# Optimizing a Trainium2 kernel written in Bass

```python
import numpy as np
import jax
import jax.numpy as jnp

def _softmax(x, axis=-1):
    return jax.nn.softmax(x, axis=axis)

def _gelu(x):
    return jax.nn.gelu(x, approximate=True)

def _silu(x):
    return jax.nn.silu(x)

def _sigmoid(x):
    return jax.nn.sigmoid(x)

def _layernorm(x, axis=-1, eps=1e-05):
    m = jnp.mean(x, axis=axis, keepdims=True)
    v = jnp.var(x, axis=axis, keepdims=True)
    return (x - m) / jnp.sqrt(v + eps)

def _scatter_add(tgt, idx, src, axis=0):
    return tgt.at[idx].add(src)

def _segment_sum(src, seg, n):
    return jax.ops.segment_sum(src, seg, n)
kernel_name = 'mk_perceiver_d2_seqx_r4_9fd466'

def setup_inputs(seed: int=0):
    np.random.seed(seed)
    _w = jnp.asarray

    def _rec_inputs():
        import jax
        import jax.numpy as jnp
        _rk = jax.random.key(seed)
        x = -0.0002928 + 1 * jax.random.normal(jax.random.fold_in(_rk, 1), (32, 32, 256), jnp.float32)
        _lenS = 32 - jax.random.randint(jax.random.fold_in(_rk, 7), (32,), 0, max(1, 32 // 4) + 1, jnp.int32)
        _lenS2 = 257 - jax.random.randint(jax.random.fold_in(_rk, 8), (32,), 0, max(1, 257 // 4) + 1, jnp.int32)
        _ctx_1024P = jax.random.normal(jax.random.fold_in(_rk, 11), (32, 16, 256), jnp.float32)
        _ctx_1024c = jax.random.dirichlet(jax.random.fold_in(_rk, 511), 0.3 * jnp.ones((16,), jnp.float32), (32, 257))
        _ctx_1024t = jnp.einsum('bsk,bkd->bsd', _ctx_1024c, _ctx_1024P)
        _ctx_1024t = _ctx_1024t * jax.lax.rsqrt(jnp.mean(jnp.square(_ctx_1024t)) + 1e-12) * 0.953939
        ctx_1024 = -1.39393e-06 + 0.999914 * (_ctx_1024t + 0.3 * jax.random.normal(jax.random.fold_in(_rk, 611), (32, 257, 256), jnp.float32))
        return (x, ctx_1024)
    x, ctx_1024 = _rec_inputs()

    def _L0_xattn_setup():
        import jax, jax.numpy as jnp
        import numpy as np
        EMBED_DIM = 256
        NUM_HEADS = 16
        HEAD_DIM = EMBED_DIM // NUM_HEADS
        B, NQ, K = (2, 512, 512)
        key = jax.random.key(seed)
        ks = jax.random.split(key, 11)
        s = 1.0 / np.sqrt(EMBED_DIM)
        return {'Q_input': jax.random.normal(ks[0], (B, NQ, EMBED_DIM), jnp.float32), 'K_input': jax.random.normal(ks[1], (B, K, EMBED_DIM), jnp.float32), 'V_input': jax.random.normal(ks[2], (B, K, EMBED_DIM), jnp.float32), 'Wq': jax.random.normal(ks[3], (EMBED_DIM, EMBED_DIM), jnp.float32) * s, 'bq': jnp.zeros((EMBED_DIM,), jnp.float32), 'Wk': jax.random.normal(ks[4], (EMBED_DIM, EMBED_DIM), jnp.float32) * s, 'bk': jnp.zeros((EMBED_DIM,), jnp.float32), 'Wv': jax.random.normal(ks[5], (EMBED_DIM, EMBED_DIM), jnp.float32) * s, 'bv': jnp.zeros((EMBED_DIM,), jnp.float32), 'Wo': jax.random.normal(ks[6], (EMBED_DIM, EMBED_DIM), jnp.float32) * s, 'bo': jnp.zeros((EMBED_DIM,), jnp.float32)}
    _L0_xattn_all = _L0_xattn_setup()
    _L0_xattn_in = {k: v for k, v in _L0_xattn_all.items() if k in ('Wq', 'bq', 'Wk', 'bk', 'Wv', 'bv', 'Wo', 'bo')}
    del _L0_xattn_all

    def _L0_attn_setup():
        import jax, jax.numpy as jnp
        import numpy as np
        B, N, D = (2, 256, 256)
        H = 4
        KD = 128
        VD = 256
        DK = KD // H
        DV = VD // H
        LR = 16
        GLN = 16.0
        EPS = 1e-05

        def _split_heads(t, h):
            b, n, hd = t.shape
            return t.reshape(b, n, h, hd // h).transpose(0, 2, 1, 3)

        def _gla_scan(q, k, v, g):
            b, h, n, dk = q.shape
            dv = v.shape[-1]
            qT = jnp.moveaxis(q, 2, 0)
            kT = jnp.moveaxis(k, 2, 0)
            vT = jnp.moveaxis(v, 2, 0)
            gT = jnp.moveaxis(g, 2, 0)

            def step(S, inp):
                qt, kt, vt, gt = inp
                S = S * jnp.exp(gt)[..., None] + kt[..., None] * vt[..., None, :]
                ot = jnp.einsum('bhk,bhkv->bhv', qt, S)
                return (S, ot)
            S0 = jnp.zeros((b, h, dk, dv), q.dtype)
            _, o = jax.lax.scan(step, S0, (qT, kT, vT, gT))
            return jnp.moveaxis(o, 0, 2)
        key = jax.random.key(seed)
        ks = jax.random.split(key, 10)
        s = 0.02
        return {'x': jax.random.normal(ks[0], (B, N, D), jnp.float32), 'Wq': jax.random.normal(ks[1], (D, KD), jnp.float32) * s, 'Wk': jax.random.normal(ks[2], (D, KD), jnp.float32) * s, 'Wv': jax.random.normal(ks[3], (D, VD), jnp.float32) * s, 'Wg': jax.random.normal(ks[4], (D, VD), jnp.float32) * s, 'Wgk1': jax.random.normal(ks[5], (D, LR), jnp.float32) * s, 'Wgk2': jax.random.normal(ks[6], (LR, KD), jnp.float32) * s, 'bgk2': jax.random.normal(ks[7], (KD,), jnp.float32) * s, 'Wout': jax.random.normal(ks[8], (VD, D), jnp.float32) * s, 'rms_w': jnp.ones((DV,), jnp.float32)}
    _L0_attn_all = _L0_attn_setup()
    _L0_attn_in = {k: v for k, v in _L0_attn_all.items() if k in ('Wq', 'Wk', 'Wv', 'Wg', 'Wgk1', 'Wgk2', 'bgk2', 'Wout', 'rms_w')}
    del _L0_attn_all

    def _L0_ffn_setup():
        import jax, jax.numpy as jnp
        import numpy as np
        D_MODEL = 256
        EXPANSION = 4
        D_HIDDEN = D_MODEL * EXPANSION
        NUM_STAGES = int(np.log2(D_HIDDEN))

        def butterfly(y, weights, dim):
            lead = y.shape[:-1]
            for stage in range(weights.shape[0]):
                s = 2 ** stage
                nb = dim // (2 * s)
                yr = y.reshape(*lead, nb, 2, s)
                a = yr[..., 0, :]
                b = yr[..., 1, :]
                w = weights[stage].reshape(nb, s, 2, 2)
                na = w[..., 0, 0] * a + w[..., 0, 1] * b
                nb2 = w[..., 1, 0] * a + w[..., 1, 1] * b
                y = jnp.stack([na, nb2], axis=-2).reshape(*lead, dim)
            return y
        key = jax.random.key(seed)
        ks = jax.random.split(key, 6)
        B, S = (4, 512)
        x = jax.random.normal(ks[0], (B, S, D_MODEL), jnp.float32)
        W_exp = jax.random.normal(ks[1], (D_MODEL, D_HIDDEN), jnp.float32) * 0.02
        b_exp = jnp.zeros((D_HIDDEN,), jnp.float32)
        up_weights = jax.random.normal(ks[2], (NUM_STAGES, D_HIDDEN // 2, 2, 2), jnp.float32) * 0.02
        up_bias = jnp.zeros((D_HIDDEN,), jnp.float32)
        down_weights = jax.random.normal(ks[3], (NUM_STAGES, D_HIDDEN // 2, 2, 2), jnp.float32) * 0.02
        W_con = jax.random.normal(ks[4], (D_HIDDEN, D_MODEL), jnp.float32) * 0.02
        b_con = jnp.zeros((D_MODEL,), jnp.float32)
        down_bias = jnp.zeros((D_MODEL,), jnp.float32)
        return dict(x=x, W_exp=W_exp, b_exp=b_exp, up_weights=up_weights, up_bias=up_bias, down_weights=down_weights, W_con=W_con, b_con=b_con, down_bias=down_bias)
    _L0_ffn_all = _L0_ffn_setup()
    _L0_ffn_in = {k: v for k, v in _L0_ffn_all.items() if k in ('W_exp', 'b_exp', 'up_weights', 'up_bias', 'down_weights', 'W_con', 'b_con', 'down_bias')}
    del _L0_ffn_all

    def _L1_xattn_setup():
        import jax, jax.numpy as jnp
        import numpy as np
        EPS = 1e-05

        def layernorm(x, g, b):
            mu = jnp.mean(x, axis=-1, keepdims=True)
            var = jnp.var(x, axis=-1, keepdims=True)
            return (x - mu) * jax.lax.rsqrt(var + EPS) * g + b
        DIM = 256
        CTX = 256
        HEADS = 12
        DHEAD = 64
        INNER = HEADS * DHEAD
        B = 4
        F = 512
        J = 256
        key = jax.random.key(seed)
        ks = jax.random.split(key, 8)
        s = lambda d: 1.0 / np.sqrt(d)
        return {'x': jax.random.normal(ks[0], (B, F, DIM), jnp.float32), 'tab_x': jax.random.normal(ks[1], (B, J, CTX), jnp.float32), 'tab_g': jnp.ones((CTX,), jnp.float32), 'tab_b': jnp.zeros((CTX,), jnp.float32), 'vid_g': jnp.ones((DIM,), jnp.float32), 'vid_b': jnp.zeros((DIM,), jnp.float32), 'Wq': jax.random.normal(ks[2], (DIM, INNER), jnp.float32) * s(DIM), 'Wk': jax.random.normal(ks[3], (CTX, INNER), jnp.float32) * s(CTX), 'Wv': jax.random.normal(ks[4], (CTX, INNER), jnp.float32) * s(CTX), 'q_g': jnp.ones((INNER,), jnp.float32), 'q_b': jnp.zeros((INNER,), jnp.float32), 'k_g': jnp.ones((INNER,), jnp.float32), 'k_b': jnp.zeros((INNER,), jnp.float32), 'Wo': jax.random.normal(ks[5], (INNER, DIM), jnp.float32) * s(INNER), 'bo': jnp.zeros((DIM,), jnp.float32)}
    _L1_xattn_all = _L1_xattn_setup()
    _L1_xattn_in = {k: v for k, v in _L1_xattn_all.items() if k in ('tab_g', 'tab_b', 'vid_g', 'vid_b', 'Wq', 'Wk', 'Wv', 'q_g', 'q_b', 'k_g', 'k_b', 'Wo', 'bo')}
    del _L1_xattn_all

    def _L1_attn_setup():
        import jax, jax.numpy as jnp
        import numpy as np
        D = 256
        H = 16
        DK = D // 2
        DV = D
        HDK = DK // H
        HDV = DV // H
        RATIO = 2
        FF = 704
        EPS = 1e-05
        ROPE_BASE = 10000.0

        def layernorm(x, w, b):
            mu = jnp.mean(x, axis=-1, keepdims=True)
            var = jnp.var(x, axis=-1, keepdims=True)
            return (x - mu) * jax.lax.rsqrt(var + EPS) * w + b

        def rope(t, cos, sin):
            half = HDK // 2
            t1, t2 = (t[..., :half], t[..., half:])
            return jnp.concatenate([t1 * cos - t2 * sin, t2 * cos + t1 * sin], axis=-1)

        def _forward(x, ln1_w, ln1_b, ln2_w, ln2_b, conv_w, Wq, Wk, Wv, Wg, Wout, router_w, w1, w3, w2):
            residual = x
            h = layernorm(x, ln1_w, ln1_b)
            h = jnp.transpose(h, (1, 0, 2))
            b, l, d = h.shape
            h_prev = jnp.pad(h, ((0, 0), (1, 0), (0, 0)))[:, :-1]
            h = jax.nn.silu(h_prev * conv_w[:, 0] + h * conv_w[:, 1])
            q = jax.nn.silu(h @ Wq)
            k = h @ Wk
            v = h @ Wv
            g = h @ Wg
            q = q.reshape(b, l, H, HDK).transpose(0, 2, 1, 3)
            k = k.reshape(b, l, H, HDK).transpose(0, 2, 1, 3)
            v = v.reshape(b, l, H, HDV).transpose(0, 2, 1, 3)
            half = HDK // 2
            inv_freq = 1.0 / ROPE_BASE ** (jnp.arange(0, half, dtype=jnp.float32) * 2.0 / HDK)
            freqs = jnp.arange(l, dtype=jnp.float32)[:, None] * inv_freq[None, :]
            cos, sin = (jnp.cos(freqs)[None, None], jnp.sin(freqs)[None, None])
            q = rope(q, cos, sin)
            k = rope(k, cos, sin)
            logits = jnp.einsum('bhld,hdr->bhlr', v, router_w)
            scores = jax.nn.softmax(logits, axis=-1)
            idx = jnp.argmax(scores, axis=-1)
            onehot = jnp.arange(RATIO) == idx[..., None]
            masked_scores = jnp.where(onehot, scores, 0.0)
            masked_indices = onehot.astype(q.dtype)
            sum_indices = jnp.cumsum(masked_indices, axis=2)
            norm_score = jnp.where(sum_indices == 0, 0.0, 1.0 / sum_indices)[..., None]
            q_exp = q[:, :, :, None, :] * masked_scores[..., None] * norm_score
            k_exp = k[:, :, :, None, :] * masked_indices[..., None]
            q_exp = q_exp.reshape(b, H, l, RATIO * HDK)
            k_exp = k_exp.reshape(b, H, l, RATIO * HDK)
            qk = jnp.einsum('bhld,bhmd->bhlm', q_exp, k_exp) * HDK ** (-0.5)
            causal = jnp.tril(jnp.ones((l, l), qk.dtype))
            qk = qk * causal
            o = jnp.einsum('bhlm,bhmd->bhld', qk, v)
            o = o.transpose(0, 2, 1, 3)
            mu = jnp.mean(o, axis=-1, keepdims=True)
            var = jnp.var(o, axis=-1, keepdims=True)
            o = (o - mu) * jax.lax.rsqrt(var + EPS)
            o = jax.nn.silu(g) * o.reshape(b, l, d)
            o = o @ Wout
            attn_out = jnp.transpose(o, (1, 0, 2)) + residual
            h2 = layernorm(attn_out, ln2_w, ln2_b)
            mlp_out = jax.nn.silu(h2 @ w1) * (h2 @ w3) @ w2
            return mlp_out + attn_out
        key = jax.random.key(seed)
        ks = jax.random.split(key, 16)
        l, b = (512, 2)
        s = 1.0 / np.sqrt(D)
        inp = {'x': jax.random.normal(ks[0], (l, b, D), jnp.float32), 'attention_mask': jnp.ones((b, l), jnp.bool_), 'ln1_w': jnp.ones((D,), jnp.float32), 'ln1_b': jnp.zeros((D,), jnp.float32), 'ln2_w': jnp.ones((D,), jnp.float32), 'ln2_b': jnp.zeros((D,), jnp.float32), 'conv_w': jax.random.normal(ks[1], (D, 2), jnp.float32) * 0.5, 'Wq': jax.random.normal(ks[2], (D, DK), jnp.float32) * s, 'Wk': jax.random.normal(ks[3], (D, DK), jnp.float32) * s, 'Wv': jax.random.normal(ks[4], (D, DV), jnp.float32) * s, 'Wg': jax.random.normal(ks[5], (D, DV), jnp.float32) * s, 'Wout': jax.random.normal(ks[6], (DV, D), jnp.float32) * s, 'router_w': jax.random.normal(ks[7], (H, HDV, RATIO), jnp.float32) * (1.0 / np.sqrt(HDV)), 'w1': jax.random.normal(ks[8], (D, FF), jnp.float32) * s, 'w3': jax.random.normal(ks[9], (D, FF), jnp.float32) * s, 'w2': jax.random.normal(ks[10], (FF, D), jnp.float32) * (1.0 / np.sqrt(FF))}
        return inp
    _L1_attn_all = _L1_attn_setup()
    _L1_attn_in = {k: v for k, v in _L1_attn_all.items() if k in ('attention_mask', 'ln1_w', 'ln1_b', 'ln2_w', 'ln2_b', 'conv_w', 'Wq', 'Wk', 'Wv', 'Wg', 'Wout', 'router_w', 'w1', 'w3', 'w2')}
    del _L1_attn_all

    def _L1_ffn_setup():
        import jax, jax.numpy as jnp
        import numpy as np
        TOP_K = 2
        key = jax.random.key(seed)
        ks = jax.random.split(key, 6)
        B, S, D, E = (8, 1024, 256, 8)
        s = 1.0 / np.sqrt(D)
        return {'x': jax.random.normal(ks[0], (B, S, D), dtype=jnp.float32), 'Wr': jax.random.normal(ks[1], (D, E), dtype=jnp.float32) * s, 'br': jnp.zeros((E,), dtype=jnp.float32), 'W1': jax.random.normal(ks[2], (E, D, D), dtype=jnp.float32) * s, 'b1': jnp.zeros((E, D), dtype=jnp.float32), 'W2': jax.random.normal(ks[3], (E, D, D), dtype=jnp.float32) * s, 'b2': jnp.zeros((E, D), dtype=jnp.float32)}
    _L1_ffn_all = _L1_ffn_setup()
    _L1_ffn_in = {k: v for k, v in _L1_ffn_all.items() if k in ('Wr', 'br', 'W1', 'b1', 'W2', 'b2')}
    del _L1_ffn_all
    return {'x': x, 'ctx_1024': ctx_1024, 'L0_xattn_Wq': _L0_xattn_in['Wq'], 'L0_xattn_bq': _L0_xattn_in['bq'], 'L0_xattn_Wk': _L0_xattn_in['Wk'], 'L0_xattn_bk': _L0_xattn_in['bk'], 'L0_xattn_Wv': _L0_xattn_in['Wv'], 'L0_xattn_bv': _L0_xattn_in['bv'], 'L0_xattn_Wo': _L0_xattn_in['Wo'], 'L0_xattn_bo': _L0_xattn_in['bo'], 'L0_attn_Wq': _L0_attn_in['Wq'], 'L0_attn_Wk': _L0_attn_in['Wk'], 'L0_attn_Wv': _L0_attn_in['Wv'], 'L0_attn_Wg': _L0_attn_in['Wg'], 'L0_attn_Wgk1': _L0_attn_in['Wgk1'], 'L0_attn_Wgk2': _L0_attn_in['Wgk2'], 'L0_attn_bgk2': _L0_attn_in['bgk2'], 'L0_attn_Wout': _L0_attn_in['Wout'], 'L0_attn_rms_w': _L0_attn_in['rms_w'], 'L0_ffn_W_exp': _L0_ffn_in['W_exp'], 'L0_ffn_b_exp': _L0_ffn_in['b_exp'], 'L0_ffn_up_weights': _L0_ffn_in['up_weights'], 'L0_ffn_up_bias': _L0_ffn_in['up_bias'], 'L0_ffn_down_weights': _L0_ffn_in['down_weights'], 'L0_ffn_W_con': _L0_ffn_in['W_con'], 'L0_ffn_b_con': _L0_ffn_in['b_con'], 'L0_ffn_down_bias': _L0_ffn_in['down_bias'], 'L1_xattn_tab_g': _L1_xattn_in['tab_g'], 'L1_xattn_tab_b': _L1_xattn_in['tab_b'], 'L1_xattn_vid_g': _L1_xattn_in['vid_g'], 'L1_xattn_vid_b': _L1_xattn_in['vid_b'], 'L1_xattn_Wq': _L1_xattn_in['Wq'], 'L1_xattn_Wk': _L1_xattn_in['Wk'], 'L1_xattn_Wv': _L1_xattn_in['Wv'], 'L1_xattn_q_g': _L1_xattn_in['q_g'], 'L1_xattn_q_b': _L1_xattn_in['q_b'], 'L1_xattn_k_g': _L1_xattn_in['k_g'], 'L1_xattn_k_b': _L1_xattn_in['k_b'], 'L1_xattn_Wo': _L1_xattn_in['Wo'], 'L1_xattn_bo': _L1_xattn_in['bo'], 'L1_attn_attention_mask': _L1_attn_in['attention_mask'], 'L1_attn_ln1_w': _L1_attn_in['ln1_w'], 'L1_attn_ln1_b': _L1_attn_in['ln1_b'], 'L1_attn_ln2_w': _L1_attn_in['ln2_w'], 'L1_attn_ln2_b': _L1_attn_in['ln2_b'], 'L1_attn_conv_w': _L1_attn_in['conv_w'], 'L1_attn_Wq': _L1_attn_in['Wq'], 'L1_attn_Wk': _L1_attn_in['Wk'], 'L1_attn_Wv': _L1_attn_in['Wv'], 'L1_attn_Wg': _L1_attn_in['Wg'], 'L1_attn_Wout': _L1_attn_in['Wout'], 'L1_attn_router_w': _L1_attn_in['router_w'], 'L1_attn_w1': _L1_attn_in['w1'], 'L1_attn_w3': _L1_attn_in['w3'], 'L1_attn_w2': _L1_attn_in['w2'], 'L1_ffn_Wr': _L1_ffn_in['Wr'], 'L1_ffn_br': _L1_ffn_in['br'], 'L1_ffn_W1': _L1_ffn_in['W1'], 'L1_ffn_b1': _L1_ffn_in['b1'], 'L1_ffn_W2': _L1_ffn_in['W2'], 'L1_ffn_b2': _L1_ffn_in['b2']}

def reference(x, ctx_1024, L0_xattn_Wq, L0_xattn_bq, L0_xattn_Wk, L0_xattn_bk, L0_xattn_Wv, L0_xattn_bv, L0_xattn_Wo, L0_xattn_bo, L0_attn_Wq, L0_attn_Wk, L0_attn_Wv, L0_attn_Wg, L0_attn_Wgk1, L0_attn_Wgk2, L0_attn_bgk2, L0_attn_Wout, L0_attn_rms_w, L0_ffn_W_exp, L0_ffn_b_exp, L0_ffn_up_weights, L0_ffn_up_bias, L0_ffn_down_weights, L0_ffn_W_con, L0_ffn_b_con, L0_ffn_down_bias, L1_xattn_tab_g, L1_xattn_tab_b, L1_xattn_vid_g, L1_xattn_vid_b, L1_xattn_Wq, L1_xattn_Wk, L1_xattn_Wv, L1_xattn_q_g, L1_xattn_q_b, L1_xattn_k_g, L1_xattn_k_b, L1_xattn_Wo, L1_xattn_bo, L1_attn_attention_mask, L1_attn_ln1_w, L1_attn_ln1_b, L1_attn_ln2_w, L1_attn_ln2_b, L1_attn_conv_w, L1_attn_Wq, L1_attn_Wk, L1_attn_Wv, L1_attn_Wg, L1_attn_Wout, L1_attn_router_w, L1_attn_w1, L1_attn_w3, L1_attn_w2, L1_ffn_Wr, L1_ffn_br, L1_ffn_W1, L1_ffn_b1, L1_ffn_W2, L1_ffn_b2):
    import jax
    import jax.numpy as jnp

    def _L0_xattn_ref(Q_input, K_input, V_input, Wq, bq, Wk, bk, Wv, bv, Wo, bo):
        import jax, jax.numpy as jnp
        import numpy as np
        EMBED_DIM = 256
        NUM_HEADS = 16
        HEAD_DIM = EMBED_DIM // NUM_HEADS
        B, NQ, K = (2, 512, 512)
        b, n_q, _ = Q_input.shape
        k = K_input.shape[1]
        Q = Q_input @ Wq.T + bq
        Kp = K_input @ Wk.T + bk
        V = V_input @ Wv.T + bv
        Q = Q.reshape(b, n_q, NUM_HEADS, HEAD_DIM).transpose(0, 2, 1, 3)
        Kp = Kp.reshape(b, k, NUM_HEADS, HEAD_DIM).transpose(0, 2, 1, 3)
        V = V.reshape(b, k, NUM_HEADS, HEAD_DIM).transpose(0, 2, 1, 3)
        scores = jnp.einsum('bhqd,bhkd->bhqk', Q, Kp) / jnp.sqrt(jnp.float32(HEAD_DIM))
        weights = jax.nn.softmax(scores, axis=-1)
        attn = jnp.einsum('bhqk,bhkd->bhqd', weights, V)
        attn = attn.transpose(0, 2, 1, 3).reshape(b, n_q, EMBED_DIM)
        return attn @ Wo.T + bo

    def _L0_attn_ref(x, Wq, Wk, Wv, Wg, Wgk1, Wgk2, bgk2, Wout, rms_w):
        import jax, jax.numpy as jnp
        import numpy as np
        B, N, D = (2, 256, 256)
        H = 4
        KD = 128
        VD = 256
        DK = KD // H
        DV = VD // H
        LR = 16
        GLN = 16.0
        EPS = 1e-05

        def _split_heads(t, h):
            b, n, hd = t.shape
            return t.reshape(b, n, h, hd // h).transpose(0, 2, 1, 3)

        def _gla_scan(q, k, v, g):
            b, h, n, dk = q.shape
            dv = v.shape[-1]
            qT = jnp.moveaxis(q, 2, 0)
            kT = jnp.moveaxis(k, 2, 0)
            vT = jnp.moveaxis(v, 2, 0)
            gT = jnp.moveaxis(g, 2, 0)

            def step(S, inp):
                qt, kt, vt, gt = inp
                S = S * jnp.exp(gt)[..., None] + kt[..., None] * vt[..., None, :]
                ot = jnp.einsum('bhk,bhkv->bhv', qt, S)
                return (S, ot)
            S0 = jnp.zeros((b, h, dk, dv), q.dtype)
            _, o = jax.lax.scan(step, S0, (qT, kT, vT, gT))
            return jnp.moveaxis(o, 0, 2)
        q = _split_heads(x @ Wq, H)
        k = _split_heads(x @ Wk, H)
        v = _split_heads(x @ Wv, H)
        g = jax.nn.log_sigmoid(x @ Wgk1 @ Wgk2 + bgk2) / GLN
        g = jnp.maximum(g, -3.0)
        g = _split_heads(g, H)
        o = _gla_scan(q, k, v, g)
        o = o.transpose(0, 2, 1, 3)
        o = o * jax.lax.rsqrt(jnp.mean(o * o, axis=-1, keepdims=True) + EPS) * rms_w
        o = o.reshape(o.shape[0], o.shape[1], VD)
        o = o * jax.nn.silu(x @ Wg)
        return o @ Wout

    def _L0_ffn_ref(x, W_exp, b_exp, up_weights, up_bias, down_weights, W_con, b_con, down_bias):
        import jax, jax.numpy as jnp
        import numpy as np
        D_MODEL = 256
        EXPANSION = 4
        D_HIDDEN = D_MODEL * EXPANSION
        NUM_STAGES = int(np.log2(D_HIDDEN))

        def butterfly(y, weights, dim):
            lead = y.shape[:-1]
            for stage in range(weights.shape[0]):
                s = 2 ** stage
                nb = dim // (2 * s)
                yr = y.reshape(*lead, nb, 2, s)
                a = yr[..., 0, :]
                b = yr[..., 1, :]
                w = weights[stage].reshape(nb, s, 2, 2)
                na = w[..., 0, 0] * a + w[..., 0, 1] * b
                nb2 = w[..., 1, 0] * a + w[..., 1, 1] * b
                y = jnp.stack([na, nb2], axis=-2).reshape(*lead, dim)
            return y
        h = jnp.einsum('bsd,dh->bsh', x, W_exp) + b_exp
        h = butterfly(h, up_weights, D_HIDDEN)
        h = jax.nn.gelu(h + up_bias, approximate=False)
        h = butterfly(h, down_weights, D_HIDDEN)
        y = jnp.einsum('bsh,hd->bsd', h, W_con) + b_con
        return y + down_bias

    def _L1_xattn_ref(x, tab_x, tab_g, tab_b, vid_g, vid_b, Wq, Wk, Wv, q_g, q_b, k_g, k_b, Wo, bo):
        import jax, jax.numpy as jnp
        import numpy as np
        EPS = 1e-05

        def layernorm(x, g, b):
            mu = jnp.mean(x, axis=-1, keepdims=True)
            var = jnp.var(x, axis=-1, keepdims=True)
            return (x - mu) * jax.lax.rsqrt(var + EPS) * g + b
        DIM = 256
        CTX = 256
        HEADS = 12
        DHEAD = 64
        INNER = HEADS * DHEAD
        B = 4
        F = 512
        J = 256
        scale = DHEAD ** (-0.5)
        kv_in = layernorm(tab_x, tab_g, tab_b)
        q = layernorm(layernorm(x, vid_g, vid_b) @ Wq, q_g, q_b)
        k = layernorm(kv_in @ Wk, k_g, k_b)
        v = kv_in @ Wv
        split = lambda t: t.reshape(t.shape[0], t.shape[1], HEADS, DHEAD).transpose(0, 2, 1, 3)
        q, k, v = (split(q) * scale, split(k), split(v))
        sim = jnp.einsum('bhid,bhjd->bhij', q, k)
        attn = jax.nn.softmax(sim, axis=-1)
        out = jnp.einsum('bhij,bhjd->bhid', attn, v)
        out = out.transpose(0, 2, 1, 3).reshape(x.shape[0], x.shape[1], INNER)
        return out @ Wo + bo

    def _L1_attn_ref(x, attention_mask, ln1_w, ln1_b, ln2_w, ln2_b, conv_w, Wq, Wk, Wv, Wg, Wout, router_w, w1, w3, w2):
        import jax, jax.numpy as jnp
        import numpy as np
        D = 256
        H = 16
        DK = D // 2
        DV = D
        HDK = DK // H
        HDV = DV // H
        RATIO = 2
        FF = 704
        EPS = 1e-05
        ROPE_BASE = 10000.0

        def layernorm(x, w, b):
            mu = jnp.mean(x, axis=-1, keepdims=True)
            var = jnp.var(x, axis=-1, keepdims=True)
            return (x - mu) * jax.lax.rsqrt(var + EPS) * w + b

        def rope(t, cos, sin):
            half = HDK // 2
            t1, t2 = (t[..., :half], t[..., half:])
            return jnp.concatenate([t1 * cos - t2 * sin, t2 * cos + t1 * sin], axis=-1)

        def _forward(x, ln1_w, ln1_b, ln2_w, ln2_b, conv_w, Wq, Wk, Wv, Wg, Wout, router_w, w1, w3, w2):
            residual = x
            h = layernorm(x, ln1_w, ln1_b)
            h = jnp.transpose(h, (1, 0, 2))
            b, l, d = h.shape
            h_prev = jnp.pad(h, ((0, 0), (1, 0), (0, 0)))[:, :-1]
            h = jax.nn.silu(h_prev * conv_w[:, 0] + h * conv_w[:, 1])
            q = jax.nn.silu(h @ Wq)
            k = h @ Wk
            v = h @ Wv
            g = h @ Wg
            q = q.reshape(b, l, H, HDK).transpose(0, 2, 1, 3)
            k = k.reshape(b, l, H, HDK).transpose(0, 2, 1, 3)
            v = v.reshape(b, l, H, HDV).transpose(0, 2, 1, 3)
            half = HDK // 2
            inv_freq = 1.0 / ROPE_BASE ** (jnp.arange(0, half, dtype=jnp.float32) * 2.0 / HDK)
            freqs = jnp.arange(l, dtype=jnp.float32)[:, None] * inv_freq[None, :]
            cos, sin = (jnp.cos(freqs)[None, None], jnp.sin(freqs)[None, None])
            q = rope(q, cos, sin)
            k = rope(k, cos, sin)
            logits = jnp.einsum('bhld,hdr->bhlr', v, router_w)
            scores = jax.nn.softmax(logits, axis=-1)
            idx = jnp.argmax(scores, axis=-1)
            onehot = jnp.arange(RATIO) == idx[..., None]
            masked_scores = jnp.where(onehot, scores, 0.0)
            masked_indices = onehot.astype(q.dtype)
            sum_indices = jnp.cumsum(masked_indices, axis=2)
            norm_score = jnp.where(sum_indices == 0, 0.0, 1.0 / sum_indices)[..., None]
            q_exp = q[:, :, :, None, :] * masked_scores[..., None] * norm_score
            k_exp = k[:, :, :, None, :] * masked_indices[..., None]
            q_exp = q_exp.reshape(b, H, l, RATIO * HDK)
            k_exp = k_exp.reshape(b, H, l, RATIO * HDK)
            qk = jnp.einsum('bhld,bhmd->bhlm', q_exp, k_exp) * HDK ** (-0.5)
            causal = jnp.tril(jnp.ones((l, l), qk.dtype))
            qk = qk * causal
            o = jnp.einsum('bhlm,bhmd->bhld', qk, v)
            o = o.transpose(0, 2, 1, 3)
            mu = jnp.mean(o, axis=-1, keepdims=True)
            var = jnp.var(o, axis=-1, keepdims=True)
            o = (o - mu) * jax.lax.rsqrt(var + EPS)
            o = jax.nn.silu(g) * o.reshape(b, l, d)
            o = o @ Wout
            attn_out = jnp.transpose(o, (1, 0, 2)) + residual
            h2 = layernorm(attn_out, ln2_w, ln2_b)
            mlp_out = jax.nn.silu(h2 @ w1) * (h2 @ w3) @ w2
            return mlp_out + attn_out
        del attention_mask
        return _forward(x, ln1_w, ln1_b, ln2_w, ln2_b, conv_w, Wq, Wk, Wv, Wg, Wout, router_w, w1, w3, w2)

    def _L1_ffn_ref(x, Wr, br, W1, b1, W2, b2):
        import jax, jax.numpy as jnp
        import numpy as np
        TOP_K = 2
        k = TOP_K
        scores0 = x[:, 0, :] @ Wr + br
        _, idx = jax.lax.top_k(scores0, k)
        W1g, b1g = (W1[idx], b1[idx])
        W2g, b2g = (W2[idx], b2[idx])
        h = jnp.einsum('bsd,bkde->bkse', x, W1g) + b1g[:, :, None, :]
        h = jax.nn.gelu(h, approximate=False)
        o = jnp.einsum('bkse,bkef->bksf', h, W2g) + b2g[:, :, None, :]
        return jnp.sum(o, axis=1) / k
    x = x + _L0_xattn_ref(_layernorm(x, axis=-1), ctx_1024, ctx_1024, L0_xattn_Wq, L0_xattn_bq, L0_xattn_Wk, L0_xattn_bk, L0_xattn_Wv, L0_xattn_bv, L0_xattn_Wo, L0_xattn_bo)
    x = x + _L0_attn_ref(_layernorm(x, axis=-1), L0_attn_Wq, L0_attn_Wk, L0_attn_Wv, L0_attn_Wg, L0_attn_Wgk1, L0_attn_Wgk2, L0_attn_bgk2, L0_attn_Wout, L0_attn_rms_w)
    x = x + _L0_ffn_ref(_layernorm(x, axis=-1), L0_ffn_W_exp, L0_ffn_b_exp, L0_ffn_up_weights, L0_ffn_up_bias, L0_ffn_down_weights, L0_ffn_W_con, L0_ffn_b_con, L0_ffn_down_bias)
    x = x + _L1_xattn_ref(_layernorm(x, axis=-1), ctx_1024, L1_xattn_tab_g, L1_xattn_tab_b, L1_xattn_vid_g, L1_xattn_vid_b, L1_xattn_Wq, L1_xattn_Wk, L1_xattn_Wv, L1_xattn_q_g, L1_xattn_q_b, L1_xattn_k_g, L1_xattn_k_b, L1_xattn_Wo, L1_xattn_bo)
    x = x + _L1_attn_ref(_layernorm(x, axis=-1), L1_attn_attention_mask, L1_attn_ln1_w, L1_attn_ln1_b, L1_attn_ln2_w, L1_attn_ln2_b, L1_attn_conv_w, L1_attn_Wq, L1_attn_Wk, L1_attn_Wv, L1_attn_Wg, L1_attn_Wout, L1_attn_router_w, L1_attn_w1, L1_attn_w3, L1_attn_w2)
    x = x + _L1_ffn_ref(_layernorm(x, axis=-1), L1_ffn_Wr, L1_ffn_br, L1_ffn_W1, L1_ffn_b1, L1_ffn_W2, L1_ffn_b2)
    return x

_drawn_inputs = setup_inputs


def setup_inputs(seed=0):
    import zlib

    import numpy as np

    out = dict(_drawn_inputs(seed))
    spreads = {'L0_xattn_bq': (0.0, 0.321),
     'L0_xattn_bk': (0.0, 2.0),
     'L0_xattn_bv': (0.0, 0.1),
     'L0_xattn_bo': (0.0, 0.1),
     'L0_attn_rms_w': (1.0, 0.6),
     'L0_ffn_b_exp': (0.0, 0.1),
     'L0_ffn_up_bias': (0.0, 0.1),
     'L0_ffn_b_con': (0.0, 0.1),
     'L0_ffn_down_bias': (0.0, 0.1),
     'L1_xattn_tab_g': (1.0, 0.2),
     'L1_xattn_tab_b': (0.0, 0.1),
     'L1_xattn_vid_g': (1.0, 0.2),
     'L1_xattn_vid_b': (0.0, 0.349),
     'L1_xattn_q_g': (1.0, 0.2),
     'L1_xattn_q_b': (0.0, 0.1),
     'L1_xattn_k_g': (1.0, 0.2),
     'L1_xattn_k_b': (0.0, 2.0),
     'L1_xattn_bo': (0.0, 0.1),
     'L1_attn_ln1_w': (1.0, 0.2),
     'L1_attn_ln1_b': (0.0, 0.1),
     'L1_attn_ln2_w': (1.0, 0.2),
     'L1_attn_ln2_b': (0.0, 0.1),
     'L1_ffn_br': (0.0, 0.1),
     'L1_ffn_b1': (0.0, 0.39),
     'L1_ffn_b2': (0.0, 0.276)}
    factors = {'L0_attn_Wgk1': 28.327, 'L0_attn_Wgk2': 28.506, 'L0_attn_bgk2': 64.0}
    for name, (base, spread) in spreads.items():
        noise = np.random.default_rng([zlib.crc32(name.encode()), seed]).standard_normal(out[name].shape)
        drawn = base * np.exp(spread * noise) if base else spread * noise
        out[name] = jnp.asarray(drawn.astype(out[name].dtype))
    for name, factor in factors.items():
        out[name] = (out[name] * factor).astype(out[name].dtype)
    return out
```

```python
from contextlib import ExitStack

import numpy as np
import concourse.bass as bass
from concourse import mybir

F32 = mybir.dt.float32
I32 = mybir.dt.int32
ALU = mybir.AluOpType
ACT = mybir.ActivationFunctionType
AX_X = mybir.AxisListType.X

P = 128
NB, S, D = 32, 32, 256
KEYS = 257
TB = P // S
NT = NB // TB
KC = D // P
EPS = 1e-5


class Steps:

    def __init__(self, sem, names):
        self.sem = sem
        self.names = names.split()
        self.per_turn = len(self.names)
        assert len(set(self.names)) == self.per_turn, names

    def first_turn(self, eng):
        eng.sem_inc(self.sem, self.per_turn)

    def after(self, name, turn):
        return (turn + 1) * self.per_turn + (self.names.index(name) + 1)


def bc(ap, pos, n):
    a = ap.unsqueeze(pos)
    return a.to_broadcast([*a.shape[:pos], n, *a.shape[pos + 1:]])


FF, FFP = 704, 768
NE = 8
WEIGHTS_L1 = {
    "L1_attn_Wqk": (D, D), "L1_attn_Wv": (D, D), "L1_attn_Wg": (D, D), "L1_attn_Wout": (D, D),
    "L1_attn_w1": (D, FFP), "L1_attn_w3": (D, FFP), "L1_attn_w2": (FFP, D),
}
WEIGHTS_CROSS = {
    "L1_xattn_Wq": (D, 768), "L1_xattn_Wk": (D, 768), "L1_xattn_Wv": (D, 768), "L1_xattn_Wo": (768, D),
}
WEIGHTS_L0 = {
    "L0_xattn_Wq": (D, D), "L0_xattn_Wk": (D, D), "L0_xattn_Wv": (D, D), "L0_xattn_Wo": (D, D),
    "L0_attn_Wq": (D, P), "L0_attn_Wk": (D, P), "L0_attn_Wv": (D, D), "L0_attn_Wg": (D, D),
    "L0_attn_Wgk1": (D, 16), "L0_attn_Wout": (D, D),
}
COLS = {
    "L0_xattn_bq": D, "L0_xattn_bk": D, "L0_xattn_bv": D, "L0_attn_bgk2": P,
    "L1_xattn_tab_g": D, "L1_xattn_tab_b": D, "L1_xattn_vid_g": D, "L1_xattn_vid_b": D,
    "L1_xattn_q_g": 768, "L1_xattn_q_b": 768, "L1_xattn_k_g": 768, "L1_xattn_k_b": 768,
    "L1_attn_ln1_w": D, "L1_attn_ln1_b": D, "L1_attn_ln2_w": D, "L1_attn_ln2_b": D, "conv0": D, "conv1": D,
    "L1_ffn_b1": NE * D,
}
ROWS = {
    "L0_xattn_bo": D, "L0_ffn_up_bias": 1024, "L0_ffn_b_con": D, "L0_ffn_down_bias": D, "L1_xattn_bo": D, "L1_ffn_br": NE,
}
REPEATED = {
    "L0_attn_rms_w": 64, "L1_xattn_tab_g": D, "L1_attn_router_w": 512,
}
MASKS = {"ident": P, "fold": S, "hmask": 4, "qmask": 8, "causal": P, "spread": 4 * P, "half": 2, "cos": 4, "sin": 4, "earlier": NE * NE}
HT = 4
HN = HT * P


def offsets(sizes):
    at, out = 0, {}
    for name, n in sizes.items():
        out[name] = at
        at += n
    return out, at


COL_AT, COL_N = offsets({n: k // P for n, k in COLS.items()})
ROW_AT, ROW_N = offsets(ROWS)
REP_AT, REP_N = offsets(REPEATED)
MASK_AT, MASK_N = offsets(MASKS)


class Core:

    def __init__(self, nc, ctx, dram):
        self.nc, self.ctx, self.dram = nc, ctx, dram
        self.PS = ctx.enter_context(nc.psum_tensor("banks", [P, 8, 512], F32))
        self.bank = [self.PS[:, n, :] for n in range(8)]
        self.waited = self.sem("waited")
        self.X = self.sb("x_sb", [P, NT, D])
        self.masks = self.sb("masks_sb", [P, MASK_N])
        self.eps, self.mhalf, self.ones = self.sb("eps", [P, 16]), self.sb("mhalf", [P, 16]), self.sb("ones", [1, P])
        self.fold, self.hmask, self.qmask = self.mask("fold"), self.mask("hmask"), self.mask("qmask")
        self.cols_sb, self.rows_sb = self.sb("cols_sb", [P, COL_N]), self.sb("rows_sb", [1, ROW_N])
        self.rep_sb = self.sb("repeated_sb", [P, REP_N])
        self.w, self.loads, self.loaded = {}, {}, {}
        self.weights(WEIGHTS_L1, ctx)
        self.cross, self.l0 = ExitStack(), ExitStack()
        self.weights(WEIGHTS_CROSS, self.cross)
        self.weights(WEIGHTS_L0, self.l0)
        self.W1e, self.W2eT = self.sb("W1e", [P, KC + 1, 1024], self.l0), self.sb("W2eT", [P, KC, 1024], self.l0)
        self.ffn_bias = self.sb("ffn_bias", [1, D], self.l0)
        self.narrow = self.sb("narrow", [16, P], self.l0)
        early = {"cols": (self.cols_sb[:, :], dram["cols"]), "rows": (self.rows_sb[:, :], dram["rows"]),
                 "repeated": (self.rep_sb[:, :], dram["repeated"]),
                 "L0_attn_Wgk2": (self.narrow[:, :], dram["L0_attn_Wgk2"])}
        late = [n for n in self.loads if not n.startswith("L0")]
        self.loads = {**early, **{n: self.loads[n] for n in self.loads if n not in late}, **{n: self.loads[n] for n in reversed(late)}}
        self.loaded.update({name: self.sem(name + "_in") for name in ["x", "masks", *early]})

    def weights(self, shapes, ctx):
        for name, (rows, columns) in shapes.items():
            self.w[name] = self.sb(name + "_sb", [P, rows // P, columns], ctx)
            self.loads[name] = (self.w[name][:, :, :], self.dram[name].rearrange("(c p) n -> p c n", p=P))
            self.loaded[name] = self.sem(name + "_in")

    def sb(self, name, shape, ctx=None):
        return (ctx or self.ctx).enter_context(self.nc.sbuf_tensor(name, shape, F32))

    def sem(self, name, ctx=None):
        return (ctx or self.ctx).enter_context(self.nc.semaphore(name))

    def steps(self, ctx, name, names):
        return Steps(self.sem(name + "_done", ctx), names)

    def mask(self, name):
        return self.masks[:, MASK_AT[name]:MASK_AT[name] + MASKS[name]]

    def ident(self):
        return self.mask("ident")

    def col(self, name, m):
        return self.cols_sb[:, COL_AT[name] + m:COL_AT[name] + m + 1]

    def cols2(self, name):
        return self.cols_sb[:, COL_AT[name]:COL_AT[name] + COLS[name] // P]

    def rep(self, name):
        return self.rep_sb[:, REP_AT[name]:REP_AT[name] + REPEATED[name]]

    def row(self, name):
        return self.rows_sb[:, ROW_AT[name]:ROW_AT[name] + ROWS[name]]


def norm_half(c, ve, dve, pool, pre, i, src, dst, st, mv, rs):
    for t in range(HT):
        op = c.nc.vector.bn_stats(st[:, t, :], src(t))
    op.then_inc(dve.sem, 1)
    ve.wait_ge(dve.sem, dve.after(pre + "stats", i))
    ve.sem_inc(c.waited)
    for t in range(HT):
        op = c.nc.vector.bn_aggr(mv[:, t, :], st[:, t, :])
    op.then_inc(dve.sem, 1)
    ve.wait_ge(pool.sem, pool.after(pre + "rstd", i))
    for t in range(HT):
        op = c.nc.vector.tensor_scalar(dst(t), src(t), mv[:, t, 0:1], rs[:, HT + t:HT + t + 1], ALU.subtract, ALU.mult)
    op.then_inc(dve.sem, 1)


def rstd_half(c, gp, pool, dve, pre, i, mv, rs):
    gp.wait_ge(dve.sem, dve.after(pre + "moments", i))
    c.nc.gpsimd.tensor_tensor(rs[:, 0:HT], mv[:, :, 1:2].rearrange("p t o -> p (t o)"), c.eps[:, 0:HT], ALU.add).then_inc(pool.sem, 1)
    gp.wait_ge(pool.sem, pool.after(pre + "vareps", i))
    c.nc.gpsimd.tensor_tensor(rs[:, HT:2 * HT], rs[:, 0:HT], c.mhalf[:, 0:HT], ALU.pow).then_inc(pool.sem, 1)


STAGES_BF = 10
F0 = 2 ** STAGES_BF


class Butterflies:

    def __init__(self, c, ctx):
        self.c = c
        self.t = [c.sb(f"bf_t{n}", [P, 3, F0 // 2], ctx) for n in range(2)]
        self.wts = [c.sb(f"bf_wts{n}", [P, 4, F0 // 2], ctx) for n in range(2)]
        self.wts_in = [c.sem(f"bf_wts_in{n}", ctx) for n in range(2)]
        self.bias_in = c.sem("bf_bias_in", ctx)
        self.up_in, self.zero, self.done = c.sem("bf_up_in", ctx), c.sem("bf_zero", ctx), c.sem("bf_done", ctx)

    def load_first(self, sp):
        c = self.c
        sp.dma_start(c.W1e[:, 0:KC, :], c.dram["W_exp"].rearrange("(c p) f -> p c f", p=P)).then_inc(self.up_in, 16)
        sp.dma_start(c.W2eT[:, :, :], c.dram["W_conT"].rearrange("(c p) f -> p c f", p=P)).then_inc(self.up_in, 16)

    def load_weights(self, eng, n):
        eng.dma_start(self.wts[n % 2][:, :, :], self.c.dram["bf_weights"][n:n + 1].to_broadcast([P, 4, F0 // 2])).then_inc(self.wts_in[n % 2], 16)


def fold_butterflies(c, gp, bf):
    nc = c.nc
    nc.gpsimd.memset(c.W1e[:, KC, :], 0.0).then_inc(bf.zero, 1)
    gp.wait_ge(bf.zero, 1)
    gp.dma_start(c.W1e[0:1, KC, :], c.dram["b_exp"]).then_inc(bf.bias_in, 16)
    for n in range(2):
        bf.load_weights(gp, n)
    gp.wait_ge(bf.bias_in, 16)
    gp.wait_ge(bf.up_in, 32)
    n = 0
    for down in range(2):
        for stage in (range(STAGES_BF) if not down else reversed(range(STAGES_BF))):
            y = c.W2eT if down else c.W1e
            chunks = y.shape[1]
            s, nb = 2 ** stage, F0 // 2 ** (stage + 1)
            yr = y[:, :, :].rearrange("p c (n two s) -> p c n two s", two=2, s=s)
            a, b = yr[:, :, :, 0, :], yr[:, :, :, 1, :]
            w = bf.wts[n % 2]
            wt = [bc(w[:, q, :].rearrange("p (n s) -> p n s", s=s), 1, chunks) for q in ((0, 2, 1, 3) if down else (0, 1, 2, 3))]
            t = [x[:, 0:chunks, :].rearrange("p c (n s) -> p c n s", s=s) for x in bf.t]
            gp.wait_ge(bf.wts_in[n % 2], 16 * (n // 2 + 1))
            nc.gpsimd.tensor_tensor(t[0], a, wt[0], ALU.mult)
            nc.gpsimd.tensor_tensor(t[1], b, wt[1], ALU.mult).then_inc(bf.done, 1)
            gp.wait_ge(bf.done, 4 * n + 1)
            nc.gpsimd.tensor_tensor(a, a, wt[2], ALU.mult)
            nc.gpsimd.tensor_tensor(b, b, wt[3], ALU.mult).then_inc(bf.done, 1)
            gp.wait_ge(bf.done, 4 * n + 2)
            if n + 2 < 2 * STAGES_BF:
                bf.load_weights(gp, n + 2)
            nc.gpsimd.tensor_tensor(b, a, b, ALU.add).then_inc(bf.done, 1)
            gp.wait_ge(bf.done, 4 * n + 3)
            nc.gpsimd.tensor_tensor(a, t[0], t[1], ALU.add).then_inc(bf.done, 1)
            gp.wait_ge(bf.done, 4 * n + 4)
            n += 1
    gp.wait_ge(c.loaded["rows"], 16)
    nc.gpsimd.tensor_tensor(c.W1e[0:1, KC, :], c.W1e[0:1, KC, :], c.row("L0_ffn_up_bias"), ALU.add)
    nc.gpsimd.tensor_tensor(c.ffn_bias[:, :], c.row("L0_ffn_b_con"), c.row("L0_ffn_down_bias"), ALU.add)


def stage_l0_cross(c):
    nc = c.nc
    with ExitStack() as ctx:
        sb = lambda name, shape: c.sb(name, shape, ctx)
        xn, xnT = sb("l0_xn", [P, NT, D]), sb("l0_xnT", [P, KC, NT * P])
        st, mv, rs = sb("l0_st", [P, NT, 6]), sb("l0_mv", [P, NT, 2]), sb("l0_rs", [P, 2 * NT])
        qT = xn[:, :, :].rearrange("p (m t) d -> p m (t d)", m=KC)
        qblk = sb("l0_qblk", [P, KC, TB, 8, S])
        ctxT = [sb(f"l0_ctxT{j}", [P, KC, KEYS]) for j in range(TB)]
        kT = [sb(f"l0_kT{n}", [P, KC, KEYS]) for n in range(2)]
        v = [sb(f"l0_v{n}", [P, 2, D]) for n in range(2)]
        lastT = sb("l0_lastT", [P, KC, NB])
        vlast = sb("l0_vlast", [TB, NT, D])
        probs = [sb(f"l0_probs{n}", [P, 4, KEYS]) for n in range(2)]
        nmax = [sb(f"l0_nmax{n}", [P, 4]) for n in range(2)]
        total = [sb(f"l0_total{n}", [P, 4]) for n in range(2)]
        plast = [sb(f"l0_plast{j}", [P, 4, TB]) for j in range(TB)]
        probsT = sb("l0_probsT", [P, 2, 512])
        plastT = sb("l0_plastT", [TB, 512])
        rinv, rmask = sb("l0_rinv", [P, 4]), sb("l0_rmask", [P, 4, 4])
        ao = sb("l0_ao", [P, 4, 4, 16])
        aT = sb("l0_aT", [P, KC, P])
        ctx_in = [c.sem(f"l0_ctx_in{j}", ctx) for j in range(TB)]
        last_in, ready = c.sem("l0_last_in", ctx), c.sem("l0_ready", ctx)
        vlast_done = c.sem("l0_vlast_done", ctx)
        J = range(TB)
        each = lambda names: " ".join(f"{n}{j}" for j in J for n in names.split())
        pe = c.steps(ctx, "l0_pe", "kT0 v0 sA0 " + " ".join(
            (f"kT{j+1} " if j < 3 else "") + f"sB{j} " + (f"v{j+1} " if j < 3 else "") + f"pT{j} "
            + (f"sA{j+1} " if j < 3 else "") + f"av{j} fold{j}" for j in J) + " out")
        dve = c.steps(ctx, "l0_dve", "qb v0 maxA0 " + " ".join(
            f"maxB{j} " + (f"v{j+1} " if j < 3 else "") + f"plast{j} rinv{j} rmask{j} pT{j} plT{j} "
            + (f"maxA{j+1} " if j < 3 else "") + f"ao{j} aT{j}" for j in J) + " res")
        act = c.steps(ctx, "l0_act", "kTa0 kTb0 e00 e10 " + " ".join(
            (f"kTa{j+1} kTb{j+1} " if j < 3 else "") + f"e2{j} e3{j} pT{j}"
            + (f" e0{j+1} e1{j+1}" if j < 3 else "") for j in J))
        pro = {n: c.sem("l0_" + n, ctx) for n in ("stats", "moments", "rstd", "norm", "xT", "xT_out", "qT", "qT_out")}
        B = c.bank
        ident = c.ident()
        ctx_bf = Butterflies(c, ctx)

        with nc.Block() as block:
            @block.sync
            def _(sp):
                sp.dma_start(c.masks[:, :], c.dram["masks"]).then_inc(c.loaded["masks"], 16)
                sp.dma_start(c.X[:, :, :], c.dram["x"]).then_inc(c.loaded["x"], 16)
                sp.dma_start(lastT[:, :, :], c.dram["ctx_lastT"].rearrange("(c p) b -> p c b", p=P)).then_inc(last_in, 16)
                for name in c.loads:
                    sp.dma_start(*c.loads[name]).then_inc(c.loaded[name], 16)
                    if name == "L0_xattn_Wo":
                        break
                ctx_bf.load_first(sp)
                with sp.Fori(0, NT) as i:
                    for j in J:
                        sp.wait_ge(pe.sem, pe.after(f"v{j}", i - 1))
                        sp.dma_start(ctxT[j][:, :, :], c.dram["ctxT"][bass.ds(i * TB + j, 1)].rearrange(
                            "b (c p) k -> p (b c) k", p=P)).then_inc(ctx_in[j], 16)
                rest = False
                for name in c.loads:
                    if rest:
                        sp.dma_start(*c.loads[name]).then_inc(c.loaded[name], 16)
                    rest = rest or name == "L0_xattn_Wo"

            @block.gpsimd
            def _(gp):
                nc.gpsimd.memset(c.eps[:, :], EPS).then_inc(ready, 1)
                nc.gpsimd.memset(c.mhalf[:, :], -0.5).then_inc(ready, 1)
                nc.gpsimd.memset(c.ones[:, :], 1.0).then_inc(ready, 1)
                for j in J:
                    nc.gpsimd.memset(plast[j][:, :, :], 0.0).then_inc(ready, 1)
                gp.wait_ge(ready, 3 + TB)
                gp.wait_ge(pro["moments"], NT)
                nc.gpsimd.tensor_tensor(rs[:, 0:NT], mv[:, :, 1:2].rearrange("p t o -> p (t o)"), c.eps[:, 0:NT],
                                        ALU.add).then_inc(pro["rstd"], 1)
                gp.wait_ge(pro["rstd"], 1)
                nc.gpsimd.tensor_tensor(rs[:, NT:2 * NT], rs[:, 0:NT], c.mhalf[:, 0:NT], ALU.pow).then_inc(pro["rstd"], 1)
                fold_butterflies(c, gp, ctx_bf)

            @block.tensor
            def _(te):
                pe.first_turn(te)
                for name in ("masks", "L0_xattn_Wq", "L0_xattn_Wk", "L0_xattn_Wv", "L0_xattn_Wo", "cols", "rows"):
                    te.wait_ge(c.loaded[name], 16)
                te.wait_ge(ready, 3 + TB)
                te.wait_ge(last_in, 16)
                for t in range(NT):
                    for k in range(KC):
                        mm = nc.tensor.matmul(B[t % 8][0:TB, 0:D], lastT[:, k, t * TB:(t + 1) * TB],
                                              c.w["L0_xattn_Wv"][:, k, :], start=(k == 0), stop=(k == KC - 1))
                    mm.then_inc(vlast_done, 1)
                te.wait_ge(ready, 3 + TB + NT)
                te.wait_ge(pro["norm"], 1)
                for k in range(KC):
                    for t in range(NT):
                        mm = nc.tensor.transpose(B[2 * k + t // 4][:, (t % 4) * P:(t % 4 + 1) * P], xn[:, t, k * P:(k + 1) * P], ident)
                mm.then_inc(pro["xT"], 1)
                te.wait_ge(pro["xT_out"], 2)
                for m in range(2):
                    for n in range(2):
                        for k in range(KC):
                            mm = nc.tensor.matmul(B[4 + 2 * m + n][:, :], c.w["L0_xattn_Wq"][:, k, m * P:(m + 1) * P],
                                                  xnT[:, k, n * 512:(n + 1) * 512], start=(k == 0), stop=(k == KC - 1))
                mm.then_inc(pro["qT"], 1)
                te.wait_ge(pro["qT_out"], 1)

                def key_product(j, i):
                    te.wait_ge(ctx_in[j], 16 * (i + 1))
                    if j == 0:
                        te.wait_ge(dve.sem, dve.after("res", i - 1))
                    else:
                        te.wait_ge(act.sem, act.after(f"kTb{j-1}", i))
                    for m in range(2):
                        for k in range(KC):
                            mm = nc.tensor.matmul(B[m][:, 0:KEYS], c.w["L0_xattn_Wk"][:, k, m * P:(m + 1) * P],
                                                  ctxT[j][:, k, :], start=(k == 0), stop=(k == KC - 1))
                    mm.then_inc(pe.sem, 1)

                def value_product(j, i):
                    te.wait_ge(dve.sem, dve.after(f"v{j-1}", i) if j else dve.after("v3", i - 1))
                    for h in range(2):
                        for k in range(KC):
                            mm = nc.tensor.matmul(B[2][:, h * D:(h + 1) * D], ctxT[j][:, k, h * P:(h + 1) * P],
                                                  c.w["L0_xattn_Wv"][:, k, :], start=(k == 0), stop=(k == KC - 1))
                    mm.then_inc(pe.sem, 1)

                def scores(j, i, half):
                    te.wait_ge(act.sem, act.after(f"kTb{j}", i))
                    if half:
                        te.wait_ge(act.sem, act.after(f"e1{j}", i))
                    else:
                        te.wait_ge(act.sem, act.after(f"e3{j-1}", i) if j else act.after("e33", i - 1))
                    if (j, half) == (0, 0):
                        te.wait_ge(dve.sem, dve.after("qb", i))
                    for g in range(2):
                        mm = nc.tensor.matmul(B[3 + g][:, 0:KEYS], qblk[:, half, j, 4 * g:4 * g + 4, :].rearrange("p h q -> p (h q)"),
                                              kT[j % 2][:, half, :], start=True, stop=True)
                    mm.then_inc(pe.sem, 1)

                def transposes(j, i):
                    te.wait_ge(act.sem, act.after(f"e3{j}", i))
                    te.wait_ge(dve.sem, dve.after(f"plast{j}", i))
                    te.wait_ge(dve.sem, dve.after(f"aT{j-1}", i) if j else dve.after("aT3", i - 1))
                    for h in range(2):
                        for g in range(4):
                            nc.tensor.transpose(B[5 + h][:, g * P:(g + 1) * P], probs[j % 2][:, g, h * P:(h + 1) * P], ident)
                    for g in range(4):
                        mm = nc.tensor.transpose(B[7][0:TB, g * P:(g + 1) * P], plast[j][:, g, :], ident)
                    mm.then_inc(pe.sem, 1)

                with te.Fori(0, NT) as i:
                    key_product(0, i)
                    value_product(0, i)
                    scores(0, i, 0)
                    for j in J:
                        if j < 3:
                            key_product(j + 1, i)
                        scores(j, i, 1)
                        if j < 3:
                            value_product(j + 1, i)
                        transposes(j, i)
                        if j < 3:
                            scores(j + 1, i, 0)
                        te.wait_ge(act.sem, act.after(f"pT{j}", i))
                        te.wait_ge(dve.sem, dve.after(f"plT{j}", i))
                        for g in range(4):
                            o = B[7][:, g * 64:(g + 1) * 64]
                            for h in range(2):
                                nc.tensor.matmul(o, probsT[:, h, g * P:(g + 1) * P], v[j % 2][:, h, g * 64:(g + 1) * 64],
                                                 start=(h == 0), stop=False)
                            mm = nc.tensor.matmul(o, plastT[:, g * P:(g + 1) * P], vlast[:, bass.ds(i, 1), g * 64:(g + 1) * 64].rearrange("p t n -> p (t n)"),
                                                  start=False, stop=True)
                        mm.then_inc(pe.sem, 1)
                        te.wait_ge(dve.sem, dve.after(f"ao{j}", i))
                        for m in range(2):
                            mm = nc.tensor.matmul(B[7][:, 256 + m * S:256 + (m + 1) * S],
                                                  ao[:, 2 * m:2 * m + 2, :, :].rearrange("p g h d -> p (g h d)"),
                                                  c.fold[:, :], start=True, stop=True)
                        mm.then_inc(pe.sem, 1)
                    te.wait_ge(dve.sem, dve.after("aT3", i))
                    for k in range(KC):
                        nc.tensor.matmul(B[0][:, 0:D], aT[:, k, :], c.w["L0_xattn_Wo"][:, k, :], start=(k == 0), stop=False)
                    nc.tensor.matmul(B[0][:, 0:D], c.ones[0:1, :], c.row("L0_xattn_bo"), start=False, stop=True).then_inc(pe.sem, 1)

            @block.scalar
            def _(sc):
                act.first_turn(sc)
                sc.wait_ge(c.loaded["cols"], 16)

                sc.wait_ge(pro["xT"], 1)
                nc.scalar.copy(xnT[:, 1, :], c.PS[:, 2:4, :].rearrange("p b n -> p (b n)")).then_inc(pro["xT_out"], 1)
                sc.wait_ge(pro["qT"], 1)
                for m in range(2):
                    op = nc.scalar.activation(qT[:, m, :], c.PS[:, 4 + 2 * m:6 + 2 * m, :].rearrange("p b n -> p (b n)"),
                                              ACT.Identity, bias=c.col("L0_xattn_bq", m))
                op.then_inc(pro["qT_out"], 1)

                def keys_out(j, i):
                    sc.wait_ge(pe.sem, pe.after(f"kT{j}", i))
                    sc.wait_ge(pe.sem, pe.after(f"sB{j-2}", i) if j > 1 else pe.after(f"sB{j+2}", i - 1))
                    for m in range(2):
                        nc.scalar.activation(kT[j % 2][:, m, :], B[m][:, 0:KEYS], ACT.Identity,
                                             bias=c.col("L0_xattn_bk", m)).then_inc(act.sem, 1)

                def exps(j, i, half):
                    sc.wait_ge(dve.sem, dve.after(("maxB" if half else "maxA") + str(j), i))
                    for g in range(2):
                        nc.scalar.activation(probs[j % 2][:, 2 * half + g, :], B[3 + g][:, 0:KEYS], ACT.Exp,
                                             bias=nmax[j % 2][:, 2 * half + g:2 * half + g + 1],
                                             accum_out=total[j % 2][:, 2 * half + g:2 * half + g + 1]).then_inc(act.sem, 1)

                with sc.Fori(0, NT) as i:
                    keys_out(0, i)
                    exps(0, i, 0)
                    for j in J:
                        if j < 3:
                            keys_out(j + 1, i)
                        exps(j, i, 1)
                        sc.wait_ge(pe.sem, pe.after(f"pT{j}", i))
                        sc.wait_ge(pe.sem, pe.after(f"av{j-1}", i) if j else pe.after("av3", i - 1))
                        nc.scalar.copy(probsT[:, 1, :], B[6][:, :]).then_inc(act.sem, 1)
                        if j < 3:
                            exps(j + 1, i, 0)

            @block.vector
            def _(ve):
                dve.first_turn(ve)
                for name in ("x", "cols", "masks"):
                    ve.wait_ge(c.loaded[name], 16)
                ve.wait_ge(ready, 3 + TB)
                for t in range(NT):
                    ve.wait_ge(vlast_done, t + 1)
                    nc.vector.tensor_copy(vlast[:, t, :], B[t % 8][0:TB, 0:D]).then_inc(ready, 1)

                for t in range(NT):
                    nc.vector.bn_stats(st[:, t, :], c.X[:, t, :]).then_inc(pro["stats"], 1)
                ve.wait_ge(pro["stats"], NT)
                for t in range(NT):
                    nc.vector.bn_aggr(mv[:, t, :], st[:, t, :]).then_inc(pro["moments"], 1)
                ve.wait_ge(pro["moments"], NT)
                ve.wait_ge(pro["rstd"], 2)
                for t in range(NT):
                    op = nc.vector.tensor_scalar(xn[:, t, :], c.X[:, t, :], mv[:, t, 0:1], rs[:, NT + t:NT + t + 1],
                                                 ALU.subtract, ALU.mult)
                op.then_inc(pro["norm"], 1)
                ve.wait_ge(pro["xT"], 1)
                nc.vector.tensor_copy(xnT[:, 0, :], c.PS[:, 0:2, :].rearrange("p b n -> p (b n)")).then_inc(pro["xT_out"], 1)
                ve.wait_ge(pro["qT_out"], 1)

                def row_max(j, i, half):
                    ve.wait_ge(pe.sem, pe.after(("sB" if half else "sA") + str(j), i))
                    nc.vector.tensor_reduce(nmax[j % 2][:, 2 * half:2 * half + 2], c.PS[:, 3:5, 0:KEYS],
                                            AX_X, ALU.max, negate=True).then_inc(dve.sem, 1)

                def values_out(j, i):
                    ve.wait_ge(pe.sem, pe.after(f"v{j}", i))
                    nc.vector.tensor_copy(v[j % 2][:, :, :].rearrange("p h n -> p (h n)"), B[2][:, :]).then_inc(dve.sem, 1)

                with ve.Fori(0, NT) as i:
                    xt = c.X[:, bass.ds(i, 1), :].rearrange("p t d -> p (t d)")
                    for m in range(2):
                        op = nc.vector.tensor_tensor(
                            qblk[:, m, :, :, :], bc(qT[:, m, bass.ds(i * P, P)].rearrange("p (b q) -> p b q", b=TB), 2, 8),
                            c.qmask[:, :].unsqueeze(1).unsqueeze(3).to_broadcast([P, TB, 8, S]), ALU.mult)
                    op.then_inc(dve.sem, 1)
                    values_out(0, i)
                    row_max(0, i, 0)
                    for j in J:
                        row_max(j, i, 1)
                        if j < 3:
                            values_out(j + 1, i)
                        ve.wait_ge(act.sem, act.after(f"e3{j}", i))
                        nc.vector.tensor_copy(plast[j][:, :, j:j + 1], probs[j % 2][:, :, KEYS - 1:KEYS]).then_inc(dve.sem, 1)
                        nc.vector.reciprocal(rinv[:, :], total[j % 2][:, :]).then_inc(dve.sem, 1)
                        ve.wait_ge(dve.sem, dve.after(f"rinv{j}", i))
                        nc.vector.tensor_tensor(rmask[:, :, :], bc(rinv[:, :], 2, 4), bc(c.hmask[:, :], 1, 4),
                                                ALU.mult).then_inc(dve.sem, 1)
                        ve.wait_ge(pe.sem, pe.after(f"pT{j}", i))
                        nc.vector.tensor_copy(probsT[:, 0, :], B[5][:, :]).then_inc(dve.sem, 1)
                        nc.vector.tensor_copy(plastT[:, :], B[7][0:TB, :]).then_inc(dve.sem, 1)
                        if j < 3:
                            row_max(j + 1, i, 0)
                        ve.wait_ge(dve.sem, dve.after(f"rmask{j}", i))
                        ve.wait_ge(pe.sem, pe.after(f"av{j}", i))
                        nc.vector.tensor_tensor(ao[:, :, :, :], B[7][:, 0:D].rearrange("p (g h d) -> p g h d", g=4, h=4),
                                                bc(rmask[:, :, :], 3, 16), ALU.mult).then_inc(dve.sem, 1)
                        ve.wait_ge(pe.sem, pe.after(f"fold{j}", i))
                        nc.vector.tensor_tensor(aT[:, :, j * S:(j + 1) * S], B[7][:, 256:256 + 2 * S].rearrange("p (m q) -> p m q", m=2),
                                                bc(c.cols2("L0_xattn_bv"), 2, S), ALU.add).then_inc(dve.sem, 1)
                    ve.wait_ge(pe.sem, pe.after("out", i))
                    nc.vector.tensor_tensor(xt, xt, B[0][:, 0:D], ALU.add).then_inc(dve.sem, 1)


def stage_l0_gla(c):
    nc = c.nc
    with ExitStack() as ctx:
        sb = lambda name, shape: c.sb(name, shape, ctx)
        xn, xnT = sb("l0a_xn", [P, HT, D]), sb("l0a_xnT", [P, KC, HN])
        st, mv, rs = sb("l0a_st", [P, HT, 6]), sb("l0a_mv", [P, HT, 2]), sb("l0a_rs", [P, 2 * HT])
        g1T = sb("l0a_g1T", [16, HN])
        neg, z, expo, lg = (sb(f"l0a_{n}", [P, HN]) for n in ("neg", "z", "expo", "lg"))
        keep = sb("l0a_keep", [P, HN])
        G, Gc = sb("l0a_G", [P, HN]), sb("l0a_Gc", [P, HN])
        eq, ek = sb("l0a_eq", [P, HN]), sb("l0a_ek", [P, HN])
        qd, kd = sb("l0a_qd", [P, HN]), sb("l0a_kd", [P, HN])
        v, gate, gatew = (sb(f"l0a_{n}", [P, HT, D]) for n in ("v", "gate", "gatew"))
        AT = sb("l0a_AT", [P, 4, HN])
        sq, y = sb("l0a_sq", [P, HT, D]), sb("l0a_y", [P, HT, D])
        yT = sb("l0a_yT", [P, KC, HN])
        ms, ms2 = sb("l0a_ms", [P, 16]), sb("l0a_ms2", [P, 3, 16])
        sixty4th = sb("l0a_64th", [P, 16])
        pe = c.steps(ctx, "l0a_pe", "xT g1 g2 gate q k v scores o yT out")
        dve = c.steps(ctx, "l0a_dve", "stats moments norm xT0 neg z mabs v0 v1 logsig logg scan center qd kd "
                      "c0 c1 c2 c3 ms y0 y1 yg yT0 res0 res1")
        act = c.steps(ctx, "l0a_act", "xT1 g1T gate0 gate1 exp ln eq ek sq0 sq1 yT1")
        pool = c.steps(ctx, "l0a_pool", "vareps rstd gatew msn mse msr")
        ready = c.sem("l0a_ready", ctx)
        B = c.bank
        ident = c.ident()
        causal = c.mask("causal")

        with nc.Block() as block:
            @block.gpsimd
            def _(gp):
                pool.first_turn(gp)
                nc.gpsimd.memset(sixty4th[:, :], 1.0 / 64).then_inc(ready, 1)
                nc.gpsimd.memset(keep[:, :], 1.0).then_inc(ready, 1)
                gp.wait_ge(ready, 2)
                nc.gpsimd.memset(keep[:, :].rearrange("p (b s) -> p b s", s=S)[:, :, 0:1], 0.0).then_inc(ready, 1)
                nc.gpsimd.memset(AT[:, :, :], 0.0).then_inc(ready, 1)
                gp.wait_ge(c.loaded["repeated"], 16)
                gp.wait_ge(ready, 4)
                with gp.Fori(0, 2) as i:
                    rstd_half(c, gp, pool, dve, "", i, mv, rs)
                    gp.wait_ge(act.sem, act.after("gate1", i))
                    gp.wait_ge(dve.sem, dve.after("yg", i - 1))
                    nc.gpsimd.tensor_tensor(gatew[:, :, :].rearrange("p t (h d) -> p (t h) d", h=4),
                                            gate[:, :, :].rearrange("p t (h d) -> p (t h) d", h=4),
                                            bc(c.rep("L0_attn_rms_w"), 1, 16), ALU.mult).then_inc(pool.sem, 1)
                    gp.wait_ge(dve.sem, dve.after("ms", i))
                    nc.gpsimd.tensor_tensor(ms2[:, 0, :], ms[:, :], sixty4th[:, :], ALU.mult).then_inc(pool.sem, 1)
                    gp.wait_ge(pool.sem, pool.after("msn", i))
                    nc.gpsimd.tensor_tensor(ms2[:, 1, :], ms2[:, 0, :], c.eps[:, :], ALU.add).then_inc(pool.sem, 1)
                    gp.wait_ge(pool.sem, pool.after("mse", i))
                    nc.gpsimd.tensor_tensor(ms2[:, 2, :], ms2[:, 1, :], c.mhalf[:, :], ALU.pow).then_inc(pool.sem, 1)

            @block.tensor
            def _(te):
                pe.first_turn(te)
                for name in c.loaded:
                    if name.startswith("L0_attn"):
                        te.wait_ge(c.loaded[name], 16)

                def feature_major(out, w, k_rhs):
                    for k in range(KC):
                        mm = nc.tensor.matmul(out, w[:, k, :], k_rhs[:, k, :], start=(k == 0), stop=(k == KC - 1))
                    return mm

                def token_major(banks, lhsT, w):
                    for t in range(HT):
                        for k in range(KC):
                            mm = nc.tensor.matmul(B[banks + t // 2][:, (t % 2) * D:(t % 2 + 1) * D], lhsT[:, k, t * P:(t + 1) * P],
                                                  w[:, k, :], start=(k == 0), stop=(k == KC - 1))
                    return mm

                with te.Fori(0, 2) as i:
                    te.wait_ge(dve.sem, dve.after("res1", i - 1))
                    te.wait_ge(dve.sem, dve.after("norm", i))
                    for t in range(HT):
                        for k in range(KC):
                            mm = nc.tensor.transpose(B[k][:, t * P:(t + 1) * P], xn[:, t, k * P:(k + 1) * P], ident)
                    mm.then_inc(pe.sem, 1)
                    te.wait_ge(dve.sem, dve.after("xT0", i))
                    te.wait_ge(act.sem, act.after("xT1", i))
                    feature_major(B[4][0:16, :], c.w["L0_attn_Wgk1"], xnT).then_inc(pe.sem, 1)
                    te.wait_ge(act.sem, act.after("g1T", i))
                    nc.tensor.matmul(B[5][:, :], c.narrow[:, :], g1T[:, :], start=True, stop=True).then_inc(pe.sem, 1)
                    token_major(0, xnT, c.w["L0_attn_Wg"]).then_inc(pe.sem, 1)
                    feature_major(B[2][:, :], c.w["L0_attn_Wq"], xnT).then_inc(pe.sem, 1)
                    feature_major(B[3][:, :], c.w["L0_attn_Wk"], xnT).then_inc(pe.sem, 1)
                    token_major(6, xnT, c.w["L0_attn_Wv"]).then_inc(pe.sem, 1)
                    te.wait_ge(act.sem, act.after("gate1", i))
                    te.wait_ge(dve.sem, dve.after("kd", i))
                    for t in range(HT):
                        for h in range(4):
                            r = slice(32 * h, 32 * h + 32)
                            mm = nc.tensor.matmul(B[h][:, t * P:(t + 1) * P], kd[r, t * P:(t + 1) * P],
                                                  qd[r, t * P:(t + 1) * P], start=True, stop=True)
                    mm.then_inc(pe.sem, 1)
                    te.wait_ge(dve.sem, dve.after("c3", i))
                    te.wait_ge(dve.sem, dve.after("v1", i))
                    for t in range(HT):
                        for h in range(4):
                            mm = nc.tensor.matmul(B[4 + t // 2][:, (t % 2) * D + h * 64:(t % 2) * D + (h + 1) * 64],
                                                  AT[:, h, t * P:(t + 1) * P], v[:, t, h * 64:(h + 1) * 64], start=True, stop=True)
                    mm.then_inc(pe.sem, 1)
                    te.wait_ge(dve.sem, dve.after("yg", i))
                    for t in range(HT):
                        for k in range(KC):
                            mm = nc.tensor.transpose(B[6 + k][:, t * P:(t + 1) * P], y[:, t, k * P:(k + 1) * P], ident)
                    mm.then_inc(pe.sem, 1)
                    te.wait_ge(dve.sem, dve.after("yT0", i))
                    te.wait_ge(act.sem, act.after("yT1", i))
                    token_major(0, yT, c.w["L0_attn_Wout"]).then_inc(pe.sem, 1)

            @block.scalar
            def _(sc):
                act.first_turn(sc)
                with sc.Fori(0, 2) as i:
                    sc.wait_ge(pe.sem, pe.after("xT", i))
                    nc.scalar.copy(xnT[:, 1, :], B[1][:, :]).then_inc(act.sem, 1)
                    sc.wait_ge(pe.sem, pe.after("g1", i))
                    nc.scalar.copy(g1T[:, :], B[4][0:16, :]).then_inc(act.sem, 1)
                    sc.wait_ge(pe.sem, pe.after("gate", i))
                    sc.wait_ge(pool.sem, pool.after("gatew", i - 1))
                    for n in range(2):
                        nc.scalar.activation(gate[:, 2 * n:2 * n + 2, :].rearrange("p t n -> p (t n)"), B[n][:, :],
                                             ACT.Silu).then_inc(act.sem, 1)
                    sc.wait_ge(dve.sem, dve.after("mabs", i))
                    nc.scalar.activation(expo[:, :], expo[:, :], ACT.Exp).then_inc(act.sem, 1)
                    sc.wait_ge(act.sem, act.after("exp", i))
                    nc.scalar.activation(lg[:, :], expo[:, :], ACT.Ln, bias=1.0).then_inc(act.sem, 1)
                    sc.wait_ge(dve.sem, dve.after("center", i))
                    nc.scalar.activation(eq[:, :], Gc[:, :], ACT.Exp).then_inc(act.sem, 1)
                    nc.scalar.activation(ek[:, :], Gc[:, :], ACT.Exp, scale=-1.0).then_inc(act.sem, 1)
                    sc.wait_ge(pe.sem, pe.after("o", i))
                    for n in range(2):
                        nc.scalar.activation(sq[:, 2 * n:2 * n + 2, :].rearrange("p t n -> p (t n)"), B[4 + n][:, :],
                                             ACT.Square).then_inc(act.sem, 1)
                    sc.wait_ge(pe.sem, pe.after("yT", i))
                    nc.scalar.copy(yT[:, 1, :], B[7][:, :]).then_inc(act.sem, 1)

            @block.vector
            def _(ve):
                dve.first_turn(ve)
                ve.wait_ge(ready, 4)
                with ve.Fori(0, 2) as i:
                    xt = lambda t: c.X[:, bass.ds(i * HT + t, 1), :].rearrange("p t d -> p (t d)")
                    norm_half(c, ve, dve, pool, "", i, xt, lambda t: xn[:, t, :], st, mv, rs)
                    ve.wait_ge(pe.sem, pe.after("xT", i))
                    nc.vector.tensor_copy(xnT[:, 0, :], B[0][:, :]).then_inc(dve.sem, 1)
                    ve.wait_ge(pe.sem, pe.after("g2", i))
                    b = c.col("L0_attn_bgk2", 0)
                    nc.vector.tensor_scalar(neg[:, :], B[5][:, :], b, 0.0, ALU.add, ALU.min).then_inc(dve.sem, 1)
                    nc.vector.tensor_scalar(z[:, :], B[5][:, :], b, None, ALU.add).then_inc(dve.sem, 1)
                    ve.wait_ge(dve.sem, dve.after("z", i))
                    nc.vector.scalar_tensor_tensor(out=expo[:, :], in0=neg[:, :], scalar=2.0, in1=z[:, :],
                                                   op0=ALU.mult, op1=ALU.subtract).then_inc(dve.sem, 1)
                    ve.wait_ge(pe.sem, pe.after("v", i))
                    for n in range(2):
                        nc.vector.tensor_copy(v[:, 2 * n:2 * n + 2, :].rearrange("p t n -> p (t n)"), B[6 + n][:, :]).then_inc(dve.sem, 1)
                    ve.wait_ge(act.sem, act.after("ln", i))
                    nc.vector.tensor_tensor(z[:, :], neg[:, :], lg[:, :], ALU.subtract).then_inc(dve.sem, 1)
                    ve.wait_ge(dve.sem, dve.after("logsig", i))
                    nc.vector.tensor_scalar(neg[:, :], z[:, :], 1.0 / 16, -3.0, ALU.mult, ALU.max).then_inc(dve.sem, 1)
                    ve.wait_ge(dve.sem, dve.after("logg", i))
                    nc.vector.tensor_tensor_scan(G[:, :], keep[:, :], neg[:, :], 0.0, ALU.mult, ALU.add).then_inc(dve.sem, 1)
                    ve.wait_ge(dve.sem, dve.after("scan", i))
                    G3 = G[:, :].rearrange("p (b s) -> p b s", s=S)
                    nc.vector.tensor_tensor(Gc[:, :].rearrange("p (b s) -> p b s", s=S), G3,
                                            G3[:, :, S // 2 - 1:S // 2].to_broadcast([P, HN // S, S]), ALU.subtract).then_inc(dve.sem, 1)
                    ve.wait_ge(pe.sem, pe.after("k", i))
                    ve.wait_ge(act.sem, act.after("ek", i))
                    nc.vector.tensor_tensor(qd[:, :], B[2][:, :], eq[:, :], ALU.mult).then_inc(dve.sem, 1)
                    nc.vector.tensor_tensor(kd[:, :], B[3][:, :], ek[:, :], ALU.mult).then_inc(dve.sem, 1)
                    ve.wait_ge(pe.sem, pe.after("scores", i))
                    ve.sem_inc(c.waited)
                    for h in range(4):
                        nc.vector.copy_predicated(AT[:, h, :].rearrange("p (t n) -> p t n", t=HT),
                                                  bc(causal, 1, HT).bitcast(I32),
                                                  B[h][:, :].rearrange("p (t n) -> p t n", t=HT)).then_inc(dve.sem, 1)
                    ve.wait_ge(act.sem, act.after("sq1", i))
                    nc.vector.tensor_reduce(ms[:, :], sq[:, :, :].rearrange("p t (h d) -> p (t h) d", h=4),
                                            AX_X, ALU.add).then_inc(dve.sem, 1)
                    ve.wait_ge(pool.sem, pool.after("msr", i))
                    for n in range(2):
                        nc.vector.tensor_tensor(y[:, 2 * n:2 * n + 2, :].rearrange("p t (h d) -> p (t h) d", h=4),
                                                B[4 + n][:, :].rearrange("p (g d) -> p g d", d=64),
                                                bc(ms2[:, 2, 8 * n:8 * n + 8], 2, 64), ALU.mult).then_inc(dve.sem, 1)
                    ve.wait_ge(dve.sem, dve.after("y1", i))
                    nc.vector.tensor_tensor(y[:, :, :], y[:, :, :], gatew[:, :, :], ALU.mult).then_inc(dve.sem, 1)
                    ve.wait_ge(pe.sem, pe.after("yT", i))
                    nc.vector.tensor_copy(yT[:, 0, :], B[6][:, :]).then_inc(dve.sem, 1)
                    ve.wait_ge(pe.sem, pe.after("out", i))
                    for n in range(2):
                        xx = c.X[:, bass.ds(i * HT + 2 * n, 2), :]
                        nc.vector.tensor_tensor(xx, xx, B[n][:, :].rearrange("p (t n) -> p t n", t=2), ALU.add).then_inc(dve.sem, 1)


def stage_l0_ffn(c):
    nc = c.nc
    FC = F0 // P
    with ExitStack() as ctx:
        sb = lambda name, shape: c.sb(name, shape, ctx)
        xn, xnT = sb("l0f_xn", [P, HT, D]), sb("l0f_xnT", [P, KC, HN])
        st, mv, rs = sb("l0f_st", [P, HT, 6]), sb("l0f_mv", [P, HT, 2]), sb("l0f_rs", [P, 2 * HT])
        W2e = sb("l0f_W2e", [P, FC, D])
        b1 = sb("l0f_b1", [P, FC])
        hT = sb("l0f_hT", [P, FC, HN])
        hid = " ".join(f"h{j}" for j in range(FC))
        pe = c.steps(ctx, "l0f_pe", f"xT {hid} out")
        dve = c.steps(ctx, "l0f_dve", "stats moments norm xT0 res0 res1")
        act = c.steps(ctx, "l0f_act", f"xT1 {hid}")
        pool = c.steps(ctx, "l0f_pool", "vareps rstd")
        prep, prep_out = c.sem("l0f_prep", ctx), c.sem("l0f_prep_out", ctx)
        B = c.bank
        ident = c.ident()
        hbank = lambda j: B[(j + 2) % 8]

        with nc.Block() as block:
            @block.gpsimd
            def _(gp):
                pool.first_turn(gp)
                with gp.Fori(0, 2) as i:
                    rstd_half(c, gp, pool, dve, "", i, mv, rs)

            @block.tensor
            def _(te):
                pe.first_turn(te)
                for j in range(FC):
                    for k in range(KC):
                        nc.tensor.transpose(B[j // 2][:, (j % 2) * D + k * P:(j % 2) * D + (k + 1) * P],
                                            c.W2eT[:, k, j * P:(j + 1) * P], ident)
                for j in range(FC):
                    mm = nc.tensor.matmul(B[4][:, j:j + 1], c.W1e[0:1, KC, j * P:(j + 1) * P], c.ones[0:1, 0:1],
                                          start=True, stop=True)
                mm.then_inc(prep, 1)
                te.wait_ge(prep_out, 2)
                with te.Fori(0, 2) as i:
                    te.wait_ge(act.sem, act.after(f"h{FC-1}", i - 1))
                    te.wait_ge(dve.sem, dve.after("norm", i))
                    for t in range(HT):
                        for k in range(KC):
                            mm = nc.tensor.transpose(B[k][:, t * P:(t + 1) * P], xn[:, t, k * P:(k + 1) * P], ident)
                    mm.then_inc(pe.sem, 1)
                    te.wait_ge(dve.sem, dve.after("xT0", i))
                    te.wait_ge(act.sem, act.after("xT1", i))
                    te.wait_ge(dve.sem, dve.after("res1", i - 1))
                    for j in range(FC):
                        for k in range(KC):
                            mm = nc.tensor.matmul(hbank(j), c.W1e[:, k, j * P:(j + 1) * P], xnT[:, k, :],
                                                  start=(k == 0), stop=(k == KC - 1))
                        mm.then_inc(pe.sem, 1)
                    te.wait_ge(act.sem, act.after(f"h{FC-1}", i))
                    for t in range(HT):
                        o = B[2 + t // 2][:, (t % 2) * D:(t % 2 + 1) * D]
                        for j in range(FC):
                            nc.tensor.matmul(o, hT[:, j, t * P:(t + 1) * P], W2e[:, j, :], start=(j == 0), stop=False)
                        mm = nc.tensor.matmul(o, c.ones[0:1, :], c.ffn_bias[:, :], start=False, stop=True)
                    mm.then_inc(pe.sem, 1)

            @block.scalar
            def _(sc):
                act.first_turn(sc)
                sc.wait_ge(prep, 1)
                nc.scalar.copy(W2e[:, FC // 2:FC, :].rearrange("p j n -> p (j n)"),
                               c.PS[:, 2:4, :].rearrange("p b n -> p (b n)")).then_inc(prep_out, 1)
                with sc.Fori(0, 2) as i:
                    sc.wait_ge(pe.sem, pe.after("xT", i))
                    nc.scalar.copy(xnT[:, 1, :], B[1][:, :]).then_inc(act.sem, 1)
                    for j in range(FC):
                        sc.wait_ge(pe.sem, pe.after(f"h{j}", i))
                        nc.scalar.activation(hT[:, j, :], hbank(j), ACT.Gelu, bias=b1[:, j:j + 1]).then_inc(act.sem, 1)

            @block.vector
            def _(ve):
                dve.first_turn(ve)
                ve.wait_ge(prep, 1)
                nc.vector.tensor_copy(W2e[:, 0:FC // 2, :].rearrange("p j n -> p (j n)"),
                                      c.PS[:, 0:2, :].rearrange("p b n -> p (b n)"))
                nc.vector.tensor_copy(b1[:, :], B[4][:, 0:FC]).then_inc(prep_out, 1)
                with ve.Fori(0, 2) as i:
                    xt = lambda t: c.X[:, bass.ds(i * HT + t, 1), :].rearrange("p t d -> p (t d)")
                    norm_half(c, ve, dve, pool, "", i, xt, lambda t: xn[:, t, :], st, mv, rs)
                    ve.wait_ge(pe.sem, pe.after("xT", i))
                    nc.vector.tensor_copy(xnT[:, 0, :], B[0][:, :]).then_inc(dve.sem, 1)
                    ve.wait_ge(pe.sem, pe.after("out", i))
                    for n in range(2):
                        xx = c.X[:, bass.ds(i * HT + 2 * n, 2), :]
                        nc.vector.tensor_tensor(xx, xx, B[2 + n][:, :].rearrange("p (t n) -> p t n", t=2), ALU.add).then_inc(dve.sem, 1)


HEADS1, HD1 = 12, 64
INNER = HEADS1 * HD1
PAIRS = INNER // P


def prepare_l1_keys(c, s):
    nc = c.nc
    with ExitStack() as ctx:
        sb = lambda name, shape: c.sb(name, shape, ctx)
        mean = sb("l1p_mean", [P, KC])
        WkcT, Cp, kgz = sb("l1p_WkcT", [P, PAIRS, D]), sb("l1p_C", [P, KC, D]), sb("l1p_kgz", [P, PAIRS, 2])
        ve_done, pe_done, act_done = (c.sem("l1p_" + n, ctx) for n in ("ve", "pe", "act"))
        B = c.bank
        Wk = c.w["L1_xattn_Wk"]
        with nc.Block() as block:
            @block.vector
            def _(ve):
                for name in ("L1_xattn_Wk", "cols", "repeated"):
                    ve.wait_ge(c.loaded[name], 16)
                nc.vector.memset(s.KB[:, :], 0.0).then_inc(ve_done, 1)
                nc.vector.tensor_reduce(mean[:, :], Wk[:, :, :], AX_X, ALU.add).then_inc(ve_done, 1)
                ve.wait_ge(ve_done, 2)
                nc.vector.tensor_scalar(mean[:, :], mean[:, :], 1.0 / INNER, None, ALU.mult).then_inc(ve_done, 1)
                ve.wait_ge(ve_done, 3)
                nc.vector.tensor_tensor(Wk[:, :, :], Wk[:, :, :], bc(mean[:, :], 2, INNER), ALU.subtract).then_inc(ve_done, 1)
                half = c.mask("half")
                nc.vector.tensor_tensor(kgz[:, :, :], bc(c.cols2("L1_xattn_k_g"), 2, 2), bc(half, 1, PAIRS), ALU.mult).then_inc(ve_done, 1)
                nc.vector.tensor_tensor(s.KB[:, :].rearrange("p (a x) -> p a x", a=PAIRS)[:, :, 0:2],
                                        bc(c.cols2("L1_xattn_k_b"), 2, 2), bc(half, 1, PAIRS), ALU.mult).then_inc(ve_done, 1)
                ve.wait_ge(pe_done, 1)
                nc.vector.tensor_copy(WkcT[:, :, :].rearrange("p (b a) c -> p b (a c)", a=2), c.PS[:, 0:3, :]).then_inc(ve_done, 1)
                ve.wait_ge(ve_done, 7)
                for h in range(HEADS1):
                    nc.vector.tensor_scalar(s.WkgZ[:, h, :], WkcT[:, h // 2, :], kgz[:, h // 2, h % 2:h % 2 + 1], None, ALU.mult)
                ve.wait_ge(pe_done, 2)
                for m in range(KC):
                    op = nc.vector.scalar_tensor_tensor(out=s.Cx[:, m, 0:D], in0=B[3][:, m * D:(m + 1) * D], scalar=1.0 / INNER,
                                                        in1=c.rep("L1_xattn_tab_g"), op0=ALU.mult, op1=ALU.mult)
                op.then_inc(ve_done, 1)
                ve.wait_ge(pe_done, 3)
                nc.vector.tensor_copy(s.Cx[:, :, D:D + 1], B[4][:, 0:KC].unsqueeze(2)).then_inc(ve_done, 1)

            @block.tensor
            def _(te):
                te.wait_ge(ve_done, 4)
                for p in range(PAIRS):
                    for k in range(KC):
                        mm = nc.tensor.transpose(B[p // 2][:, (p % 2) * D + k * P:(p % 2) * D + (k + 1) * P],
                                                 Wk[:, k, p * P:(p + 1) * P], c.ident())
                mm.then_inc(pe_done, 1)
                te.wait_ge(ve_done, 7)
                for m in range(KC):
                    for p in range(PAIRS):
                        mm = nc.tensor.matmul(B[3][:, m * D:(m + 1) * D], WkcT[:, p, m * P:(m + 1) * P], WkcT[:, p, :],
                                              start=(p == 0), stop=(p == PAIRS - 1))
                mm.then_inc(pe_done, 1)
                te.wait_ge(act_done, 1)
                for m in range(KC):
                    for k in range(KC):
                        mm = nc.tensor.matmul(B[4][:, m:m + 1], Cp[:, k, m * P:(m + 1) * P], c.col("L1_xattn_tab_b", k),
                                              start=(k == 0), stop=(k == KC - 1))
                mm.then_inc(pe_done, 1)

            @block.scalar
            def _(sc):
                sc.wait_ge(ve_done, 8)
                nc.scalar.mul(Cp[:, :, :].rearrange("p k n -> p (k n)"), B[3][:, :], 1.0 / INNER).then_inc(act_done, 1)


def prepare_l1_queries(c, s):
    nc = c.nc
    with ExitStack() as ctx:
        sb = lambda name, shape: c.sb(name, shape, ctx)
        xn, xn2, xnT = sb("l1q_xn", [P, HT, D]), sb("l1q_xn2", [P, HT, D]), sb("l1q_xnT", [P, KC, HN])
        st, mv, rs = sb("l1q_st", [P, HT, 6]), sb("l1q_mv", [P, HT, 2]), sb("l1q_rs", [P, 2 * HT])
        qst = sb("l1q_qst", [P, HT, 2, 6])
        qn = sb("l1q_qn", [P, HT, INNER])
        qbT = sb("l1q_qbT", [HEADS1, HN])
        pairs = lambda n: " ".join(f"{n}{p}" for p in range(PAIRS))
        pe = c.steps(ctx, "l1q_pe", f"xT qA qB {pairs('qT')} qb qbT")
        dve = c.steps(ctx, "l1q_dve", f"stats moments norm 2stats 2moments 2norm xT0 xT1 "
                      f"qstatsA qstatsB 3moments qnormA qnormB {pairs('qT')} qbT qbt")
        pool = c.steps(ctx, "l1q_pool", "vareps rstd 2vareps 2rstd 3vareps 3rstd")
        B = c.bank
        with nc.Block() as block:
            @block.gpsimd
            def _(gp):
                pool.first_turn(gp)
                with gp.Fori(0, 2) as i:
                    for pre in ("", "2", "3"):
                        rstd_half(c, gp, pool, dve, pre, i, mv, rs)

            @block.tensor
            def _(te):
                pe.first_turn(te)
                te.wait_ge(c.loaded["L1_xattn_Wq"], 16)
                with te.Fori(0, 2) as i:
                    te.wait_ge(dve.sem, dve.after("qbt", i - 1))
                    te.wait_ge(dve.sem, dve.after("2norm", i))
                    for t in range(HT):
                        for k in range(KC):
                            mm = nc.tensor.transpose(B[k][:, t * P:(t + 1) * P], xn2[:, t, k * P:(k + 1) * P], c.ident())
                    mm.then_inc(pe.sem, 1)
                    te.wait_ge(dve.sem, dve.after("xT1", i))
                    for n in range(2):
                        for t in range(2 * n, 2 * n + 2):
                            for a in range(2):
                                for k in range(KC):
                                    mm = nc.tensor.matmul(B[2 * t + a][:, 0:384], xnT[:, k, t * P:(t + 1) * P],
                                                          c.w["L1_xattn_Wq"][:, k, a * 384:(a + 1) * 384], start=(k == 0), stop=(k == KC - 1))
                        mm.then_inc(pe.sem, 1)
                    te.wait_ge(dve.sem, dve.after("qnormB", i))
                    for p in range(PAIRS):
                        for t in range(HT):
                            mm = nc.tensor.transpose(B[p][:, t * P:(t + 1) * P], qn[:, t, p * P:(p + 1) * P], c.ident())
                        mm.then_inc(pe.sem, 1)
                    te.wait_ge(dve.sem, dve.after(f"qT{PAIRS-1}", i))
                    for p in range(PAIRS):
                        mm = nc.tensor.matmul(B[6][0:HEADS1, :], s.KB[:, HEADS1 * p:HEADS1 * (p + 1)], s.qT[:, p, bass.ds(i * HN, HN)],
                                              start=(p == 0), stop=(p == PAIRS - 1))
                    mm.then_inc(pe.sem, 1)
                    te.wait_ge(dve.sem, dve.after("qbT", i))
                    te.sem_inc(c.waited)
                    for t in range(HT):
                        mm = nc.tensor.transpose(B[7][:, t * HEADS1:(t + 1) * HEADS1], qbT[:, t * P:(t + 1) * P],
                                                 c.ident()[0:HEADS1, 0:HEADS1])
                    mm.then_inc(pe.sem, 1)

            @block.vector
            def _(ve):
                dve.first_turn(ve)
                with ve.Fori(0, 2) as i:
                    xt = lambda t: c.X[:, bass.ds(i * HT + t, 1), :].rearrange("p t d -> p (t d)")
                    norm_half(c, ve, dve, pool, "", i, xt, lambda t: xn[:, t, :], st, mv, rs)
                    ve.wait_ge(dve.sem, dve.after("norm", i))
                    norm_half(c, ve, dve, pool, "2", i, lambda t: xn[:, t, :], lambda t: xn2[:, t, :], st, mv, rs)
                    ve.wait_ge(pe.sem, pe.after("xT", i))
                    for k in range(KC):
                        nc.vector.tensor_scalar(xnT[:, k, :], B[k][:, :], c.col("L1_xattn_vid_g", k), c.col("L1_xattn_vid_b", k),
                                                ALU.mult, ALU.add).then_inc(dve.sem, 1)
                    for n in range(2):
                        ve.wait_ge(pe.sem, pe.after("qA" if n == 0 else "qB", i))
                        for t in range(2 * n, 2 * n + 2):
                            for a in range(2):
                                op = nc.vector.bn_stats(qst[:, t, a, :], B[2 * t + a][:, 0:384])
                        op.then_inc(dve.sem, 1)
                    ve.wait_ge(dve.sem, dve.after("qstatsB", i))
                    ve.sem_inc(c.waited)
                    for t in range(HT):
                        op = nc.vector.bn_aggr(mv[:, t, :], qst[:, t, :, :].rearrange("p a n -> p (a n)"))
                    op.then_inc(dve.sem, 1)
                    ve.wait_ge(pool.sem, pool.after("3rstd", i))
                    for n in range(2):
                        for t in range(2 * n, 2 * n + 2):
                            op = nc.vector.tensor_scalar(qn[:, t, :].rearrange("p (a n) -> p a n", a=2), c.PS[:, 2 * t:2 * t + 2, 0:384],
                                                         mv[:, t, 0:1], rs[:, HT + t:HT + t + 1], ALU.subtract, ALU.mult)
                        op.then_inc(dve.sem, 1)
                    for p in range(PAIRS):
                        ve.wait_ge(pe.sem, pe.after(f"qT{p}", i))
                        nc.vector.tensor_scalar(s.qT[:, p, bass.ds(i * HN, HN)], B[p][:, :], c.col("L1_xattn_q_g", p),
                                                c.col("L1_xattn_q_b", p), ALU.mult, ALU.add).then_inc(dve.sem, 1)
                    ve.wait_ge(pe.sem, pe.after("qb", i))
                    nc.vector.tensor_copy(qbT[:, :], B[6][0:HEADS1, :]).then_inc(dve.sem, 1)
                    ve.wait_ge(pe.sem, pe.after("qbT", i))
                    nc.vector.tensor_copy(s.qb[:, bass.ds(i * HT, HT), :], B[7][:, 0:HT * HEADS1].rearrange("p (t h) -> p t h", t=HT)).then_inc(dve.sem, 1)


def stage_l1_cross(c):
    nc = c.nc
    with ExitStack() as outer:
        s = type("Shared", (), {})()
        s.WkgZ, s.Cx = c.sb("l1_WkgZ", [P, HEADS1, D], outer), c.sb("l1_Cx", [P, KC, D + 1], outer)
        s.KB = c.sb("l1_KB", [P, PAIRS * 14], outer)
        s.qT, s.qb = c.sb("l1_qT", [P, PAIRS, NT * P], outer), c.sb("l1_qb", [P, NT, HEADS1], outer)
        prepare_l1_keys(c, s)
        prepare_l1_queries(c, s)
        ctx = outer
        sb = lambda name, shape: c.sb(name, shape, ctx)
        QT = sb("l1_QT", [P, KC, TB, HEADS1, S])
        UT = sb("l1_UT", [P, KC, HEADS1, P])
        ck = [sb(f"l1_ck{n}", [P, 2, D]) for n in range(2)]
        xh = [sb(f"l1_xh{n}", [P, 2, D + 1]) for n in range(2)]
        kst, kmv, krs = sb("l1_kst", [P, 2, 6]), sb("l1_kmv", [P, 2, 2]), sb("l1_krs", [P, 4])
        cl, xl = sb("l1_cl", [TB, D]), sb("l1_xl", [TB, D + 1])
        lst, lmv, lrs = sb("l1_lst", [TB, 6]), sb("l1_lmv", [TB, 2]), sb("l1_lrs", [TB, 2])
        xlT = sb("l1_xlT", [P, KC, TB])
        kvT = [sb(f"l1_kvT{n}", [P, KC, KEYS]) for n in range(2)]
        junk, junkl = sb("l1_junk", [P, 2, D + 1]), sb("l1_junkl", [TB, D + 1])
        kvar, rk = sb("l1_kvar", [P, 2]), sb("l1_rk", [P, 4])
        lvar, rl = sb("l1_lvar", [TB, 1]), sb("l1_rl", [TB, 2])
        rkB = sb("l1_rkB", [P, KEYS])
        sco = sb("l1_sco", [P, 3, KEYS])
        probs = sb("l1_probs", [P, 3, KEYS])
        qsel, qcol = sb("l1_qsel", [P, TB, 3, 4]), sb("l1_qcol", [P, TB, 3])
        mx, top, nb = sb("l1_mx", [P, 3]), sb("l1_top", [P, 3]), sb("l1_nb", [P, 3])
        total, rinv = sb("l1_total", [P, 3]), sb("l1_rinv", [P, 3])
        plast = [sb(f"l1_plast{j}", [P, 3, TB]) for j in range(TB)]
        probsT, plastT = sb("l1_probsT", [P, 2, 384]), sb("l1_plastT", [TB, 384])
        aT = sb("l1_aT", [P, PAIRS, P])
        J = range(TB)
        nxt = lambda j, names: " ".join(f"{n}{j+1}" for n in names.split()) if j < 3 else ""
        kv_pe, kv_dve, kv_act, kv_pool = "xT Z rk", "st mo no Zdot", "kv0 kv1 rkB", "ve rs last vz rz"
        at0 = lambda names: " ".join(f"{n}0" for n in names.split())
        pe = c.steps(ctx, "l1_pe", "QT0 QT1 qb lT lZ xT0 Z0 rk0 sc0 " + " ".join(
            f"{nxt(j, 'xT Z')} pT{j} {nxt(j, 'rk sc')} U{j}" for j in J) + " V out")
        dve = c.steps(ctx, "l1_dve", "lst lmo lno QT0 qsel qcol lT lZ st0 mo0 no0 Z0 max0 top0 nb0 " + " ".join(
            f"{nxt(j, 'st mo no')} rinv{j} norm{j} pT{j} {nxt(j, 'Z')} plT{j} {nxt(j, 'max top nb')} U{j}" for j in J) + " aT res")
        act = c.steps(ctx, "l1_act", "QT1 " + at0("kv0_ kv1_ rkB") + " ea0 eb0 ec0 " + " ".join(
            f"{nxt(j, 'kv0_ kv1_')} pT{j} {nxt(j, 'rkB ea eb ec')} U{j}" for j in J) + " aT")
        pool = c.steps(ctx, "l1_pool", "lve lrs lvz lrz " + at0("ve rs last vz rz") + " " + " ".join(
            f"{nxt(j, 've rs last')} plast{j} {nxt(j, 'vz rz')}" for j in J))
        ctx_in, last_in = [c.sem(f"l1_ctx_in{n}", ctx) for n in range(TB)], c.sem("l1_last_in", ctx)
        ready = c.sem("l1_ready", ctx)
        B = c.bank
        ident = c.ident()
        spread = c.mask("spread")
        by_head = lambda b: c.PS[:, b:b + 3, :].rearrange("p k n -> p (k n)").rearrange("p (h b q) -> p h b q", h=HEADS1, b=TB)

        with nc.Block() as block:
            @block.sync
            def _(sp):
                with sp.Fori(0, NT) as i:
                    sp.wait_ge(dve.sem, dve.after("lno", i - 1))
                    sp.dma_start(cl[:, :], c.dram["ctx_last"][bass.ds(i * TB, TB)]).then_inc(last_in, 16)
                    for j in J:
                        sp.wait_ge(dve.sem, dve.after(f"no{j-2}", i) if j > 1 else dve.after(f"no{j+2}", i - 1))
                        sp.dma_start(ck[j % 2][:, :, :], c.dram["ctx"][bass.ds(i * TB + j, 1)].rearrange(
                            "b p h d -> p (b h) d")).then_inc(ctx_in[j], 16)

            @block.gpsimd
            def _(gp):
                pool.first_turn(gp)
                for n in range(2):
                    nc.gpsimd.memset(xh[n][:, :, D:D + 1], 1.0).then_inc(ready, 1)
                nc.gpsimd.memset(xl[:, D:D + 1], 1.0).then_inc(ready, 1)
                for j in J:
                    nc.gpsimd.memset(plast[j][:, :, :], 0.0).then_inc(ready, 1)
                gp.wait_ge(ready, 3 + TB)

                def root(i, step, src, tmp, dst, first, second, when):
                    gp.wait_ge(dve.sem, when)
                    n = src.shape[1]
                    nc.gpsimd.tensor_tensor(tmp, src, c.eps[0:src.shape[0], 0:n], ALU.add).then_inc(pool.sem, 1)
                    gp.wait_ge(pool.sem, pool.after(first, i))
                    nc.gpsimd.tensor_tensor(dst, tmp, c.mhalf[0:src.shape[0], 0:n], ALU.pow).then_inc(pool.sem, 1)

                def context(j, i):
                    root(i, j, kmv[:, :, 1:2].rearrange("p t o -> p (t o)"), krs[:, 0:2], krs[:, 2:4], f"ve{j}", f"rs{j}",
                         dve.after(f"mo{j}", i))
                    gp.wait_ge(dve.sem, dve.after("lT", i))
                    gp.wait_ge(pe.sem, pe.after(f"sc{j-2}", i) if j > 1 else pe.after(f"sc{j+2}", i - 1))
                    gp.sem_inc(c.waited)
                    nc.gpsimd.tensor_copy(kvT[j % 2][:, :, KEYS - 1:KEYS], xlT[:, :, j:j + 1]).then_inc(pool.sem, 1)

                def key_root(j, i):
                    root(i, j, kvar[:, :], rk[:, 0:2], rk[:, 2:4], f"vz{j}", f"rz{j}", dve.after(f"Z{j}", i))

                with gp.Fori(0, NT) as i:
                    root(i, 0, lmv[:, 1:2], lrs[:, 0:1], lrs[:, 1:2], "lve", "lrs", dve.after("lmo", i))
                    root(i, 0, lvar[:, :], rl[:, 0:1], rl[:, 1:2], "lvz", "lrz", dve.after("lZ", i))
                    context(0, i)
                    key_root(0, i)
                    for j in J:
                        if j < 3:
                            context(j + 1, i)
                        gp.wait_ge(dve.sem, dve.after(f"norm{j}", i))
                        gp.sem_inc(c.waited)
                        nc.gpsimd.tensor_copy(plast[j][:, :, j:j + 1], probs[:, :, KEYS - 1:KEYS]).then_inc(pool.sem, 1)
                        if j < 3:
                            key_root(j + 1, i)

            @block.tensor
            def _(te):
                pe.first_turn(te)
                for name in ("L1_xattn_Wv", "L1_xattn_Wo"):
                    te.wait_ge(c.loaded[name], 16)
                te.wait_ge(ready, 3 + TB)

                def context_T(j, i):
                    te.wait_ge(dve.sem, dve.after(f"no{j}", i))
                    if j != 1:
                        te.wait_ge(dve.sem, dve.after(f"plT{j-2}", i) if j else dve.after("plT3", i - 1))
                    for m in range(KC):
                        for h in range(2):
                            mm = nc.tensor.transpose(B[0][:, m * D + h * P:m * D + (h + 1) * P], xh[j % 2][:, h, m * P:(m + 1) * P], ident)
                    mm.then_inc(pe.sem, 1)

                def key_square(j, i):
                    te.wait_ge(act.sem, act.after(f"kv1_{j}", i))
                    te.wait_ge(pool.sem, pool.after(f"last{j}", i))
                    if j:
                        te.wait_ge(act.sem, act.after(f"rkB{j-1}", i))
                    for h in range(2):
                        for k in range(KC):
                            mm = nc.tensor.matmul(B[1 + h][:, 0:D + 1], kvT[j % 2][:, k, h * P:(h + 1) * P], s.Cx[:, k, :],
                                                  start=(k == 0), stop=(k == KC - 1))
                    mm.then_inc(pe.sem, 1)

                def key_scale(j, i):
                    te.wait_ge(pool.sem, pool.after(f"rz{j}", i))
                    for h in range(2):
                        nc.tensor.matmul(B[1][:, h * P:(h + 1) * P], rk[:, 2 + h:3 + h].to_broadcast([P, P]), ident, start=True, stop=True)
                    nc.tensor.matmul(B[1][:, KEYS - 1:KEYS], rl[:, 1:2].to_broadcast([TB, P]), ident[0:TB, j:j + 1],
                                     start=True, stop=True).then_inc(pe.sem, 1)

                def scores(j, i):
                    if j:
                        te.wait_ge(dve.sem, dve.after(f"max{j-1}", i))
                    for g in range(3):
                        for k in range(KC):
                            mm = nc.tensor.matmul(B[3 + g][:, 0:KEYS], QT[:, k, j, 4 * g:4 * g + 4, :].rearrange("p h q -> p (h q)"), kvT[j % 2][:, k, :],
                                                  start=(k == 0), stop=(k == KC - 1))
                    mm.then_inc(pe.sem, 1)

                with te.Fori(0, NT) as i:
                    te.wait_ge(dve.sem, dve.after("res", i - 1))
                    te.wait_ge(act.sem, act.after("aT", i - 1))
                    for m in range(KC):
                        for h in range(HEADS1):
                            mm = nc.tensor.matmul(B[3 * m + h // 4][:, (h % 4) * P:(h % 4 + 1) * P], s.WkgZ[:, h, m * P:(m + 1) * P],
                                                  s.qT[:, h // 2, bass.ds(i * P, P)], start=True, stop=True)
                        mm.then_inc(pe.sem, 1)
                    for j in J:
                        mm = nc.tensor.matmul(B[6][:, j * HEADS1:(j + 1) * HEADS1], spread[:, j * P:(j + 1) * P],
                                              s.qb[:, bass.ds(i, 1), :].rearrange("p t h -> p (t h)"), start=True, stop=True)
                    mm.then_inc(pe.sem, 1)
                    te.wait_ge(dve.sem, dve.after("lno", i))
                    te.sem_inc(c.waited)
                    for m in range(KC):
                        mm = nc.tensor.transpose(B[7][:, m * TB:(m + 1) * TB], xl[:, m * P:(m + 1) * P], ident[0:TB, 0:TB])
                    mm.then_inc(pe.sem, 1)
                    te.wait_ge(dve.sem, dve.after("lT", i))
                    for k in range(KC):
                        mm = nc.tensor.matmul(B[7][0:TB, 0:D + 1], xlT[:, k, :], s.Cx[:, k, :], start=(k == 0), stop=(k == KC - 1))
                    mm.then_inc(pe.sem, 1)
                    te.wait_ge(act.sem, act.after("QT1", i))
                    te.wait_ge(dve.sem, dve.after("QT0", i))
                    context_T(0, i)
                    key_square(0, i)
                    key_scale(0, i)
                    scores(0, i)
                    for j in J:
                        if j < 3:
                            context_T(j + 1, i)
                            key_square(j + 1, i)
                        te.wait_ge(pool.sem, pool.after(f"plast{j}", i))
                        if j:
                            te.wait_ge(act.sem, act.after(f"U{j-1}", i))
                            te.wait_ge(dve.sem, dve.after(f"U{j-1}", i))
                        if j < 3:
                            te.wait_ge(act.sem, act.after(f"kv1_{j+1}", i))
                        for g in range(3):
                            for h in range(2):
                                nc.tensor.transpose(B[6 + h][:, g * P:(g + 1) * P], probs[:, g, h * P:(h + 1) * P], ident)
                        for g in range(3):
                            mm = nc.tensor.transpose(B[0][0:TB, g * P:(g + 1) * P], plast[j][:, g, :], ident)
                        mm.then_inc(pe.sem, 1)
                        if j < 3:
                            key_scale(j + 1, i)
                            scores(j + 1, i)
                        te.wait_ge(dve.sem, dve.after(f"plT{j}", i))
                        te.wait_ge(act.sem, act.after(f"pT{j}", i))
                        for m in range(KC):
                            for h in range(2):
                                nc.tensor.matmul(B[6 + m][:, 0:384], xh[j % 2][:, h, m * P:(m + 1) * P], probsT[:, h, :],
                                                 start=(h == 0), stop=False)
                            mm = nc.tensor.matmul(B[6 + m][:, 0:384], xl[:, m * P:(m + 1) * P], plastT[:, :], start=False, stop=True)
                        mm.then_inc(pe.sem, 1)
                    te.wait_ge(act.sem, act.after("U3", i))
                    te.wait_ge(dve.sem, dve.after("U3", i))
                    for h in range(HEADS1):
                        r = slice(64 * (h % 2), 64 * (h % 2) + 64)
                        bank, at = (6, h // 2) if h < 8 else (7, h // 2 - 4)
                        for k in range(KC):
                            mm = nc.tensor.matmul(B[bank][r, at * P:(at + 1) * P], c.w["L1_xattn_Wv"][:, k, h * HD1:(h + 1) * HD1],
                                                  UT[:, k, h, :], start=(k == 0), stop=(k == KC - 1))
                    mm.then_inc(pe.sem, 1)
                    te.wait_ge(act.sem, act.after("aT", i))
                    te.wait_ge(dve.sem, dve.after("aT", i))
                    for p in range(PAIRS):
                        nc.tensor.matmul(B[3][:, 0:D], aT[:, p, :], c.w["L1_xattn_Wo"][:, p, :], start=(p == 0), stop=False)
                    nc.tensor.matmul(B[3][:, 0:D], c.ones[0:1, :], c.row("L1_xattn_bo"), start=False, stop=True).then_inc(pe.sem, 1)

            @block.scalar
            def _(sc):
                act.first_turn(sc)

                def context_out(j, i):
                    sc.wait_ge(pe.sem, pe.after(f"xT{j}", i))
                    sc.wait_ge(pe.sem, pe.after(f"sc{j-2}", i) if j > 1 else pe.after(f"sc{j+2}", i - 1))
                    for m in range(KC):
                        nc.scalar.activation(kvT[j % 2][:, m, 0:D], B[0][:, m * D:(m + 1) * D], ACT.Identity,
                                             scale=c.col("L1_xattn_tab_g", m), bias=c.col("L1_xattn_tab_b", m)).then_inc(act.sem, 1)

                def scale_out(j, i):
                    sc.wait_ge(pe.sem, pe.after(f"rk{j}", i))
                    sc.wait_ge(dve.sem, dve.after(f"max{j-1 if j else 3}", i if j else i - 1))
                    nc.scalar.copy(rkB[:, :], B[1][:, 0:KEYS]).then_inc(act.sem, 1)

                def exps(j, i):
                    sc.wait_ge(dve.sem, dve.after(f"nb{j}", i))
                    sc.wait_ge(pe.sem, pe.after(f"pT{j-1 if j else 3}", i if j else i - 1))
                    for g in range(3):
                        nc.scalar.activation(probs[:, g, :], sco[:, g, :], ACT.Exp, bias=nb[:, g:g + 1],
                                             accum_out=total[:, g:g + 1]).then_inc(act.sem, 1)

                with sc.Fori(0, NT) as i:
                    sc.wait_ge(pe.sem, pe.after("QT1", i))
                    nc.scalar.copy(QT[:, 1, :, :, :].rearrange("p b h q -> p h b q"), by_head(3)).then_inc(act.sem, 1)
                    context_out(0, i)
                    scale_out(0, i)
                    exps(0, i)
                    for j in J:
                        if j < 3:
                            context_out(j + 1, i)
                        sc.wait_ge(pe.sem, pe.after(f"pT{j}", i))
                        sc.wait_ge(pe.sem, pe.after(f"U{j-1 if j else 3}", i if j else i - 1))
                        nc.scalar.copy(probsT[:, 1, :], B[7][:, 0:384]).then_inc(act.sem, 1)
                        if j < 3:
                            scale_out(j + 1, i)
                            exps(j + 1, i)
                        sc.wait_ge(pe.sem, pe.after(f"U{j}", i))
                        nc.scalar.activation(UT[:, 1, :, j * S:(j + 1) * S], B[7][:, 0:384].rearrange("p (h q) -> p h q", h=HEADS1),
                                             ACT.Identity, scale=c.col("L1_xattn_tab_g", 1), bias=c.col("L1_xattn_tab_b", 1)).then_inc(act.sem, 1)
                    sc.wait_ge(pe.sem, pe.after("V", i))
                    nc.scalar.copy(aT[:, 4:6, :].rearrange("p a n -> p (a n)"), B[7][:, 0:2 * P]).then_inc(act.sem, 1)

            @block.vector
            def _(ve):
                dve.first_turn(ve)
                ve.wait_ge(ready, 3 + TB)

                def context_norm(j, i):
                    ve.wait_ge(ctx_in[j], 16 * (i + 1))
                    for h in range(2):
                        op = nc.vector.bn_stats(kst[:, h, :], ck[j % 2][:, h, :])
                    op.then_inc(dve.sem, 1)
                    ve.wait_ge(dve.sem, dve.after(f"st{j}", i))
                    ve.sem_inc(c.waited)
                    for h in range(2):
                        op = nc.vector.bn_aggr(kmv[:, h, :], kst[:, h, :])
                    op.then_inc(dve.sem, 1)
                    ve.wait_ge(pool.sem, pool.after(f"rs{j}", i))
                    ve.wait_ge(pe.sem, pe.after(f"U{j-2}", i) if j > 1 else pe.after(f"U{j+2}", i - 1))
                    for h in range(2):
                        op = nc.vector.tensor_scalar(xh[j % 2][:, h, 0:D], ck[j % 2][:, h, :], kmv[:, h, 0:1], krs[:, 2 + h:3 + h],
                                                     ALU.subtract, ALU.mult)
                    op.then_inc(dve.sem, 1)

                def key_variance(j, i):
                    ve.wait_ge(pe.sem, pe.after(f"Z{j}", i))
                    for h in range(2):
                        op = nc.vector.tensor_tensor_reduce(junk[:, h, :], B[1 + h][:, 0:D + 1], xh[j % 2][:, h, :], 1.0, 0.0,
                                                            ALU.mult, ALU.add, kvar[:, h:h + 1])
                    op.then_inc(dve.sem, 1)

                def row_max(j, i):
                    ve.wait_ge(act.sem, act.after(f"rkB{j}", i))
                    ve.wait_ge(act.sem, act.after(f"ec{j-1 if j else 3}", i if j else i - 1))
                    ve.wait_ge(pe.sem, pe.after(f"sc{j}", i))
                    ve.sem_inc(c.waited)
                    for g in range(3):
                        op = nc.vector.tensor_tensor_reduce(sco[:, g, :], B[3 + g][:, 0:KEYS], rkB[:, :], 1.0, -3.0e38,
                                                            ALU.mult, ALU.max, mx[:, g:g + 1])
                    op.then_inc(dve.sem, 1)
                    ve.wait_ge(dve.sem, dve.after(f"max{j}", i))
                    nc.vector.tensor_tensor(top[:, :], mx[:, :], qcol[:, j, :], ALU.add).then_inc(dve.sem, 1)
                    ve.wait_ge(dve.sem, dve.after(f"top{j}", i))
                    nc.vector.tensor_tensor(nb[:, :], qcol[:, j, :], top[:, :], ALU.subtract).then_inc(dve.sem, 1)

                with ve.Fori(0, NT) as i:
                    ve.wait_ge(last_in, 16 * (i + 1))
                    ve.wait_ge(pe.sem, pe.after("U3", i - 1))
                    ve.sem_inc(c.waited)
                    nc.vector.bn_stats(lst[:, :], cl[:, :]).then_inc(dve.sem, 1)
                    ve.wait_ge(dve.sem, dve.after("lst", i))
                    ve.sem_inc(c.waited)
                    nc.vector.bn_aggr(lmv[:, :], lst[:, :]).then_inc(dve.sem, 1)
                    ve.wait_ge(pool.sem, pool.after("lrs", i))
                    nc.vector.tensor_scalar(xl[:, 0:D], cl[:, :], lmv[:, 0:1], lrs[:, 1:2], ALU.subtract, ALU.mult).then_inc(dve.sem, 1)
                    ve.wait_ge(pe.sem, pe.after("QT0", i))
                    nc.vector.tensor_copy(QT[:, 0, :, :, :].rearrange("p b h q -> p h b q"), by_head(0)).then_inc(dve.sem, 1)
                    ve.wait_ge(pe.sem, pe.after("qb", i))
                    nc.vector.tensor_tensor(qsel[:, :, :, :].rearrange("p b g h -> p (b g) h"),
                                            B[6][:, 0:TB * HEADS1].rearrange("p (x h) -> p x h", h=4),
                                            bc(c.hmask[:, :], 1, TB * 3), ALU.mult).then_inc(dve.sem, 1)
                    ve.wait_ge(dve.sem, dve.after("qsel", i))
                    nc.vector.tensor_reduce(qcol[:, :, :].rearrange("p b g -> p (b g)"), qsel[:, :, :, :].rearrange("p b g h -> p (b g) h"),
                                            AX_X, ALU.add).then_inc(dve.sem, 1)
                    ve.wait_ge(pe.sem, pe.after("lT", i))
                    for m in range(KC):
                        op = nc.vector.tensor_scalar(xlT[:, m, :], B[7][:, m * TB:(m + 1) * TB], c.col("L1_xattn_tab_g", m),
                                                     c.col("L1_xattn_tab_b", m), ALU.mult, ALU.add)
                    op.then_inc(dve.sem, 1)
                    ve.wait_ge(pe.sem, pe.after("lZ", i))
                    nc.vector.tensor_tensor_reduce(junkl[:, :], B[7][0:TB, 0:D + 1], xl[:, :], 1.0, 0.0, ALU.mult, ALU.add,
                                                   lvar[:, :]).then_inc(dve.sem, 1)
                    context_norm(0, i)
                    key_variance(0, i)
                    row_max(0, i)
                    for j in J:
                        if j < 3:
                            context_norm(j + 1, i)
                        ve.wait_ge(act.sem, act.after(f"ec{j}", i))
                        nc.vector.reciprocal(rinv[:, :], total[:, :]).then_inc(dve.sem, 1)
                        ve.wait_ge(dve.sem, dve.after(f"rinv{j}", i))
                        for g in range(3):
                            op = nc.vector.tensor_scalar(probs[:, g, :], probs[:, g, :], rinv[:, g:g + 1], None, ALU.mult)
                        op.then_inc(dve.sem, 1)
                        ve.wait_ge(pe.sem, pe.after(f"pT{j}", i))
                        nc.vector.tensor_copy(probsT[:, 0, :], B[6][:, 0:384]).then_inc(dve.sem, 1)
                        if j < 3:
                            key_variance(j + 1, i)
                        nc.vector.tensor_copy(plastT[:, :], B[0][0:TB, 0:384]).then_inc(dve.sem, 1)
                        if j < 3:
                            row_max(j + 1, i)
                        ve.wait_ge(pe.sem, pe.after(f"U{j}", i))
                        nc.vector.tensor_scalar(UT[:, 0, :, j * S:(j + 1) * S], B[6][:, 0:384].rearrange("p (h q) -> p h q", h=HEADS1),
                                                c.col("L1_xattn_tab_g", 0), c.col("L1_xattn_tab_b", 0), ALU.mult, ALU.add).then_inc(dve.sem, 1)
                    ve.wait_ge(pe.sem, pe.after("V", i))
                    nc.vector.tensor_copy(aT[:, 0:4, :].rearrange("p a n -> p (a n)"), B[6][:, :]).then_inc(dve.sem, 1)
                    ve.wait_ge(pe.sem, pe.after("out", i))
                    xt = c.X[:, bass.ds(i, 1), :].rearrange("p t d -> p (t d)")
                    nc.vector.tensor_tensor(xt, xt, B[3][:, 0:D], ALU.add).then_inc(dve.sem, 1)


LH, LHD, LVD = 16, 8, 16
GRP = 4


def by_column(x, j):
    return x.rearrange("l (u j) d -> j l u d", j=TB)[j]


def stage_l1_linear(c):
    nc = c.nc
    with ExitStack() as ctx:
        sb = lambda name, shape: c.sb(name, shape, ctx)
        xn, xn2, hT, cT = sb("la_xn", [P, HT, D]), sb("la_xn2", [P, HT, D]), sb("la_hT", [P, KC, HN]), sb("la_cT", [P, KC, HN])
        st, mv, rs = sb("la_st", [P, HT, 6]), sb("la_mv", [P, HT, 2]), sb("la_rs", [P, 2 * HT])
        Wvr, Wtmp = sb("la_Wvr", [P, KC, 2 * LH]), sb("la_Wtmp", [P, 2 * D])
        qk, m1, m2 = (sb(f"la_{n}", [P, HT, D]) for n in ("qk", "m1", "m2"))
        v, gate = sb("la_v", [P, HT, D]), sb("la_gate", [P, HT, D])
        lg, oh, ow = (sb(f"la_{n}", [P, HT * LH, 2]) for n in ("lg", "oh", "ow"))
        dl, nabs, sc_, own, wq = (sb(f"la_{n}", [P, HT * LH]) for n in ("dl", "nabs", "sc", "own", "wq"))
        qe, ke = sb("la_qe", [P, HT, LH, 32]), sb("la_ke", [P, HT, LH, 32])
        qeT, keT = sb("la_qeT", [P, GRP, HN]), sb("la_keT", [P, GRP, HN])
        AT = [sb(f"la_AT{n}", [P, LH * P]) for n in range(2)]
        mu, ms3 = sb("la_mu", [P, HT * LH]), sb("la_ms3", [P, 3, HT * LH])
        gsc = sb("la_gsc", [P, 3, HT * LH])
        ao, y, sq = sb("la_ao", [P, HT, D]), m1, m2
        pT = sb("la_pT", [P, FFP // P, HN])
        u = [sb(f"la_u{n}", [P, HN]) for n in range(2)]
        FC = FFP // P
        T = range(HT)
        mlp = " ".join(f"u{f} w{f}" for f in range(FC))
        pe = c.steps(ctx, "la_pe", "xT qkv g lg cnt T " + " ".join(f"A{t}" for t in T) + " o1 yT out zT " + mlp + " mlp")
        dve = c.steps(ctx, "la_dve", "stats moments norm 2stats 2moments 2norm h0 h1 c0 c1 c0b c1b k v lg dl oh0 oh1 nabs m1 m2a m2b rope "
                      "one sc ow own rown wq wq2 qw qe ke T " + " ".join(f"AT{t}" for t in T) +
                      " mu mus d0 d1 ms yd yg y0 ao0 ao1 3stats 3moments 3norm z0 z1 " + " ".join(f"p{f}" for f in range(FC)) + " xa res0 res1")
        act = c.steps(ctx, "la_act", "silu q g e T sq y1 " + " ".join(f"u{f}" for f in range(FC)))
        pool = c.steps(ctx, "la_pool", "vareps rstd 2vareps 2rstd a b c 3vareps 3rstd")
        stored, turned, ready, wide, folded = (c.sem("la_" + n, ctx) for n in ("stored", "turned", "ready", "wide", "folded"))
        B = c.bank
        ident, causal = c.ident(), c.mask("causal")
        cos, sin = c.mask("cos"), c.mask("sin")

        with nc.Block() as block:
            @block.sync
            def _(sp):
                sp.dma_start(c.dram["turned"].rearrange("(t b) s d -> (b s) t d", b=TB), c.X[:, :, :]).then_inc(stored, 16)
                sp.wait_ge(stored, 16)
                for j in range(TB):
                    sp.dma_start(c.X[j * S:(j + 1) * S, :, :], by_column(c.dram["turned"], j)).then_inc(turned, 16)
                for name, (dst, src) in c.moe_loads.items():
                    sp.dma_start(dst, src).then_inc(c.loaded[name], 16)

            @block.gpsimd
            def _(gp):
                pool.first_turn(gp)
                for n, value in enumerate((1.0 / LVD, EPS, -0.5)):
                    nc.gpsimd.memset(gsc[:, n, :], value).then_inc(ready, 1)
                nc.gpsimd.memset(qe[:, :, :, :], 0.0).then_inc(ready, 1)
                nc.gpsimd.memset(ke[:, :, :, :], 0.0).then_inc(ready, 1)
                gp.wait_ge(ready, 5)
                with gp.Fori(0, 2) as i:
                    rstd_half(c, gp, pool, dve, "", i, mv, rs)
                    rstd_half(c, gp, pool, dve, "2", i, mv, rs)
                    gp.wait_ge(dve.sem, dve.after("ms", i))
                    nc.gpsimd.tensor_tensor(ms3[:, 1, :], ms3[:, 0, :], gsc[:, 0, :], ALU.mult).then_inc(pool.sem, 1)
                    gp.wait_ge(pool.sem, pool.after("a", i))
                    nc.gpsimd.tensor_tensor(ms3[:, 2, :], ms3[:, 1, :], gsc[:, 1, :], ALU.add).then_inc(pool.sem, 1)
                    gp.wait_ge(pool.sem, pool.after("b", i))
                    nc.gpsimd.tensor_tensor(ms3[:, 1, :], ms3[:, 2, :], gsc[:, 2, :], ALU.pow).then_inc(pool.sem, 1)
                    rstd_half(c, gp, pool, dve, "3", i, mv, rs)

            @block.tensor
            def _(te):
                pe.first_turn(te)
                for name in WEIGHTS_L1:
                    te.wait_ge(c.loaded[name], 16)
                te.wait_ge(folded, 3)

                def turn(dst_bank, src):
                    for t in T:
                        for k in range(KC):
                            mm = nc.tensor.transpose(B[dst_bank + k][:, t * P:(t + 1) * P], src[:, t, k * P:(k + 1) * P], ident)
                    mm.then_inc(pe.sem, 1)

                def token_major(out, lhsT, t, w):
                    for k in range(lhsT.shape[1]):
                        mm = nc.tensor.matmul(out, lhsT[:, k, t * P:(t + 1) * P], w[:, k, :], start=(k == 0), stop=(k == lhsT.shape[1] - 1))
                    return mm

                with te.Fori(0, 2) as i:
                    te.wait_ge(dve.sem, dve.after("res1", i - 1))
                    te.wait_ge(dve.sem, dve.after("2norm", i))
                    turn(0, xn2)
                    te.wait_ge(act.sem, act.after("silu", i))
                    for t in T:
                        token_major(B[t][:, 0:D], cT, t, c.w["L1_attn_Wqk"])
                        mm = token_major(B[t][:, D:2 * D], cT, t, c.w["L1_attn_Wv"])
                    mm.then_inc(pe.sem, 1)
                    for t in T:
                        mm = token_major(B[4 + t // 2][:, (t % 2) * D:(t % 2 + 1) * D], cT, t, c.w["L1_attn_Wg"])
                    mm.then_inc(pe.sem, 1)
                    for t in T:
                        mm = token_major(B[6][:, t * 2 * LH:(t + 1) * 2 * LH], cT, t, Wvr)
                    mm.then_inc(pe.sem, 1)
                    te.wait_ge(dve.sem, dve.after("oh1", i))
                    nc.tensor.matmul(B[7][:, 0:HT * 2 * LH], causal, oh[:, :, :].rearrange("p x r -> p (x r)"),
                                     start=True, stop=True).then_inc(pe.sem, 1)
                    te.wait_ge(act.sem, act.after("g", i))
                    te.wait_ge(dve.sem, dve.after("ke", i))
                    for g in range(GRP):
                        for t in T:
                            nc.tensor.transpose(B[g][:, t * P:(t + 1) * P], qe[:, t, GRP * g:GRP * (g + 1), :].rearrange("p h x -> p (h x)"), ident)
                            mm = nc.tensor.transpose(B[4 + g][:, t * P:(t + 1) * P], ke[:, t, GRP * g:GRP * (g + 1), :].rearrange("p h x -> p (h x)"), ident)
                    mm.then_inc(pe.sem, 1)
                    te.wait_ge(act.sem, act.after("T", i))
                    te.wait_ge(dve.sem, dve.after("T", i))

                    def weights(t):
                        if t:
                            te.wait_ge(dve.sem, dve.after(f"AT{t-1}", i))
                        for g in range(GRP):
                            for r in range(GRP):
                                rows = slice(32 * r, 32 * r + 32)
                                mm = nc.tensor.matmul(B[r][:, g * P:(g + 1) * P], keT[rows, g, t * P:(t + 1) * P],
                                                      qeT[rows, g, t * P:(t + 1) * P], start=True, stop=True)
                        mm.then_inc(pe.sem, 1)

                    def outputs(t):
                        te.wait_ge(dve.sem, dve.after(f"AT{t}", i))
                        for h in range(LH):
                            r, g = h % GRP, h // GRP
                            at = (r * GRP + g) * P
                            mm = nc.tensor.matmul(B[4 + t // 2][:, (t % 2) * D + h * LVD:(t % 2) * D + (h + 1) * LVD],
                                                  AT[t % 2][:, at:at + P], v[:, t, h * LVD:(h + 1) * LVD], start=True, stop=True)
                        return mm

                    for t in T:
                        weights(t)
                        if t:
                            outputs(t - 1)
                    outputs(HT - 1).then_inc(pe.sem, 1)
                    te.wait_ge(dve.sem, dve.after("yg", i))
                    turn(6, y)
                    te.wait_ge(dve.sem, dve.after("y0", i))
                    te.wait_ge(act.sem, act.after("y1", i))
                    for t in T:
                        mm = token_major(B[t // 2][:, (t % 2) * D:(t % 2 + 1) * D], hT, t, c.w["L1_attn_Wout"])
                    mm.then_inc(pe.sem, 1)
                    te.wait_ge(dve.sem, dve.after("3norm", i))
                    turn(2, xn2)
                    te.wait_ge(dve.sem, dve.after("z1", i))
                    for f in range(FC):
                        if f >= 4:
                            te.wait_ge(dve.sem, dve.after(f"p{f-4}", i))
                        for n, name in enumerate(("L1_attn_w1", "L1_attn_w3")):
                            for k in range(KC):
                                mm = nc.tensor.matmul(B[2 * (f % 4) + n][:, :], c.w[name][:, k, f * P:(f + 1) * P], cT[:, k, :],
                                                      start=(k == 0), stop=(k == KC - 1))
                            mm.then_inc(pe.sem, 1)
                    te.wait_ge(dve.sem, dve.after(f"p{FC-1}", i))
                    for t in T:
                        mm = token_major(B[t // 2][:, (t % 2) * D:(t % 2 + 1) * D], pT, t, c.w["L1_attn_w2"])
                    mm.then_inc(pe.sem, 1)

            @block.scalar
            def _(sc):
                act.first_turn(sc)
                with sc.Fori(0, 2) as i:
                    sc.wait_ge(dve.sem, dve.after("c1b", i))
                    nc.scalar.activation(cT[:, :, :], cT[:, :, :], ACT.Silu).then_inc(act.sem, 1)
                    sc.wait_ge(pe.sem, pe.after("qkv", i))
                    nc.scalar.activation(qk[:, :, 0:P], c.PS[:, 0:HT, 0:P], ACT.Silu).then_inc(act.sem, 1)
                    sc.wait_ge(pe.sem, pe.after("g", i))
                    nc.scalar.activation(gate[:, :, :].rearrange("p (b t) n -> p b (t n)", b=2), c.PS[:, 4:6, :], ACT.Silu).then_inc(act.sem, 1)
                    sc.wait_ge(dve.sem, dve.after("nabs", i))
                    nc.scalar.activation(nabs[:, :], nabs[:, :], ACT.Exp).then_inc(act.sem, 1)
                    sc.wait_ge(pe.sem, pe.after("T", i))
                    nc.scalar.copy(keT[:, :, :], c.PS[:, 4:8, :]).then_inc(act.sem, 1)
                    sc.wait_ge(dve.sem, dve.after("d1", i))
                    nc.scalar.activation(sq[:, :, :], ao[:, :, :], ACT.Square).then_inc(act.sem, 1)
                    sc.wait_ge(pe.sem, pe.after("yT", i))
                    nc.scalar.copy(hT[:, 1, :], B[7][:, :]).then_inc(act.sem, 1)
                    for f in range(FC):
                        sc.wait_ge(pe.sem, pe.after(f"u{f}", i))
                        if f >= 2:
                            sc.wait_ge(dve.sem, dve.after(f"p{f-2}", i))
                        nc.scalar.activation(u[f % 2][:, :], B[2 * (f % 4)][:, :], ACT.Silu).then_inc(act.sem, 1)

            @block.vector
            def _(ve):
                dve.first_turn(ve)
                for n in WEIGHTS_L1:
                    ve.wait_ge(c.loaded[n], 16)
                ve.wait_ge(c.loaded["repeated"], 16)
                for k in range(KC):
                    ve.wait_ge(folded, k)
                    nc.vector.tensor_tensor(Wtmp[:, :].rearrange("p (h r d) -> p h r d", r=2, d=LVD),
                                            bc(c.w["L1_attn_Wv"][:, k, :].rearrange("p (h d) -> p h d", d=LVD), 2, 2),
                                            c.rep("L1_attn_router_w").rearrange("p (h r d) -> p h r d", r=2, d=LVD), ALU.mult).then_inc(wide, 1)
                    ve.wait_ge(wide, k + 1)
                    nc.vector.tensor_reduce(Wvr[:, k, :], Wtmp[:, :].rearrange("p (x d) -> p x d", d=LVD), AX_X, ALU.add).then_inc(folded, 1)
                ve.wait_ge(turned, 16 * TB)
                nc.vector.memset(dl[:, :], 0.0).then_inc(folded, 1)
                ve.wait_ge(folded, 3)

                def step(op, name, i, wait=True):
                    op.then_inc(dve.sem, 1)
                    if wait:
                        ve.wait_ge(dve.sem, dve.after(name, i))

                with ve.Fori(0, 2) as i:
                    xt = lambda t: c.X[:, bass.ds(i * HT + t, 1), :].rearrange("p t d -> p (t d)")
                    norm_half(c, ve, dve, pool, "", i, xt, lambda t: xn[:, t, :], st, mv, rs)
                    ve.wait_ge(dve.sem, dve.after("norm", i))
                    norm_half(c, ve, dve, pool, "2", i, lambda t: xn[:, t, :], lambda t: xn2[:, t, :], st, mv, rs)
                    ve.wait_ge(pe.sem, pe.after("xT", i))
                    for k in range(KC):
                        nc.vector.tensor_scalar(hT[:, k, :], B[k][:, :], c.col("L1_attn_ln1_w", k), c.col("L1_attn_ln1_b", k),
                                                ALU.mult, ALU.add).then_inc(dve.sem, 1)
                    ve.wait_ge(dve.sem, dve.after("h1", i))
                    for k in range(KC):
                        nc.vector.tensor_scalar(cT[:, k, :], hT[:, k, :], c.col("conv1", k), None, ALU.mult).then_inc(dve.sem, 1)
                    ve.wait_ge(dve.sem, dve.after("c1", i))
                    for k in range(KC):
                        seq = lambda x: x[:, k, :].rearrange("p (b l) -> p b l", l=S)
                        nc.vector.scalar_tensor_tensor(out=seq(cT)[:, :, 1:S], in0=seq(hT)[:, :, 0:S - 1], scalar=c.col("conv0", k),
                                                       in1=seq(cT)[:, :, 1:S], op0=ALU.mult, op1=ALU.add).then_inc(dve.sem, 1)
                    ve.wait_ge(pe.sem, pe.after("qkv", i))
                    ve.wait_ge(act.sem, act.after("q", i))
                    step(nc.vector.tensor_copy(qk[:, :, P:D], c.PS[:, 0:HT, P:D]), "k", i, False)
                    step(nc.vector.tensor_copy(v[:, :, :], c.PS[:, 0:HT, D:2 * D]), "v", i, False)
                    ve.wait_ge(pe.sem, pe.after("lg", i))
                    step(nc.vector.tensor_copy(lg[:, :, :].rearrange("p x r -> p (x r)"), B[6][:, 0:HT * 2 * LH]), "lg", i)
                    l0, l1 = (lg[:, :, r:r + 1].rearrange("p x r -> p (x r)") for r in range(2))
                    step(nc.vector.tensor_tensor(dl[:, :], l0, l1, ALU.subtract), "dl", i)
                    step(nc.vector.tensor_scalar(oh[:, :, 0:1], dl[:, :].unsqueeze(2), 0.0, None, ALU.is_ge), "oh0", i, False)
                    step(nc.vector.tensor_scalar(oh[:, :, 1:2], dl[:, :].unsqueeze(2), 0.0, None, ALU.is_lt), "oh1", i, False)
                    step(nc.vector.scalar_tensor_tensor(out=nabs[:, :], in0=dl[:, :], scalar=-1.0, in1=dl[:, :],
                                                        op0=ALU.mult, op1=ALU.min), "nabs", i, False)
                    pair = lambda x: x[:, :, :].rearrange("p t (h two d) -> p (t h) two d", two=2, d=4)
                    X4 = HT * D // 8
                    ve.wait_ge(dve.sem, dve.after("k", i))
                    step(nc.vector.tensor_tensor(pair(m1), pair(qk), cos.unsqueeze(1).unsqueeze(1).to_broadcast([P, X4, 2, 4]), ALU.mult), "m1", i, False)
                    sin3 = bc(sin, 1, X4)
                    step(nc.vector.scalar_tensor_tensor(out=pair(m2)[:, :, 0, :], in0=pair(qk)[:, :, 1, :], scalar=-1.0, in1=sin3,
                                                        op0=ALU.mult, op1=ALU.mult), "m2a", i, False)
                    step(nc.vector.tensor_tensor(pair(m2)[:, :, 1, :], pair(qk)[:, :, 0, :], sin3, ALU.mult), "m2b", i)
                    step(nc.vector.tensor_tensor(qk[:, :, :], m1[:, :, :], m2[:, :, :], ALU.add), "rope", i, False)
                    ve.wait_ge(act.sem, act.after("e", i))
                    step(nc.vector.tensor_scalar(nabs[:, :], nabs[:, :], 1.0, None, ALU.add), "one", i)
                    step(nc.vector.reciprocal(sc_[:, :], nabs[:, :]), "sc", i, False)
                    ve.wait_ge(pe.sem, pe.after("cnt", i))
                    step(nc.vector.tensor_tensor(ow[:, :, :].rearrange("p x r -> p (x r)"), B[7][:, 0:HT * 2 * LH],
                                                 oh[:, :, :].rearrange("p x r -> p (x r)"), ALU.mult), "ow", i)
                    step(nc.vector.tensor_tensor(own[:, :].unsqueeze(2), ow[:, :, 0:1], ow[:, :, 1:2], ALU.add), "own", i)
                    step(nc.vector.reciprocal(own[:, :], own[:, :]), "rown", i)
                    step(nc.vector.tensor_tensor(wq[:, :], sc_[:, :], own[:, :], ALU.mult), "wq", i)
                    step(nc.vector.tensor_scalar(wq[:, :], wq[:, :], float(LHD) ** -0.5, None, ALU.mult), "wq2", i)
                    ve.wait_ge(dve.sem, dve.after("rope", i))
                    q_, k_ = qk[:, :, 0:P], qk[:, :, P:D]
                    head = lambda x: x.rearrange("p t (h d) -> p t h d", d=LHD)
                    step(nc.vector.tensor_tensor(head(m1[:, :, 0:P]), head(q_),
                                                 bc(wq[:, :].rearrange("p (t h) -> p t h", t=HT), 3, LHD), ALU.mult), "qw", i)
                    for t in T:
                        for name, dst, src in (("qe", qe, m1[:, t, 0:P]),):
                            op = nc.vector.tensor_tensor(dst[:, t, :, 0:2 * LHD].rearrange("p h (r d) -> p h r d", r=2),
                                                         bc(src.rearrange("p (h d) -> p h d", d=LHD), 2, 2),
                                                         bc(oh[:, t * LH:(t + 1) * LH, :], 3, LHD), ALU.mult)
                    op.then_inc(dve.sem, 1)
                    for t in T:
                        op = nc.vector.tensor_tensor(ke[:, t, :, 0:2 * LHD].rearrange("p h (r d) -> p h r d", r=2),
                                                     bc(qk[:, t, P:D].rearrange("p (h d) -> p h d", d=LHD), 2, 2),
                                                     bc(oh[:, t * LH:(t + 1) * LH, :], 3, LHD), ALU.mult)
                    op.then_inc(dve.sem, 1)
                    ve.wait_ge(pe.sem, pe.after("T", i))
                    step(nc.vector.tensor_copy(qeT[:, :, :], c.PS[:, 0:4, :]), "T", i, False)
                    for t in T:
                        ve.wait_ge(pe.sem, pe.after(f"A{t}", i))
                        step(nc.vector.tensor_tensor(AT[t % 2][:, :].rearrange("p (x n) -> p x n", n=P),
                                                     c.PS[:, 0:4, :].rearrange("p b n -> p (b n)").rearrange("p (x n) -> p x n", n=P),
                                                     bc(causal, 1, LH), ALU.mult), f"AT{t}", i, False)
                    ve.wait_ge(pe.sem, pe.after("o1", i))
                    heads = lambda x: x.rearrange("p (x d) -> p x d", d=LVD)
                    o2 = c.PS[:, 4:6, :].rearrange("p b n -> p (b n)")
                    step(nc.vector.tensor_reduce(mu[:, :], heads(o2), AX_X, ALU.add), "mu", i)
                    step(nc.vector.tensor_scalar(mu[:, :], mu[:, :], 1.0 / LVD, None, ALU.mult), "mus", i)
                    for n in range(2):
                        step(nc.vector.tensor_tensor(heads(ao[:, 2 * n:2 * n + 2, :].rearrange("p t n -> p (t n)")), heads(B[4 + n][:, :]),
                                                     bc(mu[:, 2 * LH * n:2 * LH * (n + 1)], 2, LVD), ALU.subtract), f"d{n}", i, False)
                    ve.wait_ge(act.sem, act.after("sq", i))
                    step(nc.vector.tensor_reduce(ms3[:, 0, :], heads(sq[:, :, :].rearrange("p t n -> p (t n)")), AX_X, ALU.add), "ms", i, False)
                    ve.wait_ge(pool.sem, pool.after("c", i))
                    step(nc.vector.tensor_tensor(heads(y[:, :, :].rearrange("p t n -> p (t n)")), heads(ao[:, :, :].rearrange("p t n -> p (t n)")),
                                                 bc(ms3[:, 1, :], 2, LVD), ALU.mult), "yd", i)
                    step(nc.vector.tensor_tensor(y[:, :, :], y[:, :, :], gate[:, :, :], ALU.mult), "yg", i, False)
                    ve.wait_ge(pe.sem, pe.after("yT", i))
                    step(nc.vector.tensor_copy(hT[:, 0, :], B[6][:, :]), "y0", i, False)
                    ve.wait_ge(pe.sem, pe.after("out", i))
                    for n in range(2):
                        step(nc.vector.tensor_tensor(ao[:, 2 * n:2 * n + 2, :].rearrange("p t n -> p (t n)"), B[n][:, :],
                                                     xn[:, 2 * n:2 * n + 2, :].rearrange("p t n -> p (t n)"), ALU.add), f"ao{n}", i)
                    norm_half(c, ve, dve, pool, "3", i, lambda t: ao[:, t, :], lambda t: xn2[:, t, :], st, mv, rs)
                    ve.wait_ge(pe.sem, pe.after("zT", i))
                    for k in range(KC):
                        step(nc.vector.tensor_scalar(cT[:, k, :], B[2 + k][:, :], c.col("L1_attn_ln2_w", k), c.col("L1_attn_ln2_b", k),
                                                     ALU.mult, ALU.add), f"z{k}", i, False)
                    for f in range(FC):
                        ve.wait_ge(pe.sem, pe.after(f"w{f}", i))
                        ve.wait_ge(act.sem, act.after(f"u{f}", i))
                        step(nc.vector.tensor_tensor(pT[:, f, :], u[f % 2][:, :], B[2 * (f % 4) + 1][:, :], ALU.mult), f"p{f}", i, False)
                    xx = c.X[:, bass.ds(i * HT, HT), :]
                    step(nc.vector.tensor_tensor(xx, xx, ao[:, :, :], ALU.add), "xa", i)
                    ve.wait_ge(pe.sem, pe.after("mlp", i))
                    for n in range(2):
                        xx = c.X[:, bass.ds(i * HT + 2 * n, 2), :]
                        step(nc.vector.tensor_tensor(xx, xx, B[n][:, :].rearrange("p (t n) -> p t n", t=2), ALU.add), f"res{n}", i, False)


def stage_moe(c):
    nc = c.nc
    with ExitStack() as ctx:
        sb = lambda name, shape: c.sb(name, shape, ctx)
        xn, xnT = sb("mo_xn", [P, HT, D]), sb("mo_xnT", [P, KC, HN])
        st, mv, rs = sb("mo_st", [P, HT, 6]), sb("mo_mv", [P, HT, 2]), sb("mo_rs", [P, 2 * HT])
        fst, fmv, frs = sb("mo_fst", [P, 6]), sb("mo_fmv", [P, 2]), sb("mo_frs", [P, 2])
        fn, fT = sb("mo_fn", [P, D]), sb("mo_fT", [P, KC, TB, S])
        sco = sb("mo_sco", [P, NE])
        more, same, rank = sb("mo_more", [P, NE, NE]), sb("mo_same", [P, NE, NE]), sb("mo_rank", [P, NE])
        G, GT, bias2 = sb("mo_G", [P, NE]), sb("mo_GT", [NE, P]), sb("mo_bias2", [P, D])
        hT = [sb(f"mo_hT{n}", [P, KC, HN]) for n in range(2)]
        E = range(NE)
        pe = c.steps(ctx, "mo_pe", "xT h0 " + " ".join((f"h{e+1} " if e < NE - 1 else "") + f"o{e}" for e in E))
        dve = c.steps(ctx, "mo_dve", "stats moments norm xT0 bias " + " ".join(f"a{e} b{e}" for e in E))
        act = c.steps(ctx, "mo_act", "xT1 " + " ".join(f"h{e}" for e in E))
        pool = c.steps(ctx, "mo_pool", "vareps rstd")
        rv, rp, rg = (c.sem("mo_route_" + n, ctx) for n in ("dve", "pe", "pool"))
        B = c.bank
        ident = c.ident()

        with nc.Block() as block:
            @block.gpsimd
            def _(gp):
                pool.first_turn(gp)
                gp.wait_ge(rv, 2)
                nc.gpsimd.tensor_tensor(frs[:, 0:1], fmv[:, 1:2], c.eps[:, 0:1], ALU.add).then_inc(rg, 1)
                gp.wait_ge(rg, 1)
                nc.gpsimd.tensor_tensor(frs[:, 1:2], frs[:, 0:1], c.mhalf[:, 0:1], ALU.pow).then_inc(rg, 1)
                with gp.Fori(0, 2) as i:
                    rstd_half(c, gp, pool, dve, "", i, mv, rs)

            @block.tensor
            def _(te):
                pe.first_turn(te)
                for name in c.moe_loads:
                    te.wait_ge(c.loaded[name], 16)
                te.wait_ge(rv, 3)
                for k in range(KC):
                    mm = nc.tensor.transpose(B[0][:, k * P:(k + 1) * P], fn[:, k * P:(k + 1) * P], ident)
                mm.then_inc(rp, 1)
                te.wait_ge(rv, 4)
                for k in range(KC):
                    nc.tensor.matmul(B[1][:, 0:NE], fT[:, k, :, :].rearrange("p b s -> p (b s)"), c.Wr[:, k, :], start=(k == 0), stop=False)
                nc.tensor.matmul(B[1][:, 0:NE], c.ones[0:1, :], c.row("L1_ffn_br"), start=False, stop=True).then_inc(rp, 1)
                te.wait_ge(rv, 11)
                nc.tensor.transpose(B[2][0:NE, 0:P], G[:, :], ident).then_inc(rp, 1)
                te.wait_ge(rv, 12)
                nc.tensor.matmul(B[3][:, 0:D], GT[:, :], c.moe_b2[:, :], start=True, stop=True).then_inc(rp, 1)
                te.wait_ge(rv, 13)

                def hidden(e, i):
                    if e >= 2:
                        te.wait_ge(act.sem, act.after(f"h{e-2}", i))
                    for m in range(KC):
                        for k in range(KC):
                            mm = nc.tensor.matmul(B[2 * (e % 2) + m][:, :], c.moe_W1[:, KC * e + k, m * P:(m + 1) * P], xnT[:, k, :],
                                                  start=(k == 0), stop=(k == KC - 1))
                    mm.then_inc(pe.sem, 1)

                with te.Fori(0, 2) as i:
                    te.wait_ge(act.sem, act.after(f"h{NE-1}", i - 1))
                    te.wait_ge(dve.sem, dve.after("norm", i))
                    for t in range(HT):
                        for k in range(KC):
                            mm = nc.tensor.transpose(B[k][:, t * P:(t + 1) * P], xn[:, t, k * P:(k + 1) * P], ident)
                    mm.then_inc(pe.sem, 1)
                    te.wait_ge(dve.sem, dve.after("xT0", i))
                    te.wait_ge(act.sem, act.after("xT1", i))
                    hidden(0, i)
                    for e in E:
                        if e < NE - 1:
                            hidden(e + 1, i)
                        te.wait_ge(act.sem, act.after(f"h{e}", i))
                        te.wait_ge(dve.sem, dve.after(f"b{e-2}", i) if e >= 2 else dve.after(f"b{e+NE-2}", i - 1))
                        for t in range(HT):
                            for k in range(KC):
                                mm = nc.tensor.matmul(B[4 + 2 * (e % 2) + t // 2][:, (t % 2) * D:(t % 2 + 1) * D],
                                                      hT[e % 2][:, k, t * P:(t + 1) * P], c.moe_W2[:, KC * e + k, :],
                                                      start=(k == 0), stop=(k == KC - 1))
                        mm.then_inc(pe.sem, 1)

            @block.scalar
            def _(sc):
                act.first_turn(sc)
                with sc.Fori(0, 2) as i:
                    sc.wait_ge(pe.sem, pe.after("xT", i))
                    nc.scalar.copy(xnT[:, 1, :], B[1][:, :]).then_inc(act.sem, 1)
                    for e in E:
                        sc.wait_ge(pe.sem, pe.after(f"h{e}", i))
                        sc.wait_ge(pe.sem, pe.after(f"o{e-2}", i) if e >= 2 else pe.after(f"o{e+NE-2}", i - 1))
                        for m in range(KC):
                            op = nc.scalar.activation(hT[e % 2][:, m, :], B[2 * (e % 2) + m][:, :], ACT.Gelu,
                                                      bias=c.col("L1_ffn_b1", KC * e + m))
                        op.then_inc(act.sem, 1)

            @block.vector
            def _(ve):
                dve.first_turn(ve)
                nc.vector.bn_stats(fst[:, :], c.X[:, 0, :]).then_inc(rv, 1)
                ve.wait_ge(rv, 1)
                nc.vector.bn_aggr(fmv[:, :], fst[:, :]).then_inc(rv, 1)
                ve.wait_ge(rg, 2)
                nc.vector.tensor_scalar(fn[:, :], c.X[:, 0, :], fmv[:, 0:1], frs[:, 1:2], ALU.subtract, ALU.mult).then_inc(rv, 1)
                ve.wait_ge(rp, 1)
                nc.vector.tensor_copy(fT[:, :, :, :], bc(B[0][:, 0:D].rearrange("p (k n) -> p k n", k=KC)[:, :, 0:S], 2, TB)).then_inc(rv, 1)
                ve.wait_ge(rp, 2)
                nc.vector.tensor_copy(sco[:, :], B[1][:, 0:NE]).then_inc(rv, 1)
                ve.wait_ge(rv, 5)
                other, self_ = bc(sco[:, :], 1, NE), bc(sco[:, :], 2, NE)
                nc.vector.tensor_tensor(more[:, :, :], other, self_, ALU.is_gt).then_inc(rv, 1)
                nc.vector.tensor_tensor(same[:, :, :], other, self_, ALU.is_equal).then_inc(rv, 1)
                ve.wait_ge(rv, 7)
                nc.vector.tensor_tensor(same[:, :, :], same[:, :, :], c.mask("earlier").rearrange("p (e j) -> p e j", e=NE), ALU.mult).then_inc(rv, 1)
                ve.wait_ge(rv, 8)
                nc.vector.tensor_tensor(more[:, :, :], more[:, :, :], same[:, :, :], ALU.add).then_inc(rv, 1)
                ve.wait_ge(rv, 9)
                nc.vector.tensor_reduce(rank[:, :], more[:, :, :], AX_X, ALU.add).then_inc(rv, 1)
                ve.wait_ge(rv, 10)
                nc.vector.tensor_scalar(G[:, :], rank[:, :], 2.0, 0.5, ALU.is_lt, ALU.mult).then_inc(rv, 1)
                ve.wait_ge(rp, 3)
                nc.vector.tensor_copy(GT[:, :], B[2][0:NE, 0:P]).then_inc(rv, 1)
                ve.wait_ge(rp, 4)
                nc.vector.tensor_copy(bias2[:, :], B[3][:, 0:D]).then_inc(rv, 1)
                ve.wait_ge(rv, 13)
                with ve.Fori(0, 2) as i:
                    xt = lambda t: c.X[:, bass.ds(i * HT + t, 1), :].rearrange("p t d -> p (t d)")
                    norm_half(c, ve, dve, pool, "", i, xt, lambda t: xn[:, t, :], st, mv, rs)
                    ve.wait_ge(pe.sem, pe.after("xT", i))
                    nc.vector.tensor_copy(xnT[:, 0, :], B[0][:, :]).then_inc(dve.sem, 1)
                    xx = c.X[:, bass.ds(i * HT, HT), :]
                    nc.vector.tensor_tensor(xx, xx, bc(bias2[:, :], 1, HT), ALU.add).then_inc(dve.sem, 1)
                    ve.wait_ge(dve.sem, dve.after("bias", i))
                    for e in E:
                        ve.wait_ge(pe.sem, pe.after(f"o{e}", i))
                        if e:
                            ve.wait_ge(dve.sem, dve.after(f"b{e-1}", i))
                        for n in range(2):
                            xx = c.X[:, bass.ds(i * HT + 2 * n, 2), :]
                            nc.vector.scalar_tensor_tensor(out=xx, in0=B[4 + 2 * (e % 2) + n][:, :].rearrange("p (t n) -> p t n", t=2),
                                                           scalar=G[:, e:e + 1], in1=xx, op0=ALU.mult, op1=ALU.add).then_inc(dve.sem, 1)


def build(nc, dram):
    with ExitStack() as ctx:
        c = Core(nc, ctx, dram)
        for n, stage in enumerate(STAGES):
            stage(c)
            if n == 2:
                c.l0.close()
            if n == 3:
                c.cross.close()
                c.moe_W1, c.moe_W2 = c.sb("moe_W1_sb", [P, NE * KC, D]), c.sb("moe_W2_sb", [P, NE * KC, D])
                c.moe_b2, c.Wr = c.sb("moe_b2_sb", [NE, D]), c.sb("moe_Wr_sb", [P, KC, NE])
                c.moe_loads = {
                    "moe_W1": (c.moe_W1[:, :, :], dram["moe_W1"].rearrange("(c p) n -> p c n", p=P)),
                    "moe_W2": (c.moe_W2[:, :, :], dram["moe_W2"].rearrange("(c p) n -> p c n", p=P)),
                    "moe_b2": (c.moe_b2[:, :], dram["moe_b2"]),
                    "moe_Wr": (c.Wr[:, :, :], dram["L1_ffn_Wr"].rearrange("(c p) n -> p c n", p=P)),
                }
                c.loaded.update({n: c.sem(n + "_in") for n in c.moe_loads})
        stored = c.sem("stored")
        with nc.Block() as block:
            @block.sync
            def _(sp):
                for j in range(TB):
                    sp.dma_start(by_column(dram["out"], j), c.X[j * S:(j + 1) * S, :, :]).then_inc(stored, 16)
                sp.wait_ge(stored, 16 * TB)


STAGES = [stage_l0_cross, stage_l0_gla, stage_l0_ffn, stage_l1_cross, stage_l1_linear, stage_moe]


def masks():
    p = np.arange(P)
    inv_freq = 1.0 / np.float32(10000.0) ** (np.arange(0, 4, dtype=np.float32) * np.float32(2.0) / np.float32(8.0))
    angles = (p[:, None] % S).astype(np.float32) * inv_freq.astype(np.float32)[None]
    m = {
        "ident": np.eye(P),
        "fold": p[:, None] % S == np.arange(S),
        "hmask": p[:, None] // S == np.arange(4),
        "qmask": (p[:, None] // 16 == np.arange(8)) * 0.25,
        "causal": (p[:, None] // S == p // S) & (p[:, None] <= p),
        "spread": np.concatenate([p[:, None] == b * S + p % S for b in range(TB)], axis=1),
        "half": (p[:, None] // 64 == np.arange(2)) * 0.125,
        "cos": np.cos(angles), "sin": np.sin(angles),
        "earlier": np.broadcast_to((np.arange(NE)[None, :] < np.arange(NE)[:, None]).reshape(1, -1), (P, NE * NE)),
    }
    return np.concatenate([m[n].astype(np.float32) for n in MASKS], axis=1)


def kernel(**inputs):
    import concourse.bacc as _bacc
    from concourse.bass_utils import run_bass_kernel_spmd as _run

    a = {n: np.asarray(v) for n, v in inputs.items()}
    ctx = a["ctx_1024"]
    a["conv0"], a["conv1"] = a["L1_attn_conv_w"].T
    a["L1_attn_router_w"] = a["L1_attn_router_w"].transpose(0, 2, 1)
    a["L1_attn_Wqk"] = np.concatenate([a["L1_attn_Wq"], a["L1_attn_Wk"]], axis=1)
    for n in ("L1_attn_w1", "L1_attn_w3"):
        a[n] = np.pad(a[n], ((0, 0), (0, FFP - FF)))
    a["L1_attn_w2"] = np.pad(a["L1_attn_w2"], ((0, FFP - FF), (0, 0)))
    a["moe_W1"], a["moe_W2"] = a["L1_ffn_W1"].reshape(NE * D, D), a["L1_ffn_W2"].reshape(NE * D, D)
    arrays = {
        "x": a["x"].reshape(NT, P, D).transpose(1, 0, 2),
        "ctxT": ctx.transpose(0, 2, 1),
        "ctx_lastT": ctx[:, KEYS - 1].T,
        "masks": masks(),
        "cols": np.concatenate([a[n].reshape(-1, P).T for n in COLS], axis=1),
        "repeated": np.broadcast_to(np.concatenate([a[n].reshape(-1) for n in REPEATED]), (P, REP_N)),
        "ctx": ctx[:, 0:KEYS - 1].reshape(NB, 2, P, D).transpose(0, 2, 1, 3),
        "ctx_last": ctx[:, KEYS - 1],
        "W_exp": a["L0_ffn_W_exp"],
        "W_conT": a["L0_ffn_W_con"].T,
        "b_exp": a["L0_ffn_b_exp"][None],
        "bf_weights": np.concatenate([w.reshape(STAGES_BF, F0 // 2, 4).transpose(0, 2, 1) for w in
                                      (a["L0_ffn_up_weights"], a["L0_ffn_down_weights"][::-1])]),
        "L0_attn_Wgk2": a["L0_attn_Wgk2"],
        "rows": np.concatenate([a[n] for n in ROWS])[None],
    }
    arrays["moe_b2"], arrays["L1_ffn_Wr"] = a["L1_ffn_b2"], a["L1_ffn_Wr"]
    arrays["moe_W1"], arrays["moe_W2"] = a["moe_W1"], a["moe_W2"]
    for n in (*WEIGHTS_L0, *WEIGHTS_CROSS, *WEIGHTS_L1):
        arrays[n] = a[n].T if n.startswith("L0_xattn") else a[n]
    nc = _bacc.Bacc("TRN2", target_bir_lowering=False, num_devices=1)
    dram, feed = {}, {}
    for n, v in arrays.items():
        feed["in_" + n] = np.ascontiguousarray(v)
        dram[n] = nc.dram_tensor("in_" + n, v.shape, F32, kind="ExternalInput").ap()
    dram["turned"] = nc.dram_tensor("turned", (NB, S, D), F32, kind="Internal").ap()
    dram["out"] = nc.dram_tensor("out_0", (NB, S, D), F32, kind="ExternalOutput").ap()
    build(nc, dram)
    r = _run(nc, [feed], core_ids=[0])
    return r.results[0]["out_0"]
```

```python
from contextlib import ExitStack

import numpy as np
import concourse.bass as bass
from concourse import mybir

F32 = mybir.dt.float32
I32 = mybir.dt.int32
ALU = mybir.AluOpType
ACT = mybir.ActivationFunctionType
AX_X = mybir.AxisListType.X

P = 128
NB, S, D = 32, 32, 256
KEYS = 257
TB = P // S
NT = NB // TB
KC = D // P
EPS = 1e-5


class Steps:

    def __init__(self, sem, names):
        self.sem = sem
        self.names = [n.removesuffix("'") for n in names.split()]
        self.ahead = {n.removesuffix("'") for n in names.split() if n.endswith("'")}
        self.per_turn = len(self.names)
        self.counted = 0
        assert len(set(self.names)) == self.per_turn, names

    def skip_to(self, eng, name, steps):
        at = self.names.index(name)
        if self.counted:
            eng.wait_ge(self.sem, self.counted)
        eng.sem_inc(self.sem, at - self.counted)
        self.counted = at + steps

    def skip_to_end(self, eng):
        eng.wait_ge(self.sem, self.counted)
        if self.counted < self.per_turn:
            eng.sem_inc(self.sem, self.per_turn - self.counted)

    def first_turn(self, eng):
        eng.sem_inc(self.sem, self.per_turn)

    def after(self, name, turn):
        return (turn + (0 if name in self.ahead else 1)) * self.per_turn + (self.names.index(name) + 1)


def bc(ap, pos, n):
    a = ap.unsqueeze(pos)
    return a.to_broadcast([*a.shape[:pos], n, *a.shape[pos + 1:]])


FF, FFP = 704, 768
NE = 8
WEIGHTS_L1 = {
    "L1_attn_Wqk": (D, D), "L1_attn_Wv": (D, D), "L1_attn_Wg": (D, D), "L1_attn_Wout": (D, D),
    "L1_attn_w1": (D, FFP), "L1_attn_w3": (D, FFP), "L1_attn_w2": (FFP, D),
}
WEIGHTS_CROSS = {
    "L1_xattn_Wq": (D, 768), "L1_xattn_Wk": (D, 768), "L1_xattn_Wv": (D, 768), "L1_xattn_Wo": (768, D),
}
WEIGHTS_L0 = {
    "L0_xattn_Wq": (D, D), "L0_xattn_Wk": (D, D), "L0_xattn_Wv": (D, D), "L0_xattn_Wo": (D, D),
    "L0_attn_Wq": (D, P), "L0_attn_Wk": (D, P), "L0_attn_Wv": (D, D), "L0_attn_Wg": (D, D),
    "L0_attn_Wgk1": (D, 16), "L0_attn_Wout": (D, D),
}
COLS = {
    "L0_xattn_bq": D, "L0_xattn_bk": D, "L0_xattn_bv": D, "L0_attn_bgk2": P,
    "L1_xattn_tab_g": D, "L1_xattn_tab_b": D, "L1_xattn_vid_g": D, "L1_xattn_vid_b": D,
    "L1_xattn_q_g": 768, "L1_xattn_q_b": 768, "L1_xattn_k_g": 768, "L1_xattn_k_b": 768,
    "L1_attn_ln1_w": D, "L1_attn_ln1_b": D, "L1_attn_ln2_w": D, "L1_attn_ln2_b": D, "conv0": D, "conv1": D,
    "L1_ffn_b1": NE * D,
}
ROWS = {
    "L0_xattn_bo": D, "L0_ffn_up_bias": 1024, "L0_ffn_b_con": D, "L0_ffn_down_bias": D, "L1_xattn_bo": D, "L1_ffn_br": NE,
}
REPEATED = {
    "L0_attn_rms_w": 64, "L1_xattn_tab_g": D, "L1_attn_router_w": 512,
}
MASKS = {"ident": P, "fold": S, "hmask": 4, "qmask": 8, "causal": P, "spread": 4 * P, "half": 2, "cos": 4, "sin": 4, "earlier": NE * NE}
HT = 4
HN = HT * P


def offsets(sizes):
    at, out = 0, {}
    for name, n in sizes.items():
        out[name] = at
        at += n
    return out, at


COL_AT, COL_N = offsets({n: k // P for n, k in COLS.items()})
ROW_AT, ROW_N = offsets(ROWS)
REP_AT, REP_N = offsets(REPEATED)
MASK_AT, MASK_N = offsets(MASKS)


class Core:

    def __init__(self, nc, ctx, dram):
        self.nc, self.ctx, self.dram = nc, ctx, dram
        self.PS = ctx.enter_context(nc.psum_tensor("banks", [P, 8, 512], F32))
        self.bank = [self.PS[:, n, :] for n in range(8)]
        self.waited = self.sem("waited")
        self.X = self.sb("x_sb", [P, NT, D])
        self.masks = self.sb("masks_sb", [P, MASK_N])
        self.eps, self.mhalf, self.ones = self.sb("eps", [P, 16]), self.sb("mhalf", [P, 16]), self.sb("ones", [1, P])
        self.fold, self.hmask, self.qmask = self.mask("fold"), self.mask("hmask"), self.mask("qmask")
        self.cols_sb, self.rows_sb = self.sb("cols_sb", [P, COL_N]), self.sb("rows_sb", [1, ROW_N])
        self.rep_sb = self.sb("repeated_sb", [P, REP_N])
        self.w, self.loads, self.loaded = {}, {}, {}
        self.weights(WEIGHTS_L1, ctx)
        self.cross, self.l0 = ExitStack(), ExitStack()
        self.weights(WEIGHTS_CROSS, self.cross)
        self.weights(WEIGHTS_L0, self.l0)
        self.W1e, self.W2eT = self.sb("W1e", [P, KC + 1, 1024], self.l0), self.sb("W2eT", [P, KC, 1024], self.l0)
        self.ffn_bias = self.sb("ffn_bias", [1, D], self.l0)
        self.narrow = self.sb("narrow", [16, P], self.l0)
        early = {"cols": (self.cols_sb[:, :], dram["cols"]), "rows": (self.rows_sb[:, :], dram["rows"]),
                 "repeated": (self.rep_sb[:, :], dram["repeated"]),
                 "L0_attn_Wgk2": (self.narrow[:, :], dram["L0_attn_Wgk2"])}
        late = [n for n in self.loads if not n.startswith("L0")]
        self.loads = {**early, **{n: self.loads[n] for n in self.loads if n not in late}, **{n: self.loads[n] for n in reversed(late)}}
        self.loaded.update({name: self.sem(name + "_in") for name in ["x", "masks", *early]})

    def weights(self, shapes, ctx):
        for name, (rows, columns) in shapes.items():
            self.w[name] = self.sb(name + "_sb", [P, rows // P, columns], ctx)
            self.loads[name] = (self.w[name][:, :, :], self.dram[name].rearrange("(c p) n -> p c n", p=P))
            self.loaded[name] = self.sem(name + "_in")

    def sb(self, name, shape, ctx=None):
        return (ctx or self.ctx).enter_context(self.nc.sbuf_tensor(name, shape, F32))

    def sem(self, name, ctx=None):
        return (ctx or self.ctx).enter_context(self.nc.semaphore(name))

    def steps(self, ctx, name, names):
        return Steps(self.sem(name + "_done", ctx), names)

    def mask(self, name):
        return self.masks[:, MASK_AT[name]:MASK_AT[name] + MASKS[name]]

    def ident(self):
        return self.mask("ident")

    def col(self, name, m):
        return self.cols_sb[:, COL_AT[name] + m:COL_AT[name] + m + 1]

    def cols2(self, name):
        return self.cols_sb[:, COL_AT[name]:COL_AT[name] + COLS[name] // P]

    def rep(self, name):
        return self.rep_sb[:, REP_AT[name]:REP_AT[name] + REPEATED[name]]

    def row(self, name):
        return self.rows_sb[:, ROW_AT[name]:ROW_AT[name] + ROWS[name]]


def norm_half(c, ve, dve, pool, pre, i, src, dst, st, mv, rs):
    for t in range(HT):
        op = c.nc.vector.bn_stats(st[:, t, :], src(t))
    op.then_inc(dve.sem, 1)
    ve.wait_ge(dve.sem, dve.after(pre + "stats", i))
    ve.sem_inc(c.waited)
    for t in range(HT):
        op = c.nc.vector.bn_aggr(mv[:, t, :], st[:, t, :])
    op.then_inc(dve.sem, 1)
    ve.wait_ge(pool.sem, pool.after(pre + "rstd", i))
    for t in range(HT):
        op = c.nc.vector.tensor_scalar(dst(t), src(t), mv[:, t, 0:1], rs[:, HT + t:HT + t + 1], ALU.subtract, ALU.mult)
    op.then_inc(dve.sem, 1)


def rstd_half(c, gp, pool, dve, pre, i, mv, rs):
    gp.wait_ge(dve.sem, dve.after(pre + "moments", i))
    c.nc.gpsimd.tensor_tensor(rs[:, 0:HT], mv[:, :, 1:2].rearrange("p t o -> p (t o)"), c.eps[:, 0:HT], ALU.add).then_inc(pool.sem, 1)
    gp.wait_ge(pool.sem, pool.after(pre + "vareps", i))
    c.nc.gpsimd.tensor_tensor(rs[:, HT:2 * HT], rs[:, 0:HT], c.mhalf[:, 0:HT], ALU.pow).then_inc(pool.sem, 1)


STAGES_BF = 10
F0 = 2 ** STAGES_BF


class Butterflies:

    def __init__(self, c, ctx):
        self.c = c
        self.t = [c.sb(f"bf_t{n}", [P, 3, F0 // 2], ctx) for n in range(2)]
        self.wts = [c.sb(f"bf_wts{n}", [P, 4, F0 // 2], ctx) for n in range(2)]
        self.wts_in = [c.sem(f"bf_wts_in{n}", ctx) for n in range(2)]
        self.bias_in = c.sem("bf_bias_in", ctx)
        self.up_in, self.zero, self.done = c.sem("bf_up_in", ctx), c.sem("bf_zero", ctx), c.sem("bf_done", ctx)

    def load_first(self, sp):
        c = self.c
        sp.dma_start(c.W1e[:, 0:KC, :], c.dram["W_exp"].rearrange("(c p) f -> p c f", p=P)).then_inc(self.up_in, 16)
        sp.dma_start(c.W2eT[:, :, :], c.dram["W_conT"].rearrange("(c p) f -> p c f", p=P)).then_inc(self.up_in, 16)

    def load_weights(self, eng, n):
        eng.dma_start(self.wts[n % 2][:, :, :], self.c.dram["bf_weights"][n:n + 1].to_broadcast([P, 4, F0 // 2])).then_inc(self.wts_in[n % 2], 16)


def fold_butterflies(c, gp, bf):
    nc = c.nc
    nc.gpsimd.memset(c.W1e[:, KC, :], 0.0).then_inc(bf.zero, 1)
    gp.wait_ge(bf.zero, 1)
    gp.dma_start(c.W1e[0:1, KC, :], c.dram["b_exp"]).then_inc(bf.bias_in, 16)
    for n in range(2):
        bf.load_weights(gp, n)
    gp.wait_ge(bf.bias_in, 16)
    gp.wait_ge(bf.up_in, 32)
    n = 0
    for down in range(2):
        for stage in (range(STAGES_BF) if not down else reversed(range(STAGES_BF))):
            y = c.W2eT if down else c.W1e
            chunks = y.shape[1]
            s, nb = 2 ** stage, F0 // 2 ** (stage + 1)
            yr = y[:, :, :].rearrange("p c (n two s) -> p c n two s", two=2, s=s)
            a, b = yr[:, :, :, 0, :], yr[:, :, :, 1, :]
            w = bf.wts[n % 2]
            wt = [bc(w[:, q, :].rearrange("p (n s) -> p n s", s=s), 1, chunks) for q in ((0, 2, 1, 3) if down else (0, 1, 2, 3))]
            t = [x[:, 0:chunks, :].rearrange("p c (n s) -> p c n s", s=s) for x in bf.t]
            gp.wait_ge(bf.wts_in[n % 2], 16 * (n // 2 + 1))
            nc.gpsimd.tensor_tensor(t[0], a, wt[0], ALU.mult)
            nc.gpsimd.tensor_tensor(t[1], b, wt[1], ALU.mult).then_inc(bf.done, 1)
            gp.wait_ge(bf.done, 4 * n + 1)
            nc.gpsimd.tensor_tensor(a, a, wt[2], ALU.mult)
            nc.gpsimd.tensor_tensor(b, b, wt[3], ALU.mult).then_inc(bf.done, 1)
            gp.wait_ge(bf.done, 4 * n + 2)
            if n + 2 < 2 * STAGES_BF:
                bf.load_weights(gp, n + 2)
            nc.gpsimd.tensor_tensor(b, a, b, ALU.add).then_inc(bf.done, 1)
            gp.wait_ge(bf.done, 4 * n + 3)
            nc.gpsimd.tensor_tensor(a, t[0], t[1], ALU.add).then_inc(bf.done, 1)
            gp.wait_ge(bf.done, 4 * n + 4)
            n += 1
    gp.wait_ge(c.loaded["rows"], 16)
    nc.gpsimd.tensor_tensor(c.W1e[0:1, KC, :], c.W1e[0:1, KC, :], c.row("L0_ffn_up_bias"), ALU.add)
    nc.gpsimd.tensor_tensor(c.ffn_bias[:, :], c.row("L0_ffn_b_con"), c.row("L0_ffn_down_bias"), ALU.add)


def stage_l0_cross(c):
    nc = c.nc
    with ExitStack() as ctx:
        sb = lambda name, shape: c.sb(name, shape, ctx)
        xn, xnT = sb("l0_xn", [P, NT + 1, D]), sb("l0_xnT", [P, KC, NT * P])
        st, mv, rs = sb("l0_st", [P, NT, 6]), sb("l0_mv", [P, NT, 2]), sb("l0_rs", [P, 2 * NT])
        qT = xn[:, :, :].rearrange("p t d -> p (t d)").rearrange("p (m n) -> p m n", m=KC)
        qblk = sb("l0_qblk", [P, KC, TB, 8, S])
        ctxT = [sb(f"l0_ctxT{j}", [P, KC, KEYS]) for j in range(TB)]
        kT = [sb(f"l0_kT{n}", [P, KC, KEYS]) for n in range(2)]
        v = [sb(f"l0_v{n}", [P, 2, D]) for n in range(2)]
        lastT = sb("l0_lastT", [P, KC, NB])
        klast, vlast = sb("l0_klast", [P, KC, NB + TB]), sb("l0_vlast", [TB, NT, D])
        probs = [sb(f"l0_probs{n}", [P, 4, KEYS]) for n in range(2)]
        nmax = [sb(f"l0_nmax{n}", [P, 4]) for n in range(2)]
        total = [sb(f"l0_total{n}", [P, 4]) for n in range(2)]
        plast = [sb(f"l0_plast{j}", [P, 4, TB]) for j in range(TB)]
        probsT = sb("l0_probsT", [P, 2, 512])
        plastT = sb("l0_plastT", [TB, 512])
        rinv, rmask = sb("l0_rinv", [P, 4]), sb("l0_rmask", [P, 4, 4])
        ao = [sb(f"l0_ao{n}", [P, 4, 4, 16]) for n in range(2)]
        aT = sb("l0_aT", [P, KC, P])
        ctx_in = [c.sem(f"l0_ctx_in{j}", ctx) for j in range(TB)]
        last_in, ready = c.sem("l0_last_in", ctx), c.sem("l0_ready", ctx)
        vlast_done = c.sem("l0_vlast_done", ctx)
        J = range(TB)
        pe = c.steps(ctx, "l0_pe", "v1 pT0 kT2 s1 av0 v2 pT1 kT3 s2 fold0 av1 v3 pT2 kT0' s3 fold1 av2 v0' pT3 "
                     "kT1' fold2 av3 s0' fold3 out")
        dve = c.steps(ctx, "l0_dve", "v1 plast0 rinv0 rmask0 pT0 plT0 max1 ao0 plast1 rinv1 rmask1 v2 pT1 plT1 "
                      "max2 ao1 aT0 plast2 rinv2 rmask2 v3 pT2 plT2 max3 qb' ao2 aT1 plast3 rinv3 rmask3 v0' pT3 plT3 "
                      "ao3 aT2 max0' aT3 res")
        act = c.steps(ctx, "l0_act", "e0 pT0 kT2 e1 pT1 kT3 e2 pT2 kT0' e3 pT3 kT1'")
        pro = {n: c.sem("l0_" + n, ctx) for n in ("stats", "moments", "rstd", "norm", "xT", "xT_out", "qT", "qT_out", "klast", "klast_out")}
        B = c.bank
        ident = c.ident()
        ctx_bf = Butterflies(c, ctx)

        with nc.Block() as block:
            @block.sync
            def _(sp):
                sp.dma_start(c.masks[:, :], c.dram["masks"]).then_inc(c.loaded["masks"], 16)
                sp.dma_start(c.X[:, :, :], c.dram["x"]).then_inc(c.loaded["x"], 16)
                sp.dma_start(lastT[:, :, :], c.dram["ctx_lastT"].rearrange("(c p) b -> p c b", p=P)).then_inc(last_in, 16)
                for name in c.loads:
                    sp.dma_start(*c.loads[name]).then_inc(c.loaded[name], 16)
                    if name == "L0_xattn_Wo":
                        break
                ctx_bf.load_first(sp)

                def load_context(j, t):
                    sp.dma_start(ctxT[j][:, :, :], c.dram["ctxT"][bass.ds(t * TB + j, 1)].rearrange(
                        "b (c p) k -> p (b c) k", p=P)).then_inc(ctx_in[j], 16)

                load_context(0, 0)
                load_context(1, 0)
                with sp.Fori(0, NT) as i:
                    for j, t in ((2, i), (3, i), (0, i + 1), (1, i + 1)):
                        sp.wait_ge(pe.sem, pe.after(f"v{j}", t - 1))
                        load_context(j, t)
                rest = False
                for name in c.loads:
                    if rest:
                        sp.dma_start(*c.loads[name]).then_inc(c.loaded[name], 16)
                    rest = rest or name == "L0_xattn_Wo"

            @block.gpsimd
            def _(gp):
                nc.gpsimd.memset(c.eps[:, :], EPS).then_inc(ready, 1)
                nc.gpsimd.memset(c.mhalf[:, :], -0.5).then_inc(ready, 1)
                nc.gpsimd.memset(c.ones[:, :], 1.0).then_inc(ready, 1)
                for j in J:
                    nc.gpsimd.memset(plast[j][:, :, :], 0.0).then_inc(ready, 1)
                gp.wait_ge(ready, 3 + TB)
                gp.wait_ge(pro["moments"], NT)
                nc.gpsimd.tensor_tensor(rs[:, 0:NT], mv[:, :, 1:2].rearrange("p t o -> p (t o)"), c.eps[:, 0:NT],
                                        ALU.add).then_inc(pro["rstd"], 1)
                gp.wait_ge(pro["rstd"], 1)
                nc.gpsimd.tensor_tensor(rs[:, NT:2 * NT], rs[:, 0:NT], c.mhalf[:, 0:NT], ALU.pow).then_inc(pro["rstd"], 1)
                fold_butterflies(c, gp, ctx_bf)

            @block.tensor
            def _(te):
                for name in ("masks", "L0_xattn_Wq", "L0_xattn_Wk", "L0_xattn_Wv", "L0_xattn_Wo", "cols", "rows"):
                    te.wait_ge(c.loaded[name], 16)
                te.wait_ge(ready, 3 + TB)
                te.wait_ge(last_in, 16)
                for t in range(NT):
                    for k in range(KC):
                        mm = nc.tensor.matmul(B[t % 8][0:TB, 0:D], lastT[:, k, t * TB:(t + 1) * TB],
                                              c.w["L0_xattn_Wv"][:, k, :], start=(k == 0), stop=(k == KC - 1))
                    mm.then_inc(vlast_done, 1)
                te.wait_ge(ready, 3 + TB + NT)
                te.wait_ge(pro["norm"], 1)
                for k in range(KC):
                    for t in range(NT):
                        mm = nc.tensor.transpose(B[2 * k + t // 4][:, (t % 4) * P:(t % 4 + 1) * P], xn[:, t, k * P:(k + 1) * P], ident)
                mm.then_inc(pro["xT"], 1)
                te.wait_ge(pro["xT_out"], 2)
                for m in range(2):
                    for n in range(2):
                        for k in range(KC):
                            mm = nc.tensor.matmul(B[4 + 2 * m + n][:, :], c.w["L0_xattn_Wq"][:, k, m * P:(m + 1) * P],
                                                  xnT[:, k, n * 512:(n + 1) * 512], start=(k == 0), stop=(k == KC - 1))
                mm.then_inc(pro["qT"], 1)
                te.wait_ge(pro["qT_out"], 2)
                for m in range(2):
                    for k in range(KC):
                        mm = nc.tensor.matmul(B[6][:, m * NB:(m + 1) * NB], c.w["L0_xattn_Wk"][:, k, m * P:(m + 1) * P], lastT[:, k, :],
                                              start=(k == 0), stop=(k == KC - 1))
                mm.then_inc(pro["klast"], 1)

                def keys(j, t):
                    te.wait_ge(ctx_in[j], 16 * (t + 1))
                    te.wait_ge(dve.sem, dve.after(f"v{j-1}", t) if j else dve.after("v3", t - 1))
                    for m in range(2):
                        for k in range(KC):
                            mm = nc.tensor.matmul(B[0][:, m * D:(m + 1) * D], c.w["L0_xattn_Wk"][:, k, m * P:(m + 1) * P],
                                                  ctxT[j][:, k, 0:D], start=(k == 0), stop=(k == KC - 1))
                    mm.then_inc(pe.sem, 1)

                def values(j, t):
                    te.wait_ge(act.sem, act.after(f"kT{j}", t))
                    for h in range(2):
                        for k in range(KC):
                            mm = nc.tensor.matmul(B[0][:, h * D:(h + 1) * D], ctxT[j][:, k, h * P:(h + 1) * P],
                                                  c.w["L0_xattn_Wv"][:, k, :], start=(k == 0), stop=(k == KC - 1))
                    mm.then_inc(pe.sem, 1)

                def scores(j, t):
                    te.wait_ge(act.sem, act.after(f"kT{j}", t))
                    te.wait_ge(act.sem, act.after(f"e{j-1}", t) if j else act.after("e3", t - 1))
                    if j == 0:
                        te.wait_ge(dve.sem, dve.after("qb", t))
                    for g in range(4):
                        mm = nc.tensor.matmul(B[1 + g][:, 0:KEYS], qblk[:, g // 2, j, 4 * (g % 2):4 * (g % 2) + 4, :].rearrange("p h q -> p (h q)"),
                                              kT[j % 2][:, g // 2, :], start=True, stop=True)
                    mm.then_inc(pe.sem, 1)

                def transposes(j, i):
                    te.wait_ge(act.sem, act.after(f"e{j}", i))
                    te.wait_ge(dve.sem, dve.after(f"plast{j}", i))
                    te.wait_ge(dve.sem, dve.after(f"ao{j-1}", i) if j else dve.after("res", i - 1))
                    if j > 1:
                        te.wait_ge(dve.sem, dve.after(f"aT{j-2}", i))
                    for h in range(2):
                        for g in range(4):
                            nc.tensor.transpose(B[5 + h][:, g * P:(g + 1) * P], probs[j % 2][:, g, h * P:(h + 1) * P], ident)
                    for g in range(4):
                        mm = nc.tensor.transpose(B[7][0:TB, g * P:(g + 1) * P], plast[j][:, g, :], ident)
                    mm.then_inc(pe.sem, 1)

                def weighted(j, i):
                    te.wait_ge(act.sem, act.after(f"pT{j}", i))
                    te.wait_ge(dve.sem, dve.after(f"plT{j}", i))
                    for g in range(4):
                        o = B[7][:, g * 64:(g + 1) * 64]
                        for h in range(2):
                            nc.tensor.matmul(o, probsT[:, h, g * P:(g + 1) * P], v[j % 2][:, h, g * 64:(g + 1) * 64],
                                             start=(h == 0), stop=False)
                        mm = nc.tensor.matmul(o, plastT[:, g * P:(g + 1) * P], vlast[:, bass.ds(i, 1), g * 64:(g + 1) * 64].rearrange("p t n -> p (t n)"),
                                              start=False, stop=True)
                    mm.then_inc(pe.sem, 1)

                def fold_heads(j, i):
                    te.wait_ge(dve.sem, dve.after(f"ao{j}", i))
                    if j < 3:
                        te.wait_ge(dve.sem, dve.after(f"plT{j+1}", i))
                    for m in range(2):
                        mm = nc.tensor.matmul(B[7][:, D + m * S:D + (m + 1) * S],
                                              ao[j % 2][:, 2 * m:2 * m + 2, :, :].rearrange("p g h d -> p (g h d)"),
                                              c.fold[:, :], start=True, stop=True)
                    mm.then_inc(pe.sem, 1)

                pe.skip_to(te, "kT0", 1)
                keys(0, 0)
                pe.skip_to(te, "v0", 1)
                values(0, 0)
                pe.skip_to(te, "kT1", 1)
                keys(1, 0)
                pe.skip_to(te, "s0", 1)
                scores(0, 0)
                pe.skip_to_end(te)
                with te.Fori(0, NT) as i:
                    values(1, i)
                    transposes(0, i)
                    for j in range(3):
                        after_next = (j + 2, i) if j < 2 else (0, i + 1)
                        keys(*after_next)
                        scores(j + 1, i)
                        if j:
                            fold_heads(j - 1, i)
                        weighted(j, i)
                        values(*after_next)
                        transposes(j + 1, i)
                    keys(1, i + 1)
                    fold_heads(2, i)
                    weighted(3, i)
                    scores(0, i + 1)
                    te.wait_ge(dve.sem, dve.after("aT2", i))
                    fold_heads(3, i)
                    te.wait_ge(dve.sem, dve.after("aT3", i))
                    for k in range(KC):
                        nc.tensor.matmul(B[7][:, 0:D], aT[:, k, :], c.w["L0_xattn_Wo"][:, k, :], start=(k == 0), stop=False)
                    nc.tensor.matmul(B[7][:, 0:D], c.ones[0:1, :], c.row("L0_xattn_bo"), start=False, stop=True).then_inc(pe.sem, 1)

            @block.scalar
            def _(sc):
                sc.wait_ge(c.loaded["cols"], 16)

                sc.wait_ge(pro["xT"], 1)
                nc.scalar.copy(xnT[:, 1, :], c.PS[:, 2:4, :].rearrange("p b n -> p (b n)")).then_inc(pro["xT_out"], 1)
                sc.wait_ge(pro["qT"], 1)
                for m in range(2):
                    op = nc.scalar.activation(qT[:, m, 0:NT * P], c.PS[:, 4 + 2 * m:6 + 2 * m, :].rearrange("p b n -> p (b n)"),
                                              ACT.Identity, bias=c.col("L0_xattn_bq", m))
                op.then_inc(pro["qT_out"], 1)

                sc.wait_ge(pro["klast"], 1)
                for m in range(2):
                    op = nc.scalar.activation(klast[:, m, 0:NB], B[6][:, m * NB:(m + 1) * NB], ACT.Identity, bias=c.col("L0_xattn_bk", m))
                op.then_inc(pro["klast_out"], 1)
                sc.wait_ge(pro["klast_out"], 1)

                def keys_out(j, t):
                    sc.wait_ge(pe.sem, pe.after(f"kT{j}", t))
                    sc.wait_ge(pe.sem, pe.after(f"s{j-2}", t) if j > 1 else pe.after(f"s{j+2}", t - 1))
                    sc.sem_inc(c.waited)
                    for m in range(2):
                        nc.scalar.activation(kT[j % 2][:, m, 0:D], B[0][:, m * D:(m + 1) * D], ACT.Identity,
                                             bias=c.col("L0_xattn_bk", m))
                    nc.scalar.copy(kT[j % 2][:, :, D:D + 1], klast[:, :, bass.ds(t * TB + j, 1)]).then_inc(act.sem, 1)

                def exps(j, i):
                    sc.wait_ge(dve.sem, dve.after(f"max{j}", i))
                    sc.wait_ge(pe.sem, pe.after(f"pT{j-2}", i) if j > 1 else pe.after(f"pT{j+2}", i - 1))
                    for g in range(4):
                        op = nc.scalar.activation(probs[j % 2][:, g, :], B[1 + g][:, 0:KEYS], ACT.Exp, bias=nmax[j % 2][:, g:g + 1],
                                                  accum_out=total[j % 2][:, g:g + 1])
                    op.then_inc(act.sem, 1)

                act.skip_to(sc, "kT0", 1)
                keys_out(0, 0)
                act.skip_to(sc, "kT1", 1)
                keys_out(1, 0)
                act.skip_to_end(sc)
                with sc.Fori(0, NT) as i:
                    for j in J:
                        if j:
                            keys_out(*((j + 1, i) if j < 3 else (0, i + 1)))
                        exps(j, i)
                        sc.wait_ge(pe.sem, pe.after(f"pT{j}", i))
                        sc.wait_ge(pe.sem, pe.after(f"av{j-1}", i) if j else pe.after("av3", i - 1))
                        nc.scalar.copy(probsT[:, 1, :], B[6][:, :]).then_inc(act.sem, 1)
                    keys_out(1, i + 1)

            @block.vector
            def _(ve):
                for name in ("x", "cols", "masks"):
                    ve.wait_ge(c.loaded[name], 16)
                ve.wait_ge(ready, 3 + TB)
                for t in range(NT):
                    ve.wait_ge(vlast_done, t + 1)
                    nc.vector.tensor_copy(vlast[:, t, :], B[t % 8][0:TB, 0:D]).then_inc(ready, 1)

                for t in range(NT):
                    nc.vector.bn_stats(st[:, t, :], c.X[:, t, :]).then_inc(pro["stats"], 1)
                ve.wait_ge(pro["stats"], NT)
                for t in range(NT):
                    nc.vector.bn_aggr(mv[:, t, :], st[:, t, :]).then_inc(pro["moments"], 1)
                ve.wait_ge(pro["moments"], NT)
                ve.wait_ge(pro["rstd"], 2)
                for t in range(NT):
                    op = nc.vector.tensor_scalar(xn[:, t, :], c.X[:, t, :], mv[:, t, 0:1], rs[:, NT + t:NT + t + 1],
                                                 ALU.subtract, ALU.mult)
                op.then_inc(pro["norm"], 1)
                ve.wait_ge(pro["xT"], 1)
                nc.vector.tensor_copy(xnT[:, 0, :], c.PS[:, 0:2, :].rearrange("p b n -> p (b n)")).then_inc(pro["xT_out"], 1)
                nc.vector.memset(qT[:, :, NT * P:(NT + 1) * P], 0.0)
                nc.vector.memset(klast[:, :, NB:NB + TB], 0.0).then_inc(pro["qT_out"], 1)
                ve.wait_ge(pro["qT_out"], 2)

                def row_max(j, t):
                    ve.wait_ge(pe.sem, pe.after(f"s{j}", t))
                    nc.vector.tensor_reduce(nmax[j % 2][:, :], c.PS[:, 1:5, 0:KEYS], AX_X, ALU.max, negate=True).then_inc(dve.sem, 1)

                def values_out(j, t):
                    ve.wait_ge(pe.sem, pe.after(f"v{j}", t))
                    ve.wait_ge(pe.sem, pe.after(f"av{j-2}", t) if j > 1 else pe.after(f"av{j+2}", t - 1))
                    nc.vector.tensor_copy(v[j % 2][:, :, :].rearrange("p h n -> p (h n)"), B[0][:, :]).then_inc(dve.sem, 1)

                def block_queries(t):
                    ve.wait_ge(pe.sem, pe.after("s3", t - 1))
                    for m in range(2):
                        op = nc.vector.tensor_tensor(
                            qblk[:, m, :, :, :], bc(qT[:, m, bass.ds(t * P, P)].rearrange("p (b q) -> p b q", b=TB), 2, 8),
                            c.qmask[:, :].unsqueeze(1).unsqueeze(3).to_broadcast([P, TB, 8, S]), ALU.mult)
                    op.then_inc(dve.sem, 1)

                def last_and_sums(j, i):
                    ve.wait_ge(act.sem, act.after(f"e{j}", i))
                    nc.vector.tensor_copy(plast[j][:, :, j:j + 1], probs[j % 2][:, :, KEYS - 1:KEYS]).then_inc(dve.sem, 1)
                    nc.vector.reciprocal(rinv[:, :], total[j % 2][:, :]).then_inc(dve.sem, 1)
                    ve.wait_ge(dve.sem, dve.after(f"rinv{j}", i))
                    nc.vector.tensor_tensor(rmask[:, :, :], bc(rinv[:, :], 2, 4), bc(c.hmask[:, :], 1, 4),
                                            ALU.mult).then_inc(dve.sem, 1)

                def probs_out(j, i):
                    ve.wait_ge(pe.sem, pe.after(f"pT{j}", i))
                    nc.vector.tensor_copy(probsT[:, 0, :], B[5][:, :]).then_inc(dve.sem, 1)
                    nc.vector.tensor_copy(plastT[:, :], B[7][0:TB, :]).then_inc(dve.sem, 1)

                def normalize(j, i):
                    ve.wait_ge(pe.sem, pe.after(f"av{j}", i))
                    nc.vector.tensor_tensor(ao[j % 2][:, :, :, :], B[7][:, 0:D].rearrange("p (g h d) -> p g h d", g=4, h=4),
                                            bc(rmask[:, :, :], 3, 16), ALU.mult).then_inc(dve.sem, 1)

                def folded_out(j, i):
                    ve.wait_ge(pe.sem, pe.after(f"av{j+1}" if j < 3 else "fold3", i))
                    nc.vector.tensor_tensor(aT[:, :, j * S:(j + 1) * S], B[7][:, D:D + 2 * S].rearrange("p (m q) -> p m q", m=2),
                                            bc(c.cols2("L0_xattn_bv"), 2, S), ALU.add).then_inc(dve.sem, 1)

                dve.skip_to(ve, "qb", 1)
                block_queries(0)
                dve.skip_to(ve, "v0", 1)
                values_out(0, 0)
                dve.skip_to(ve, "max0", 1)
                row_max(0, 0)
                dve.skip_to_end(ve)
                with ve.Fori(0, NT) as i:
                    xt = c.X[:, bass.ds(i, 1), :].rearrange("p t d -> p (t d)")
                    values_out(1, i)
                    last_and_sums(0, i)
                    probs_out(0, i)
                    for j in range(3):
                        row_max(j + 1, i)
                        if j == 2:
                            block_queries(i + 1)
                        normalize(j, i)
                        if j:
                            folded_out(j - 1, i)
                        last_and_sums(j + 1, i)
                        values_out(*((j + 2, i) if j < 2 else (0, i + 1)))
                        probs_out(j + 1, i)
                    normalize(3, i)
                    folded_out(2, i)
                    row_max(0, i + 1)
                    folded_out(3, i)
                    ve.wait_ge(pe.sem, pe.after("out", i))
                    nc.vector.tensor_tensor(xt, xt, B[7][:, 0:D], ALU.add).then_inc(dve.sem, 1)


def stage_l0_gla(c):
    nc = c.nc
    with ExitStack() as ctx:
        sb = lambda name, shape: c.sb(name, shape, ctx)
        xn, xnT = sb("l0a_xn", [P, HT, D]), sb("l0a_xnT", [P, KC, HN])
        st, mv, rs = sb("l0a_st", [P, HT, 6]), sb("l0a_mv", [P, HT, 2]), sb("l0a_rs", [P, 2 * HT])
        g1T = sb("l0a_g1T", [16, HN])
        neg, z, expo, lg = (sb(f"l0a_{n}", [P, HN]) for n in ("neg", "z", "expo", "lg"))
        keep = sb("l0a_keep", [P, HN])
        G, Gc = sb("l0a_G", [P, HN]), sb("l0a_Gc", [P, HN])
        eq, ek = sb("l0a_eq", [P, HN]), sb("l0a_ek", [P, HN])
        qd, kd = sb("l0a_qd", [P, HN]), sb("l0a_kd", [P, HN])
        v, gate, gatew = (sb(f"l0a_{n}", [P, HT, D]) for n in ("v", "gate", "gatew"))
        AT = sb("l0a_AT", [P, 4, HN])
        sq, y = sb("l0a_sq", [P, HT, D]), sb("l0a_y", [P, HT, D])
        yT = sb("l0a_yT", [P, KC, HN])
        ms, ms2 = sb("l0a_ms", [P, 16]), sb("l0a_ms2", [P, 3, 16])
        sixty4th = sb("l0a_64th", [P, 16])
        pe = c.steps(ctx, "l0a_pe", "xT g1 g2 gate q k v scores o yT out")
        dve = c.steps(ctx, "l0a_dve", "stats moments norm xT0 neg z mabs v0 v1 logsig logg scan center qd kd "
                      "c0 c1 c2 c3 ms y0 y1 yg yT0 res0 res1")
        act = c.steps(ctx, "l0a_act", "xT1 g1T gate0 gate1 exp ln eq ek sq0 sq1 yT1")
        pool = c.steps(ctx, "l0a_pool", "vareps rstd gatew msn mse msr")
        ready = c.sem("l0a_ready", ctx)
        B = c.bank
        ident = c.ident()
        causal = c.mask("causal")

        with nc.Block() as block:
            @block.gpsimd
            def _(gp):
                pool.first_turn(gp)
                nc.gpsimd.memset(sixty4th[:, :], 1.0 / 64).then_inc(ready, 1)
                nc.gpsimd.memset(keep[:, :], 1.0).then_inc(ready, 1)
                gp.wait_ge(ready, 2)
                nc.gpsimd.memset(keep[:, :].rearrange("p (b s) -> p b s", s=S)[:, :, 0:1], 0.0).then_inc(ready, 1)
                nc.gpsimd.memset(AT[:, :, :], 0.0).then_inc(ready, 1)
                gp.wait_ge(c.loaded["repeated"], 16)
                gp.wait_ge(ready, 4)
                with gp.Fori(0, 2) as i:
                    rstd_half(c, gp, pool, dve, "", i, mv, rs)
                    gp.wait_ge(act.sem, act.after("gate1", i))
                    gp.wait_ge(dve.sem, dve.after("yg", i - 1))
                    nc.gpsimd.tensor_tensor(gatew[:, :, :].rearrange("p t (h d) -> p (t h) d", h=4),
                                            gate[:, :, :].rearrange("p t (h d) -> p (t h) d", h=4),
                                            bc(c.rep("L0_attn_rms_w"), 1, 16), ALU.mult).then_inc(pool.sem, 1)
                    gp.wait_ge(dve.sem, dve.after("ms", i))
                    nc.gpsimd.tensor_tensor(ms2[:, 0, :], ms[:, :], sixty4th[:, :], ALU.mult).then_inc(pool.sem, 1)
                    gp.wait_ge(pool.sem, pool.after("msn", i))
                    nc.gpsimd.tensor_tensor(ms2[:, 1, :], ms2[:, 0, :], c.eps[:, :], ALU.add).then_inc(pool.sem, 1)
                    gp.wait_ge(pool.sem, pool.after("mse", i))
                    nc.gpsimd.tensor_tensor(ms2[:, 2, :], ms2[:, 1, :], c.mhalf[:, :], ALU.pow).then_inc(pool.sem, 1)

            @block.tensor
            def _(te):
                pe.first_turn(te)
                for name in c.loaded:
                    if name.startswith("L0_attn"):
                        te.wait_ge(c.loaded[name], 16)

                def feature_major(out, w, k_rhs):
                    for k in range(KC):
                        mm = nc.tensor.matmul(out, w[:, k, :], k_rhs[:, k, :], start=(k == 0), stop=(k == KC - 1))
                    return mm

                def token_major(banks, lhsT, w):
                    for t in range(HT):
                        for k in range(KC):
                            mm = nc.tensor.matmul(B[banks + t // 2][:, (t % 2) * D:(t % 2 + 1) * D], lhsT[:, k, t * P:(t + 1) * P],
                                                  w[:, k, :], start=(k == 0), stop=(k == KC - 1))
                    return mm

                with te.Fori(0, 2) as i:
                    te.wait_ge(dve.sem, dve.after("res1", i - 1))
                    te.wait_ge(dve.sem, dve.after("norm", i))
                    for t in range(HT):
                        for k in range(KC):
                            mm = nc.tensor.transpose(B[k][:, t * P:(t + 1) * P], xn[:, t, k * P:(k + 1) * P], ident)
                    mm.then_inc(pe.sem, 1)
                    te.wait_ge(dve.sem, dve.after("xT0", i))
                    te.wait_ge(act.sem, act.after("xT1", i))
                    feature_major(B[4][0:16, :], c.w["L0_attn_Wgk1"], xnT).then_inc(pe.sem, 1)
                    te.wait_ge(act.sem, act.after("g1T", i))
                    nc.tensor.matmul(B[5][:, :], c.narrow[:, :], g1T[:, :], start=True, stop=True).then_inc(pe.sem, 1)
                    token_major(0, xnT, c.w["L0_attn_Wg"]).then_inc(pe.sem, 1)
                    feature_major(B[2][:, :], c.w["L0_attn_Wq"], xnT).then_inc(pe.sem, 1)
                    feature_major(B[3][:, :], c.w["L0_attn_Wk"], xnT).then_inc(pe.sem, 1)
                    token_major(6, xnT, c.w["L0_attn_Wv"]).then_inc(pe.sem, 1)
                    te.wait_ge(act.sem, act.after("gate1", i))
                    te.wait_ge(dve.sem, dve.after("kd", i))
                    for t in range(HT):
                        for h in range(4):
                            r = slice(32 * h, 32 * h + 32)
                            mm = nc.tensor.matmul(B[h][:, t * P:(t + 1) * P], kd[r, t * P:(t + 1) * P],
                                                  qd[r, t * P:(t + 1) * P], start=True, stop=True)
                    mm.then_inc(pe.sem, 1)
                    te.wait_ge(dve.sem, dve.after("c3", i))
                    te.wait_ge(dve.sem, dve.after("v1", i))
                    for t in range(HT):
                        for h in range(4):
                            mm = nc.tensor.matmul(B[4 + t // 2][:, (t % 2) * D + h * 64:(t % 2) * D + (h + 1) * 64],
                                                  AT[:, h, t * P:(t + 1) * P], v[:, t, h * 64:(h + 1) * 64], start=True, stop=True)
                    mm.then_inc(pe.sem, 1)
                    te.wait_ge(dve.sem, dve.after("yg", i))
                    for t in range(HT):
                        for k in range(KC):
                            mm = nc.tensor.transpose(B[6 + k][:, t * P:(t + 1) * P], y[:, t, k * P:(k + 1) * P], ident)
                    mm.then_inc(pe.sem, 1)
                    te.wait_ge(dve.sem, dve.after("yT0", i))
                    te.wait_ge(act.sem, act.after("yT1", i))
                    token_major(0, yT, c.w["L0_attn_Wout"]).then_inc(pe.sem, 1)

            @block.scalar
            def _(sc):
                act.first_turn(sc)
                with sc.Fori(0, 2) as i:
                    sc.wait_ge(pe.sem, pe.after("xT", i))
                    nc.scalar.copy(xnT[:, 1, :], B[1][:, :]).then_inc(act.sem, 1)
                    sc.wait_ge(pe.sem, pe.after("g1", i))
                    nc.scalar.copy(g1T[:, :], B[4][0:16, :]).then_inc(act.sem, 1)
                    sc.wait_ge(pe.sem, pe.after("gate", i))
                    sc.wait_ge(pool.sem, pool.after("gatew", i - 1))
                    for n in range(2):
                        nc.scalar.activation(gate[:, 2 * n:2 * n + 2, :].rearrange("p t n -> p (t n)"), B[n][:, :],
                                             ACT.Silu).then_inc(act.sem, 1)
                    sc.wait_ge(dve.sem, dve.after("mabs", i))
                    nc.scalar.activation(expo[:, :], expo[:, :], ACT.Exp).then_inc(act.sem, 1)
                    sc.wait_ge(act.sem, act.after("exp", i))
                    nc.scalar.activation(lg[:, :], expo[:, :], ACT.Ln, bias=1.0).then_inc(act.sem, 1)
                    sc.wait_ge(dve.sem, dve.after("center", i))
                    nc.scalar.activation(eq[:, :], Gc[:, :], ACT.Exp).then_inc(act.sem, 1)
                    nc.scalar.activation(ek[:, :], Gc[:, :], ACT.Exp, scale=-1.0).then_inc(act.sem, 1)
                    sc.wait_ge(pe.sem, pe.after("o", i))
                    for n in range(2):
                        nc.scalar.activation(sq[:, 2 * n:2 * n + 2, :].rearrange("p t n -> p (t n)"), B[4 + n][:, :],
                                             ACT.Square).then_inc(act.sem, 1)
                    sc.wait_ge(pe.sem, pe.after("yT", i))
                    nc.scalar.copy(yT[:, 1, :], B[7][:, :]).then_inc(act.sem, 1)

            @block.vector
            def _(ve):
                dve.first_turn(ve)
                ve.wait_ge(ready, 4)
                with ve.Fori(0, 2) as i:
                    xt = lambda t: c.X[:, bass.ds(i * HT + t, 1), :].rearrange("p t d -> p (t d)")
                    norm_half(c, ve, dve, pool, "", i, xt, lambda t: xn[:, t, :], st, mv, rs)
                    ve.wait_ge(pe.sem, pe.after("xT", i))
                    nc.vector.tensor_copy(xnT[:, 0, :], B[0][:, :]).then_inc(dve.sem, 1)
                    ve.wait_ge(pe.sem, pe.after("g2", i))
                    b = c.col("L0_attn_bgk2", 0)
                    nc.vector.tensor_scalar(neg[:, :], B[5][:, :], b, 0.0, ALU.add, ALU.min).then_inc(dve.sem, 1)
                    nc.vector.tensor_scalar(z[:, :], B[5][:, :], b, None, ALU.add).then_inc(dve.sem, 1)
                    ve.wait_ge(dve.sem, dve.after("z", i))
                    nc.vector.scalar_tensor_tensor(out=expo[:, :], in0=neg[:, :], scalar=2.0, in1=z[:, :],
                                                   op0=ALU.mult, op1=ALU.subtract).then_inc(dve.sem, 1)
                    ve.wait_ge(pe.sem, pe.after("v", i))
                    for n in range(2):
                        nc.vector.tensor_copy(v[:, 2 * n:2 * n + 2, :].rearrange("p t n -> p (t n)"), B[6 + n][:, :]).then_inc(dve.sem, 1)
                    ve.wait_ge(act.sem, act.after("ln", i))
                    nc.vector.tensor_tensor(z[:, :], neg[:, :], lg[:, :], ALU.subtract).then_inc(dve.sem, 1)
                    ve.wait_ge(dve.sem, dve.after("logsig", i))
                    nc.vector.tensor_scalar(neg[:, :], z[:, :], 1.0 / 16, -3.0, ALU.mult, ALU.max).then_inc(dve.sem, 1)
                    ve.wait_ge(dve.sem, dve.after("logg", i))
                    nc.vector.tensor_tensor_scan(G[:, :], keep[:, :], neg[:, :], 0.0, ALU.mult, ALU.add).then_inc(dve.sem, 1)
                    ve.wait_ge(dve.sem, dve.after("scan", i))
                    G3 = G[:, :].rearrange("p (b s) -> p b s", s=S)
                    nc.vector.tensor_tensor(Gc[:, :].rearrange("p (b s) -> p b s", s=S), G3,
                                            G3[:, :, S // 2 - 1:S // 2].to_broadcast([P, HN // S, S]), ALU.subtract).then_inc(dve.sem, 1)
                    ve.wait_ge(pe.sem, pe.after("k", i))
                    ve.wait_ge(act.sem, act.after("ek", i))
                    nc.vector.tensor_tensor(qd[:, :], B[2][:, :], eq[:, :], ALU.mult).then_inc(dve.sem, 1)
                    nc.vector.tensor_tensor(kd[:, :], B[3][:, :], ek[:, :], ALU.mult).then_inc(dve.sem, 1)
                    ve.wait_ge(pe.sem, pe.after("scores", i))
                    ve.sem_inc(c.waited)
                    for h in range(4):
                        nc.vector.copy_predicated(AT[:, h, :].rearrange("p (t n) -> p t n", t=HT),
                                                  bc(causal, 1, HT).bitcast(I32),
                                                  B[h][:, :].rearrange("p (t n) -> p t n", t=HT)).then_inc(dve.sem, 1)
                    ve.wait_ge(act.sem, act.after("sq1", i))
                    nc.vector.tensor_reduce(ms[:, :], sq[:, :, :].rearrange("p t (h d) -> p (t h) d", h=4),
                                            AX_X, ALU.add).then_inc(dve.sem, 1)
                    ve.wait_ge(pool.sem, pool.after("msr", i))
                    for n in range(2):
                        nc.vector.tensor_tensor(y[:, 2 * n:2 * n + 2, :].rearrange("p t (h d) -> p (t h) d", h=4),
                                                B[4 + n][:, :].rearrange("p (g d) -> p g d", d=64),
                                                bc(ms2[:, 2, 8 * n:8 * n + 8], 2, 64), ALU.mult).then_inc(dve.sem, 1)
                    ve.wait_ge(dve.sem, dve.after("y1", i))
                    nc.vector.tensor_tensor(y[:, :, :], y[:, :, :], gatew[:, :, :], ALU.mult).then_inc(dve.sem, 1)
                    ve.wait_ge(pe.sem, pe.after("yT", i))
                    nc.vector.tensor_copy(yT[:, 0, :], B[6][:, :]).then_inc(dve.sem, 1)
                    ve.wait_ge(pe.sem, pe.after("out", i))
                    for n in range(2):
                        xx = c.X[:, bass.ds(i * HT + 2 * n, 2), :]
                        nc.vector.tensor_tensor(xx, xx, B[n][:, :].rearrange("p (t n) -> p t n", t=2), ALU.add).then_inc(dve.sem, 1)


def stage_l0_ffn(c):
    nc = c.nc
    FC = F0 // P
    with ExitStack() as ctx:
        sb = lambda name, shape: c.sb(name, shape, ctx)
        xn, xnT = sb("l0f_xn", [P, HT, D]), sb("l0f_xnT", [P, KC, HN])
        st, mv, rs = sb("l0f_st", [P, HT, 6]), sb("l0f_mv", [P, HT, 2]), sb("l0f_rs", [P, 2 * HT])
        W2e = sb("l0f_W2e", [P, FC, D])
        b1 = sb("l0f_b1", [P, FC])
        hT = sb("l0f_hT", [P, FC, HN])
        hid = " ".join(f"h{j}" for j in range(FC))
        pe = c.steps(ctx, "l0f_pe", f"xT {hid} out")
        dve = c.steps(ctx, "l0f_dve", "stats moments norm xT0 res0 res1")
        act = c.steps(ctx, "l0f_act", f"xT1 {hid}")
        pool = c.steps(ctx, "l0f_pool", "vareps rstd")
        prep, prep_out = c.sem("l0f_prep", ctx), c.sem("l0f_prep_out", ctx)
        B = c.bank
        ident = c.ident()
        hbank = lambda j: B[(j + 2) % 8]

        with nc.Block() as block:
            @block.gpsimd
            def _(gp):
                pool.first_turn(gp)
                with gp.Fori(0, 2) as i:
                    rstd_half(c, gp, pool, dve, "", i, mv, rs)

            @block.tensor
            def _(te):
                pe.first_turn(te)
                for j in range(FC):
                    for k in range(KC):
                        nc.tensor.transpose(B[j // 2][:, (j % 2) * D + k * P:(j % 2) * D + (k + 1) * P],
                                            c.W2eT[:, k, j * P:(j + 1) * P], ident)
                for j in range(FC):
                    mm = nc.tensor.matmul(B[4][:, j:j + 1], c.W1e[0:1, KC, j * P:(j + 1) * P], c.ones[0:1, 0:1],
                                          start=True, stop=True)
                mm.then_inc(prep, 1)
                te.wait_ge(prep_out, 2)
                with te.Fori(0, 2) as i:
                    te.wait_ge(act.sem, act.after(f"h{FC-1}", i - 1))
                    te.wait_ge(dve.sem, dve.after("norm", i))
                    for t in range(HT):
                        for k in range(KC):
                            mm = nc.tensor.transpose(B[k][:, t * P:(t + 1) * P], xn[:, t, k * P:(k + 1) * P], ident)
                    mm.then_inc(pe.sem, 1)
                    te.wait_ge(dve.sem, dve.after("xT0", i))
                    te.wait_ge(act.sem, act.after("xT1", i))
                    te.wait_ge(dve.sem, dve.after("res1", i - 1))
                    for j in range(FC):
                        for k in range(KC):
                            mm = nc.tensor.matmul(hbank(j), c.W1e[:, k, j * P:(j + 1) * P], xnT[:, k, :],
                                                  start=(k == 0), stop=(k == KC - 1))
                        mm.then_inc(pe.sem, 1)
                    te.wait_ge(act.sem, act.after(f"h{FC-1}", i))
                    for t in range(HT):
                        o = B[2 + t // 2][:, (t % 2) * D:(t % 2 + 1) * D]
                        for j in range(FC):
                            nc.tensor.matmul(o, hT[:, j, t * P:(t + 1) * P], W2e[:, j, :], start=(j == 0), stop=False)
                        mm = nc.tensor.matmul(o, c.ones[0:1, :], c.ffn_bias[:, :], start=False, stop=True)
                    mm.then_inc(pe.sem, 1)

            @block.scalar
            def _(sc):
                act.first_turn(sc)
                sc.wait_ge(prep, 1)
                nc.scalar.copy(W2e[:, FC // 2:FC, :].rearrange("p j n -> p (j n)"),
                               c.PS[:, 2:4, :].rearrange("p b n -> p (b n)")).then_inc(prep_out, 1)
                with sc.Fori(0, 2) as i:
                    sc.wait_ge(pe.sem, pe.after("xT", i))
                    nc.scalar.copy(xnT[:, 1, :], B[1][:, :]).then_inc(act.sem, 1)
                    for j in range(FC):
                        sc.wait_ge(pe.sem, pe.after(f"h{j}", i))
                        nc.scalar.activation(hT[:, j, :], hbank(j), ACT.Gelu, bias=b1[:, j:j + 1]).then_inc(act.sem, 1)

            @block.vector
            def _(ve):
                dve.first_turn(ve)
                ve.wait_ge(prep, 1)
                nc.vector.tensor_copy(W2e[:, 0:FC // 2, :].rearrange("p j n -> p (j n)"),
                                      c.PS[:, 0:2, :].rearrange("p b n -> p (b n)"))
                nc.vector.tensor_copy(b1[:, :], B[4][:, 0:FC]).then_inc(prep_out, 1)
                with ve.Fori(0, 2) as i:
                    xt = lambda t: c.X[:, bass.ds(i * HT + t, 1), :].rearrange("p t d -> p (t d)")
                    norm_half(c, ve, dve, pool, "", i, xt, lambda t: xn[:, t, :], st, mv, rs)
                    ve.wait_ge(pe.sem, pe.after("xT", i))
                    nc.vector.tensor_copy(xnT[:, 0, :], B[0][:, :]).then_inc(dve.sem, 1)
                    ve.wait_ge(pe.sem, pe.after("out", i))
                    for n in range(2):
                        xx = c.X[:, bass.ds(i * HT + 2 * n, 2), :]
                        nc.vector.tensor_tensor(xx, xx, B[2 + n][:, :].rearrange("p (t n) -> p t n", t=2), ALU.add).then_inc(dve.sem, 1)


HEADS1, HD1 = 12, 64
INNER = HEADS1 * HD1
PAIRS = INNER // P


def prepare_l1_keys(c, s):
    nc = c.nc
    with ExitStack() as ctx:
        sb = lambda name, shape: c.sb(name, shape, ctx)
        mean = sb("l1p_mean", [P, KC])
        WkcT, Cp, kgz = sb("l1p_WkcT", [P, PAIRS, D]), sb("l1p_C", [P, KC, D]), sb("l1p_kgz", [P, PAIRS, 2])
        ve_done, pe_done, act_done = (c.sem("l1p_" + n, ctx) for n in ("ve", "pe", "act"))
        B = c.bank
        Wk = c.w["L1_xattn_Wk"]
        with nc.Block() as block:
            @block.vector
            def _(ve):
                for name in ("L1_xattn_Wk", "cols", "repeated"):
                    ve.wait_ge(c.loaded[name], 16)
                nc.vector.memset(s.qT[:, :, NT * P:(NT + 1) * P], 0.0)
                nc.vector.memset(s.qb[:, NT, :], 0.0)
                nc.vector.memset(s.KB[:, :], 0.0).then_inc(ve_done, 1)
                nc.vector.tensor_reduce(mean[:, :], Wk[:, :, :], AX_X, ALU.add).then_inc(ve_done, 1)
                ve.wait_ge(ve_done, 2)
                nc.vector.tensor_scalar(mean[:, :], mean[:, :], 1.0 / INNER, None, ALU.mult).then_inc(ve_done, 1)
                ve.wait_ge(ve_done, 3)
                nc.vector.tensor_tensor(Wk[:, :, :], Wk[:, :, :], bc(mean[:, :], 2, INNER), ALU.subtract).then_inc(ve_done, 1)
                half = c.mask("half")
                nc.vector.tensor_tensor(kgz[:, :, :], bc(c.cols2("L1_xattn_k_g"), 2, 2), bc(half, 1, PAIRS), ALU.mult).then_inc(ve_done, 1)
                nc.vector.tensor_tensor(s.KB[:, :].rearrange("p (a x) -> p a x", a=PAIRS)[:, :, 0:2],
                                        bc(c.cols2("L1_xattn_k_b"), 2, 2), bc(half, 1, PAIRS), ALU.mult).then_inc(ve_done, 1)
                ve.wait_ge(pe_done, 1)
                nc.vector.tensor_copy(WkcT[:, :, :].rearrange("p (b a) c -> p b (a c)", a=2), c.PS[:, 0:3, :]).then_inc(ve_done, 1)
                ve.wait_ge(ve_done, 7)
                for h in range(HEADS1):
                    nc.vector.tensor_scalar(s.WkgZ[:, h, :], WkcT[:, h // 2, :], kgz[:, h // 2, h % 2:h % 2 + 1], None, ALU.mult)
                ve.wait_ge(pe_done, 2)
                for m in range(KC):
                    op = nc.vector.scalar_tensor_tensor(out=s.Cx[:, m, 0:D], in0=B[3][:, m * D:(m + 1) * D], scalar=1.0 / INNER,
                                                        in1=c.rep("L1_xattn_tab_g"), op0=ALU.mult, op1=ALU.mult)
                op.then_inc(ve_done, 1)
                ve.wait_ge(pe_done, 3)
                nc.vector.tensor_copy(s.Cx[:, :, D:D + 1], B[4][:, 0:KC].unsqueeze(2)).then_inc(ve_done, 1)

            @block.tensor
            def _(te):
                te.wait_ge(ve_done, 4)
                for p in range(PAIRS):
                    for k in range(KC):
                        mm = nc.tensor.transpose(B[p // 2][:, (p % 2) * D + k * P:(p % 2) * D + (k + 1) * P],
                                                 Wk[:, k, p * P:(p + 1) * P], c.ident())
                mm.then_inc(pe_done, 1)
                te.wait_ge(ve_done, 7)
                for m in range(KC):
                    for p in range(PAIRS):
                        mm = nc.tensor.matmul(B[3][:, m * D:(m + 1) * D], WkcT[:, p, m * P:(m + 1) * P], WkcT[:, p, :],
                                              start=(p == 0), stop=(p == PAIRS - 1))
                mm.then_inc(pe_done, 1)
                te.wait_ge(act_done, 1)
                for m in range(KC):
                    for k in range(KC):
                        mm = nc.tensor.matmul(B[4][:, m:m + 1], Cp[:, k, m * P:(m + 1) * P], c.col("L1_xattn_tab_b", k),
                                              start=(k == 0), stop=(k == KC - 1))
                mm.then_inc(pe_done, 1)

            @block.scalar
            def _(sc):
                sc.wait_ge(ve_done, 8)
                nc.scalar.mul(Cp[:, :, :].rearrange("p k n -> p (k n)"), B[3][:, :], 1.0 / INNER).then_inc(act_done, 1)


def prepare_l1_queries(c, s):
    nc = c.nc
    with ExitStack() as ctx:
        sb = lambda name, shape: c.sb(name, shape, ctx)
        xn, xn2, xnT = sb("l1q_xn", [P, HT, D]), sb("l1q_xn2", [P, HT, D]), sb("l1q_xnT", [P, KC, HN])
        st, mv, rs = sb("l1q_st", [P, HT, 6]), sb("l1q_mv", [P, HT, 2]), sb("l1q_rs", [P, 2 * HT])
        qst = sb("l1q_qst", [P, HT, 2, 6])
        qn = sb("l1q_qn", [P, HT, INNER])
        qbT = sb("l1q_qbT", [HEADS1, HN])
        pairs = lambda n: " ".join(f"{n}{p}" for p in range(PAIRS))
        pe = c.steps(ctx, "l1q_pe", f"xT qA qB {pairs('qT')} qb qbT")
        dve = c.steps(ctx, "l1q_dve", f"stats moments norm 2stats 2moments 2norm xT0 xT1 "
                      f"qstatsA qstatsB 3moments qnormA qnormB {pairs('qT')} qbT qbt")
        pool = c.steps(ctx, "l1q_pool", "vareps rstd 2vareps 2rstd 3vareps 3rstd")
        B = c.bank
        with nc.Block() as block:
            @block.gpsimd
            def _(gp):
                pool.first_turn(gp)
                with gp.Fori(0, 2) as i:
                    for pre in ("", "2", "3"):
                        rstd_half(c, gp, pool, dve, pre, i, mv, rs)

            @block.tensor
            def _(te):
                pe.first_turn(te)
                te.wait_ge(c.loaded["L1_xattn_Wq"], 16)
                with te.Fori(0, 2) as i:
                    te.wait_ge(dve.sem, dve.after("qbt", i - 1))
                    te.wait_ge(dve.sem, dve.after("2norm", i))
                    for t in range(HT):
                        for k in range(KC):
                            mm = nc.tensor.transpose(B[k][:, t * P:(t + 1) * P], xn2[:, t, k * P:(k + 1) * P], c.ident())
                    mm.then_inc(pe.sem, 1)
                    te.wait_ge(dve.sem, dve.after("xT1", i))
                    for n in range(2):
                        for t in range(2 * n, 2 * n + 2):
                            for a in range(2):
                                for k in range(KC):
                                    mm = nc.tensor.matmul(B[2 * t + a][:, 0:384], xnT[:, k, t * P:(t + 1) * P],
                                                          c.w["L1_xattn_Wq"][:, k, a * 384:(a + 1) * 384], start=(k == 0), stop=(k == KC - 1))
                        mm.then_inc(pe.sem, 1)
                    te.wait_ge(dve.sem, dve.after("qnormB", i))
                    for p in range(PAIRS):
                        for t in range(HT):
                            mm = nc.tensor.transpose(B[p][:, t * P:(t + 1) * P], qn[:, t, p * P:(p + 1) * P], c.ident())
                        mm.then_inc(pe.sem, 1)
                    te.wait_ge(dve.sem, dve.after(f"qT{PAIRS-1}", i))
                    for p in range(PAIRS):
                        mm = nc.tensor.matmul(B[6][0:HEADS1, :], s.KB[:, HEADS1 * p:HEADS1 * (p + 1)], s.qT[:, p, bass.ds(i * HN, HN)],
                                              start=(p == 0), stop=(p == PAIRS - 1))
                    mm.then_inc(pe.sem, 1)
                    te.wait_ge(dve.sem, dve.after("qbT", i))
                    te.sem_inc(c.waited)
                    for t in range(HT):
                        mm = nc.tensor.transpose(B[7][:, t * HEADS1:(t + 1) * HEADS1], qbT[:, t * P:(t + 1) * P],
                                                 c.ident()[0:HEADS1, 0:HEADS1])
                    mm.then_inc(pe.sem, 1)

            @block.vector
            def _(ve):
                dve.first_turn(ve)
                with ve.Fori(0, 2) as i:
                    xt = lambda t: c.X[:, bass.ds(i * HT + t, 1), :].rearrange("p t d -> p (t d)")
                    norm_half(c, ve, dve, pool, "", i, xt, lambda t: xn[:, t, :], st, mv, rs)
                    ve.wait_ge(dve.sem, dve.after("norm", i))
                    norm_half(c, ve, dve, pool, "2", i, lambda t: xn[:, t, :], lambda t: xn2[:, t, :], st, mv, rs)
                    ve.wait_ge(pe.sem, pe.after("xT", i))
                    for k in range(KC):
                        nc.vector.tensor_scalar(xnT[:, k, :], B[k][:, :], c.col("L1_xattn_vid_g", k), c.col("L1_xattn_vid_b", k),
                                                ALU.mult, ALU.add).then_inc(dve.sem, 1)
                    for n in range(2):
                        ve.wait_ge(pe.sem, pe.after("qA" if n == 0 else "qB", i))
                        for t in range(2 * n, 2 * n + 2):
                            for a in range(2):
                                op = nc.vector.bn_stats(qst[:, t, a, :], B[2 * t + a][:, 0:384])
                        op.then_inc(dve.sem, 1)
                    ve.wait_ge(dve.sem, dve.after("qstatsB", i))
                    ve.sem_inc(c.waited)
                    for t in range(HT):
                        op = nc.vector.bn_aggr(mv[:, t, :], qst[:, t, :, :].rearrange("p a n -> p (a n)"))
                    op.then_inc(dve.sem, 1)
                    ve.wait_ge(pool.sem, pool.after("3rstd", i))
                    for n in range(2):
                        for t in range(2 * n, 2 * n + 2):
                            op = nc.vector.tensor_scalar(qn[:, t, :].rearrange("p (a n) -> p a n", a=2), c.PS[:, 2 * t:2 * t + 2, 0:384],
                                                         mv[:, t, 0:1], rs[:, HT + t:HT + t + 1], ALU.subtract, ALU.mult)
                        op.then_inc(dve.sem, 1)
                    for p in range(PAIRS):
                        ve.wait_ge(pe.sem, pe.after(f"qT{p}", i))
                        nc.vector.tensor_scalar(s.qT[:, p, bass.ds(i * HN, HN)], B[p][:, :], c.col("L1_xattn_q_g", p),
                                                c.col("L1_xattn_q_b", p), ALU.mult, ALU.add).then_inc(dve.sem, 1)
                    ve.wait_ge(pe.sem, pe.after("qb", i))
                    nc.vector.tensor_copy(qbT[:, :], B[6][0:HEADS1, :]).then_inc(dve.sem, 1)
                    ve.wait_ge(pe.sem, pe.after("qbT", i))
                    nc.vector.tensor_copy(s.qb[:, bass.ds(i * HT, HT), :], B[7][:, 0:HT * HEADS1].rearrange("p (t h) -> p t h", t=HT)).then_inc(dve.sem, 1)


def stage_l1_cross(c):
    nc = c.nc
    with ExitStack() as outer:
        s = type("Shared", (), {})()
        s.WkgZ, s.Cx = c.sb("l1_WkgZ", [P, HEADS1, D], outer), c.sb("l1_Cx", [P, KC, D + 1], outer)
        s.KB = c.sb("l1_KB", [P, PAIRS * 14], outer)
        s.qT, s.qb = c.sb("l1_qT", [P, PAIRS, (NT + 1) * P], outer), c.sb("l1_qb", [P, NT + 1, HEADS1], outer)
        prepare_l1_keys(c, s)
        prepare_l1_queries(c, s)
        ctx = outer
        sb = lambda name, shape: c.sb(name, shape, ctx)
        QT = sb("l1_QT", [P, KC, TB, HEADS1, S])
        UT = sb("l1_UT", [P, KC, HEADS1, P])
        ck, xh = (sb(f"l1_{n}", [P, TB, 2, w]) for n, w in (("ck", D), ("xh", D + 1)))
        kst, kmv, krs = sb("l1_kst", [P, 2, 6]), sb("l1_kmv", [P, 2, 2]), sb("l1_krs", [P, 4])
        cl, xl = sb("l1_cl", [TB, D]), sb("l1_xl", [TB, D + 1])
        lst, lmv, lrs = sb("l1_lst", [TB, 6]), sb("l1_lmv", [TB, 2]), sb("l1_lrs", [TB, 2])
        xlT = sb("l1_xlT", [P, KC, TB])
        kvT = sb("l1_kvT", [P, TB, KC, KEYS])
        junk, junkl = sb("l1_junk", [P, 2, D + 1]), sb("l1_junkl", [TB, D + 1])
        kvar, rk = sb("l1_kvar", [P, 2]), sb("l1_rk", [P, 4])
        lvar, rl = sb("l1_lvar", [TB, 1]), sb("l1_rl", [TB, 2])
        rkB = sb("l1_rkB", [P, KEYS])
        sco = sb("l1_sco", [P, 3, KEYS])
        probs = sb("l1_probs", [P, 3, KEYS])
        qsel, qcol = sb("l1_qsel", [P, TB, 3, 4]), sb("l1_qcol", [P, TB, 3])
        mx, top, nb = sb("l1_mx", [P, 3]), sb("l1_top", [P, 3]), sb("l1_nb", [P, 3])
        total, rinv = sb("l1_total", [P, 3]), sb("l1_rinv", [P, 3])
        plast = [sb(f"l1_plast{j}", [P, 3, TB]) for j in range(TB)]
        probsT, plastT = sb("l1_probsT", [P, 2, 384]), sb("l1_plastT", [TB, 384])
        aT = sb("l1_aT", [P, PAIRS, P])
        J = range(TB)
        pe = c.steps(ctx, "l1_pe", "rk0 sc0 Z1 pT0 rk1 sc1 xT2 U0 Z2 pT1 rk2 sc2 xT3 U1 Z3 pT2 rk3 sc3 U2 pT3 "
                     "QT0' U3 QT1' lT' V lZ' xT0' Z0' out xT1' qb'")
        dve = c.steps(ctx, "l1_dve", "max0 top0 nb0 rinv0 norm0 Z1 pT0 plT0 max1 top1 nb1 st3 mo3 no3 rinv1 norm1 U0 Z2 "
                      "pT1 plT1 max2 top2 nb2 st0' mo0' no0' rinv2 norm2 U1 Z3 pT2 plT2 max3 top3 nb3 st1' mo1' no1' rinv3 norm3 U2 "
                      "pT3 plT3 QT0' lst' lmo' U3 st2' mo2' no2' lno' lT' aT lZ' Z0' res qsel' qcol'")
        act = c.steps(ctx, "l1_act", "rkB0 ea0 eb0 ec0 pT0 rkB1 kv0_2 kv1_2 ea1 eb1 ec1 U0 pT1 rkB2 kv0_3 kv1_3 ea2 eb2 ec2 U1 "
                      "pT2 rkB3 ea3 eb3 ec3 U2 pT3 U3 QT1' aT kv0_0' kv1_0' kv0_1' kv1_1'")
        pool = c.steps(ctx, "l1_pool", "plast0 vz1 rz1 ve3 rs3 plast1 vz2 rz2 ve0' rs0' plast2 vz3 rz3 ve1' rs1' plast3 "
                       "lve' lrs' ve2' rs2' last' lvz' lrz' vz0' rz0'")
        ctx_in, last_in = [c.sem(f"l1_ctx_in{n}", ctx) for n in range(TB)], c.sem("l1_last_in", ctx)
        ready = c.sem("l1_ready", ctx)
        B = c.bank
        ident = c.ident()
        spread = c.mask("spread")
        by_head = lambda b: c.PS[:, b:b + 3, :].rearrange("p k n -> p (k n)").rearrange("p (h b q) -> p h b q", h=HEADS1, b=TB)

        with nc.Block() as block:
            @block.sync
            def _(sp):
                def load_last(t):
                    sp.dma_start(cl[:, :], c.dram["ctx_last"][bass.ds(t * TB, TB)]).then_inc(last_in, 16)

                def load_context(j, t):
                    sp.dma_start(ck[:, j, :, :], c.dram["ctx"][bass.ds(t * TB + j, 1)].rearrange(
                        "b p h d -> p (b h) d")).then_inc(ctx_in[j], 16)

                for j in range(3):
                    load_context(j, 0)
                load_last(0)
                with sp.Fori(0, NT) as i:
                    for j, t in ((0, i + 1), (1, i + 1), (3, i), (2, i + 1)):
                        sp.wait_ge(dve.sem, dve.after(f"no{j}", t - 1))
                        load_context(j, t)
                    sp.wait_ge(dve.sem, dve.after("lno", i))
                    load_last(i + 1)

            @block.gpsimd
            def _(gp):
                nc.gpsimd.memset(xh[:, :, :, D:D + 1], 1.0).then_inc(ready, 1)
                nc.gpsimd.memset(xl[:, D:D + 1], 1.0).then_inc(ready, 1)
                for j in J:
                    nc.gpsimd.memset(plast[j][:, :, :], 0.0).then_inc(ready, 1)
                gp.wait_ge(ready, 2 + TB)

                def root(i, step, src, tmp, dst, first, second, when):
                    gp.wait_ge(dve.sem, when)
                    n = src.shape[1]
                    nc.gpsimd.tensor_tensor(tmp, src, c.eps[0:src.shape[0], 0:n], ALU.add).then_inc(pool.sem, 1)
                    gp.wait_ge(pool.sem, pool.after(first, i))
                    nc.gpsimd.tensor_tensor(dst, tmp, c.mhalf[0:src.shape[0], 0:n], ALU.pow).then_inc(pool.sem, 1)

                def context_root(j, i):
                    root(i, j, kmv[:, :, 1:2].rearrange("p t o -> p (t o)"), krs[:, 0:2], krs[:, 2:4], f"ve{j}", f"rs{j}",
                         dve.after(f"mo{j}", i))

                def key_root(j, i):
                    root(i, j, kvar[:, :], rk[:, 0:2], rk[:, 2:4], f"vz{j}", f"rz{j}", dve.after(f"Z{j}", i))

                def last_keys(t):
                    gp.wait_ge(dve.sem, dve.after("lT", t))
                    gp.wait_ge(pe.sem, pe.after("sc3", t - 1))
                    gp.sem_inc(c.waited)
                    nc.gpsimd.tensor_copy(kvT[:, :, :, KEYS - 1:KEYS].rearrange("p b k o -> p b (k o)"), xlT[:, :, :].rearrange("p k b -> p b k")).then_inc(pool.sem, 1)
                    root(t, 0, lvar[:, :], rl[:, 0:1], rl[:, 1:2], "lvz", "lrz", dve.after("lZ", t))

                def last_root(t):
                    root(t, 0, lmv[:, 1:2], lrs[:, 0:1], lrs[:, 1:2], "lve", "lrs", dve.after("lmo", t))

                for j in range(2):
                    pool.skip_to(gp, f"ve{j}", 2)
                    context_root(j, 0)
                pool.skip_to(gp, "lve", 9)
                last_root(0)
                context_root(2, 0)
                last_keys(0)
                key_root(0, 0)
                with gp.Fori(0, NT) as i:
                    for j in J:
                        gp.wait_ge(dve.sem, dve.after(f"norm{j}", i))
                        gp.sem_inc(c.waited)
                        nc.gpsimd.tensor_copy(plast[j][:, :, j:j + 1], probs[:, :, KEYS - 1:KEYS]).then_inc(pool.sem, 1)
                        if j < 3:
                            key_root(j + 1, i)
                        if j == 0:
                            context_root(3, i)
                        elif j < 3:
                            context_root(j - 1, i + 1)
                    last_root(i + 1)
                    context_root(2, i + 1)
                    last_keys(i + 1)
                    key_root(0, i + 1)

            @block.tensor
            def _(te):
                for name in ("L1_xattn_Wv", "L1_xattn_Wo"):
                    te.wait_ge(c.loaded[name], 16)
                te.wait_ge(ready, 2 + TB)

                def context_T(j, i):
                    te.wait_ge(dve.sem, dve.after(f"no{j}", i))
                    if j:
                        te.wait_ge(act.sem, act.after(f"kv1_{j-1}", i))
                    if j != 1:
                        te.wait_ge(dve.sem, dve.after(f"plT{j-2}", i) if j else dve.after("plT3", i - 1))
                    for m in range(KC):
                        for h in range(2):
                            mm = nc.tensor.transpose(B[0][:, m * D + h * P:m * D + (h + 1) * P], xh[:, j, h, m * P:(m + 1) * P], ident)
                    mm.then_inc(pe.sem, 1)

                def key_square(j, i):
                    te.wait_ge(act.sem, act.after(f"kv1_{j}", i))
                    te.wait_ge(act.sem, act.after(f"rkB{j-1}", i) if j else act.after("rkB3", i - 1))
                    if j == 0:
                        te.wait_ge(dve.sem, dve.after("lZ", i))
                        te.wait_ge(pool.sem, pool.after("last", i))
                    for h in range(2):
                        for k in range(KC):
                            mm = nc.tensor.matmul(B[1 + h][:, 0:D + 1], kvT[:, j, k, h * P:(h + 1) * P], s.Cx[:, k, :],
                                                  start=(k == 0), stop=(k == KC - 1))
                    mm.then_inc(pe.sem, 1)

                def key_scale(j, i):
                    te.wait_ge(pool.sem, pool.after(f"rz{j}", i))
                    for h in range(2):
                        nc.tensor.matmul(B[1][:, h * P:(h + 1) * P], rk[:, 2 + h:3 + h].to_broadcast([P, P]), ident, start=True, stop=True)
                    nc.tensor.matmul(B[1][:, KEYS - 1:KEYS], rl[:, 1:2].to_broadcast([TB, P]), ident[0:TB, j:j + 1],
                                     start=True, stop=True).then_inc(pe.sem, 1)

                def scores(j, i):
                    if j:
                        te.wait_ge(dve.sem, dve.after(f"max{j-1}", i))
                    else:
                        te.wait_ge(act.sem, act.after("QT1", i))
                    for g in range(3):
                        for k in range(KC):
                            mm = nc.tensor.matmul(B[3 + g][:, 0:KEYS], QT[:, k, j, 4 * g:4 * g + 4, :].rearrange("p h q -> p (h q)"), kvT[:, j, k, :],
                                                  start=(k == 0), stop=(k == KC - 1))
                    mm.then_inc(pe.sem, 1)

                def probs_T(j, i):
                    te.wait_ge(pool.sem, pool.after(f"plast{j}", i))
                    if j:
                        te.wait_ge(act.sem, act.after(f"U{j-1}", i))
                        te.wait_ge(dve.sem, dve.after(f"U{j-1}", i))
                    else:
                        te.wait_ge(dve.sem, dve.after("res", i - 1))
                        te.wait_ge(dve.sem, dve.after("qsel", i))
                    if j < 3:
                        te.wait_ge(act.sem, act.after(f"kv1_{j+1}", i))
                    for g in range(3):
                        for h in range(2):
                            nc.tensor.transpose(B[6 + h][:, g * P:(g + 1) * P], probs[:, g, h * P:(h + 1) * P], ident)
                    for g in range(3):
                        mm = nc.tensor.transpose(B[0][0:TB, g * P:(g + 1) * P], plast[j][:, g, :], ident)
                    mm.then_inc(pe.sem, 1)

                def mixed_context(j, i):
                    te.wait_ge(dve.sem, dve.after(f"plT{j}", i))
                    te.wait_ge(act.sem, act.after(f"pT{j}", i))
                    for m in range(KC):
                        for h in range(2):
                            nc.tensor.matmul(B[6 + m][:, 0:384], xh[:, j, h, m * P:(m + 1) * P], probsT[:, h, :],
                                             start=(h == 0), stop=False)
                        mm = nc.tensor.matmul(B[6 + m][:, 0:384], xl[:, m * P:(m + 1) * P], plastT[:, :], start=False, stop=True)
                    mm.then_inc(pe.sem, 1)

                def heads_queries(m, t):
                    te.wait_ge(dve.sem, dve.after("QT0", t) if m else dve.after("max3", t - 1))
                    for h in range(HEADS1):
                        mm = nc.tensor.matmul(B[3 + h // 4][:, (h % 4) * P:(h % 4 + 1) * P], s.WkgZ[:, h, m * P:(m + 1) * P],
                                              s.qT[:, h // 2, bass.ds(t * P, P)], start=True, stop=True)
                    mm.then_inc(pe.sem, 1)

                def last_keys_T(t):
                    te.wait_ge(dve.sem, dve.after("lno", t))
                    te.sem_inc(c.waited)
                    for m in range(KC):
                        mm = nc.tensor.transpose(B[2][:, m * TB:(m + 1) * TB], xl[:, m * P:(m + 1) * P], ident[0:TB, 0:TB])
                    mm.then_inc(pe.sem, 1)

                def last_keys_square(t):
                    te.wait_ge(dve.sem, dve.after("lT", t))
                    for k in range(KC):
                        mm = nc.tensor.matmul(B[2][0:TB, 0:D + 1], xlT[:, k, :], s.Cx[:, k, :], start=(k == 0), stop=(k == KC - 1))
                    mm.then_inc(pe.sem, 1)

                def queries_bias(t):
                    for j in J:
                        mm = nc.tensor.matmul(B[6][:, j * HEADS1:(j + 1) * HEADS1], spread[:, j * P:(j + 1) * P],
                                              s.qb[:, bass.ds(t, 1), :].rearrange("p t h -> p (t h)"), start=True, stop=True)
                    mm.then_inc(pe.sem, 1)

                pe.skip_to(te, "QT0", 1)
                heads_queries(0, 0)
                pe.skip_to(te, "QT1", 2)
                heads_queries(1, 0)
                last_keys_T(0)
                pe.skip_to(te, "lZ", 3)
                last_keys_square(0)
                context_T(0, 0)
                key_square(0, 0)
                pe.skip_to(te, "xT1", 2)
                context_T(1, 0)
                queries_bias(0)
                with te.Fori(0, NT) as i:
                    key_scale(0, i)
                    scores(0, i)
                    key_square(1, i)
                    probs_T(0, i)
                    for j in J:
                        if j < 3:
                            key_scale(j + 1, i)
                            scores(j + 1, i)
                        else:
                            heads_queries(0, i + 1)
                        if j < 2:
                            context_T(j + 2, i)
                        mixed_context(j, i)
                        if j < 2:
                            key_square(j + 2, i)
                        if j < 3:
                            probs_T(j + 1, i)
                    heads_queries(1, i + 1)
                    last_keys_T(i + 1)
                    te.wait_ge(act.sem, act.after("U3", i))
                    te.wait_ge(dve.sem, dve.after("U3", i))
                    for h in range(HEADS1):
                        r = slice(64 * (h % 2), 64 * (h % 2) + 64)
                        bank, at = (6, h // 2) if h < 8 else (7, h // 2 - 4)
                        for k in range(KC):
                            mm = nc.tensor.matmul(B[bank][r, at * P:(at + 1) * P], c.w["L1_xattn_Wv"][:, k, h * HD1:(h + 1) * HD1],
                                                  UT[:, k, h, :], start=(k == 0), stop=(k == KC - 1))
                    mm.then_inc(pe.sem, 1)
                    last_keys_square(i + 1)
                    context_T(0, i + 1)
                    key_square(0, i + 1)
                    te.wait_ge(act.sem, act.after("aT", i))
                    te.wait_ge(dve.sem, dve.after("aT", i))
                    o = B[7][:, D:2 * D]
                    for p in range(PAIRS):
                        nc.tensor.matmul(o, aT[:, p, :], c.w["L1_xattn_Wo"][:, p, :], start=(p == 0), stop=False)
                    nc.tensor.matmul(o, c.ones[0:1, :], c.row("L1_xattn_bo"), start=False, stop=True).then_inc(pe.sem, 1)
                    context_T(1, i + 1)
                    queries_bias(i + 1)

            @block.scalar
            def _(sc):
                def context_out(j, i):
                    sc.wait_ge(pe.sem, pe.after(f"xT{j}", i))
                    sc.wait_ge(pe.sem, pe.after(f"sc{j}", i - 1))
                    for m in range(KC):
                        nc.scalar.activation(kvT[:, j, m, 0:D], B[0][:, m * D:(m + 1) * D], ACT.Identity,
                                             scale=c.col("L1_xattn_tab_g", m), bias=c.col("L1_xattn_tab_b", m)).then_inc(act.sem, 1)

                def scale_out(j, i):
                    sc.wait_ge(pe.sem, pe.after(f"rk{j}", i))
                    sc.wait_ge(dve.sem, dve.after(f"max{j-1 if j else 3}", i if j else i - 1))
                    nc.scalar.copy(rkB[:, :], B[1][:, 0:KEYS]).then_inc(act.sem, 1)

                def exps(j, i):
                    sc.wait_ge(dve.sem, dve.after(f"nb{j}", i))
                    sc.wait_ge(pe.sem, pe.after(f"pT{j-1 if j else 3}", i if j else i - 1))
                    for g in range(3):
                        nc.scalar.activation(probs[:, g, :], sco[:, g, :], ACT.Exp, bias=nb[:, g:g + 1],
                                             accum_out=total[:, g:g + 1]).then_inc(act.sem, 1)

                def heads_queries_out(t):
                    sc.wait_ge(pe.sem, pe.after("QT1", t))
                    nc.scalar.copy(QT[:, 1, :, :, :].rearrange("p b h q -> p h b q"), by_head(3)).then_inc(act.sem, 1)

                act.skip_to(sc, "QT1", 1)
                heads_queries_out(0)
                act.skip_to(sc, "kv0_0", 4)
                context_out(0, 0)
                context_out(1, 0)
                with sc.Fori(0, NT) as i:
                    scale_out(0, i)
                    exps(0, i)
                    for j in J:
                        sc.wait_ge(pe.sem, pe.after(f"pT{j}", i))
                        sc.wait_ge(pe.sem, pe.after(f"U{j-1 if j else 3}", i if j else i - 1))
                        nc.scalar.copy(probsT[:, 1, :], B[7][:, 0:384]).then_inc(act.sem, 1)
                        if j < 3:
                            scale_out(j + 1, i)
                        if j < 2:
                            context_out(j + 2, i)
                        if j < 3:
                            exps(j + 1, i)
                        sc.wait_ge(pe.sem, pe.after(f"U{j}", i))
                        nc.scalar.activation(UT[:, 1, :, j * S:(j + 1) * S], B[7][:, 0:384].rearrange("p (h q) -> p h q", h=HEADS1),
                                             ACT.Identity, scale=c.col("L1_xattn_tab_g", 1), bias=c.col("L1_xattn_tab_b", 1)).then_inc(act.sem, 1)
                    heads_queries_out(i + 1)
                    sc.wait_ge(pe.sem, pe.after("V", i))
                    nc.scalar.copy(aT[:, 4:6, :].rearrange("p a n -> p (a n)"), B[7][:, 0:2 * P]).then_inc(act.sem, 1)
                    context_out(0, i + 1)
                    context_out(1, i + 1)

            @block.vector
            def _(ve):
                ve.wait_ge(ready, 2 + TB)

                def context_norm(j, i):
                    ve.wait_ge(ctx_in[j], 16 * (i + 1))
                    for h in range(2):
                        op = nc.vector.bn_stats(kst[:, h, :], ck[:, j, h, :])
                    op.then_inc(dve.sem, 1)
                    ve.wait_ge(dve.sem, dve.after(f"st{j}", i))
                    ve.sem_inc(c.waited)
                    for h in range(2):
                        op = nc.vector.bn_aggr(kmv[:, h, :], kst[:, h, :])
                    op.then_inc(dve.sem, 1)
                    ve.wait_ge(pool.sem, pool.after(f"rs{j}", i))
                    ve.wait_ge(pe.sem, pe.after(f"U{j}", i - 1))
                    for h in range(2):
                        op = nc.vector.tensor_scalar(xh[:, j, h, 0:D], ck[:, j, h, :], kmv[:, h, 0:1], krs[:, 2 + h:3 + h],
                                                     ALU.subtract, ALU.mult)
                    op.then_inc(dve.sem, 1)

                def key_variance(j, i):
                    ve.wait_ge(pe.sem, pe.after(f"Z{j}", i))
                    for h in range(2):
                        op = nc.vector.tensor_tensor_reduce(junk[:, h, :], B[1 + h][:, 0:D + 1], xh[:, j, h, :], 1.0, 0.0,
                                                            ALU.mult, ALU.add, kvar[:, h:h + 1])
                    op.then_inc(dve.sem, 1)

                def row_max(j, i):
                    ve.wait_ge(act.sem, act.after(f"rkB{j}", i))
                    ve.wait_ge(act.sem, act.after(f"ec{j-1 if j else 3}", i if j else i - 1))
                    ve.wait_ge(pe.sem, pe.after(f"sc{j}", i))
                    ve.sem_inc(c.waited)
                    for g in range(3):
                        op = nc.vector.tensor_tensor_reduce(sco[:, g, :], B[3 + g][:, 0:KEYS], rkB[:, :], 1.0, -3.0e38,
                                                            ALU.mult, ALU.max, mx[:, g:g + 1])
                    op.then_inc(dve.sem, 1)
                    ve.wait_ge(dve.sem, dve.after(f"max{j}", i))
                    nc.vector.tensor_tensor(top[:, :], mx[:, :], qcol[:, j, :], ALU.add).then_inc(dve.sem, 1)
                    ve.wait_ge(dve.sem, dve.after(f"top{j}", i))
                    nc.vector.tensor_tensor(nb[:, :], qcol[:, j, :], top[:, :], ALU.subtract).then_inc(dve.sem, 1)

                def normalize(j, i):
                    ve.wait_ge(act.sem, act.after(f"ec{j}", i))
                    nc.vector.reciprocal(rinv[:, :], total[:, :]).then_inc(dve.sem, 1)
                    ve.wait_ge(dve.sem, dve.after(f"rinv{j}", i))
                    for g in range(3):
                        op = nc.vector.tensor_scalar(probs[:, g, :], probs[:, g, :], rinv[:, g:g + 1], None, ALU.mult)
                    op.then_inc(dve.sem, 1)

                def last_stats(t):
                    ve.wait_ge(last_in, 16 * (t + 1))
                    nc.vector.bn_stats(lst[:, :], cl[:, :]).then_inc(dve.sem, 1)
                    ve.wait_ge(dve.sem, dve.after("lst", t))
                    ve.sem_inc(c.waited)
                    nc.vector.bn_aggr(lmv[:, :], lst[:, :]).then_inc(dve.sem, 1)

                def last_norm(t):
                    ve.wait_ge(pool.sem, pool.after("lrs", t))
                    ve.wait_ge(pe.sem, pe.after("U3", t - 1))
                    nc.vector.tensor_scalar(xl[:, 0:D], cl[:, :], lmv[:, 0:1], lrs[:, 1:2], ALU.subtract, ALU.mult).then_inc(dve.sem, 1)
                    ve.wait_ge(pe.sem, pe.after("lT", t))
                    for m in range(KC):
                        op = nc.vector.tensor_scalar(xlT[:, m, :], B[2][:, m * TB:(m + 1) * TB], c.col("L1_xattn_tab_g", m),
                                                     c.col("L1_xattn_tab_b", m), ALU.mult, ALU.add)
                    op.then_inc(dve.sem, 1)

                def last_variance(t):
                    ve.wait_ge(pe.sem, pe.after("lZ", t))
                    nc.vector.tensor_tensor_reduce(junkl[:, :], B[2][0:TB, 0:D + 1], xl[:, :], 1.0, 0.0, ALU.mult, ALU.add,
                                                   lvar[:, :]).then_inc(dve.sem, 1)

                def heads_queries_out(t):
                    ve.wait_ge(pe.sem, pe.after("QT0", t))
                    nc.vector.tensor_copy(QT[:, 0, :, :, :].rearrange("p b h q -> p h b q"), by_head(3)).then_inc(dve.sem, 1)

                def queries_bias_out(t):
                    ve.wait_ge(pe.sem, pe.after("qb", t))
                    nc.vector.tensor_tensor(qsel[:, :, :, :].rearrange("p b g h -> p (b g) h"),
                                            B[6][:, 0:TB * HEADS1].rearrange("p (x h) -> p x h", h=4),
                                            bc(c.hmask[:, :], 1, TB * 3), ALU.mult).then_inc(dve.sem, 1)
                    ve.wait_ge(dve.sem, dve.after("qsel", t))
                    nc.vector.tensor_reduce(qcol[:, :, :].rearrange("p b g -> p (b g)"), qsel[:, :, :, :].rearrange("p b g h -> p (b g) h"),
                                            AX_X, ALU.add).then_inc(dve.sem, 1)

                for j in range(2):
                    dve.skip_to(ve, f"st{j}", 3)
                    context_norm(j, 0)
                dve.skip_to(ve, "QT0", 3)
                heads_queries_out(0)
                last_stats(0)
                dve.skip_to(ve, "st2", 5)
                context_norm(2, 0)
                last_norm(0)
                dve.skip_to(ve, "lZ", 2)
                last_variance(0)
                key_variance(0, 0)
                dve.skip_to(ve, "qsel", 2)
                queries_bias_out(0)
                with ve.Fori(0, NT) as i:
                    row_max(0, i)
                    normalize(0, i)
                    key_variance(1, i)
                    for j in J:
                        ve.wait_ge(pe.sem, pe.after(f"pT{j}", i))
                        nc.vector.tensor_copy(probsT[:, 0, :], B[6][:, 0:384]).then_inc(dve.sem, 1)
                        nc.vector.tensor_copy(plastT[:, :], B[0][0:TB, 0:384]).then_inc(dve.sem, 1)
                        if j < 3:
                            row_max(j + 1, i)
                            if j == 0:
                                context_norm(3, i)
                            else:
                                context_norm(j - 1, i + 1)
                            normalize(j + 1, i)
                        else:
                            heads_queries_out(i + 1)
                            last_stats(i + 1)
                        ve.wait_ge(pe.sem, pe.after(f"U{j}", i))
                        nc.vector.tensor_scalar(UT[:, 0, :, j * S:(j + 1) * S], B[6][:, 0:384].rearrange("p (h q) -> p h q", h=HEADS1),
                                                c.col("L1_xattn_tab_g", 0), c.col("L1_xattn_tab_b", 0), ALU.mult, ALU.add).then_inc(dve.sem, 1)
                        if j < 2:
                            key_variance(j + 2, i)
                    context_norm(2, i + 1)
                    last_norm(i + 1)
                    ve.wait_ge(pe.sem, pe.after("V", i))
                    nc.vector.tensor_copy(aT[:, 0:4, :].rearrange("p a n -> p (a n)"), B[6][:, :]).then_inc(dve.sem, 1)
                    last_variance(i + 1)
                    key_variance(0, i + 1)
                    ve.wait_ge(pe.sem, pe.after("out", i))
                    xt = c.X[:, bass.ds(i, 1), :].rearrange("p t d -> p (t d)")
                    nc.vector.tensor_tensor(xt, xt, B[7][:, D:2 * D], ALU.add).then_inc(dve.sem, 1)
                    queries_bias_out(i + 1)


LH, LHD, LVD = 16, 8, 16
GRP = 4


def by_column(x, j):
    return x.rearrange("l (u j) d -> j l u d", j=TB)[j]


def stage_l1_linear(c):
    nc = c.nc
    with ExitStack() as ctx:
        sb = lambda name, shape: c.sb(name, shape, ctx)
        xn, xn2, hT, cT = sb("la_xn", [P, HT, D]), sb("la_xn2", [P, HT, D]), sb("la_hT", [P, KC, HN]), sb("la_cT", [P, KC, HN])
        st, mv, rs = sb("la_st", [P, HT, 6]), sb("la_mv", [P, HT, 2]), sb("la_rs", [P, 2 * HT])
        Wvr, Wtmp = sb("la_Wvr", [P, KC, 2 * LH]), sb("la_Wtmp", [P, 2 * D])
        qk, m1, m2 = (sb(f"la_{n}", [P, HT, D]) for n in ("qk", "m1", "m2"))
        v, gate = sb("la_v", [P, HT, D]), sb("la_gate", [P, HT, D])
        lg, oh, ow = (sb(f"la_{n}", [P, HT * LH, 2]) for n in ("lg", "oh", "ow"))
        dl, nabs, sc_, own, wq = (sb(f"la_{n}", [P, HT * LH]) for n in ("dl", "nabs", "sc", "own", "wq"))
        qe, ke = sb("la_qe", [P, HT, LH, 32]), sb("la_ke", [P, HT, LH, 32])
        qeT, keT = sb("la_qeT", [P, GRP, HN]), sb("la_keT", [P, GRP, HN])
        AT = [sb(f"la_AT{n}", [P, LH * P]) for n in range(2)]
        mu, ms3 = sb("la_mu", [P, HT * LH]), sb("la_ms3", [P, 3, HT * LH])
        gsc = sb("la_gsc", [P, 3, HT * LH])
        ao, y, sq = sb("la_ao", [P, HT, D]), m1, m2
        pT = sb("la_pT", [P, FFP // P, HN])
        u = [sb(f"la_u{n}", [P, HN]) for n in range(2)]
        FC = FFP // P
        T = range(HT)
        mlp = " ".join(f"u{f} w{f}" for f in range(FC))
        pe = c.steps(ctx, "la_pe", "xT qkv g lg cnt T " + " ".join(f"A{t}" for t in T) + " o1 yT out zT " + mlp + " mlp")
        dve = c.steps(ctx, "la_dve", "stats moments norm 2stats 2moments 2norm h0 h1 c0 c1 c0b c1b k v lg dl oh0 oh1 nabs m1 m2a m2b rope "
                      "one sc ow own rown wq wq2 qw qe ke T " + " ".join(f"AT{t}" for t in T) +
                      " mu mus d0 d1 ms yd yg y0 ao0 ao1 3stats 3moments 3norm z0 z1 " + " ".join(f"p{f}" for f in range(FC)) + " xa res0 res1")
        act = c.steps(ctx, "la_act", "silu q g e T sq y1 " + " ".join(f"u{f}" for f in range(FC)))
        pool = c.steps(ctx, "la_pool", "vareps rstd 2vareps 2rstd a b c 3vareps 3rstd")
        stored, turned, ready, wide, folded = (c.sem("la_" + n, ctx) for n in ("stored", "turned", "ready", "wide", "folded"))
        B = c.bank
        ident, causal = c.ident(), c.mask("causal")
        cos, sin = c.mask("cos"), c.mask("sin")

        with nc.Block() as block:
            @block.sync
            def _(sp):
                sp.dma_start(c.dram["turned"].rearrange("(t b) s d -> (b s) t d", b=TB), c.X[:, :, :]).then_inc(stored, 16)
                sp.wait_ge(stored, 16)
                for j in range(TB):
                    sp.dma_start(c.X[j * S:(j + 1) * S, :, :], by_column(c.dram["turned"], j)).then_inc(turned, 16)
                for name, (dst, src) in c.moe_loads.items():
                    sp.dma_start(dst, src).then_inc(c.loaded[name], 16)

            @block.gpsimd
            def _(gp):
                pool.first_turn(gp)
                for n, value in enumerate((1.0 / LVD, EPS, -0.5)):
                    nc.gpsimd.memset(gsc[:, n, :], value).then_inc(ready, 1)
                nc.gpsimd.memset(qe[:, :, :, :], 0.0).then_inc(ready, 1)
                nc.gpsimd.memset(ke[:, :, :, :], 0.0).then_inc(ready, 1)
                gp.wait_ge(ready, 5)
                with gp.Fori(0, 2) as i:
                    rstd_half(c, gp, pool, dve, "", i, mv, rs)
                    rstd_half(c, gp, pool, dve, "2", i, mv, rs)
                    gp.wait_ge(dve.sem, dve.after("ms", i))
                    nc.gpsimd.tensor_tensor(ms3[:, 1, :], ms3[:, 0, :], gsc[:, 0, :], ALU.mult).then_inc(pool.sem, 1)
                    gp.wait_ge(pool.sem, pool.after("a", i))
                    nc.gpsimd.tensor_tensor(ms3[:, 2, :], ms3[:, 1, :], gsc[:, 1, :], ALU.add).then_inc(pool.sem, 1)
                    gp.wait_ge(pool.sem, pool.after("b", i))
                    nc.gpsimd.tensor_tensor(ms3[:, 1, :], ms3[:, 2, :], gsc[:, 2, :], ALU.pow).then_inc(pool.sem, 1)
                    rstd_half(c, gp, pool, dve, "3", i, mv, rs)

            @block.tensor
            def _(te):
                pe.first_turn(te)
                for name in WEIGHTS_L1:
                    te.wait_ge(c.loaded[name], 16)
                te.wait_ge(folded, 3)

                def turn(dst_bank, src):
                    for t in T:
                        for k in range(KC):
                            mm = nc.tensor.transpose(B[dst_bank + k][:, t * P:(t + 1) * P], src[:, t, k * P:(k + 1) * P], ident)
                    mm.then_inc(pe.sem, 1)

                def token_major(out, lhsT, t, w):
                    for k in range(lhsT.shape[1]):
                        mm = nc.tensor.matmul(out, lhsT[:, k, t * P:(t + 1) * P], w[:, k, :], start=(k == 0), stop=(k == lhsT.shape[1] - 1))
                    return mm

                with te.Fori(0, 2) as i:
                    te.wait_ge(dve.sem, dve.after("res1", i - 1))
                    te.wait_ge(dve.sem, dve.after("2norm", i))
                    turn(0, xn2)
                    te.wait_ge(act.sem, act.after("silu", i))
                    for t in T:
                        token_major(B[t][:, 0:D], cT, t, c.w["L1_attn_Wqk"])
                        mm = token_major(B[t][:, D:2 * D], cT, t, c.w["L1_attn_Wv"])
                    mm.then_inc(pe.sem, 1)
                    for t in T:
                        mm = token_major(B[4 + t // 2][:, (t % 2) * D:(t % 2 + 1) * D], cT, t, c.w["L1_attn_Wg"])
                    mm.then_inc(pe.sem, 1)
                    for t in T:
                        mm = token_major(B[6][:, t * 2 * LH:(t + 1) * 2 * LH], cT, t, Wvr)
                    mm.then_inc(pe.sem, 1)
                    te.wait_ge(dve.sem, dve.after("oh1", i))
                    nc.tensor.matmul(B[7][:, 0:HT * 2 * LH], causal, oh[:, :, :].rearrange("p x r -> p (x r)"),
                                     start=True, stop=True).then_inc(pe.sem, 1)
                    te.wait_ge(act.sem, act.after("g", i))
                    te.wait_ge(dve.sem, dve.after("ke", i))
                    for g in range(GRP):
                        for t in T:
                            nc.tensor.transpose(B[g][:, t * P:(t + 1) * P], qe[:, t, GRP * g:GRP * (g + 1), :].rearrange("p h x -> p (h x)"), ident)
                            mm = nc.tensor.transpose(B[4 + g][:, t * P:(t + 1) * P], ke[:, t, GRP * g:GRP * (g + 1), :].rearrange("p h x -> p (h x)"), ident)
                    mm.then_inc(pe.sem, 1)
                    te.wait_ge(act.sem, act.after("T", i))
                    te.wait_ge(dve.sem, dve.after("T", i))

                    def weights(t):
                        if t:
                            te.wait_ge(dve.sem, dve.after(f"AT{t-1}", i))
                        for g in range(GRP):
                            for r in range(GRP):
                                rows = slice(32 * r, 32 * r + 32)
                                mm = nc.tensor.matmul(B[r][:, g * P:(g + 1) * P], keT[rows, g, t * P:(t + 1) * P],
                                                      qeT[rows, g, t * P:(t + 1) * P], start=True, stop=True)
                        mm.then_inc(pe.sem, 1)

                    def outputs(t):
                        te.wait_ge(dve.sem, dve.after(f"AT{t}", i))
                        for h in range(LH):
                            r, g = h % GRP, h // GRP
                            at = (r * GRP + g) * P
                            mm = nc.tensor.matmul(B[4 + t // 2][:, (t % 2) * D + h * LVD:(t % 2) * D + (h + 1) * LVD],
                                                  AT[t % 2][:, at:at + P], v[:, t, h * LVD:(h + 1) * LVD], start=True, stop=True)
                        return mm

                    for t in T:
                        weights(t)
                        if t:
                            outputs(t - 1)
                    outputs(HT - 1).then_inc(pe.sem, 1)
                    te.wait_ge(dve.sem, dve.after("yg", i))
                    turn(6, y)
                    te.wait_ge(dve.sem, dve.after("y0", i))
                    te.wait_ge(act.sem, act.after("y1", i))
                    for t in T:
                        mm = token_major(B[t // 2][:, (t % 2) * D:(t % 2 + 1) * D], hT, t, c.w["L1_attn_Wout"])
                    mm.then_inc(pe.sem, 1)
                    te.wait_ge(dve.sem, dve.after("3norm", i))
                    turn(2, xn2)
                    te.wait_ge(dve.sem, dve.after("z1", i))
                    for f in range(FC):
                        if f >= 4:
                            te.wait_ge(dve.sem, dve.after(f"p{f-4}", i))
                        for n, name in enumerate(("L1_attn_w1", "L1_attn_w3")):
                            for k in range(KC):
                                mm = nc.tensor.matmul(B[2 * (f % 4) + n][:, :], c.w[name][:, k, f * P:(f + 1) * P], cT[:, k, :],
                                                      start=(k == 0), stop=(k == KC - 1))
                            mm.then_inc(pe.sem, 1)
                    te.wait_ge(dve.sem, dve.after(f"p{FC-1}", i))
                    for t in T:
                        mm = token_major(B[t // 2][:, (t % 2) * D:(t % 2 + 1) * D], pT, t, c.w["L1_attn_w2"])
                    mm.then_inc(pe.sem, 1)

            @block.scalar
            def _(sc):
                act.first_turn(sc)
                with sc.Fori(0, 2) as i:
                    sc.wait_ge(dve.sem, dve.after("c1b", i))
                    nc.scalar.activation(cT[:, :, :], cT[:, :, :], ACT.Silu).then_inc(act.sem, 1)
                    sc.wait_ge(pe.sem, pe.after("qkv", i))
                    nc.scalar.activation(qk[:, :, 0:P], c.PS[:, 0:HT, 0:P], ACT.Silu).then_inc(act.sem, 1)
                    sc.wait_ge(pe.sem, pe.after("g", i))
                    nc.scalar.activation(gate[:, :, :].rearrange("p (b t) n -> p b (t n)", b=2), c.PS[:, 4:6, :], ACT.Silu).then_inc(act.sem, 1)
                    sc.wait_ge(dve.sem, dve.after("nabs", i))
                    nc.scalar.activation(nabs[:, :], nabs[:, :], ACT.Exp).then_inc(act.sem, 1)
                    sc.wait_ge(pe.sem, pe.after("T", i))
                    nc.scalar.copy(keT[:, :, :], c.PS[:, 4:8, :]).then_inc(act.sem, 1)
                    sc.wait_ge(dve.sem, dve.after("d1", i))
                    nc.scalar.activation(sq[:, :, :], ao[:, :, :], ACT.Square).then_inc(act.sem, 1)
                    sc.wait_ge(pe.sem, pe.after("yT", i))
                    nc.scalar.copy(hT[:, 1, :], B[7][:, :]).then_inc(act.sem, 1)
                    for f in range(FC):
                        sc.wait_ge(pe.sem, pe.after(f"u{f}", i))
                        if f >= 2:
                            sc.wait_ge(dve.sem, dve.after(f"p{f-2}", i))
                        nc.scalar.activation(u[f % 2][:, :], B[2 * (f % 4)][:, :], ACT.Silu).then_inc(act.sem, 1)

            @block.vector
            def _(ve):
                dve.first_turn(ve)
                for n in WEIGHTS_L1:
                    ve.wait_ge(c.loaded[n], 16)
                ve.wait_ge(c.loaded["repeated"], 16)
                for k in range(KC):
                    ve.wait_ge(folded, k)
                    nc.vector.tensor_tensor(Wtmp[:, :].rearrange("p (h r d) -> p h r d", r=2, d=LVD),
                                            bc(c.w["L1_attn_Wv"][:, k, :].rearrange("p (h d) -> p h d", d=LVD), 2, 2),
                                            c.rep("L1_attn_router_w").rearrange("p (h r d) -> p h r d", r=2, d=LVD), ALU.mult).then_inc(wide, 1)
                    ve.wait_ge(wide, k + 1)
                    nc.vector.tensor_reduce(Wvr[:, k, :], Wtmp[:, :].rearrange("p (x d) -> p x d", d=LVD), AX_X, ALU.add).then_inc(folded, 1)
                ve.wait_ge(turned, 16 * TB)
                nc.vector.memset(dl[:, :], 0.0).then_inc(folded, 1)
                ve.wait_ge(folded, 3)

                def step(op, name, i, wait=True):
                    op.then_inc(dve.sem, 1)
                    if wait:
                        ve.wait_ge(dve.sem, dve.after(name, i))

                with ve.Fori(0, 2) as i:
                    xt = lambda t: c.X[:, bass.ds(i * HT + t, 1), :].rearrange("p t d -> p (t d)")
                    norm_half(c, ve, dve, pool, "", i, xt, lambda t: xn[:, t, :], st, mv, rs)
                    ve.wait_ge(dve.sem, dve.after("norm", i))
                    norm_half(c, ve, dve, pool, "2", i, lambda t: xn[:, t, :], lambda t: xn2[:, t, :], st, mv, rs)
                    ve.wait_ge(pe.sem, pe.after("xT", i))
                    for k in range(KC):
                        nc.vector.tensor_scalar(hT[:, k, :], B[k][:, :], c.col("L1_attn_ln1_w", k), c.col("L1_attn_ln1_b", k),
                                                ALU.mult, ALU.add).then_inc(dve.sem, 1)
                    ve.wait_ge(dve.sem, dve.after("h1", i))
                    for k in range(KC):
                        nc.vector.tensor_scalar(cT[:, k, :], hT[:, k, :], c.col("conv1", k), None, ALU.mult).then_inc(dve.sem, 1)
                    ve.wait_ge(dve.sem, dve.after("c1", i))
                    for k in range(KC):
                        seq = lambda x: x[:, k, :].rearrange("p (b l) -> p b l", l=S)
                        nc.vector.scalar_tensor_tensor(out=seq(cT)[:, :, 1:S], in0=seq(hT)[:, :, 0:S - 1], scalar=c.col("conv0", k),
                                                       in1=seq(cT)[:, :, 1:S], op0=ALU.mult, op1=ALU.add).then_inc(dve.sem, 1)
                    ve.wait_ge(pe.sem, pe.after("qkv", i))
                    ve.wait_ge(act.sem, act.after("q", i))
                    step(nc.vector.tensor_copy(qk[:, :, P:D], c.PS[:, 0:HT, P:D]), "k", i, False)
                    step(nc.vector.tensor_copy(v[:, :, :], c.PS[:, 0:HT, D:2 * D]), "v", i, False)
                    ve.wait_ge(pe.sem, pe.after("lg", i))
                    step(nc.vector.tensor_copy(lg[:, :, :].rearrange("p x r -> p (x r)"), B[6][:, 0:HT * 2 * LH]), "lg", i)
                    l0, l1 = (lg[:, :, r:r + 1].rearrange("p x r -> p (x r)") for r in range(2))
                    step(nc.vector.tensor_tensor(dl[:, :], l0, l1, ALU.subtract), "dl", i)
                    step(nc.vector.tensor_scalar(oh[:, :, 0:1], dl[:, :].unsqueeze(2), 0.0, None, ALU.is_ge), "oh0", i, False)
                    step(nc.vector.tensor_scalar(oh[:, :, 1:2], dl[:, :].unsqueeze(2), 0.0, None, ALU.is_lt), "oh1", i, False)
                    step(nc.vector.scalar_tensor_tensor(out=nabs[:, :], in0=dl[:, :], scalar=-1.0, in1=dl[:, :],
                                                        op0=ALU.mult, op1=ALU.min), "nabs", i, False)
                    pair = lambda x: x[:, :, :].rearrange("p t (h two d) -> p (t h) two d", two=2, d=4)
                    X4 = HT * D // 8
                    ve.wait_ge(dve.sem, dve.after("k", i))
                    step(nc.vector.tensor_tensor(pair(m1), pair(qk), cos.unsqueeze(1).unsqueeze(1).to_broadcast([P, X4, 2, 4]), ALU.mult), "m1", i, False)
                    sin3 = bc(sin, 1, X4)
                    step(nc.vector.scalar_tensor_tensor(out=pair(m2)[:, :, 0, :], in0=pair(qk)[:, :, 1, :], scalar=-1.0, in1=sin3,
                                                        op0=ALU.mult, op1=ALU.mult), "m2a", i, False)
                    step(nc.vector.tensor_tensor(pair(m2)[:, :, 1, :], pair(qk)[:, :, 0, :], sin3, ALU.mult), "m2b", i)
                    step(nc.vector.tensor_tensor(qk[:, :, :], m1[:, :, :], m2[:, :, :], ALU.add), "rope", i, False)
                    ve.wait_ge(act.sem, act.after("e", i))
                    step(nc.vector.tensor_scalar(nabs[:, :], nabs[:, :], 1.0, None, ALU.add), "one", i)
                    step(nc.vector.reciprocal(sc_[:, :], nabs[:, :]), "sc", i, False)
                    ve.wait_ge(pe.sem, pe.after("cnt", i))
                    step(nc.vector.tensor_tensor(ow[:, :, :].rearrange("p x r -> p (x r)"), B[7][:, 0:HT * 2 * LH],
                                                 oh[:, :, :].rearrange("p x r -> p (x r)"), ALU.mult), "ow", i)
                    step(nc.vector.tensor_tensor(own[:, :].unsqueeze(2), ow[:, :, 0:1], ow[:, :, 1:2], ALU.add), "own", i)
                    step(nc.vector.reciprocal(own[:, :], own[:, :]), "rown", i)
                    step(nc.vector.tensor_tensor(wq[:, :], sc_[:, :], own[:, :], ALU.mult), "wq", i)
                    step(nc.vector.tensor_scalar(wq[:, :], wq[:, :], float(LHD) ** -0.5, None, ALU.mult), "wq2", i)
                    ve.wait_ge(dve.sem, dve.after("rope", i))
                    q_, k_ = qk[:, :, 0:P], qk[:, :, P:D]
                    head = lambda x: x.rearrange("p t (h d) -> p t h d", d=LHD)
                    step(nc.vector.tensor_tensor(head(m1[:, :, 0:P]), head(q_),
                                                 bc(wq[:, :].rearrange("p (t h) -> p t h", t=HT), 3, LHD), ALU.mult), "qw", i)
                    for t in T:
                        for name, dst, src in (("qe", qe, m1[:, t, 0:P]),):
                            op = nc.vector.tensor_tensor(dst[:, t, :, 0:2 * LHD].rearrange("p h (r d) -> p h r d", r=2),
                                                         bc(src.rearrange("p (h d) -> p h d", d=LHD), 2, 2),
                                                         bc(oh[:, t * LH:(t + 1) * LH, :], 3, LHD), ALU.mult)
                    op.then_inc(dve.sem, 1)
                    for t in T:
                        op = nc.vector.tensor_tensor(ke[:, t, :, 0:2 * LHD].rearrange("p h (r d) -> p h r d", r=2),
                                                     bc(qk[:, t, P:D].rearrange("p (h d) -> p h d", d=LHD), 2, 2),
                                                     bc(oh[:, t * LH:(t + 1) * LH, :], 3, LHD), ALU.mult)
                    op.then_inc(dve.sem, 1)
                    ve.wait_ge(pe.sem, pe.after("T", i))
                    step(nc.vector.tensor_copy(qeT[:, :, :], c.PS[:, 0:4, :]), "T", i, False)
                    for t in T:
                        ve.wait_ge(pe.sem, pe.after(f"A{t}", i))
                        step(nc.vector.tensor_tensor(AT[t % 2][:, :].rearrange("p (x n) -> p x n", n=P),
                                                     c.PS[:, 0:4, :].rearrange("p b n -> p (b n)").rearrange("p (x n) -> p x n", n=P),
                                                     bc(causal, 1, LH), ALU.mult), f"AT{t}", i, False)
                    ve.wait_ge(pe.sem, pe.after("o1", i))
                    heads = lambda x: x.rearrange("p (x d) -> p x d", d=LVD)
                    o2 = c.PS[:, 4:6, :].rearrange("p b n -> p (b n)")
                    step(nc.vector.tensor_reduce(mu[:, :], heads(o2), AX_X, ALU.add), "mu", i)
                    step(nc.vector.tensor_scalar(mu[:, :], mu[:, :], 1.0 / LVD, None, ALU.mult), "mus", i)
                    for n in range(2):
                        step(nc.vector.tensor_tensor(heads(ao[:, 2 * n:2 * n + 2, :].rearrange("p t n -> p (t n)")), heads(B[4 + n][:, :]),
                                                     bc(mu[:, 2 * LH * n:2 * LH * (n + 1)], 2, LVD), ALU.subtract), f"d{n}", i, False)
                    ve.wait_ge(act.sem, act.after("sq", i))
                    step(nc.vector.tensor_reduce(ms3[:, 0, :], heads(sq[:, :, :].rearrange("p t n -> p (t n)")), AX_X, ALU.add), "ms", i, False)
                    ve.wait_ge(pool.sem, pool.after("c", i))
                    step(nc.vector.tensor_tensor(heads(y[:, :, :].rearrange("p t n -> p (t n)")), heads(ao[:, :, :].rearrange("p t n -> p (t n)")),
                                                 bc(ms3[:, 1, :], 2, LVD), ALU.mult), "yd", i)
                    step(nc.vector.tensor_tensor(y[:, :, :], y[:, :, :], gate[:, :, :], ALU.mult), "yg", i, False)
                    ve.wait_ge(pe.sem, pe.after("yT", i))
                    step(nc.vector.tensor_copy(hT[:, 0, :], B[6][:, :]), "y0", i, False)
                    ve.wait_ge(pe.sem, pe.after("out", i))
                    for n in range(2):
                        step(nc.vector.tensor_tensor(ao[:, 2 * n:2 * n + 2, :].rearrange("p t n -> p (t n)"), B[n][:, :],
                                                     xn[:, 2 * n:2 * n + 2, :].rearrange("p t n -> p (t n)"), ALU.add), f"ao{n}", i)
                    norm_half(c, ve, dve, pool, "3", i, lambda t: ao[:, t, :], lambda t: xn2[:, t, :], st, mv, rs)
                    ve.wait_ge(pe.sem, pe.after("zT", i))
                    for k in range(KC):
                        step(nc.vector.tensor_scalar(cT[:, k, :], B[2 + k][:, :], c.col("L1_attn_ln2_w", k), c.col("L1_attn_ln2_b", k),
                                                     ALU.mult, ALU.add), f"z{k}", i, False)
                    for f in range(FC):
                        ve.wait_ge(pe.sem, pe.after(f"w{f}", i))
                        ve.wait_ge(act.sem, act.after(f"u{f}", i))
                        step(nc.vector.tensor_tensor(pT[:, f, :], u[f % 2][:, :], B[2 * (f % 4) + 1][:, :], ALU.mult), f"p{f}", i, False)
                    xx = c.X[:, bass.ds(i * HT, HT), :]
                    step(nc.vector.tensor_tensor(xx, xx, ao[:, :, :], ALU.add), "xa", i)
                    ve.wait_ge(pe.sem, pe.after("mlp", i))
                    for n in range(2):
                        xx = c.X[:, bass.ds(i * HT + 2 * n, 2), :]
                        step(nc.vector.tensor_tensor(xx, xx, B[n][:, :].rearrange("p (t n) -> p t n", t=2), ALU.add), f"res{n}", i, False)


def stage_moe(c):
    nc = c.nc
    with ExitStack() as ctx:
        sb = lambda name, shape: c.sb(name, shape, ctx)
        xn, xnT = sb("mo_xn", [P, HT, D]), sb("mo_xnT", [P, KC, HN])
        st, mv, rs = sb("mo_st", [P, HT, 6]), sb("mo_mv", [P, HT, 2]), sb("mo_rs", [P, 2 * HT])
        fst, fmv, frs = sb("mo_fst", [P, 6]), sb("mo_fmv", [P, 2]), sb("mo_frs", [P, 2])
        fn, fT = sb("mo_fn", [P, D]), sb("mo_fT", [P, KC, TB, S])
        sco = sb("mo_sco", [P, NE])
        more, same, rank = sb("mo_more", [P, NE, NE]), sb("mo_same", [P, NE, NE]), sb("mo_rank", [P, NE])
        G, GT, bias2 = sb("mo_G", [P, NE]), sb("mo_GT", [NE, P]), sb("mo_bias2", [P, D])
        hT = [sb(f"mo_hT{n}", [P, KC, HN]) for n in range(2)]
        E = range(NE)
        pe = c.steps(ctx, "mo_pe", "xT h0 " + " ".join((f"h{e+1} " if e < NE - 1 else "") + f"o{e}" for e in E))
        dve = c.steps(ctx, "mo_dve", "stats moments norm xT0 bias " + " ".join(f"a{e} b{e}" for e in E))
        act = c.steps(ctx, "mo_act", "xT1 " + " ".join(f"h{e}" for e in E))
        pool = c.steps(ctx, "mo_pool", "vareps rstd")
        rv, rp, rg = (c.sem("mo_route_" + n, ctx) for n in ("dve", "pe", "pool"))
        B = c.bank
        ident = c.ident()

        with nc.Block() as block:
            @block.gpsimd
            def _(gp):
                pool.first_turn(gp)
                gp.wait_ge(rv, 2)
                nc.gpsimd.tensor_tensor(frs[:, 0:1], fmv[:, 1:2], c.eps[:, 0:1], ALU.add).then_inc(rg, 1)
                gp.wait_ge(rg, 1)
                nc.gpsimd.tensor_tensor(frs[:, 1:2], frs[:, 0:1], c.mhalf[:, 0:1], ALU.pow).then_inc(rg, 1)
                with gp.Fori(0, 2) as i:
                    rstd_half(c, gp, pool, dve, "", i, mv, rs)

            @block.tensor
            def _(te):
                pe.first_turn(te)
                for name in c.moe_loads:
                    te.wait_ge(c.loaded[name], 16)
                te.wait_ge(rv, 3)
                for k in range(KC):
                    mm = nc.tensor.transpose(B[0][:, k * P:(k + 1) * P], fn[:, k * P:(k + 1) * P], ident)
                mm.then_inc(rp, 1)
                te.wait_ge(rv, 4)
                for k in range(KC):
                    nc.tensor.matmul(B[1][:, 0:NE], fT[:, k, :, :].rearrange("p b s -> p (b s)"), c.Wr[:, k, :], start=(k == 0), stop=False)
                nc.tensor.matmul(B[1][:, 0:NE], c.ones[0:1, :], c.row("L1_ffn_br"), start=False, stop=True).then_inc(rp, 1)
                te.wait_ge(rv, 11)
                nc.tensor.transpose(B[2][0:NE, 0:P], G[:, :], ident).then_inc(rp, 1)
                te.wait_ge(rv, 12)
                nc.tensor.matmul(B[3][:, 0:D], GT[:, :], c.moe_b2[:, :], start=True, stop=True).then_inc(rp, 1)
                te.wait_ge(rv, 13)

                def hidden(e, i):
                    if e >= 2:
                        te.wait_ge(act.sem, act.after(f"h{e-2}", i))
                    for m in range(KC):
                        for k in range(KC):
                            mm = nc.tensor.matmul(B[2 * (e % 2) + m][:, :], c.moe_W1[:, KC * e + k, m * P:(m + 1) * P], xnT[:, k, :],
                                                  start=(k == 0), stop=(k == KC - 1))
                    mm.then_inc(pe.sem, 1)

                with te.Fori(0, 2) as i:
                    te.wait_ge(act.sem, act.after(f"h{NE-1}", i - 1))
                    te.wait_ge(dve.sem, dve.after("norm", i))
                    for t in range(HT):
                        for k in range(KC):
                            mm = nc.tensor.transpose(B[k][:, t * P:(t + 1) * P], xn[:, t, k * P:(k + 1) * P], ident)
                    mm.then_inc(pe.sem, 1)
                    te.wait_ge(dve.sem, dve.after("xT0", i))
                    te.wait_ge(act.sem, act.after("xT1", i))
                    hidden(0, i)
                    for e in E:
                        if e < NE - 1:
                            hidden(e + 1, i)
                        te.wait_ge(act.sem, act.after(f"h{e}", i))
                        te.wait_ge(dve.sem, dve.after(f"b{e-2}", i) if e >= 2 else dve.after(f"b{e+NE-2}", i - 1))
                        for t in range(HT):
                            for k in range(KC):
                                mm = nc.tensor.matmul(B[4 + 2 * (e % 2) + t // 2][:, (t % 2) * D:(t % 2 + 1) * D],
                                                      hT[e % 2][:, k, t * P:(t + 1) * P], c.moe_W2[:, KC * e + k, :],
                                                      start=(k == 0), stop=(k == KC - 1))
                        mm.then_inc(pe.sem, 1)

            @block.scalar
            def _(sc):
                act.first_turn(sc)
                with sc.Fori(0, 2) as i:
                    sc.wait_ge(pe.sem, pe.after("xT", i))
                    nc.scalar.copy(xnT[:, 1, :], B[1][:, :]).then_inc(act.sem, 1)
                    for e in E:
                        sc.wait_ge(pe.sem, pe.after(f"h{e}", i))
                        sc.wait_ge(pe.sem, pe.after(f"o{e-2}", i) if e >= 2 else pe.after(f"o{e+NE-2}", i - 1))
                        for m in range(KC):
                            op = nc.scalar.activation(hT[e % 2][:, m, :], B[2 * (e % 2) + m][:, :], ACT.Gelu,
                                                      bias=c.col("L1_ffn_b1", KC * e + m))
                        op.then_inc(act.sem, 1)

            @block.vector
            def _(ve):
                dve.first_turn(ve)
                nc.vector.bn_stats(fst[:, :], c.X[:, 0, :]).then_inc(rv, 1)
                ve.wait_ge(rv, 1)
                nc.vector.bn_aggr(fmv[:, :], fst[:, :]).then_inc(rv, 1)
                ve.wait_ge(rg, 2)
                nc.vector.tensor_scalar(fn[:, :], c.X[:, 0, :], fmv[:, 0:1], frs[:, 1:2], ALU.subtract, ALU.mult).then_inc(rv, 1)
                ve.wait_ge(rp, 1)
                nc.vector.tensor_copy(fT[:, :, :, :], bc(B[0][:, 0:D].rearrange("p (k n) -> p k n", k=KC)[:, :, 0:S], 2, TB)).then_inc(rv, 1)
                ve.wait_ge(rp, 2)
                nc.vector.tensor_copy(sco[:, :], B[1][:, 0:NE]).then_inc(rv, 1)
                ve.wait_ge(rv, 5)
                other, self_ = bc(sco[:, :], 1, NE), bc(sco[:, :], 2, NE)
                nc.vector.tensor_tensor(more[:, :, :], other, self_, ALU.is_gt).then_inc(rv, 1)
                nc.vector.tensor_tensor(same[:, :, :], other, self_, ALU.is_equal).then_inc(rv, 1)
                ve.wait_ge(rv, 7)
                nc.vector.tensor_tensor(same[:, :, :], same[:, :, :], c.mask("earlier").rearrange("p (e j) -> p e j", e=NE), ALU.mult).then_inc(rv, 1)
                ve.wait_ge(rv, 8)
                nc.vector.tensor_tensor(more[:, :, :], more[:, :, :], same[:, :, :], ALU.add).then_inc(rv, 1)
                ve.wait_ge(rv, 9)
                nc.vector.tensor_reduce(rank[:, :], more[:, :, :], AX_X, ALU.add).then_inc(rv, 1)
                ve.wait_ge(rv, 10)
                nc.vector.tensor_scalar(G[:, :], rank[:, :], 2.0, 0.5, ALU.is_lt, ALU.mult).then_inc(rv, 1)
                ve.wait_ge(rp, 3)
                nc.vector.tensor_copy(GT[:, :], B[2][0:NE, 0:P]).then_inc(rv, 1)
                ve.wait_ge(rp, 4)
                nc.vector.tensor_copy(bias2[:, :], B[3][:, 0:D]).then_inc(rv, 1)
                ve.wait_ge(rv, 13)
                with ve.Fori(0, 2) as i:
                    xt = lambda t: c.X[:, bass.ds(i * HT + t, 1), :].rearrange("p t d -> p (t d)")
                    norm_half(c, ve, dve, pool, "", i, xt, lambda t: xn[:, t, :], st, mv, rs)
                    ve.wait_ge(pe.sem, pe.after("xT", i))
                    nc.vector.tensor_copy(xnT[:, 0, :], B[0][:, :]).then_inc(dve.sem, 1)
                    xx = c.X[:, bass.ds(i * HT, HT), :]
                    nc.vector.tensor_tensor(xx, xx, bc(bias2[:, :], 1, HT), ALU.add).then_inc(dve.sem, 1)
                    ve.wait_ge(dve.sem, dve.after("bias", i))
                    for e in E:
                        ve.wait_ge(pe.sem, pe.after(f"o{e}", i))
                        if e:
                            ve.wait_ge(dve.sem, dve.after(f"b{e-1}", i))
                        for n in range(2):
                            xx = c.X[:, bass.ds(i * HT + 2 * n, 2), :]
                            nc.vector.scalar_tensor_tensor(out=xx, in0=B[4 + 2 * (e % 2) + n][:, :].rearrange("p (t n) -> p t n", t=2),
                                                           scalar=G[:, e:e + 1], in1=xx, op0=ALU.mult, op1=ALU.add).then_inc(dve.sem, 1)


def build(nc, dram):
    with ExitStack() as ctx:
        c = Core(nc, ctx, dram)
        for n, stage in enumerate(STAGES):
            stage(c)
            if n == 2:
                c.l0.close()
            if n == 3:
                c.cross.close()
                c.moe_W1, c.moe_W2 = c.sb("moe_W1_sb", [P, NE * KC, D]), c.sb("moe_W2_sb", [P, NE * KC, D])
                c.moe_b2, c.Wr = c.sb("moe_b2_sb", [NE, D]), c.sb("moe_Wr_sb", [P, KC, NE])
                c.moe_loads = {
                    "moe_W1": (c.moe_W1[:, :, :], dram["moe_W1"].rearrange("(c p) n -> p c n", p=P)),
                    "moe_W2": (c.moe_W2[:, :, :], dram["moe_W2"].rearrange("(c p) n -> p c n", p=P)),
                    "moe_b2": (c.moe_b2[:, :], dram["moe_b2"]),
                    "moe_Wr": (c.Wr[:, :, :], dram["L1_ffn_Wr"].rearrange("(c p) n -> p c n", p=P)),
                }
                c.loaded.update({n: c.sem(n + "_in") for n in c.moe_loads})
        stored = c.sem("stored")
        with nc.Block() as block:
            @block.sync
            def _(sp):
                for j in range(TB):
                    sp.dma_start(by_column(dram["out"], j), c.X[j * S:(j + 1) * S, :, :]).then_inc(stored, 16)
                sp.wait_ge(stored, 16 * TB)


STAGES = [stage_l0_cross, stage_l0_gla, stage_l0_ffn, stage_l1_cross, stage_l1_linear, stage_moe]


def masks():
    p = np.arange(P)
    inv_freq = 1.0 / np.float32(10000.0) ** (np.arange(0, 4, dtype=np.float32) * np.float32(2.0) / np.float32(8.0))
    angles = (p[:, None] % S).astype(np.float32) * inv_freq.astype(np.float32)[None]
    m = {
        "ident": np.eye(P),
        "fold": p[:, None] % S == np.arange(S),
        "hmask": p[:, None] // S == np.arange(4),
        "qmask": (p[:, None] // 16 == np.arange(8)) * 0.25,
        "causal": (p[:, None] // S == p // S) & (p[:, None] <= p),
        "spread": np.concatenate([p[:, None] == b * S + p % S for b in range(TB)], axis=1),
        "half": (p[:, None] // 64 == np.arange(2)) * 0.125,
        "cos": np.cos(angles), "sin": np.sin(angles),
        "earlier": np.broadcast_to((np.arange(NE)[None, :] < np.arange(NE)[:, None]).reshape(1, -1), (P, NE * NE)),
    }
    return np.concatenate([m[n].astype(np.float32) for n in MASKS], axis=1)


def kernel(**inputs):
    import concourse.bacc as _bacc
    from concourse.bass_utils import run_bass_kernel_spmd as _run

    a = {n: np.asarray(v) for n, v in inputs.items()}
    ctx = a["ctx_1024"]
    a["conv0"], a["conv1"] = a["L1_attn_conv_w"].T
    a["L1_attn_router_w"] = a["L1_attn_router_w"].transpose(0, 2, 1)
    a["L1_attn_Wqk"] = np.concatenate([a["L1_attn_Wq"], a["L1_attn_Wk"]], axis=1)
    for n in ("L1_attn_w1", "L1_attn_w3"):
        a[n] = np.pad(a[n], ((0, 0), (0, FFP - FF)))
    a["L1_attn_w2"] = np.pad(a["L1_attn_w2"], ((0, FFP - FF), (0, 0)))
    a["moe_W1"], a["moe_W2"] = a["L1_ffn_W1"].reshape(NE * D, D), a["L1_ffn_W2"].reshape(NE * D, D)
    arrays = {
        "x": a["x"].reshape(NT, P, D).transpose(1, 0, 2),
        "ctxT": np.pad(ctx.transpose(0, 2, 1), ((0, TB), (0, 0), (0, 0))),
        "ctx_lastT": ctx[:, KEYS - 1].T,
        "masks": masks(),
        "cols": np.concatenate([a[n].reshape(-1, P).T for n in COLS], axis=1),
        "repeated": np.broadcast_to(np.concatenate([a[n].reshape(-1) for n in REPEATED]), (P, REP_N)),
        "ctx": np.pad(ctx[:, 0:KEYS - 1].reshape(NB, 2, P, D).transpose(0, 2, 1, 3), ((0, TB), (0, 0), (0, 0), (0, 0))),
        "ctx_last": np.pad(ctx[:, KEYS - 1], ((0, TB), (0, 0))),
        "W_exp": a["L0_ffn_W_exp"],
        "W_conT": a["L0_ffn_W_con"].T,
        "b_exp": a["L0_ffn_b_exp"][None],
        "bf_weights": np.concatenate([w.reshape(STAGES_BF, F0 // 2, 4).transpose(0, 2, 1) for w in
                                      (a["L0_ffn_up_weights"], a["L0_ffn_down_weights"][::-1])]),
        "L0_attn_Wgk2": a["L0_attn_Wgk2"],
        "rows": np.concatenate([a[n] for n in ROWS])[None],
    }
    arrays["moe_b2"], arrays["L1_ffn_Wr"] = a["L1_ffn_b2"], a["L1_ffn_Wr"]
    arrays["moe_W1"], arrays["moe_W2"] = a["moe_W1"], a["moe_W2"]
    for n in (*WEIGHTS_L0, *WEIGHTS_CROSS, *WEIGHTS_L1):
        arrays[n] = a[n].T if n.startswith("L0_xattn") else a[n]
    nc = _bacc.Bacc("TRN2", target_bir_lowering=False, num_devices=1)
    dram, feed = {}, {}
    for n, v in arrays.items():
        feed["in_" + n] = np.ascontiguousarray(v)
        dram[n] = nc.dram_tensor("in_" + n, v.shape, F32, kind="ExternalInput").ap()
    dram["turned"] = nc.dram_tensor("turned", (NB, S, D), F32, kind="Internal").ap()
    dram["out"] = nc.dram_tensor("out_0", (NB, S, D), F32, kind="ExternalOutput").ap()
    build(nc, dram)
    r = _run(nc, [feed], core_ids=[0])
    return r.results[0]["out_0"]
```

```python
from contextlib import ExitStack

import numpy as np
import concourse.bass as bass
from concourse import mybir

F32 = mybir.dt.float32
I32 = mybir.dt.int32
ALU = mybir.AluOpType
ACT = mybir.ActivationFunctionType
AX_X = mybir.AxisListType.X

P = 128
NB, S, D = 32, 32, 256
KEYS = 257
TB = P // S
NT = NB // TB
KC = D // P
EPS = 1e-5


class Steps:

    def __init__(self, sem, names):
        self.sem = sem
        self.names = [n.removesuffix("'") for n in names.split()]
        self.ahead = {n.removesuffix("'") for n in names.split() if n.endswith("'")}
        self.per_turn = len(self.names)
        self.counted = 0
        assert len(set(self.names)) == self.per_turn, names

    def skip_to(self, eng, name, steps):
        at = self.names.index(name)
        if self.counted:
            eng.wait_ge(self.sem, self.counted)
        if at > self.counted:
            eng.sem_inc(self.sem, at - self.counted)
        self.counted = at + steps

    def skip_to_end(self, eng):
        eng.wait_ge(self.sem, self.counted)
        if self.counted < self.per_turn:
            eng.sem_inc(self.sem, self.per_turn - self.counted)

    def first_turn(self, eng):
        eng.sem_inc(self.sem, self.per_turn)

    def after(self, name, turn):
        return (turn + (0 if name in self.ahead else 1)) * self.per_turn + (self.names.index(name) + 1)


def bc(ap, pos, n):
    a = ap.unsqueeze(pos)
    return a.to_broadcast([*a.shape[:pos], n, *a.shape[pos + 1:]])


FF, FFP = 704, 768
NE = 8
WEIGHTS_L1 = {
    "L1_attn_Wqk": (D, D), "L1_attn_Wv": (D, D), "L1_attn_Wg": (D, D), "L1_attn_Wout": (D, D),
    "L1_attn_w1": (D, FFP), "L1_attn_w3": (D, FFP), "L1_attn_w2": (FFP, D),
}
WEIGHTS_CROSS = {
    "L1_xattn_Wq": (D, 768), "L1_xattn_Wk": (D, 768), "L1_xattn_Wv": (D, 768), "L1_xattn_Wo": (768, D),
}
WEIGHTS_L0 = {
    "L0_xattn_Wq": (D, D), "L0_xattn_Wk": (D, D), "L0_xattn_Wv": (D, D), "L0_xattn_Wo": (D, D),
    "L0_attn_Wq": (D, P), "L0_attn_Wk": (D, P), "L0_attn_Wv": (D, D), "L0_attn_Wg": (D, D),
    "L0_attn_Wgk1": (D, 16), "L0_attn_Wout": (D, D),
}
COLS = {
    "L0_xattn_bq": D, "L0_xattn_bk": D, "L0_xattn_bv": D, "L0_attn_bgk2": P,
    "L1_xattn_tab_g": D, "L1_xattn_tab_b": D, "L1_xattn_vid_g": D, "L1_xattn_vid_b": D,
    "L1_xattn_q_g": 768, "L1_xattn_q_b": 768, "L1_xattn_k_g": 768, "L1_xattn_k_b": 768,
    "L1_attn_ln1_w": D, "L1_attn_ln1_b": D, "L1_attn_ln2_w": D, "L1_attn_ln2_b": D, "conv0": D, "conv1": D,
    "L1_ffn_b1": NE * D,
}
ROWS = {
    "L0_xattn_bo": D, "L0_ffn_up_bias": 1024, "L0_ffn_b_con": D, "L0_ffn_down_bias": D, "L1_xattn_bo": D, "L1_ffn_br": NE,
}
REPEATED = {
    "L0_attn_rms_w": 64, "L1_xattn_tab_g": D, "L1_attn_router_w": 512,
}
MASKS = {"ident": P, "fold": S, "hmask": 4, "qmask": 8, "causal": P, "spread": 4 * P, "half": 2, "cos": 4, "sin": 4, "earlier": NE * NE}
HT = 4
HN = HT * P


def offsets(sizes):
    at, out = 0, {}
    for name, n in sizes.items():
        out[name] = at
        at += n
    return out, at


COL_AT, COL_N = offsets({n: k // P for n, k in COLS.items()})
ROW_AT, ROW_N = offsets(ROWS)
REP_AT, REP_N = offsets(REPEATED)
MASK_AT, MASK_N = offsets(MASKS)


class Core:

    def __init__(self, nc, ctx, dram):
        self.nc, self.ctx, self.dram = nc, ctx, dram
        self.PS = ctx.enter_context(nc.psum_tensor("banks", [P, 8, 512], F32))
        self.bank = [self.PS[:, n, :] for n in range(8)]
        self.waited = self.sem("waited")
        self.X = self.sb("x_sb", [P, NT, D])
        self.masks = self.sb("masks_sb", [P, MASK_N])
        self.eps, self.mhalf, self.ones = self.sb("eps", [P, 16]), self.sb("mhalf", [P, 16]), self.sb("ones", [1, P])
        self.fold, self.hmask, self.qmask = self.mask("fold"), self.mask("hmask"), self.mask("qmask")
        self.cols_sb, self.rows_sb = self.sb("cols_sb", [P, COL_N]), self.sb("rows_sb", [1, ROW_N])
        self.rep_sb = self.sb("repeated_sb", [P, REP_N])
        self.stored_tiles = self.sem("stored_tiles")
        self.w, self.loads, self.loaded = {}, {}, {}
        self.weights(WEIGHTS_L1, ctx)
        self.xn = self.w["L1_attn_w1"][:, :, :].rearrange("p c n -> p (c n)")[:, 0:HT * D].rearrange("p (t d) -> p t d", t=HT)
        self.w1_load = self.loads.pop("L1_attn_w1")
        self.cross, self.l0 = ExitStack(), ExitStack()
        self.weights(WEIGHTS_CROSS, self.cross)
        self.weights(WEIGHTS_L0, self.l0)
        self.W1e, self.W2eT = self.sb("W1e", [P, KC + 1, 1024], self.l0), self.sb("W2eT", [P, KC, 1024], self.l0)
        self.ffn_bias = self.sb("ffn_bias", [1, D], self.l0)
        self.narrow = self.sb("narrow", [16, P], self.l0)
        early = {"cols": (self.cols_sb[:, :], dram["cols"]), "rows": (self.rows_sb[:, :], dram["rows"]),
                 "repeated": (self.rep_sb[:, :], dram["repeated"]),
                 "L0_attn_Wgk2": (self.narrow[:, :], dram["L0_attn_Wgk2"])}
        late = [n for n in self.loads if not n.startswith("L0")]
        self.loads = {**early, **{n: self.loads[n] for n in self.loads if n not in late}, **{n: self.loads[n] for n in reversed(late)}}
        self.loaded.update({name: self.sem(name + "_in") for name in ["x", "masks", *early]})

    def weights(self, shapes, ctx):
        for name, (rows, columns) in shapes.items():
            self.w[name] = self.sb(name + "_sb", [P, rows // P, columns], ctx)
            self.loads[name] = (self.w[name][:, :, :], self.dram[name].rearrange("(c p) n -> p c n", p=P))
            self.loaded[name] = self.sem(name + "_in")

    def allocate_experts(self):
        self.xn_late = self.sb("xn_late", [P, HT, D])
        self.moe_W1, self.moe_W2 = self.sb("moe_W1_sb", [P, NE * KC, D]), self.sb("moe_W2_sb", [P, NE * KC, D])
        self.moe_b2, self.Wr = self.sb("moe_b2_sb", [NE, D]), self.sb("moe_Wr_sb", [P, KC, NE])
        self.moe_loads = {
            "moe_W1": (self.moe_W1[:, :, :], self.dram["moe_W1"].rearrange("(c p) n -> p c n", p=P)),
            "moe_W2": (self.moe_W2[:, :, :], self.dram["moe_W2"].rearrange("(c p) n -> p c n", p=P)),
            "moe_b2": (self.moe_b2[:, :], self.dram["moe_b2"]),
            "moe_Wr": (self.Wr[:, :, :], self.dram["L1_ffn_Wr"].rearrange("(c p) n -> p c n", p=P)),
        }
        self.loaded.update({n: self.sem(n + "_in") for n in self.moe_loads})

    def sb(self, name, shape, ctx=None):
        return (ctx or self.ctx).enter_context(self.nc.sbuf_tensor(name, shape, F32))

    def sem(self, name, ctx=None):
        return (ctx or self.ctx).enter_context(self.nc.semaphore(name))

    def steps(self, ctx, name, names):
        return Steps(self.sem(name + "_done", ctx), names)

    def mask(self, name):
        return self.masks[:, MASK_AT[name]:MASK_AT[name] + MASKS[name]]

    def ident(self):
        return self.mask("ident")

    def col(self, name, m):
        return self.cols_sb[:, COL_AT[name] + m:COL_AT[name] + m + 1]

    def cols2(self, name):
        return self.cols_sb[:, COL_AT[name]:COL_AT[name] + COLS[name] // P]

    def rep(self, name):
        return self.rep_sb[:, REP_AT[name]:REP_AT[name] + REPEATED[name]]

    def row(self, name):
        return self.rows_sb[:, ROW_AT[name]:ROW_AT[name] + ROWS[name]]


def half_tiles(c, i):
    return lambda t: c.X[:, bass.ds(i * HT + t, 1), :].rearrange("p t d -> p (t d)")


def norm_half(c, ve, dve, pool, pre, i, src, dst, st, mv, rs):
    ve.sem_inc(c.waited)
    for t in range(HT):
        op = c.nc.vector.bn_stats(st[:, t, :], src(t))
    op.then_inc(dve.sem, 1)
    ve.wait_ge(dve.sem, dve.after(pre + "stats", i))
    ve.sem_inc(c.waited)
    for t in range(HT):
        op = c.nc.vector.bn_aggr(mv[:, t, :], st[:, t, :])
    op.then_inc(dve.sem, 1)
    ve.wait_ge(pool.sem, pool.after(pre + "rstd", i))
    ve.sem_inc(c.waited)
    for t in range(HT):
        op = c.nc.vector.tensor_scalar(dst(t), src(t), mv[:, t, 0:1], rs[:, HT + t:HT + t + 1], ALU.subtract, ALU.mult)
    op.then_inc(dve.sem, 1)


def rstd_half(c, gp, pool, dve, pre, i, mv, rs):
    gp.wait_ge(dve.sem, dve.after(pre + "moments", i))
    c.nc.gpsimd.tensor_tensor(rs[:, 0:HT], mv[:, :, 1:2].rearrange("p t o -> p (t o)"), c.eps[:, 0:HT], ALU.add).then_inc(pool.sem, 1)
    gp.wait_ge(pool.sem, pool.after(pre + "vareps", i))
    c.nc.gpsimd.tensor_tensor(rs[:, HT:2 * HT], rs[:, 0:HT], c.mhalf[:, 0:HT], ALU.pow).then_inc(pool.sem, 1)


STAGES_BF = 10
F0 = 2 ** STAGES_BF


class Butterflies:

    def __init__(self, c, ctx):
        self.c = c
        self.t = [c.sb(f"bf_t{n}", [P, 3, F0 // 2], ctx) for n in range(2)]
        self.wts = [c.sb(f"bf_wts{n}", [P, 4, F0 // 2], ctx) for n in range(2)]
        self.wts_in = [c.sem(f"bf_wts_in{n}", ctx) for n in range(2)]
        self.bias_in = c.sem("bf_bias_in", ctx)
        self.up_in, self.zero, self.done = c.sem("bf_up_in", ctx), c.sem("bf_zero", ctx), c.sem("bf_done", ctx)

    def load_first(self, sp):
        c = self.c
        sp.dma_start(c.W1e[:, 0:KC, :], c.dram["W_exp"].rearrange("(c p) f -> p c f", p=P)).then_inc(self.up_in, 16)
        sp.dma_start(c.W2eT[:, :, :], c.dram["W_conT"].rearrange("(c p) f -> p c f", p=P)).then_inc(self.up_in, 16)

    def load_weights(self, eng, n):
        eng.dma_start(self.wts[n % 2][:, :, :], self.c.dram["bf_weights"][n:n + 1].to_broadcast([P, 4, F0 // 2])).then_inc(self.wts_in[n % 2], 16)


def start_butterflies(c, gp, bf):
    c.nc.gpsimd.memset(c.W1e[:, KC, :], 0.0).then_inc(bf.zero, 1)
    gp.wait_ge(bf.zero, 1)
    gp.dma_start(c.W1e[0:1, KC, :], c.dram["b_exp"]).then_inc(bf.bias_in, 16)
    for n in range(2):
        bf.load_weights(gp, n)


def fold_butterflies(c, gp, bf):
    nc = c.nc
    gp.wait_ge(bf.bias_in, 16)
    gp.wait_ge(bf.up_in, 32)
    n = 0
    for down in range(2):
        for stage in (range(STAGES_BF) if not down else reversed(range(STAGES_BF))):
            y = c.W2eT if down else c.W1e
            chunks = y.shape[1]
            s, nb = 2 ** stage, F0 // 2 ** (stage + 1)
            yr = y[:, :, :].rearrange("p c (n two s) -> p c n two s", two=2, s=s)
            a, b = yr[:, :, :, 0, :], yr[:, :, :, 1, :]
            w = bf.wts[n % 2]
            wt = [bc(w[:, q, :].rearrange("p (n s) -> p n s", s=s), 1, chunks) for q in ((0, 2, 1, 3) if down else (0, 1, 2, 3))]
            t = [x[:, 0:chunks, :].rearrange("p c (n s) -> p c n s", s=s) for x in bf.t]
            gp.wait_ge(bf.wts_in[n % 2], 16 * (n // 2 + 1))
            nc.gpsimd.tensor_tensor(t[0], a, wt[0], ALU.mult)
            nc.gpsimd.tensor_tensor(t[1], b, wt[1], ALU.mult).then_inc(bf.done, 1)
            gp.wait_ge(bf.done, 4 * n + 1)
            nc.gpsimd.tensor_tensor(a, a, wt[2], ALU.mult)
            nc.gpsimd.tensor_tensor(b, b, wt[3], ALU.mult).then_inc(bf.done, 1)
            gp.wait_ge(bf.done, 4 * n + 2)
            if n + 2 < 2 * STAGES_BF:
                bf.load_weights(gp, n + 2)
            nc.gpsimd.tensor_tensor(b, a, b, ALU.add).then_inc(bf.done, 1)
            gp.wait_ge(bf.done, 4 * n + 3)
            nc.gpsimd.tensor_tensor(a, t[0], t[1], ALU.add).then_inc(bf.done, 1)
            gp.wait_ge(bf.done, 4 * n + 4)
            n += 1
    gp.wait_ge(c.loaded["rows"], 16)
    nc.gpsimd.tensor_tensor(c.W1e[0:1, KC, :], c.W1e[0:1, KC, :], c.row("L0_ffn_up_bias"), ALU.add)
    nc.gpsimd.tensor_tensor(c.ffn_bias[:, :], c.row("L0_ffn_b_con"), c.row("L0_ffn_down_bias"), ALU.add)


def stage_l0_cross(c):
    nc = c.nc
    with ExitStack() as ctx:
        sb = lambda name, shape: c.sb(name, shape, ctx)
        xn, xnT = sb("l0_xn", [P, NT + 1, D]), sb("l0_xnT", [P, KC, NT * P])
        st, mv, rs = sb("l0_st", [P, NT, 6]), sb("l0_mv", [P, NT, 2]), sb("l0_rs", [P, 2 * NT])
        qT = xn[:, :, :].rearrange("p t d -> p (t d)").rearrange("p (m n) -> p m n", m=KC)
        qblk = sb("l0_qblk", [P, KC, TB, 8, S])
        ctxT = [sb(f"l0_ctxT{j}", [P, KC, KEYS]) for j in range(TB)]
        kT = [sb(f"l0_kT{n}", [P, KC, KEYS]) for n in range(2)]
        v = [sb(f"l0_v{n}", [P, 2, D]) for n in range(2)]
        lastT = sb("l0_lastT", [P, KC, NB])
        klast, vlast = sb("l0_klast", [P, KC, NB + TB]), sb("l0_vlast", [TB, NT, D])
        probs = [sb(f"l0_probs{n}", [P, 4, KEYS]) for n in range(2)]
        nmax = [sb(f"l0_nmax{n}", [P, 4]) for n in range(2)]
        total = [sb(f"l0_total{n}", [P, 4]) for n in range(2)]
        plast = [sb(f"l0_plast{j}", [P, 4, TB]) for j in range(TB)]
        probsT = sb("l0_probsT", [P, 2, 512])
        plastT = sb("l0_plastT", [TB, 512])
        rinv, rmask = sb("l0_rinv", [P, 4]), sb("l0_rmask", [P, 4, 4])
        ao = [sb(f"l0_ao{n}", [P, 4, 4, 16]) for n in range(2)]
        aT = sb("l0_aT", [P, KC, P])
        ctx_in = [c.sem(f"l0_ctx_in{j}", ctx) for j in range(TB)]
        last_in, ready = c.sem("l0_last_in", ctx), c.sem("l0_ready", ctx)
        vlast_done = c.sem("l0_vlast_done", ctx)
        J = range(TB)
        pe = c.steps(ctx, "l0_pe", "v1 pT0 kT2 s1 av0 v2 pT1 kT3 s2 fold0 av1 v3 pT2 kT0' s3 fold1 av2 v0' pT3 "
                     "kT1' fold2 av3 s0' fold3 out")
        dve = c.steps(ctx, "l0_dve", "v1 plast0 rinv0 rmask0 pT0 plT0 max1 ao0 plast1 rinv1 rmask1 v2 pT1 plT1 "
                      "max2 ao1 aT0 plast2 rinv2 rmask2 v3 pT2 plT2 max3 qb' ao2 aT1 plast3 rinv3 rmask3 v0' pT3 plT3 "
                      "ao3 aT2 max0' aT3 res")
        act = c.steps(ctx, "l0_act", "e0 pT0 kT2 e1 pT1 kT3 e2 pT2 kT0' e3 pT3 kT1'")
        pro = {n: c.sem("l0_" + n, ctx) for n in ("stats", "moments", "rstd", "norm", "xT", "xT_out", "qT", "qT_out", "klast", "klast_out")}
        B = c.bank
        ident = c.ident()
        ctx_bf = Butterflies(c, ctx)

        with nc.Block() as block:
            @block.sync
            def _(sp):
                sp.dma_start(c.masks[:, :], c.dram["masks"]).then_inc(c.loaded["masks"], 16)
                sp.dma_start(c.X[:, 0:NT, :], c.dram["x"]).then_inc(c.loaded["x"], 16)
                sp.dma_start(lastT[:, :, :], c.dram["ctx_lastT"].rearrange("(c p) b -> p c b", p=P)).then_inc(last_in, 16)
                for name in c.loads:
                    sp.dma_start(*c.loads[name]).then_inc(c.loaded[name], 16)
                    if name == "L0_xattn_Wo":
                        break
                ctx_bf.load_first(sp)

                def load_context(j, t):
                    sp.dma_start(ctxT[j][:, :, :], c.dram["ctxT"][bass.ds(t * TB + j, 1)].rearrange(
                        "b (c p) k -> p (b c) k", p=P)).then_inc(ctx_in[j], 16)

                load_context(0, 0)
                load_context(1, 0)
                with sp.Fori(0, NT) as i:
                    for j, t in ((2, i), (3, i), (0, i + 1), (1, i + 1)):
                        sp.wait_ge(pe.sem, pe.after(f"v{j}", t - 1))
                        load_context(j, t)
                rest = False
                for name in c.loads:
                    if rest:
                        sp.dma_start(*c.loads[name]).then_inc(c.loaded[name], 16)
                    rest = rest or name == "L0_xattn_Wo"

            @block.gpsimd
            def _(gp):
                nc.gpsimd.memset(c.eps[:, :], EPS).then_inc(ready, 1)
                nc.gpsimd.memset(c.mhalf[:, :], -0.5).then_inc(ready, 1)
                nc.gpsimd.memset(c.ones[:, :], 1.0).then_inc(ready, 1)
                for j in J:
                    nc.gpsimd.memset(plast[j][:, :, :], 0.0).then_inc(ready, 1)
                gp.wait_ge(ready, 3 + TB)
                start_butterflies(c, gp, ctx_bf)
                gp.wait_ge(pro["moments"], NT)
                nc.gpsimd.tensor_tensor(rs[:, 0:NT], mv[:, :, 1:2].rearrange("p t o -> p (t o)"), c.eps[:, 0:NT],
                                        ALU.add).then_inc(pro["rstd"], 1)
                gp.wait_ge(pro["rstd"], 1)
                nc.gpsimd.tensor_tensor(rs[:, NT:2 * NT], rs[:, 0:NT], c.mhalf[:, 0:NT], ALU.pow).then_inc(pro["rstd"], 1)
                fold_butterflies(c, gp, ctx_bf)

            @block.tensor
            def _(te):
                for name in ("masks", "L0_xattn_Wq", "L0_xattn_Wk", "L0_xattn_Wv", "L0_xattn_Wo", "cols", "rows"):
                    te.wait_ge(c.loaded[name], 16)
                te.wait_ge(ready, 3 + TB)
                te.wait_ge(last_in, 16)
                for t in range(NT):
                    for k in range(KC):
                        mm = nc.tensor.matmul(B[t % 8][0:TB, 0:D], lastT[:, k, t * TB:(t + 1) * TB],
                                              c.w["L0_xattn_Wv"][:, k, :], start=(k == 0), stop=(k == KC - 1))
                    mm.then_inc(vlast_done, 1)
                te.wait_ge(ready, 3 + TB + NT)
                te.wait_ge(pro["norm"], 1)
                for k in range(KC):
                    for t in range(NT):
                        mm = nc.tensor.transpose(B[2 * k + t // 4][:, (t % 4) * P:(t % 4 + 1) * P], xn[:, t, k * P:(k + 1) * P], ident)
                mm.then_inc(pro["xT"], 1)
                te.wait_ge(pro["xT_out"], 2)
                for m in range(2):
                    for n in range(2):
                        for k in range(KC):
                            mm = nc.tensor.matmul(B[4 + 2 * m + n][:, :], c.w["L0_xattn_Wq"][:, k, m * P:(m + 1) * P],
                                                  xnT[:, k, n * 512:(n + 1) * 512], start=(k == 0), stop=(k == KC - 1))
                mm.then_inc(pro["qT"], 1)
                te.wait_ge(pro["qT_out"], 2)
                for m in range(2):
                    for k in range(KC):
                        mm = nc.tensor.matmul(B[6][:, m * NB:(m + 1) * NB], c.w["L0_xattn_Wk"][:, k, m * P:(m + 1) * P], lastT[:, k, :],
                                              start=(k == 0), stop=(k == KC - 1))
                mm.then_inc(pro["klast"], 1)

                def keys(j, t):
                    te.wait_ge(ctx_in[j], 16 * (t + 1))
                    te.wait_ge(dve.sem, dve.after(f"v{j-1}", t) if j else dve.after("v3", t - 1))
                    for m in range(2):
                        for k in range(KC):
                            mm = nc.tensor.matmul(B[0][:, m * D:(m + 1) * D], c.w["L0_xattn_Wk"][:, k, m * P:(m + 1) * P],
                                                  ctxT[j][:, k, 0:D], start=(k == 0), stop=(k == KC - 1))
                    mm.then_inc(pe.sem, 1)

                def values(j, t):
                    te.wait_ge(act.sem, act.after(f"kT{j}", t))
                    for h in range(2):
                        for k in range(KC):
                            mm = nc.tensor.matmul(B[0][:, h * D:(h + 1) * D], ctxT[j][:, k, h * P:(h + 1) * P],
                                                  c.w["L0_xattn_Wv"][:, k, :], start=(k == 0), stop=(k == KC - 1))
                    mm.then_inc(pe.sem, 1)

                def scores(j, t):
                    te.wait_ge(act.sem, act.after(f"kT{j}", t))
                    te.wait_ge(act.sem, act.after(f"e{j-1}", t) if j else act.after("e3", t - 1))
                    if j == 0:
                        te.wait_ge(dve.sem, dve.after("qb", t))
                    for g in range(4):
                        mm = nc.tensor.matmul(B[1 + g][:, 0:KEYS], qblk[:, g // 2, j, 4 * (g % 2):4 * (g % 2) + 4, :].rearrange("p h q -> p (h q)"),
                                              kT[j % 2][:, g // 2, :], start=True, stop=True)
                    mm.then_inc(pe.sem, 1)

                def transposes(j, i):
                    te.wait_ge(act.sem, act.after(f"e{j}", i))
                    te.wait_ge(dve.sem, dve.after(f"plast{j}", i))
                    te.wait_ge(dve.sem, dve.after(f"ao{j-1}", i) if j else dve.after("res", i - 1))
                    if j > 1:
                        te.wait_ge(dve.sem, dve.after(f"aT{j-2}", i))
                    for h in range(2):
                        for g in range(4):
                            nc.tensor.transpose(B[5 + h][:, g * P:(g + 1) * P], probs[j % 2][:, g, h * P:(h + 1) * P], ident)
                    for g in range(4):
                        mm = nc.tensor.transpose(B[7][0:TB, g * P:(g + 1) * P], plast[j][:, g, :], ident)
                    mm.then_inc(pe.sem, 1)

                def weighted(j, i):
                    te.wait_ge(act.sem, act.after(f"pT{j}", i))
                    te.wait_ge(dve.sem, dve.after(f"plT{j}", i))
                    for g in range(4):
                        o = B[7][:, g * 64:(g + 1) * 64]
                        for h in range(2):
                            nc.tensor.matmul(o, probsT[:, h, g * P:(g + 1) * P], v[j % 2][:, h, g * 64:(g + 1) * 64],
                                             start=(h == 0), stop=False)
                        mm = nc.tensor.matmul(o, plastT[:, g * P:(g + 1) * P], vlast[:, bass.ds(i, 1), g * 64:(g + 1) * 64].rearrange("p t n -> p (t n)"),
                                              start=False, stop=True)
                    mm.then_inc(pe.sem, 1)

                def fold_heads(j, i):
                    te.wait_ge(dve.sem, dve.after(f"ao{j}", i))
                    if j < 3:
                        te.wait_ge(dve.sem, dve.after(f"plT{j+1}", i))
                    for m in range(2):
                        mm = nc.tensor.matmul(B[7][:, D + m * S:D + (m + 1) * S],
                                              ao[j % 2][:, 2 * m:2 * m + 2, :, :].rearrange("p g h d -> p (g h d)"),
                                              c.fold[:, :], start=True, stop=True)
                    mm.then_inc(pe.sem, 1)

                pe.skip_to(te, "kT0", 1)
                keys(0, 0)
                pe.skip_to(te, "v0", 1)
                values(0, 0)
                pe.skip_to(te, "kT1", 1)
                keys(1, 0)
                pe.skip_to(te, "s0", 1)
                scores(0, 0)
                pe.skip_to_end(te)
                with te.Fori(0, NT) as i:
                    values(1, i)
                    transposes(0, i)
                    for j in range(3):
                        after_next = (j + 2, i) if j < 2 else (0, i + 1)
                        keys(*after_next)
                        scores(j + 1, i)
                        if j:
                            fold_heads(j - 1, i)
                        weighted(j, i)
                        values(*after_next)
                        transposes(j + 1, i)
                    keys(1, i + 1)
                    fold_heads(2, i)
                    weighted(3, i)
                    scores(0, i + 1)
                    te.wait_ge(dve.sem, dve.after("aT2", i))
                    fold_heads(3, i)
                    te.wait_ge(dve.sem, dve.after("aT3", i))
                    for k in range(KC):
                        nc.tensor.matmul(B[7][:, 0:D], aT[:, k, :], c.w["L0_xattn_Wo"][:, k, :], start=(k == 0), stop=False)
                    nc.tensor.matmul(B[7][:, 0:D], c.ones[0:1, :], c.row("L0_xattn_bo"), start=False, stop=True).then_inc(pe.sem, 1)

            @block.scalar
            def _(sc):
                sc.wait_ge(c.loaded["cols"], 16)

                sc.wait_ge(pro["xT"], 1)
                nc.scalar.copy(xnT[:, 1, :], c.PS[:, 2:4, :].rearrange("p b n -> p (b n)")).then_inc(pro["xT_out"], 1)
                sc.wait_ge(pro["qT"], 1)
                for m in range(2):
                    op = nc.scalar.activation(qT[:, m, 0:NT * P], c.PS[:, 4 + 2 * m:6 + 2 * m, :].rearrange("p b n -> p (b n)"),
                                              ACT.Identity, bias=c.col("L0_xattn_bq", m))
                op.then_inc(pro["qT_out"], 1)

                sc.wait_ge(pro["klast"], 1)
                for m in range(2):
                    op = nc.scalar.activation(klast[:, m, 0:NB], B[6][:, m * NB:(m + 1) * NB], ACT.Identity, bias=c.col("L0_xattn_bk", m))
                op.then_inc(pro["klast_out"], 1)
                sc.wait_ge(pro["klast_out"], 1)

                def keys_out(j, t):
                    sc.wait_ge(pe.sem, pe.after(f"kT{j}", t))
                    sc.wait_ge(pe.sem, pe.after(f"s{j-2}", t) if j > 1 else pe.after(f"s{j+2}", t - 1))
                    sc.sem_inc(c.waited)
                    for m in range(2):
                        nc.scalar.activation(kT[j % 2][:, m, 0:D], B[0][:, m * D:(m + 1) * D], ACT.Identity,
                                             bias=c.col("L0_xattn_bk", m))
                    nc.scalar.copy(kT[j % 2][:, :, D:D + 1], klast[:, :, bass.ds(t * TB + j, 1)]).then_inc(act.sem, 1)

                def exps(j, i):
                    sc.wait_ge(dve.sem, dve.after(f"max{j}", i))
                    sc.wait_ge(pe.sem, pe.after(f"pT{j-2}", i) if j > 1 else pe.after(f"pT{j+2}", i - 1))
                    for g in range(4):
                        op = nc.scalar.activation(probs[j % 2][:, g, :], B[1 + g][:, 0:KEYS], ACT.Exp, bias=nmax[j % 2][:, g:g + 1],
                                                  accum_out=total[j % 2][:, g:g + 1])
                    op.then_inc(act.sem, 1)

                act.skip_to(sc, "kT0", 1)
                keys_out(0, 0)
                act.skip_to(sc, "kT1", 1)
                keys_out(1, 0)
                act.skip_to_end(sc)
                with sc.Fori(0, NT) as i:
                    for j in J:
                        if j:
                            keys_out(*((j + 1, i) if j < 3 else (0, i + 1)))
                        exps(j, i)
                        sc.wait_ge(pe.sem, pe.after(f"pT{j}", i))
                        sc.wait_ge(pe.sem, pe.after(f"av{j-1}", i) if j else pe.after("av3", i - 1))
                        nc.scalar.copy(probsT[:, 1, :], B[6][:, :]).then_inc(act.sem, 1)
                    keys_out(1, i + 1)

            @block.vector
            def _(ve):
                for name in ("x", "cols", "masks"):
                    ve.wait_ge(c.loaded[name], 16)
                ve.wait_ge(ready, 3 + TB)
                for t in range(NT):
                    nc.vector.bn_stats(st[:, t, :], c.X[:, t, :]).then_inc(pro["stats"], 1)
                ve.wait_ge(pro["stats"], NT)
                for t in range(NT):
                    nc.vector.bn_aggr(mv[:, t, :], st[:, t, :]).then_inc(pro["moments"], 1)
                ve.wait_ge(pro["moments"], NT)
                for t in range(NT):
                    ve.wait_ge(vlast_done, t + 1)
                    nc.vector.tensor_copy(vlast[:, t, :], B[t % 8][0:TB, 0:D]).then_inc(ready, 1)

                ve.wait_ge(pro["rstd"], 2)
                for t in range(NT):
                    op = nc.vector.tensor_scalar(xn[:, t, :], c.X[:, t, :], mv[:, t, 0:1], rs[:, NT + t:NT + t + 1],
                                                 ALU.subtract, ALU.mult)
                op.then_inc(pro["norm"], 1)
                ve.wait_ge(pro["xT"], 1)
                nc.vector.tensor_copy(xnT[:, 0, :], c.PS[:, 0:2, :].rearrange("p b n -> p (b n)")).then_inc(pro["xT_out"], 1)
                nc.vector.memset(qT[:, :, NT * P:(NT + 1) * P], 0.0)
                nc.vector.memset(klast[:, :, NB:NB + TB], 0.0).then_inc(pro["qT_out"], 1)
                ve.wait_ge(pro["qT_out"], 2)

                def row_max(j, t):
                    ve.wait_ge(pe.sem, pe.after(f"s{j}", t))
                    nc.vector.tensor_reduce(nmax[j % 2][:, :], c.PS[:, 1:5, 0:KEYS], AX_X, ALU.max, negate=True).then_inc(dve.sem, 1)

                def values_out(j, t):
                    ve.wait_ge(pe.sem, pe.after(f"v{j}", t))
                    ve.wait_ge(pe.sem, pe.after(f"av{j-2}", t) if j > 1 else pe.after(f"av{j+2}", t - 1))
                    nc.vector.tensor_copy(v[j % 2][:, :, :].rearrange("p h n -> p (h n)"), B[0][:, :]).then_inc(dve.sem, 1)

                def block_queries(t):
                    ve.wait_ge(pe.sem, pe.after("s3", t - 1))
                    for m in range(2):
                        op = nc.vector.tensor_tensor(
                            qblk[:, m, :, :, :], bc(qT[:, m, bass.ds(t * P, P)].rearrange("p (b q) -> p b q", b=TB), 2, 8),
                            c.qmask[:, :].unsqueeze(1).unsqueeze(3).to_broadcast([P, TB, 8, S]), ALU.mult)
                    op.then_inc(dve.sem, 1)

                def last_and_sums(j, i):
                    ve.wait_ge(act.sem, act.after(f"e{j}", i))
                    nc.vector.tensor_copy(plast[j][:, :, j:j + 1], probs[j % 2][:, :, KEYS - 1:KEYS]).then_inc(dve.sem, 1)
                    nc.vector.reciprocal(rinv[:, :], total[j % 2][:, :]).then_inc(dve.sem, 1)
                    ve.wait_ge(dve.sem, dve.after(f"rinv{j}", i))
                    nc.vector.tensor_tensor(rmask[:, :, :], bc(rinv[:, :], 2, 4), bc(c.hmask[:, :], 1, 4),
                                            ALU.mult).then_inc(dve.sem, 1)

                def probs_out(j, i):
                    ve.wait_ge(pe.sem, pe.after(f"pT{j}", i))
                    nc.vector.tensor_copy(probsT[:, 0, :], B[5][:, :]).then_inc(dve.sem, 1)
                    nc.vector.tensor_copy(plastT[:, :], B[7][0:TB, :]).then_inc(dve.sem, 1)

                def normalize(j, i):
                    ve.wait_ge(pe.sem, pe.after(f"av{j}", i))
                    nc.vector.tensor_tensor(ao[j % 2][:, :, :, :], B[7][:, 0:D].rearrange("p (g h d) -> p g h d", g=4, h=4),
                                            bc(rmask[:, :, :], 3, 16), ALU.mult).then_inc(dve.sem, 1)

                def folded_out(j, i):
                    ve.wait_ge(pe.sem, pe.after(f"av{j+1}" if j < 3 else "fold3", i))
                    nc.vector.tensor_tensor(aT[:, :, j * S:(j + 1) * S], B[7][:, D:D + 2 * S].rearrange("p (m q) -> p m q", m=2),
                                            bc(c.cols2("L0_xattn_bv"), 2, S), ALU.add).then_inc(dve.sem, 1)

                dve.skip_to(ve, "qb", 1)
                block_queries(0)
                dve.skip_to(ve, "v0", 1)
                values_out(0, 0)
                dve.skip_to(ve, "max0", 1)
                row_max(0, 0)
                dve.skip_to_end(ve)
                with ve.Fori(0, NT) as i:
                    xt = c.X[:, bass.ds(i, 1), :].rearrange("p t d -> p (t d)")
                    values_out(1, i)
                    last_and_sums(0, i)
                    probs_out(0, i)
                    for j in range(3):
                        row_max(j + 1, i)
                        if j == 2:
                            block_queries(i + 1)
                        normalize(j, i)
                        if j:
                            folded_out(j - 1, i)
                        last_and_sums(j + 1, i)
                        values_out(*((j + 2, i) if j < 2 else (0, i + 1)))
                        probs_out(j + 1, i)
                    normalize(3, i)
                    folded_out(2, i)
                    row_max(0, i + 1)
                    folded_out(3, i)
                    ve.wait_ge(pe.sem, pe.after("out", i))
                    nc.vector.tensor_tensor(xt, xt, B[7][:, 0:D], ALU.add).then_inc(dve.sem, 1)


def stage_l0_gla(c):
    nc = c.nc
    with ExitStack() as ctx:
        sb = lambda name, shape: c.sb(name, shape, ctx)
        xn, xnT = c.xn, sb("l0a_xnT", [P, KC, HN])
        st, mv, rs = sb("l0a_st", [P, HT, 6]), sb("l0a_mv", [P, HT, 2]), sb("l0a_rs", [P, 2 * HT])
        g1T = sb("l0a_g1T", [16, HN])
        neg, z, expo, lg = (sb(f"l0a_{n}", [P, HN]) for n in ("neg", "z", "expo", "lg"))
        keep = sb("l0a_keep", [P, HN])
        G, Gc = sb("l0a_G", [P, HN]), sb("l0a_Gc", [P, HN])
        eq, ek = sb("l0a_eq", [P, HN]), sb("l0a_ek", [P, HN])
        qd, kd = sb("l0a_qd", [P, HN]), sb("l0a_kd", [P, HN])
        v, gate, gatew = (sb(f"l0a_{n}", [P, HT, D]) for n in ("v", "gate", "gatew"))
        AT = sb("l0a_AT", [P, 4, HN])
        sq, y = sb("l0a_sq", [P, HT, D]), sb("l0a_y", [P, HT, D])
        yT = sb("l0a_yT", [P, KC, HN])
        ms, ms2 = sb("l0a_ms", [P, 16]), sb("l0a_ms2", [P, 3, 16])
        sixty4th = sb("l0a_64th", [P, 16])
        pe = c.steps(ctx, "l0a_pe", "xT g1 g2 q k v gate scores o yT out")
        dve = c.steps(ctx, "l0a_dve", "xT0 neg z mabs logsig logg scan center qd kd v0 v1 stats' moments' norm' "
                      "c0 c1 c2 c3 ms y0 y1 yg yT0 res0 res1")
        act = c.steps(ctx, "l0a_act", "xT1 g1T exp ln eq ek gate0 gate1 sq0 sq1 yT1")
        pool = c.steps(ctx, "l0a_pool", "vareps' rstd' gatew msn mse msr")
        ready = c.sem("l0a_ready", ctx)
        B = c.bank
        ident = c.ident()
        causal = c.mask("causal")

        with nc.Block() as block:
            @block.gpsimd
            def _(gp):
                pool.skip_to(gp, "vareps", 2)
                rstd_half(c, gp, pool, dve, "", 0, mv, rs)
                pool.skip_to_end(gp)
                nc.gpsimd.memset(sixty4th[:, :], 1.0 / 64).then_inc(ready, 1)
                nc.gpsimd.memset(keep[:, :], 1.0).then_inc(ready, 1)
                gp.wait_ge(ready, 2)
                nc.gpsimd.memset(keep[:, :].rearrange("p (b s) -> p b s", s=S)[:, :, 0:1], 0.0).then_inc(ready, 1)
                nc.gpsimd.memset(AT[:, :, :], 0.0).then_inc(ready, 1)
                gp.wait_ge(c.loaded["repeated"], 16)
                gp.wait_ge(ready, 4)
                with gp.Fori(0, 2) as i:
                    rstd_half(c, gp, pool, dve, "", i + 1, mv, rs)
                    gp.wait_ge(act.sem, act.after("gate1", i))
                    gp.wait_ge(dve.sem, dve.after("yg", i - 1))
                    nc.gpsimd.tensor_tensor(gatew[:, :, :].rearrange("p t (h d) -> p (t h) d", h=4),
                                            gate[:, :, :].rearrange("p t (h d) -> p (t h) d", h=4),
                                            bc(c.rep("L0_attn_rms_w"), 1, 16), ALU.mult).then_inc(pool.sem, 1)
                    gp.wait_ge(dve.sem, dve.after("ms", i))
                    nc.gpsimd.tensor_tensor(ms2[:, 0, :], ms[:, :], sixty4th[:, :], ALU.mult).then_inc(pool.sem, 1)
                    gp.wait_ge(pool.sem, pool.after("msn", i))
                    nc.gpsimd.tensor_tensor(ms2[:, 1, :], ms2[:, 0, :], c.eps[:, :], ALU.add).then_inc(pool.sem, 1)
                    gp.wait_ge(pool.sem, pool.after("mse", i))
                    nc.gpsimd.tensor_tensor(ms2[:, 2, :], ms2[:, 1, :], c.mhalf[:, :], ALU.pow).then_inc(pool.sem, 1)

            @block.tensor
            def _(te):
                pe.first_turn(te)
                for name in c.loaded:
                    if name.startswith("L0_attn"):
                        te.wait_ge(c.loaded[name], 16)

                def feature_major(out, w, k_rhs):
                    for k in range(KC):
                        mm = nc.tensor.matmul(out, w[:, k, :], k_rhs[:, k, :], start=(k == 0), stop=(k == KC - 1))
                    return mm

                def token_major(banks, lhsT, w):
                    for t in range(HT):
                        for k in range(KC):
                            mm = nc.tensor.matmul(B[banks + t // 2][:, (t % 2) * D:(t % 2 + 1) * D], lhsT[:, k, t * P:(t + 1) * P],
                                                  w[:, k, :], start=(k == 0), stop=(k == KC - 1))
                    return mm

                with te.Fori(0, 2) as i:
                    te.wait_ge(dve.sem, dve.after("res1", i - 1))
                    te.wait_ge(dve.sem, dve.after("norm", i))
                    for t in range(HT):
                        for k in range(KC):
                            mm = nc.tensor.transpose(B[k][:, t * P:(t + 1) * P], xn[:, t, k * P:(k + 1) * P], ident)
                    mm.then_inc(pe.sem, 1)
                    te.wait_ge(dve.sem, dve.after("xT0", i))
                    te.wait_ge(act.sem, act.after("xT1", i))
                    feature_major(B[4][0:16, :], c.w["L0_attn_Wgk1"], xnT).then_inc(pe.sem, 1)
                    te.wait_ge(act.sem, act.after("g1T", i))
                    nc.tensor.matmul(B[5][:, :], c.narrow[:, :], g1T[:, :], start=True, stop=True).then_inc(pe.sem, 1)
                    feature_major(B[2][:, :], c.w["L0_attn_Wq"], xnT).then_inc(pe.sem, 1)
                    feature_major(B[3][:, :], c.w["L0_attn_Wk"], xnT).then_inc(pe.sem, 1)
                    token_major(6, xnT, c.w["L0_attn_Wv"]).then_inc(pe.sem, 1)
                    te.wait_ge(dve.sem, dve.after("z", i))
                    token_major(4, xnT, c.w["L0_attn_Wg"]).then_inc(pe.sem, 1)
                    te.wait_ge(dve.sem, dve.after("kd", i))
                    for t in range(HT):
                        for h in range(4):
                            r = slice(32 * h, 32 * h + 32)
                            mm = nc.tensor.matmul(B[h][:, t * P:(t + 1) * P], kd[r, t * P:(t + 1) * P],
                                                  qd[r, t * P:(t + 1) * P], start=True, stop=True)
                    mm.then_inc(pe.sem, 1)
                    te.wait_ge(act.sem, act.after("gate1", i))
                    te.wait_ge(dve.sem, dve.after("v1", i))
                    for h in range(4):
                        te.wait_ge(dve.sem, dve.after(f"c{h}", i))
                        for t in range(HT):
                            mm = nc.tensor.matmul(B[4 + t // 2][:, (t % 2) * D + h * 64:(t % 2) * D + (h + 1) * 64],
                                                  AT[:, h, t * P:(t + 1) * P], v[:, t, h * 64:(h + 1) * 64], start=True, stop=True)
                    mm.then_inc(pe.sem, 1)
                    te.wait_ge(dve.sem, dve.after("yg", i))
                    for t in range(HT):
                        for k in range(KC):
                            mm = nc.tensor.transpose(B[6 + k][:, t * P:(t + 1) * P], y[:, t, k * P:(k + 1) * P], ident)
                    mm.then_inc(pe.sem, 1)
                    te.wait_ge(dve.sem, dve.after("yT0", i))
                    te.wait_ge(act.sem, act.after("yT1", i))
                    token_major(0, yT, c.w["L0_attn_Wout"]).then_inc(pe.sem, 1)

            @block.scalar
            def _(sc):
                act.first_turn(sc)
                with sc.Fori(0, 2) as i:
                    sc.wait_ge(pe.sem, pe.after("xT", i))
                    nc.scalar.copy(xnT[:, 1, :], B[1][:, :]).then_inc(act.sem, 1)
                    sc.wait_ge(pe.sem, pe.after("g1", i))
                    nc.scalar.copy(g1T[:, :], B[4][0:16, :]).then_inc(act.sem, 1)
                    sc.wait_ge(dve.sem, dve.after("mabs", i))
                    nc.scalar.activation(expo[:, :], expo[:, :], ACT.Exp).then_inc(act.sem, 1)
                    sc.wait_ge(act.sem, act.after("exp", i))
                    nc.scalar.activation(lg[:, :], expo[:, :], ACT.Ln, bias=1.0).then_inc(act.sem, 1)
                    sc.wait_ge(dve.sem, dve.after("center", i))
                    nc.scalar.activation(eq[:, :], Gc[:, :], ACT.Exp).then_inc(act.sem, 1)
                    nc.scalar.activation(ek[:, :], Gc[:, :], ACT.Exp, scale=-1.0).then_inc(act.sem, 1)
                    sc.wait_ge(pe.sem, pe.after("gate", i))
                    sc.wait_ge(pool.sem, pool.after("gatew", i - 1))
                    for n in range(2):
                        nc.scalar.activation(gate[:, 2 * n:2 * n + 2, :].rearrange("p t n -> p (t n)"), B[4 + n][:, :],
                                             ACT.Silu).then_inc(act.sem, 1)
                    sc.wait_ge(pe.sem, pe.after("o", i))
                    for n in range(2):
                        nc.scalar.activation(sq[:, 2 * n:2 * n + 2, :].rearrange("p t n -> p (t n)"), B[4 + n][:, :],
                                             ACT.Square).then_inc(act.sem, 1)
                    sc.wait_ge(pe.sem, pe.after("yT", i))
                    nc.scalar.copy(yT[:, 1, :], B[7][:, :]).then_inc(act.sem, 1)

            @block.vector
            def _(ve):
                dve.skip_to(ve, "stats", 3)
                norm_half(c, ve, dve, pool, "", 0, half_tiles(c, 0), lambda t: xn[:, t, :], st, mv, rs)
                dve.skip_to_end(ve)
                ve.wait_ge(ready, 4)
                with ve.Fori(0, 2) as i:
                    ve.wait_ge(pe.sem, pe.after("xT", i))
                    nc.vector.tensor_copy(xnT[:, 0, :], B[0][:, :]).then_inc(dve.sem, 1)
                    ve.wait_ge(pe.sem, pe.after("g2", i))
                    b = c.col("L0_attn_bgk2", 0)
                    nc.vector.tensor_scalar(neg[:, :], B[5][:, :], b, 0.0, ALU.add, ALU.min).then_inc(dve.sem, 1)
                    nc.vector.tensor_scalar(z[:, :], B[5][:, :], b, None, ALU.add).then_inc(dve.sem, 1)
                    ve.wait_ge(dve.sem, dve.after("z", i))
                    nc.vector.scalar_tensor_tensor(out=expo[:, :], in0=neg[:, :], scalar=2.0, in1=z[:, :],
                                                   op0=ALU.mult, op1=ALU.subtract).then_inc(dve.sem, 1)
                    ve.wait_ge(act.sem, act.after("ln", i))
                    nc.vector.tensor_tensor(z[:, :], neg[:, :], lg[:, :], ALU.subtract).then_inc(dve.sem, 1)
                    ve.wait_ge(dve.sem, dve.after("logsig", i))
                    nc.vector.tensor_scalar(neg[:, :], z[:, :], 1.0 / 16, -3.0, ALU.mult, ALU.max).then_inc(dve.sem, 1)
                    ve.wait_ge(dve.sem, dve.after("logg", i))
                    nc.vector.tensor_tensor_scan(G[:, :], keep[:, :], neg[:, :], 0.0, ALU.mult, ALU.add).then_inc(dve.sem, 1)
                    ve.wait_ge(dve.sem, dve.after("scan", i))
                    G3 = G[:, :].rearrange("p (b s) -> p b s", s=S)
                    nc.vector.tensor_tensor(Gc[:, :].rearrange("p (b s) -> p b s", s=S), G3,
                                            G3[:, :, S // 2 - 1:S // 2].to_broadcast([P, HN // S, S]), ALU.subtract).then_inc(dve.sem, 1)
                    ve.wait_ge(pe.sem, pe.after("k", i))
                    ve.wait_ge(act.sem, act.after("ek", i))
                    nc.vector.tensor_tensor(qd[:, :], B[2][:, :], eq[:, :], ALU.mult).then_inc(dve.sem, 1)
                    nc.vector.tensor_tensor(kd[:, :], B[3][:, :], ek[:, :], ALU.mult).then_inc(dve.sem, 1)
                    ve.wait_ge(pe.sem, pe.after("v", i))
                    for n in range(2):
                        nc.vector.tensor_copy(v[:, 2 * n:2 * n + 2, :].rearrange("p t n -> p (t n)"), B[6 + n][:, :]).then_inc(dve.sem, 1)
                    ve.wait_ge(dve.sem, dve.after("res1", i - 1))
                    norm_half(c, ve, dve, pool, "", i + 1, half_tiles(c, 1 - i), lambda t: xn[:, t, :], st, mv, rs)
                    ve.wait_ge(pe.sem, pe.after("scores", i))
                    ve.sem_inc(c.waited)
                    for h in range(4):
                        nc.vector.copy_predicated(AT[:, h, :].rearrange("p (t n) -> p t n", t=HT),
                                                  bc(causal, 1, HT).bitcast(I32),
                                                  B[h][:, :].rearrange("p (t n) -> p t n", t=HT)).then_inc(dve.sem, 1)
                    ve.wait_ge(act.sem, act.after("sq1", i))
                    nc.vector.tensor_reduce(ms[:, :], sq[:, :, :].rearrange("p t (h d) -> p (t h) d", h=4),
                                            AX_X, ALU.add).then_inc(dve.sem, 1)
                    ve.wait_ge(pool.sem, pool.after("msr", i))
                    for n in range(2):
                        nc.vector.tensor_tensor(y[:, 2 * n:2 * n + 2, :].rearrange("p t (h d) -> p (t h) d", h=4),
                                                B[4 + n][:, :].rearrange("p (g d) -> p g d", d=64),
                                                bc(ms2[:, 2, 8 * n:8 * n + 8], 2, 64), ALU.mult).then_inc(dve.sem, 1)
                    ve.wait_ge(dve.sem, dve.after("y1", i))
                    nc.vector.tensor_tensor(y[:, :, :], y[:, :, :], gatew[:, :, :], ALU.mult).then_inc(dve.sem, 1)
                    ve.wait_ge(pe.sem, pe.after("yT", i))
                    nc.vector.tensor_copy(yT[:, 0, :], B[6][:, :]).then_inc(dve.sem, 1)
                    ve.wait_ge(pe.sem, pe.after("out", i))
                    for n in range(2):
                        xx = c.X[:, bass.ds(i * HT + 2 * n, 2), :]
                        nc.vector.tensor_tensor(xx, xx, B[n][:, :].rearrange("p (t n) -> p t n", t=2), ALU.add).then_inc(dve.sem, 1)


def stage_l0_ffn(c):
    nc = c.nc
    FC = F0 // P
    with ExitStack() as ctx:
        sb = lambda name, shape: c.sb(name, shape, ctx)
        xn, xnT = c.xn, sb("l0f_xnT", [P, KC, HN])
        st, mv, rs = sb("l0f_st", [P, HT, 6]), sb("l0f_mv", [P, HT, 2]), sb("l0f_rs", [P, 2 * HT])
        W2e = sb("l0f_W2e", [P, FC, D])
        b1 = sb("l0f_b1", [P, FC])
        hT = sb("l0f_hT", [P, FC, HN])
        hid = " ".join(f"h{j}" for j in range(FC))
        pe = c.steps(ctx, "l0f_pe", f"xT {hid} out")
        dve = c.steps(ctx, "l0f_dve", "xT0 stats' moments' norm' res0 res1")
        act = c.steps(ctx, "l0f_act", f"xT1 {hid}")
        pool = c.steps(ctx, "l0f_pool", "vareps' rstd'")
        prep, prep_out = c.sem("l0f_prep", ctx), c.sem("l0f_prep_out", ctx)
        B = c.bank
        ident = c.ident()
        hbank = lambda j: B[(j + 2) % 8]

        with nc.Block() as block:
            @block.gpsimd
            def _(gp):
                pool.first_turn(gp)
                with gp.Fori(0, 2) as i:
                    rstd_half(c, gp, pool, dve, "", i + 1, mv, rs)

            @block.tensor
            def _(te):
                pe.first_turn(te)
                for j in range(FC):
                    for k in range(KC):
                        nc.tensor.transpose(B[j // 2][:, (j % 2) * D + k * P:(j % 2) * D + (k + 1) * P],
                                            c.W2eT[:, k, j * P:(j + 1) * P], ident)
                for j in range(FC):
                    mm = nc.tensor.matmul(B[4][:, j:j + 1], c.W1e[0:1, KC, j * P:(j + 1) * P], c.ones[0:1, 0:1],
                                          start=True, stop=True)
                mm.then_inc(prep, 1)
                te.wait_ge(prep_out, 2)
                with te.Fori(0, 2) as i:
                    te.wait_ge(act.sem, act.after(f"h{FC-1}", i - 1))
                    te.wait_ge(dve.sem, dve.after("norm", i))
                    for t in range(HT):
                        for k in range(KC):
                            mm = nc.tensor.transpose(B[k][:, t * P:(t + 1) * P], xn[:, t, k * P:(k + 1) * P], ident)
                    mm.then_inc(pe.sem, 1)
                    te.wait_ge(dve.sem, dve.after("xT0", i))
                    te.wait_ge(act.sem, act.after("xT1", i))
                    te.wait_ge(dve.sem, dve.after("res1", i - 1))
                    for j in range(FC):
                        for k in range(KC):
                            mm = nc.tensor.matmul(hbank(j), c.W1e[:, k, j * P:(j + 1) * P], xnT[:, k, :],
                                                  start=(k == 0), stop=(k == KC - 1))
                        mm.then_inc(pe.sem, 1)
                    te.wait_ge(act.sem, act.after(f"h{FC-1}", i))
                    for t in range(HT):
                        o = B[2 + t // 2][:, (t % 2) * D:(t % 2 + 1) * D]
                        for j in range(FC):
                            nc.tensor.matmul(o, hT[:, j, t * P:(t + 1) * P], W2e[:, j, :], start=(j == 0), stop=False)
                        mm = nc.tensor.matmul(o, c.ones[0:1, :], c.ffn_bias[:, :], start=False, stop=True)
                    mm.then_inc(pe.sem, 1)

            @block.scalar
            def _(sc):
                act.first_turn(sc)
                sc.wait_ge(prep, 1)
                nc.scalar.copy(W2e[:, FC // 2:FC, :].rearrange("p j n -> p (j n)"),
                               c.PS[:, 2:4, :].rearrange("p b n -> p (b n)")).then_inc(prep_out, 1)
                with sc.Fori(0, 2) as i:
                    sc.wait_ge(pe.sem, pe.after("xT", i))
                    nc.scalar.copy(xnT[:, 1, :], B[1][:, :]).then_inc(act.sem, 1)
                    for j in range(FC):
                        sc.wait_ge(pe.sem, pe.after(f"h{j}", i))
                        nc.scalar.activation(hT[:, j, :], hbank(j), ACT.Gelu, bias=b1[:, j:j + 1]).then_inc(act.sem, 1)

            @block.vector
            def _(ve):
                dve.first_turn(ve)
                ve.wait_ge(prep, 1)
                nc.vector.tensor_copy(W2e[:, 0:FC // 2, :].rearrange("p j n -> p (j n)"),
                                      c.PS[:, 0:2, :].rearrange("p b n -> p (b n)"))
                nc.vector.tensor_copy(b1[:, :], B[4][:, 0:FC]).then_inc(prep_out, 1)
                with ve.Fori(0, 2) as i:
                    ve.wait_ge(pe.sem, pe.after("xT", i))
                    nc.vector.tensor_copy(xnT[:, 0, :], B[0][:, :]).then_inc(dve.sem, 1)
                    ve.wait_ge(dve.sem, dve.after("res1", i - 1))
                    norm_half(c, ve, dve, pool, "", i + 1, half_tiles(c, 1 - i), lambda t: xn[:, t, :], st, mv, rs)
                    ve.wait_ge(pe.sem, pe.after("out", i))
                    for n in range(2):
                        xx = c.X[:, bass.ds(i * HT + 2 * n, 2), :]
                        nc.vector.tensor_tensor(xx, xx, B[2 + n][:, :].rearrange("p (t n) -> p t n", t=2), ALU.add).then_inc(dve.sem, 1)


HEADS1, HD1 = 12, 64
INNER = HEADS1 * HD1
PAIRS = INNER // P


def prepare_l1_keys(c, s):
    nc = c.nc
    with ExitStack() as ctx:
        sb = lambda name, shape: c.sb(name, shape, ctx)
        mean = sb("l1p_mean", [P, KC])
        WkcT, Cp, kgz = sb("l1p_WkcT", [P, PAIRS, D]), sb("l1p_C", [P, KC, D]), sb("l1p_kgz", [P, PAIRS, 2])
        ve_done, pe_done, act_done = (c.sem("l1p_" + n, ctx) for n in ("ve", "pe", "act"))
        B = c.bank
        Wk = c.w["L1_xattn_Wk"]
        with nc.Block() as block:
            @block.vector
            def _(ve):
                for name in ("L1_xattn_Wk", "cols", "repeated"):
                    ve.wait_ge(c.loaded[name], 16)
                nc.vector.memset(s.qT[:, :, NT * P:(NT + 1) * P], 0.0)
                nc.vector.memset(s.qb[:, NT, :], 0.0)
                nc.vector.memset(s.KB[:, :], 0.0).then_inc(ve_done, 1)
                nc.vector.tensor_reduce(mean[:, :], Wk[:, :, :], AX_X, ALU.add).then_inc(ve_done, 1)
                ve.wait_ge(ve_done, 2)
                nc.vector.tensor_scalar(mean[:, :], mean[:, :], 1.0 / INNER, None, ALU.mult).then_inc(ve_done, 1)
                ve.wait_ge(ve_done, 3)
                nc.vector.tensor_tensor(Wk[:, :, :], Wk[:, :, :], bc(mean[:, :], 2, INNER), ALU.subtract).then_inc(ve_done, 1)
                half = c.mask("half")
                nc.vector.tensor_tensor(kgz[:, :, :], bc(c.cols2("L1_xattn_k_g"), 2, 2), bc(half, 1, PAIRS), ALU.mult).then_inc(ve_done, 1)
                nc.vector.tensor_tensor(s.KB[:, :].rearrange("p (a x) -> p a x", a=PAIRS)[:, :, 0:2],
                                        bc(c.cols2("L1_xattn_k_b"), 2, 2), bc(half, 1, PAIRS), ALU.mult).then_inc(ve_done, 1)
                ve.wait_ge(pe_done, 1)
                nc.vector.tensor_copy(WkcT[:, :, :].rearrange("p (b a) c -> p b (a c)", a=2), c.PS[:, 0:3, :]).then_inc(ve_done, 1)
                ve.wait_ge(ve_done, 7)
                for h in range(HEADS1):
                    nc.vector.tensor_scalar(s.WkgZ[:, h, :], WkcT[:, h // 2, :], kgz[:, h // 2, h % 2:h % 2 + 1], None, ALU.mult)
                ve.wait_ge(pe_done, 2)
                for m in range(KC):
                    op = nc.vector.scalar_tensor_tensor(out=s.Cx[:, m, 0:D], in0=B[3][:, m * D:(m + 1) * D], scalar=1.0 / INNER,
                                                        in1=c.rep("L1_xattn_tab_g"), op0=ALU.mult, op1=ALU.mult)
                op.then_inc(ve_done, 1)
                ve.wait_ge(pe_done, 3)
                nc.vector.tensor_copy(s.Cx[:, :, D:D + 1], B[4][:, 0:KC].unsqueeze(2)).then_inc(ve_done, 1)

            @block.tensor
            def _(te):
                te.wait_ge(ve_done, 4)
                for p in range(PAIRS):
                    for k in range(KC):
                        mm = nc.tensor.transpose(B[p // 2][:, (p % 2) * D + k * P:(p % 2) * D + (k + 1) * P],
                                                 Wk[:, k, p * P:(p + 1) * P], c.ident())
                mm.then_inc(pe_done, 1)
                te.wait_ge(ve_done, 7)
                for m in range(KC):
                    for p in range(PAIRS):
                        mm = nc.tensor.matmul(B[3][:, m * D:(m + 1) * D], WkcT[:, p, m * P:(m + 1) * P], WkcT[:, p, :],
                                              start=(p == 0), stop=(p == PAIRS - 1))
                mm.then_inc(pe_done, 1)
                te.wait_ge(act_done, 1)
                for m in range(KC):
                    for k in range(KC):
                        mm = nc.tensor.matmul(B[4][:, m:m + 1], Cp[:, k, m * P:(m + 1) * P], c.col("L1_xattn_tab_b", k),
                                              start=(k == 0), stop=(k == KC - 1))
                mm.then_inc(pe_done, 1)

            @block.scalar
            def _(sc):
                sc.wait_ge(ve_done, 8)
                nc.scalar.mul(Cp[:, :, :].rearrange("p k n -> p (k n)"), B[3][:, :], 1.0 / INNER).then_inc(act_done, 1)


def prepare_l1_queries(c, s):
    nc = c.nc
    with ExitStack() as ctx:
        sb = lambda name, shape: c.sb(name, shape, ctx)
        xn, xn2, xnT = c.xn, sb("l1q_xn2", [P, HT, D]), sb("l1q_xnT", [P, KC, HN])
        st, mv, rs = sb("l1q_st", [P, HT, 6]), sb("l1q_mv", [P, HT, 2]), sb("l1q_rs", [P, 2 * HT])
        qst = sb("l1q_qst", [P, HT, 2, 6])
        qn = sb("l1q_qn", [P, HT, INNER])
        shift = sb("l1q_shift", [P, HT // 2])
        qbT = sb("l1q_qbT", [HEADS1, HN])
        pairs = lambda n: " ".join(f"{n}{p}" for p in range(PAIRS))
        pe = c.steps(ctx, "l1q_pe", f"xT qA qB {pairs('qT')} qb qbT")
        dve = c.steps(ctx, "l1q_dve", "xT0 stats' moments' norm' 2stats' 2moments' 2norm' "
                      "qstatsA qstatsB 3moments shift qnormA qT0 qT2 qT4 qbT qbt")
        act = c.steps(ctx, "l1q_act", "xT1 qnormB qT1 qT3 qT5")
        pool = c.steps(ctx, "l1q_pool", "vareps' rstd' 2vareps' 2rstd' 3vareps 3rstd")
        B = c.bank
        with nc.Block() as block:
            @block.gpsimd
            def _(gp):
                pool.skip_to(gp, "2vareps", 2)
                rstd_half(c, gp, pool, dve, "2", 0, mv, rs)
                pool.skip_to_end(gp)
                with gp.Fori(0, 2) as i:
                    for pre in ("", "2"):
                        rstd_half(c, gp, pool, dve, pre, i + 1, mv, rs)
                    rstd_half(c, gp, pool, dve, "3", i, mv, rs)

            @block.tensor
            def _(te):
                pe.first_turn(te)
                te.wait_ge(c.loaded["L1_xattn_Wq"], 16)
                with te.Fori(0, 2) as i:
                    te.wait_ge(dve.sem, dve.after("qbt", i - 1))
                    te.wait_ge(dve.sem, dve.after("2norm", i))
                    for t in range(HT):
                        for k in range(KC):
                            mm = nc.tensor.transpose(B[k][:, t * P:(t + 1) * P], xn2[:, t, k * P:(k + 1) * P], c.ident())
                    mm.then_inc(pe.sem, 1)
                    te.wait_ge(dve.sem, dve.after("xT0", i))
                    te.wait_ge(act.sem, act.after("xT1", i))
                    for n in range(2):
                        for t in range(2 * n, 2 * n + 2):
                            for a in range(2):
                                for k in range(KC):
                                    mm = nc.tensor.matmul(B[2 * t + a][:, 0:384], xnT[:, k, t * P:(t + 1) * P],
                                                          c.w["L1_xattn_Wq"][:, k, a * 384:(a + 1) * 384], start=(k == 0), stop=(k == KC - 1))
                        mm.then_inc(pe.sem, 1)
                    te.wait_ge(dve.sem, dve.after("qnormA", i))
                    te.wait_ge(act.sem, act.after("qnormB", i))
                    for p in range(PAIRS):
                        for t in range(HT):
                            mm = nc.tensor.transpose(B[p][:, t * P:(t + 1) * P], qn[:, t, p * P:(p + 1) * P], c.ident())
                        mm.then_inc(pe.sem, 1)
                    te.wait_ge(dve.sem, dve.after("qT4", i))
                    te.wait_ge(act.sem, act.after("qT5", i))
                    for p in range(PAIRS):
                        mm = nc.tensor.matmul(B[6][0:HEADS1, :], s.KB[:, HEADS1 * p:HEADS1 * (p + 1)], s.qT[:, p, bass.ds(i * HN, HN)],
                                              start=(p == 0), stop=(p == PAIRS - 1))
                    mm.then_inc(pe.sem, 1)
                    te.wait_ge(dve.sem, dve.after("qbT", i))
                    te.sem_inc(c.waited)
                    for t in range(HT):
                        mm = nc.tensor.transpose(B[7][:, t * HEADS1:(t + 1) * HEADS1], qbT[:, t * P:(t + 1) * P],
                                                 c.ident()[0:HEADS1, 0:HEADS1])
                    mm.then_inc(pe.sem, 1)

            @block.scalar
            def _(sc):
                act.first_turn(sc)
                with sc.Fori(0, 2) as i:
                    sc.wait_ge(pe.sem, pe.after("xT", i))
                    nc.scalar.activation(xnT[:, 1, :], B[1][:, :], ACT.Identity, scale=c.col("L1_xattn_vid_g", 1),
                                         bias=c.col("L1_xattn_vid_b", 1)).then_inc(act.sem, 1)
                    sc.wait_ge(dve.sem, dve.after("shift", i))
                    for t in (2, 3):
                        op = nc.scalar.activation(qn[:, t, :].rearrange("p (a n) -> p a n", a=2), c.PS[:, 2 * t:2 * t + 2, 0:384],
                                                  ACT.Identity, scale=rs[:, HT + t:HT + t + 1], bias=shift[:, t - 2:t - 1])
                    op.then_inc(act.sem, 1)
                    for p in (1, 3, 5):
                        sc.wait_ge(pe.sem, pe.after(f"qT{p}", i))
                        sc.sem_inc(c.waited)
                        nc.scalar.activation(s.qT[:, p, bass.ds(i * HN, HN)], B[p][:, :], ACT.Identity, scale=c.col("L1_xattn_q_g", p),
                                             bias=c.col("L1_xattn_q_b", p)).then_inc(act.sem, 1)

            @block.vector
            def _(ve):
                def second_norm(i):
                    norm_half(c, ve, dve, pool, "2", i, lambda t: xn[:, t, :], lambda t: xn2[:, t, :], st, mv, rs)

                dve.skip_to(ve, "2stats", 3)
                second_norm(0)
                dve.skip_to_end(ve)
                with ve.Fori(0, 2) as i:
                    ve.wait_ge(pe.sem, pe.after("xT", i))
                    nc.vector.tensor_scalar(xnT[:, 0, :], B[0][:, :], c.col("L1_xattn_vid_g", 0), c.col("L1_xattn_vid_b", 0),
                                            ALU.mult, ALU.add).then_inc(dve.sem, 1)
                    norm_half(c, ve, dve, pool, "", i + 1, half_tiles(c, 1 - i), lambda t: xn[:, t, :], st, mv, rs)
                    ve.wait_ge(dve.sem, dve.after("norm", i + 1))
                    second_norm(i + 1)
                    for n in range(2):
                        ve.wait_ge(pe.sem, pe.after("qA" if n == 0 else "qB", i))
                        for t in range(2 * n, 2 * n + 2):
                            for a in range(2):
                                op = nc.vector.bn_stats(qst[:, t, a, :], B[2 * t + a][:, 0:384])
                        op.then_inc(dve.sem, 1)
                    ve.wait_ge(dve.sem, dve.after("qstatsB", i))
                    ve.sem_inc(c.waited)
                    for t in range(HT):
                        op = nc.vector.bn_aggr(mv[:, t, :], qst[:, t, :, :].rearrange("p a n -> p (a n)"))
                    op.then_inc(dve.sem, 1)
                    ve.wait_ge(pool.sem, pool.after("3rstd", i))
                    nc.vector.scalar_tensor_tensor(out=shift[:, :], in0=mv[:, 2:4, 0:1].rearrange("p t o -> p (t o)"), scalar=-1.0,
                                                   in1=rs[:, HT + 2:HT + 4], op0=ALU.mult, op1=ALU.mult).then_inc(dve.sem, 1)
                    for t in range(2):
                        op = nc.vector.tensor_scalar(qn[:, t, :].rearrange("p (a n) -> p a n", a=2), c.PS[:, 2 * t:2 * t + 2, 0:384],
                                                     mv[:, t, 0:1], rs[:, HT + t:HT + t + 1], ALU.subtract, ALU.mult)
                    op.then_inc(dve.sem, 1)
                    for p in (0, 2, 4):
                        ve.wait_ge(pe.sem, pe.after(f"qT{p}", i))
                        nc.vector.tensor_scalar(s.qT[:, p, bass.ds(i * HN, HN)], B[p][:, :], c.col("L1_xattn_q_g", p),
                                                c.col("L1_xattn_q_b", p), ALU.mult, ALU.add).then_inc(dve.sem, 1)
                    ve.wait_ge(pe.sem, pe.after("qb", i))
                    nc.vector.tensor_copy(qbT[:, :], B[6][0:HEADS1, :]).then_inc(dve.sem, 1)
                    ve.wait_ge(pe.sem, pe.after("qbT", i))
                    nc.vector.tensor_copy(s.qb[:, bass.ds(i * HT, HT), :], B[7][:, 0:HT * HEADS1].rearrange("p (t h) -> p t h", t=HT)).then_inc(dve.sem, 1)


def stage_l1_cross(c):
    nc = c.nc
    with ExitStack() as outer:
        s = type("Shared", (), {})()
        s.WkgZ, s.Cx = c.sb("l1_WkgZ", [P, HEADS1, D], outer), c.sb("l1_Cx", [P, KC, D + 1], outer)
        s.KB = c.sb("l1_KB", [P, PAIRS * 14], outer)
        s.qT, s.qb = c.sb("l1_qT", [P, PAIRS, (NT + 1) * P], outer), c.sb("l1_qb", [P, NT + 1, HEADS1], outer)
        prepare_l1_keys(c, s)
        prepare_l1_queries(c, s)
        ctx = outer
        sb = lambda name, shape: c.sb(name, shape, ctx)
        QT = sb("l1_QT", [P, KC, TB, HEADS1, S])
        UT = sb("l1_UT", [P, KC, HEADS1, P])
        ck, xh = (sb(f"l1_{n}", [P, TB, 2, w]) for n, w in (("ck", D), ("xh", D + 1)))
        kst, kmv, krs = sb("l1_kst", [P, 2, 6]), sb("l1_kmv", [P, 2, 2]), sb("l1_krs", [P, 4])
        cl, xl = sb("l1_cl", [TB, D]), sb("l1_xl", [TB, D + 1])
        lst, lmv, lrs = sb("l1_lst", [TB, 6]), sb("l1_lmv", [TB, 2]), sb("l1_lrs", [TB, 2])
        xlT = sb("l1_xlT", [P, KC, TB])
        kvT = sb("l1_kvT", [P, TB, KC, KEYS])
        junk, junkl = sb("l1_junk", [P, 2, D + 1]), sb("l1_junkl", [TB, D + 1])
        kvar, rk = sb("l1_kvar", [P, 2]), sb("l1_rk", [P, 4])
        lvar, rl = sb("l1_lvar", [TB, 1]), sb("l1_rl", [TB, 2])
        rkB = sb("l1_rkB", [P, KEYS])
        sco = sb("l1_sco", [P, 3, KEYS])
        probs = sb("l1_probs", [P, 3, KEYS])
        qsel, qcol = sb("l1_qsel", [P, TB, 3, 4]), sb("l1_qcol", [P, TB, 3])
        mx, top, nb = sb("l1_mx", [P, 3]), sb("l1_top", [P, 3]), sb("l1_nb", [P, 3])
        total, rinv = sb("l1_total", [P, 3]), sb("l1_rinv", [P, 3])
        plast = [sb(f"l1_plast{j}", [P, 3, TB]) for j in range(TB)]
        probsT, plastT = sb("l1_probsT", [P, 2, 384]), sb("l1_plastT", [TB, 384])
        aT = sb("l1_aT", [P, PAIRS, P])
        J = range(TB)
        pe = c.steps(ctx, "l1_pe", "Z1 pT0 rk1 sc1 xT2 U0 Z2 pT1 rk2 sc2 xT3 U1 Z3 pT2 rk3 sc3 U2 QT0' pT3 U3 QT1' "
                     "V lT' xT0' lZ' qb' Z0' xT1' sc0' rk0' out")
        dve = c.steps(ctx, "l1_dve", "rinv0 norm0 Z1 pT0 plT0 max1 top1 nb1 st3 mo3 no3 rinv1 norm1 U0 Z2 "
                      "pT1 plT1 max2 top2 nb2 st0' mo0' no0' rinv2 norm2 U1 Z3 pT2 plT2 max3 top3 nb3 st1' mo1' no1' rinv3 norm3 U2 "
                      "pT3 plT3 QT0' lst' lmo' U3 lno' st2' mo2' no2' aT lT' lZ' qsel' qcol' Z0' max0' top0' nb0' res")
        act = c.steps(ctx, "l1_act", "ea0 eb0 ec0 pT0 rkB1 kv0_2 kv1_2 ea1 eb1 ec1 U0 pT1 rkB2 kv0_3 kv1_3 ea2 eb2 ec2 U1 "
                      "pT2 rkB3 ea3 eb3 ec3 U2 pT3 U3 QT1' aT kv0_0' kv1_0' kv0_1' kv1_1' rkB0'")
        pool = c.steps(ctx, "l1_pool", "plast0 vz1 rz1 ve3 rs3 plast1 vz2 rz2 ve0' rs0' plast2 vz3 rz3 ve1' rs1' plast3 "
                       "lve' lrs' ve2' rs2' last' lvz' lrz' vz0' rz0'")
        ctx_in, last_in = [c.sem(f"l1_ctx_in{n}", ctx) for n in range(TB)], c.sem("l1_last_in", ctx)
        ready = c.sem("l1_ready", ctx)
        B = c.bank
        ident = c.ident()
        spread = c.mask("spread")
        by_head = lambda b: c.PS[:, b:b + 3, :].rearrange("p k n -> p (k n)").rearrange("p (h b q) -> p h b q", h=HEADS1, b=TB)

        with nc.Block() as block:
            @block.sync
            def _(sp):
                def load_last(t):
                    sp.dma_start(cl[:, :], c.dram["ctx_last"][bass.ds(t * TB, TB)]).then_inc(last_in, 16)

                def load_context(j, t):
                    sp.dma_start(ck[:, j, :, :], c.dram["ctx"][bass.ds(t * TB + j, 1)].rearrange(
                        "b p h d -> p (b h) d")).then_inc(ctx_in[j], 16)

                for j in range(3):
                    load_context(j, 0)
                load_last(0)
                sp.dma_start(*c.w1_load).then_inc(c.loaded["L1_attn_w1"], 16)
                with sp.Fori(0, NT) as i:
                    for j, t in ((0, i + 1), (1, i + 1), (3, i), (2, i + 1)):
                        sp.wait_ge(dve.sem, dve.after(f"no{j}", t - 1))
                        load_context(j, t)
                    sp.wait_ge(dve.sem, dve.after("lno", i))
                    load_last(i + 1)
                    sp.wait_ge(dve.sem, dve.after("res", i))
                    sp.dma_start(c.dram["turned"][bass.ds(i * TB, TB)].rearrange("b s d -> (b s) d"),
                                 c.X[:, bass.ds(i, 1), :].rearrange("p t d -> p (t d)")).then_inc(c.stored_tiles, 16)

            @block.gpsimd
            def _(gp):
                nc.gpsimd.memset(xh[:, :, :, D:D + 1], 1.0).then_inc(ready, 1)
                nc.gpsimd.memset(xl[:, D:D + 1], 1.0).then_inc(ready, 1)
                for j in J:
                    nc.gpsimd.memset(plast[j][:, :, :], 0.0).then_inc(ready, 1)
                gp.wait_ge(ready, 2 + TB)

                def root(i, step, src, tmp, dst, first, second, when):
                    gp.wait_ge(dve.sem, when)
                    n = src.shape[1]
                    nc.gpsimd.tensor_tensor(tmp, src, c.eps[0:src.shape[0], 0:n], ALU.add).then_inc(pool.sem, 1)
                    gp.wait_ge(pool.sem, pool.after(first, i))
                    nc.gpsimd.tensor_tensor(dst, tmp, c.mhalf[0:src.shape[0], 0:n], ALU.pow).then_inc(pool.sem, 1)

                def context_root(j, i):
                    root(i, j, kmv[:, :, 1:2].rearrange("p t o -> p (t o)"), krs[:, 0:2], krs[:, 2:4], f"ve{j}", f"rs{j}",
                         dve.after(f"mo{j}", i))

                def key_root(j, i):
                    root(i, j, kvar[:, :], rk[:, 0:2], rk[:, 2:4], f"vz{j}", f"rz{j}", dve.after(f"Z{j}", i))

                def last_keys(t):
                    gp.wait_ge(dve.sem, dve.after("lT", t))
                    gp.wait_ge(pe.sem, pe.after("sc3", t - 1))
                    gp.sem_inc(c.waited)
                    nc.gpsimd.tensor_copy(kvT[:, :, :, KEYS - 1:KEYS].rearrange("p b k o -> p b (k o)"), xlT[:, :, :].rearrange("p k b -> p b k")).then_inc(pool.sem, 1)
                    root(t, 0, lvar[:, :], rl[:, 0:1], rl[:, 1:2], "lvz", "lrz", dve.after("lZ", t))

                def last_root(t):
                    root(t, 0, lmv[:, 1:2], lrs[:, 0:1], lrs[:, 1:2], "lve", "lrs", dve.after("lmo", t))

                for j in range(2):
                    pool.skip_to(gp, f"ve{j}", 2)
                    context_root(j, 0)
                pool.skip_to(gp, "lve", 9)
                last_root(0)
                context_root(2, 0)
                last_keys(0)
                key_root(0, 0)
                with gp.Fori(0, NT) as i:
                    for j in J:
                        gp.wait_ge(dve.sem, dve.after(f"norm{j}", i))
                        gp.sem_inc(c.waited)
                        nc.gpsimd.tensor_copy(plast[j][:, :, j:j + 1], probs[:, :, KEYS - 1:KEYS]).then_inc(pool.sem, 1)
                        if j < 3:
                            key_root(j + 1, i)
                        if j == 0:
                            context_root(3, i)
                        elif j < 3:
                            context_root(j - 1, i + 1)
                    last_root(i + 1)
                    context_root(2, i + 1)
                    last_keys(i + 1)
                    key_root(0, i + 1)

            @block.tensor
            def _(te):
                for name in ("L1_xattn_Wv", "L1_xattn_Wo"):
                    te.wait_ge(c.loaded[name], 16)
                te.wait_ge(ready, 2 + TB)

                def context_T(j, i):
                    te.wait_ge(dve.sem, dve.after(f"no{j}", i))
                    if j:
                        te.wait_ge(act.sem, act.after(f"kv1_{j-1}", i))
                    if j != 1:
                        te.wait_ge(dve.sem, dve.after(f"plT{j-2}", i) if j else dve.after("plT3", i - 1))
                    for m in range(KC):
                        for h in range(2):
                            mm = nc.tensor.transpose(B[0][:, m * D + h * P:m * D + (h + 1) * P], xh[:, j, h, m * P:(m + 1) * P], ident)
                    mm.then_inc(pe.sem, 1)

                def key_square(j, i):
                    te.wait_ge(act.sem, act.after(f"kv1_{j}", i))
                    te.wait_ge(act.sem, act.after(f"rkB{j-1}", i) if j else act.after("rkB3", i - 1))
                    if j == 0:
                        te.wait_ge(dve.sem, dve.after("lZ", i))
                        te.wait_ge(pool.sem, pool.after("last", i))
                    for h in range(2):
                        for k in range(KC):
                            mm = nc.tensor.matmul(B[1 + h][:, 0:D + 1], kvT[:, j, k, h * P:(h + 1) * P], s.Cx[:, k, :],
                                                  start=(k == 0), stop=(k == KC - 1))
                    mm.then_inc(pe.sem, 1)

                def key_scale(j, i):
                    te.wait_ge(pool.sem, pool.after(f"rz{j}", i))
                    for h in range(2):
                        nc.tensor.matmul(B[1][:, h * P:(h + 1) * P], rk[:, 2 + h:3 + h].to_broadcast([P, P]), ident, start=True, stop=True)
                    nc.tensor.matmul(B[1][:, KEYS - 1:KEYS], rl[:, 1:2].to_broadcast([TB, P]), ident[0:TB, j:j + 1],
                                     start=True, stop=True).then_inc(pe.sem, 1)

                def scores(j, i):
                    if j:
                        te.wait_ge(dve.sem, dve.after(f"max{j-1}", i))
                    else:
                        te.wait_ge(act.sem, act.after("QT1", i))
                    for g in range(3):
                        for k in range(KC):
                            mm = nc.tensor.matmul(B[3 + g][:, 0:KEYS], QT[:, k, j, 4 * g:4 * g + 4, :].rearrange("p h q -> p (h q)"), kvT[:, j, k, :],
                                                  start=(k == 0), stop=(k == KC - 1))
                    mm.then_inc(pe.sem, 1)

                def probs_T(j, i):
                    te.wait_ge(pool.sem, pool.after(f"plast{j}", i))
                    if j:
                        te.wait_ge(act.sem, act.after(f"U{j-1}", i))
                        te.wait_ge(dve.sem, dve.after(f"U{j-1}", i))
                    else:
                        te.wait_ge(dve.sem, dve.after("res", i - 1))
                        te.wait_ge(dve.sem, dve.after("qsel", i))
                    if j < 3:
                        te.wait_ge(act.sem, act.after(f"kv1_{j+1}", i))
                    for g in range(3):
                        for h in range(2):
                            nc.tensor.transpose(B[6 + h][:, g * P:(g + 1) * P], probs[:, g, h * P:(h + 1) * P], ident)
                    for g in range(3):
                        mm = nc.tensor.transpose(B[0][0:TB, g * P:(g + 1) * P], plast[j][:, g, :], ident)
                    mm.then_inc(pe.sem, 1)

                def mixed_context(j, i):
                    te.wait_ge(dve.sem, dve.after(f"plT{j}", i))
                    te.wait_ge(act.sem, act.after(f"pT{j}", i))
                    for m in range(KC):
                        for h in range(2):
                            nc.tensor.matmul(B[6 + m][:, 0:384], xh[:, j, h, m * P:(m + 1) * P], probsT[:, h, :],
                                             start=(h == 0), stop=False)
                        mm = nc.tensor.matmul(B[6 + m][:, 0:384], xl[:, m * P:(m + 1) * P], plastT[:, :], start=False, stop=True)
                    mm.then_inc(pe.sem, 1)

                def heads_queries(m, t):
                    te.wait_ge(dve.sem, dve.after("QT0", t) if m else dve.after("max3", t - 1))
                    for h in range(HEADS1):
                        mm = nc.tensor.matmul(B[3 + h // 4][:, (h % 4) * P:(h % 4 + 1) * P], s.WkgZ[:, h, m * P:(m + 1) * P],
                                              s.qT[:, h // 2, bass.ds(t * P, P)], start=True, stop=True)
                    mm.then_inc(pe.sem, 1)

                def last_keys_T(t):
                    te.wait_ge(dve.sem, dve.after("lno", t))
                    te.sem_inc(c.waited)
                    for m in range(KC):
                        mm = nc.tensor.transpose(B[2][:, m * TB:(m + 1) * TB], xl[:, m * P:(m + 1) * P], ident[0:TB, 0:TB])
                    mm.then_inc(pe.sem, 1)

                def last_keys_square(t):
                    te.wait_ge(dve.sem, dve.after("lT", t))
                    for k in range(KC):
                        mm = nc.tensor.matmul(B[2][0:TB, 0:D + 1], xlT[:, k, :], s.Cx[:, k, :], start=(k == 0), stop=(k == KC - 1))
                    mm.then_inc(pe.sem, 1)

                def queries_bias(t):
                    te.wait_ge(dve.sem, dve.after("aT", t - 1))
                    for j in J:
                        mm = nc.tensor.matmul(B[6][:, j * HEADS1:(j + 1) * HEADS1], spread[:, j * P:(j + 1) * P],
                                              s.qb[:, bass.ds(t, 1), :].rearrange("p t h -> p (t h)"), start=True, stop=True)
                    mm.then_inc(pe.sem, 1)

                def next_contexts(t):
                    last_keys_T(t)
                    context_T(0, t)
                    last_keys_square(t)
                    queries_bias(t)
                    key_square(0, t)
                    context_T(1, t)
                    scores(0, t)
                    key_scale(0, t)

                pe.skip_to(te, "QT0", 1)
                heads_queries(0, 0)
                pe.skip_to(te, "QT1", 1)
                heads_queries(1, 0)
                pe.skip_to(te, "lT", 8)
                next_contexts(0)
                pe.skip_to_end(te)
                with te.Fori(0, NT) as i:
                    key_square(1, i)
                    probs_T(0, i)
                    for j in J:
                        if j < 3:
                            key_scale(j + 1, i)
                            scores(j + 1, i)
                        if j < 2:
                            context_T(j + 2, i)
                        mixed_context(j, i)
                        if j < 2:
                            key_square(j + 2, i)
                        elif j == 2:
                            heads_queries(0, i + 1)
                        if j < 3:
                            probs_T(j + 1, i)
                    heads_queries(1, i + 1)
                    te.wait_ge(act.sem, act.after("U3", i))
                    te.wait_ge(dve.sem, dve.after("U3", i))
                    for h in range(HEADS1):
                        r = slice(64 * (h % 2), 64 * (h % 2) + 64)
                        bank, at = (6, h // 2) if h < 8 else (7, h // 2 - 4)
                        for k in range(KC):
                            mm = nc.tensor.matmul(B[bank][r, at * P:(at + 1) * P], c.w["L1_xattn_Wv"][:, k, h * HD1:(h + 1) * HD1],
                                                  UT[:, k, h, :], start=(k == 0), stop=(k == KC - 1))
                    mm.then_inc(pe.sem, 1)
                    next_contexts(i + 1)
                    te.wait_ge(act.sem, act.after("aT", i))
                    te.wait_ge(dve.sem, dve.after("aT", i))
                    o = B[7][:, D:2 * D]
                    for p in range(PAIRS):
                        nc.tensor.matmul(o, aT[:, p, :], c.w["L1_xattn_Wo"][:, p, :], start=(p == 0), stop=False)
                    nc.tensor.matmul(o, c.ones[0:1, :], c.row("L1_xattn_bo"), start=False, stop=True).then_inc(pe.sem, 1)
            @block.scalar
            def _(sc):
                def context_out(j, i):
                    sc.wait_ge(pe.sem, pe.after(f"xT{j}", i))
                    if j:
                        sc.wait_ge(pe.sem, pe.after(f"sc{j}", i - 1))
                    for m in range(KC):
                        nc.scalar.activation(kvT[:, j, m, 0:D], B[0][:, m * D:(m + 1) * D], ACT.Identity,
                                             scale=c.col("L1_xattn_tab_g", m), bias=c.col("L1_xattn_tab_b", m)).then_inc(act.sem, 1)

                def scale_out(j, i):
                    sc.wait_ge(pe.sem, pe.after(f"rk{j}", i))
                    sc.wait_ge(dve.sem, dve.after(f"max{j-1 if j else 3}", i if j else i - 1))
                    nc.scalar.copy(rkB[:, :], B[1][:, 0:KEYS]).then_inc(act.sem, 1)

                def exps(j, i):
                    sc.wait_ge(dve.sem, dve.after(f"nb{j}", i))
                    sc.wait_ge(pe.sem, pe.after(f"pT{j-1 if j else 3}", i if j else i - 1))
                    for g in range(3):
                        nc.scalar.activation(probs[:, g, :], sco[:, g, :], ACT.Exp, bias=nb[:, g:g + 1],
                                             accum_out=total[:, g:g + 1]).then_inc(act.sem, 1)

                def heads_queries_out(t):
                    sc.wait_ge(pe.sem, pe.after("QT1", t))
                    nc.scalar.copy(QT[:, 1, :, :, :].rearrange("p b h q -> p h b q"), by_head(3)).then_inc(act.sem, 1)

                act.skip_to(sc, "QT1", 1)
                heads_queries_out(0)
                act.skip_to(sc, "kv0_0", 5)
                context_out(0, 0)
                context_out(1, 0)
                scale_out(0, 0)
                with sc.Fori(0, NT) as i:
                    exps(0, i)
                    for j in J:
                        sc.wait_ge(pe.sem, pe.after(f"pT{j}", i))
                        sc.wait_ge(pe.sem, pe.after(f"U{j-1 if j else 3}", i if j else i - 1))
                        nc.scalar.copy(probsT[:, 1, :], B[7][:, 0:384]).then_inc(act.sem, 1)
                        if j < 3:
                            scale_out(j + 1, i)
                        if j < 2:
                            context_out(j + 2, i)
                        if j < 3:
                            exps(j + 1, i)
                        sc.wait_ge(pe.sem, pe.after(f"U{j}", i))
                        nc.scalar.activation(UT[:, 1, :, j * S:(j + 1) * S], B[7][:, 0:384].rearrange("p (h q) -> p h q", h=HEADS1),
                                             ACT.Identity, scale=c.col("L1_xattn_tab_g", 1), bias=c.col("L1_xattn_tab_b", 1)).then_inc(act.sem, 1)
                    heads_queries_out(i + 1)
                    sc.wait_ge(pe.sem, pe.after("V", i))
                    nc.scalar.copy(aT[:, 4:6, :].rearrange("p a n -> p (a n)"), B[7][:, 0:2 * P]).then_inc(act.sem, 1)
                    context_out(0, i + 1)
                    context_out(1, i + 1)
                    scale_out(0, i + 1)

            @block.vector
            def _(ve):
                ve.wait_ge(ready, 2 + TB)

                def context_norm(j, i):
                    ve.wait_ge(ctx_in[j], 16 * (i + 1))
                    for h in range(2):
                        op = nc.vector.bn_stats(kst[:, h, :], ck[:, j, h, :])
                    op.then_inc(dve.sem, 1)
                    ve.wait_ge(dve.sem, dve.after(f"st{j}", i))
                    ve.sem_inc(c.waited)
                    for h in range(2):
                        op = nc.vector.bn_aggr(kmv[:, h, :], kst[:, h, :])
                    op.then_inc(dve.sem, 1)
                    ve.wait_ge(pool.sem, pool.after(f"rs{j}", i))
                    ve.wait_ge(pe.sem, pe.after(f"U{j}", i - 1))
                    for h in range(2):
                        op = nc.vector.tensor_scalar(xh[:, j, h, 0:D], ck[:, j, h, :], kmv[:, h, 0:1], krs[:, 2 + h:3 + h],
                                                     ALU.subtract, ALU.mult)
                    op.then_inc(dve.sem, 1)

                def key_variance(j, i):
                    ve.wait_ge(pe.sem, pe.after(f"Z{j}", i))
                    for h in range(2):
                        op = nc.vector.tensor_tensor_reduce(junk[:, h, :], B[1 + h][:, 0:D + 1], xh[:, j, h, :], 1.0, 0.0,
                                                            ALU.mult, ALU.add, kvar[:, h:h + 1])
                    op.then_inc(dve.sem, 1)

                def row_max(j, i):
                    ve.wait_ge(act.sem, act.after(f"rkB{j}", i))
                    ve.wait_ge(act.sem, act.after(f"ec{j-1 if j else 3}", i if j else i - 1))
                    ve.wait_ge(pe.sem, pe.after(f"sc{j}", i))
                    ve.sem_inc(c.waited)
                    for g in range(3):
                        op = nc.vector.tensor_tensor_reduce(sco[:, g, :], B[3 + g][:, 0:KEYS], rkB[:, :], 1.0, -3.0e38,
                                                            ALU.mult, ALU.max, mx[:, g:g + 1])
                    op.then_inc(dve.sem, 1)
                    ve.wait_ge(dve.sem, dve.after(f"max{j}", i))
                    nc.vector.tensor_tensor(top[:, :], mx[:, :], qcol[:, j, :], ALU.add).then_inc(dve.sem, 1)
                    ve.wait_ge(dve.sem, dve.after(f"top{j}", i))
                    nc.vector.tensor_tensor(nb[:, :], qcol[:, j, :], top[:, :], ALU.subtract).then_inc(dve.sem, 1)

                def normalize(j, i):
                    ve.wait_ge(act.sem, act.after(f"ec{j}", i))
                    nc.vector.reciprocal(rinv[:, :], total[:, :]).then_inc(dve.sem, 1)
                    ve.wait_ge(dve.sem, dve.after(f"rinv{j}", i))
                    for g in range(3):
                        op = nc.vector.tensor_scalar(probs[:, g, :], probs[:, g, :], rinv[:, g:g + 1], None, ALU.mult)
                    op.then_inc(dve.sem, 1)

                def last_stats(t):
                    ve.wait_ge(last_in, 16 * (t + 1))
                    nc.vector.bn_stats(lst[:, :], cl[:, :]).then_inc(dve.sem, 1)
                    ve.wait_ge(dve.sem, dve.after("lst", t))
                    ve.sem_inc(c.waited)
                    nc.vector.bn_aggr(lmv[:, :], lst[:, :]).then_inc(dve.sem, 1)

                def last_norm(t):
                    ve.wait_ge(pool.sem, pool.after("lrs", t))
                    ve.wait_ge(pe.sem, pe.after("U3", t - 1))
                    nc.vector.tensor_scalar(xl[:, 0:D], cl[:, :], lmv[:, 0:1], lrs[:, 1:2], ALU.subtract, ALU.mult).then_inc(dve.sem, 1)

                def last_T(t):
                    ve.wait_ge(pe.sem, pe.after("lT", t))
                    for m in range(KC):
                        op = nc.vector.tensor_scalar(xlT[:, m, :], B[2][:, m * TB:(m + 1) * TB], c.col("L1_xattn_tab_g", m),
                                                     c.col("L1_xattn_tab_b", m), ALU.mult, ALU.add)
                    op.then_inc(dve.sem, 1)

                def last_variance(t):
                    ve.wait_ge(pe.sem, pe.after("lZ", t))
                    nc.vector.tensor_tensor_reduce(junkl[:, :], B[2][0:TB, 0:D + 1], xl[:, :], 1.0, 0.0, ALU.mult, ALU.add,
                                                   lvar[:, :]).then_inc(dve.sem, 1)

                def heads_queries_out(t):
                    ve.wait_ge(pe.sem, pe.after("QT0", t))
                    nc.vector.tensor_copy(QT[:, 0, :, :, :].rearrange("p b h q -> p h b q"), by_head(3)).then_inc(dve.sem, 1)

                def queries_bias_out(t):
                    ve.wait_ge(pe.sem, pe.after("qb", t))
                    nc.vector.tensor_tensor(qsel[:, :, :, :].rearrange("p b g h -> p (b g) h"),
                                            B[6][:, 0:TB * HEADS1].rearrange("p (x h) -> p x h", h=4),
                                            bc(c.hmask[:, :], 1, TB * 3), ALU.mult).then_inc(dve.sem, 1)
                    ve.wait_ge(dve.sem, dve.after("qsel", t))
                    nc.vector.tensor_reduce(qcol[:, :, :].rearrange("p b g -> p (b g)"), qsel[:, :, :, :].rearrange("p b g h -> p (b g) h"),
                                            AX_X, ALU.add).then_inc(dve.sem, 1)

                for j in range(2):
                    dve.skip_to(ve, f"st{j}", 3)
                    context_norm(j, 0)
                dve.skip_to(ve, "QT0", 3)
                heads_queries_out(0)
                last_stats(0)
                def next_contexts(t):
                    last_T(t)
                    last_variance(t)
                    queries_bias_out(t)
                    key_variance(0, t)
                    row_max(0, t)

                dve.skip_to(ve, "lno", 4)
                last_norm(0)
                context_norm(2, 0)
                dve.skip_to(ve, "lT", 8)
                next_contexts(0)
                dve.skip_to_end(ve)
                with ve.Fori(0, NT) as i:
                    normalize(0, i)
                    key_variance(1, i)
                    for j in J:
                        ve.wait_ge(pe.sem, pe.after(f"pT{j}", i))
                        nc.vector.tensor_copy(probsT[:, 0, :], B[6][:, 0:384]).then_inc(dve.sem, 1)
                        nc.vector.tensor_copy(plastT[:, :], B[0][0:TB, 0:384]).then_inc(dve.sem, 1)
                        if j < 3:
                            row_max(j + 1, i)
                            if j == 0:
                                context_norm(3, i)
                            else:
                                context_norm(j - 1, i + 1)
                            normalize(j + 1, i)
                        else:
                            heads_queries_out(i + 1)
                            last_stats(i + 1)
                        ve.wait_ge(pe.sem, pe.after(f"U{j}", i))
                        nc.vector.tensor_scalar(UT[:, 0, :, j * S:(j + 1) * S], B[6][:, 0:384].rearrange("p (h q) -> p h q", h=HEADS1),
                                                c.col("L1_xattn_tab_g", 0), c.col("L1_xattn_tab_b", 0), ALU.mult, ALU.add).then_inc(dve.sem, 1)
                        if j < 2:
                            key_variance(j + 2, i)
                    last_norm(i + 1)
                    context_norm(2, i + 1)
                    ve.wait_ge(pe.sem, pe.after("V", i))
                    nc.vector.tensor_copy(aT[:, 0:4, :].rearrange("p a n -> p (a n)"), B[6][:, :]).then_inc(dve.sem, 1)
                    next_contexts(i + 1)
                    ve.wait_ge(pe.sem, pe.after("out", i))
                    xt = c.X[:, bass.ds(i, 1), :].rearrange("p t d -> p (t d)")
                    nc.vector.tensor_tensor(xt, xt, B[7][:, D:2 * D], ALU.add).then_inc(dve.sem, 1)


LH, LHD, LVD = 16, 8, 16
GRP = 8


def by_column(x, j):
    return x.rearrange("l (u j) d -> j l u d", j=TB)[j]


def stage_l1_linear(c):
    nc = c.nc
    with ExitStack() as ctx:
        sb = lambda name, shape: c.sb(name, shape, ctx)
        xn, xn2, hT, cT = c.xn_late, sb("la_xn2", [P, HT, D]), sb("la_hT", [P, KC, HN]), sb("la_cT", [P, KC, HN])
        st, mv, rs = sb("la_st", [P, HT, 6]), sb("la_mv", [P, HT, 2]), sb("la_rs", [P, 2 * HT])
        Wvr, Wtmp = sb("la_Wvr", [P, KC, 2 * LH]), sb("la_Wtmp", [P, 2 * D])
        qk, m1, m2 = (sb(f"la_{n}", [P, HT, D]) for n in ("qk", "m1", "m2"))
        v, gate = sb("la_v", [P, HT, D]), sb("la_gate", [P, HT, D])
        lg, oh, ow = (sb(f"la_{n}", [P, HT * LH, 2]) for n in ("lg", "oh", "ow"))
        dl, nabs, sc_, own, wq = (sb(f"la_{n}", [P, HT * LH]) for n in ("dl", "nabs", "sc", "own", "wq"))
        qe, ke = sb("la_qe", [P, HT, LH, 2 * LHD]), sb("la_ke", [P, HT, LH, 2 * LHD])
        CH = LH // GRP
        qeT, keT = sb("la_qeT", [P, CH, HN]), sb("la_keT", [P, CH, HN])
        qblk = [sb(f"la_qblk{n}", [P, CH, GRP, P]) for n in range(2)]
        AT = [sb(f"la_AT{n}", [P, LH * P]) for n in range(2)]
        mu, ms, dev = (sb(f"la_{n}", [P, HT * LH]) for n in ("mu", "ms", "dev"))
        ao, y, sq = sb("la_ao", [P, HT, D]), m1, m2
        pT = sb("la_pT", [P, FFP // P, HN])
        u = [sb(f"la_u{n}", [P, HN]) for n in range(2)]
        FC = FFP // P
        T = range(HT)
        mlp = " ".join(f"u{f} w{f}" for f in range(FC))
        pe = c.steps(ctx, "la_pe", "xT lg qkv cnt g T A0a A0b A1a A1b A2a A2b oA A3a A3b oB yT out zT " + mlp + " mlp")
        dve = c.steps(ctx, "la_dve", "h0 h1 c0 c1 c0b c1b lg dl oh0 oh1 nabs one sc ow own rown wq wq2 "
                      "k m1 m2a m2b rope qw qe ke qB0 T v AT0a AT0b AT1a AT1b AT2a AT2b mu0 mus0 d0 AT3a AT3b ms0 mu1 mus1 d1 ms1 "
                      "mse rdev yd yg y0 ao0 ao1 3stats 3moments 3norm z0 z1 stats' moments' norm' 2stats' 2moments' 2norm' "
                      + " ".join(f"p{f}" for f in range(FC)) + " xa res0 res1")
        act = c.steps(ctx, "la_act", "silu e q g T qB1 qB2 qB3 sq0 sq1 dev y1 " + " ".join(f"u{f}" for f in range(FC)))
        pool = c.steps(ctx, "la_pool", "3vareps 3rstd vareps' rstd' 2vareps' 2rstd'")
        turned, wide, folded = (c.sem("la_" + n, ctx) for n in ("turned", "wide", "folded"))
        B = c.bank
        ident, causal = c.ident(), c.mask("causal")
        cos, sin = c.mask("cos"), c.mask("sin")

        with nc.Block() as block:
            @block.sync
            def _(sp):
                sp.wait_ge(c.stored_tiles, 16 * NT)
                for j in range(TB):
                    sp.dma_start(c.X[j * S:(j + 1) * S, 0:NT, :], by_column(c.dram["turned"], j)).then_inc(turned, 16)
                for name, (dst, src) in c.moe_loads.items():
                    sp.dma_start(dst, src).then_inc(c.loaded[name], 16)

            @block.gpsimd
            def _(gp):
                pool.skip_to(gp, "vareps", 4)
                rstd_half(c, gp, pool, dve, "", 0, mv, rs)
                rstd_half(c, gp, pool, dve, "2", 0, mv, rs)
                with gp.Fori(0, 2) as i:
                    rstd_half(c, gp, pool, dve, "3", i, mv, rs)
                    rstd_half(c, gp, pool, dve, "", i + 1, mv, rs)
                    rstd_half(c, gp, pool, dve, "2", i + 1, mv, rs)

            @block.tensor
            def _(te):
                pe.first_turn(te)
                for name in WEIGHTS_L1:
                    te.wait_ge(c.loaded[name], 16)
                te.wait_ge(folded, 3)

                def turn(dst_bank, src):
                    for t in T:
                        for k in range(KC):
                            mm = nc.tensor.transpose(B[dst_bank + k][:, t * P:(t + 1) * P], src[:, t, k * P:(k + 1) * P], ident)
                    mm.then_inc(pe.sem, 1)

                def token_major(out, lhsT, t, w):
                    for k in range(lhsT.shape[1]):
                        mm = nc.tensor.matmul(out, lhsT[:, k, t * P:(t + 1) * P], w[:, k, :], start=(k == 0), stop=(k == lhsT.shape[1] - 1))
                    return mm

                with te.Fori(0, 2) as i:
                    te.wait_ge(dve.sem, dve.after("res1", i - 1))
                    te.wait_ge(dve.sem, dve.after("2norm", i))
                    turn(0, xn2)
                    te.wait_ge(act.sem, act.after("silu", i))
                    for t in T:
                        mm = token_major(B[6][:, t * 2 * LH:(t + 1) * 2 * LH], cT, t, Wvr)
                    mm.then_inc(pe.sem, 1)
                    for t in T:
                        token_major(B[t][:, 0:D], cT, t, c.w["L1_attn_Wqk"])
                        mm = token_major(B[t][:, D:2 * D], cT, t, c.w["L1_attn_Wv"])
                    mm.then_inc(pe.sem, 1)
                    te.wait_ge(dve.sem, dve.after("oh1", i))
                    nc.tensor.matmul(B[7][:, 0:HT * 2 * LH], causal, oh[:, :, :].rearrange("p x r -> p (x r)"),
                                     start=True, stop=True).then_inc(pe.sem, 1)
                    for t in T:
                        mm = token_major(B[4 + t // 2][:, (t % 2) * D:(t % 2 + 1) * D], cT, t, c.w["L1_attn_Wg"])
                    mm.then_inc(pe.sem, 1)
                    te.wait_ge(act.sem, act.after("g", i))
                    te.wait_ge(dve.sem, dve.after("ke", i))
                    for g in range(CH):
                        for t in T:
                            heads = slice(GRP * g, GRP * (g + 1))
                            nc.tensor.transpose(B[6 + g][:, t * P:(t + 1) * P], qe[:, t, heads, :].rearrange("p h x -> p (h x)"), ident)
                            mm = nc.tensor.transpose(B[4 + g][:, t * P:(t + 1) * P], ke[:, t, heads, :].rearrange("p h x -> p (h x)"), ident)
                    mm.then_inc(pe.sem, 1)
                    te.wait_ge(act.sem, act.after("T", i))

                    def weights(t):
                        if t:
                            te.wait_ge(act.sem, act.after(f"qB{t}", i))
                        else:
                            te.wait_ge(dve.sem, dve.after("v", i))
                        for g in range(CH):
                            if t:
                                te.wait_ge(dve.sem, dve.after(f"AT{t-1}{'ab'[g]}", i))
                            for n in range(2):
                                mm = nc.tensor.matmul(B[2 * g + n][:, :], keT[:, g, t * P:(t + 1) * P],
                                                      qblk[t % 2][:, g, 4 * n:4 * n + 4, :].rearrange("p h q -> p (h q)"), start=True, stop=True)
                            mm.then_inc(pe.sem, 1)

                    def outputs(t):
                        te.wait_ge(dve.sem, dve.after(f"AT{t}b", i))
                        for h in range(LH):
                            mm = nc.tensor.matmul(B[4 + t // 2][:, (t % 2) * D + h * LVD:(t % 2) * D + (h + 1) * LVD],
                                                  AT[t % 2][:, h * P:(h + 1) * P], v[:, t, h * LVD:(h + 1) * LVD], start=True, stop=True)
                        if t % 2:
                            mm.then_inc(pe.sem, 1)

                    for t in T:
                        weights(t)
                        if t:
                            outputs(t - 1)
                    outputs(HT - 1)
                    te.wait_ge(dve.sem, dve.after("yg", i))
                    turn(6, y)
                    te.wait_ge(dve.sem, dve.after("y0", i))
                    te.wait_ge(act.sem, act.after("y1", i))
                    for t in T:
                        mm = token_major(B[t // 2][:, (t % 2) * D:(t % 2 + 1) * D], hT, t, c.w["L1_attn_Wout"])
                    mm.then_inc(pe.sem, 1)
                    te.wait_ge(dve.sem, dve.after("3norm", i))
                    turn(2, xn2)
                    te.wait_ge(dve.sem, dve.after("z1", i))
                    for f in range(FC):
                        if f >= 4:
                            te.wait_ge(dve.sem, dve.after(f"p{f-4}", i))
                        for n, name in enumerate(("L1_attn_w1", "L1_attn_w3")):
                            for k in range(KC):
                                mm = nc.tensor.matmul(B[2 * (f % 4) + n][:, :], c.w[name][:, k, f * P:(f + 1) * P], cT[:, k, :],
                                                      start=(k == 0), stop=(k == KC - 1))
                            mm.then_inc(pe.sem, 1)
                    te.wait_ge(dve.sem, dve.after(f"p{FC-1}", i))
                    for t in T:
                        mm = token_major(B[t // 2][:, (t % 2) * D:(t % 2 + 1) * D], pT, t, c.w["L1_attn_w2"])
                    mm.then_inc(pe.sem, 1)

            @block.scalar
            def _(sc):
                act.first_turn(sc)
                with sc.Fori(0, 2) as i:
                    sc.wait_ge(dve.sem, dve.after("c1b", i))
                    nc.scalar.activation(cT[:, :, :], cT[:, :, :], ACT.Silu).then_inc(act.sem, 1)
                    sc.wait_ge(dve.sem, dve.after("nabs", i))
                    nc.scalar.activation(nabs[:, :], nabs[:, :], ACT.Exp).then_inc(act.sem, 1)
                    sc.wait_ge(pe.sem, pe.after("qkv", i))
                    nc.scalar.activation(qk[:, :, 0:P], c.PS[:, 0:HT, 0:P], ACT.Silu).then_inc(act.sem, 1)
                    sc.wait_ge(pe.sem, pe.after("g", i))
                    nc.scalar.activation(gate[:, :, :].rearrange("p (b t) n -> p b (t n)", b=2), c.PS[:, 4:6, :], ACT.Silu).then_inc(act.sem, 1)
                    sc.wait_ge(pe.sem, pe.after("T", i))
                    nc.scalar.copy(keT[:, :, :], c.PS[:, 4:4 + CH, :]).then_inc(act.sem, 1)
                    sc.wait_ge(dve.sem, dve.after("T", i))
                    for t in range(1, HT):
                        if t > 1:
                            sc.wait_ge(pe.sem, pe.after(f"A{t-2}b", i))
                        for r in range(GRP):
                            op = nc.scalar.mul(qblk[t % 2][:, :, r, :], qeT[:, :, t * P:(t + 1) * P], c.qmask[:, r:r + 1])
                        op.then_inc(act.sem, 1)
                    for n in range(2):
                        sc.wait_ge(dve.sem, dve.after(f"d{n}", i))
                        nc.scalar.activation(sq[:, 2 * n:2 * n + 2, :], ao[:, 2 * n:2 * n + 2, :], ACT.Square).then_inc(act.sem, 1)
                    sc.wait_ge(dve.sem, dve.after("mse", i))
                    nc.scalar.activation(dev[:, :], ms[:, :], ACT.Sqrt).then_inc(act.sem, 1)
                    sc.wait_ge(pe.sem, pe.after("yT", i))
                    nc.scalar.copy(hT[:, 1, :], B[7][:, :]).then_inc(act.sem, 1)
                    for f in range(FC):
                        sc.wait_ge(pe.sem, pe.after(f"u{f}", i))
                        if f >= 2:
                            sc.wait_ge(dve.sem, dve.after(f"p{f-2}", i))
                        nc.scalar.activation(u[f % 2][:, :], B[2 * (f % 4)][:, :], ACT.Silu).then_inc(act.sem, 1)

            @block.vector
            def _(ve):
                for n in WEIGHTS_L1:
                    ve.wait_ge(c.loaded[n], 16)
                ve.wait_ge(c.loaded["repeated"], 16)
                for k in range(KC):
                    ve.wait_ge(folded, k)
                    nc.vector.tensor_tensor(Wtmp[:, :].rearrange("p (h r d) -> p h r d", r=2, d=LVD),
                                            bc(c.w["L1_attn_Wv"][:, k, :].rearrange("p (h d) -> p h d", d=LVD), 2, 2),
                                            c.rep("L1_attn_router_w").rearrange("p (h r d) -> p h r d", r=2, d=LVD), ALU.mult).then_inc(wide, 1)
                    ve.wait_ge(wide, k + 1)
                    nc.vector.tensor_reduce(Wvr[:, k, :], Wtmp[:, :].rearrange("p (x d) -> p x d", d=LVD), AX_X, ALU.add).then_inc(folded, 1)
                ve.wait_ge(turned, 16 * TB)
                nc.vector.memset(dl[:, :], 0.0).then_inc(folded, 1)
                ve.wait_ge(folded, 3)

                def norms(i, half):
                    norm_half(c, ve, dve, pool, "", i, half_tiles(c, half), lambda t: xn[:, t, :], st, mv, rs)
                    ve.wait_ge(dve.sem, dve.after("norm", i))
                    norm_half(c, ve, dve, pool, "2", i, lambda t: xn[:, t, :], lambda t: xn2[:, t, :], st, mv, rs)

                dve.skip_to(ve, "stats", 6)
                norms(0, 0)
                dve.skip_to_end(ve)

                def step(op, name, i, wait=True):
                    op.then_inc(dve.sem, 1)
                    if wait:
                        ve.wait_ge(dve.sem, dve.after(name, i))

                with ve.Fori(0, 2) as i:
                    ve.wait_ge(pe.sem, pe.after("xT", i))
                    for k in range(KC):
                        nc.vector.tensor_scalar(hT[:, k, :], B[k][:, :], c.col("L1_attn_ln1_w", k), c.col("L1_attn_ln1_b", k),
                                                ALU.mult, ALU.add).then_inc(dve.sem, 1)
                    ve.wait_ge(dve.sem, dve.after("h1", i))
                    for k in range(KC):
                        nc.vector.tensor_scalar(cT[:, k, :], hT[:, k, :], c.col("conv1", k), None, ALU.mult).then_inc(dve.sem, 1)
                    ve.wait_ge(dve.sem, dve.after("c1", i))
                    for k in range(KC):
                        seq = lambda x: x[:, k, :].rearrange("p (b l) -> p b l", l=S)
                        nc.vector.scalar_tensor_tensor(out=seq(cT)[:, :, 1:S], in0=seq(hT)[:, :, 0:S - 1], scalar=c.col("conv0", k),
                                                       in1=seq(cT)[:, :, 1:S], op0=ALU.mult, op1=ALU.add).then_inc(dve.sem, 1)
                    ve.wait_ge(pe.sem, pe.after("lg", i))
                    step(nc.vector.tensor_copy(lg[:, :, :].rearrange("p x r -> p (x r)"), B[6][:, 0:HT * 2 * LH]), "lg", i)
                    l0, l1 = (lg[:, :, r:r + 1].rearrange("p x r -> p (x r)") for r in range(2))
                    step(nc.vector.tensor_tensor(dl[:, :], l0, l1, ALU.subtract), "dl", i)
                    step(nc.vector.tensor_scalar(oh[:, :, 0:1], dl[:, :].unsqueeze(2), 0.0, None, ALU.is_ge), "oh0", i, False)
                    step(nc.vector.tensor_scalar(oh[:, :, 1:2], dl[:, :].unsqueeze(2), 0.0, None, ALU.is_lt), "oh1", i, False)
                    step(nc.vector.scalar_tensor_tensor(out=nabs[:, :], in0=dl[:, :], scalar=-1.0, in1=dl[:, :],
                                                        op0=ALU.mult, op1=ALU.min), "nabs", i, False)
                    ve.wait_ge(act.sem, act.after("e", i))
                    step(nc.vector.tensor_scalar(nabs[:, :], nabs[:, :], 1.0, None, ALU.add), "one", i)
                    step(nc.vector.reciprocal(sc_[:, :], nabs[:, :]), "sc", i, False)
                    ve.wait_ge(pe.sem, pe.after("cnt", i))
                    step(nc.vector.tensor_tensor(ow[:, :, :].rearrange("p x r -> p (x r)"), B[7][:, 0:HT * 2 * LH],
                                                 oh[:, :, :].rearrange("p x r -> p (x r)"), ALU.mult), "ow", i)
                    step(nc.vector.tensor_tensor(own[:, :].unsqueeze(2), ow[:, :, 0:1], ow[:, :, 1:2], ALU.add), "own", i)
                    step(nc.vector.reciprocal(own[:, :], own[:, :]), "rown", i)
                    step(nc.vector.tensor_tensor(wq[:, :], sc_[:, :], own[:, :], ALU.mult), "wq", i)
                    step(nc.vector.tensor_scalar(wq[:, :], wq[:, :], 4 * float(LHD) ** -0.5, None, ALU.mult), "wq2", i)
                    ve.wait_ge(pe.sem, pe.after("qkv", i))
                    ve.wait_ge(act.sem, act.after("q", i))
                    step(nc.vector.tensor_copy(qk[:, :, P:D], c.PS[:, 0:HT, P:D]), "k", i, False)
                    pair = lambda x: x[:, :, :].rearrange("p t (h two d) -> p (t h) two d", two=2, d=4)
                    X4 = HT * D // 8
                    ve.wait_ge(dve.sem, dve.after("k", i))
                    step(nc.vector.tensor_tensor(pair(m1), pair(qk), cos.unsqueeze(1).unsqueeze(1).to_broadcast([P, X4, 2, 4]), ALU.mult), "m1", i, False)
                    sin3 = bc(sin, 1, X4)
                    step(nc.vector.scalar_tensor_tensor(out=pair(m2)[:, :, 0, :], in0=pair(qk)[:, :, 1, :], scalar=-1.0, in1=sin3,
                                                        op0=ALU.mult, op1=ALU.mult), "m2a", i, False)
                    step(nc.vector.tensor_tensor(pair(m2)[:, :, 1, :], pair(qk)[:, :, 0, :], sin3, ALU.mult), "m2b", i)
                    step(nc.vector.tensor_tensor(qk[:, :, :], m1[:, :, :], m2[:, :, :], ALU.add), "rope", i, False)
                    ve.wait_ge(dve.sem, dve.after("rope", i))
                    head = lambda x: x.rearrange("p t (h d) -> p t h d", d=LHD)
                    step(nc.vector.tensor_tensor(head(m1[:, :, 0:P]), head(qk[:, :, 0:P]),
                                                 bc(wq[:, :].rearrange("p (t h) -> p t h", t=HT), 3, LHD), ALU.mult), "qw", i)
                    for t in T:
                        op = nc.vector.tensor_tensor(qe[:, t, :, :].rearrange("p h (r d) -> p h r d", r=2),
                                                     bc(m1[:, t, 0:P].rearrange("p (h d) -> p h d", d=LHD), 2, 2),
                                                     bc(oh[:, t * LH:(t + 1) * LH, :], 3, LHD), ALU.mult)
                    op.then_inc(dve.sem, 1)
                    for t in T:
                        op = nc.vector.tensor_tensor(ke[:, t, :, :].rearrange("p h (r d) -> p h r d", r=2),
                                                     bc(qk[:, t, P:D].rearrange("p (h d) -> p h d", d=LHD), 2, 2),
                                                     bc(oh[:, t * LH:(t + 1) * LH, :], 3, LHD), ALU.mult)
                    op.then_inc(dve.sem, 1)
                    ve.wait_ge(pe.sem, pe.after("T", i))
                    step(nc.vector.tensor_tensor(qblk[0][:, :, :, :], bc(c.PS[:, 6:6 + CH, 0:P], 2, GRP),
                                                 c.qmask.unsqueeze(1).unsqueeze(3).to_broadcast([P, CH, GRP, P]), ALU.mult), "qB0", i, False)
                    step(nc.vector.tensor_copy(qeT[:, :, :], c.PS[:, 6:6 + CH, :]), "T", i, False)
                    step(nc.vector.tensor_copy(v[:, :, :], c.PS[:, 0:HT, D:2 * D]), "v", i, False)
                    heads = lambda x: x.rearrange("p (x d) -> p x d", d=LVD)
                    two = lambda x, n: x[:, 2 * n:2 * n + 2, :].rearrange("p t n -> p (t n)")
                    of = lambda n: slice(2 * LH * n, 2 * LH * (n + 1))

                    def centre(n):
                        ve.wait_ge(pe.sem, pe.after("oB" if n else "oA", i))
                        step(nc.vector.tensor_reduce(mu[:, of(n)], heads(B[4 + n][:, :]), AX_X, ALU.add), f"mu{n}", i)
                        step(nc.vector.tensor_scalar(mu[:, of(n)], mu[:, of(n)], 1.0 / LVD, None, ALU.mult), f"mus{n}", i)
                        step(nc.vector.tensor_tensor(heads(two(ao, n)), heads(B[4 + n][:, :]), bc(mu[:, of(n)], 2, LVD), ALU.subtract), f"d{n}", i, False)

                    def squares(n):
                        ve.wait_ge(act.sem, act.after(f"sq{n}", i))
                        step(nc.vector.tensor_reduce(ms[:, of(n)], heads(two(sq, n)), AX_X, ALU.add), f"ms{n}", i, n == 1)

                    for t in T:
                        if t == HT - 1:
                            centre(0)
                        for g in range(CH):
                            half = "ab"[g]
                            ve.wait_ge(pe.sem, pe.after(f"A{t}{half}", i))
                            step(nc.vector.tensor_tensor(AT[t % 2][:, g * GRP * P:(g + 1) * GRP * P].rearrange("p (x n) -> p x n", n=P),
                                                         c.PS[:, 2 * g:2 * g + 2, :].rearrange("p b n -> p (b n)").rearrange("p (x n) -> p x n", n=P),
                                                         bc(causal, 1, GRP), ALU.mult), f"AT{t}{half}", i, False)
                    squares(0)
                    centre(1)
                    squares(1)
                    step(nc.vector.tensor_scalar(ms[:, :], ms[:, :], 1.0 / LVD, EPS, ALU.mult, ALU.add), "mse", i, False)
                    ve.wait_ge(act.sem, act.after("dev", i))
                    step(nc.vector.reciprocal(dev[:, :], dev[:, :]), "rdev", i)
                    step(nc.vector.tensor_tensor(heads(y[:, :, :].rearrange("p t n -> p (t n)")), heads(ao[:, :, :].rearrange("p t n -> p (t n)")),
                                                 bc(dev[:, :], 2, LVD), ALU.mult), "yd", i)
                    step(nc.vector.tensor_tensor(y[:, :, :], y[:, :, :], gate[:, :, :], ALU.mult), "yg", i, False)
                    ve.wait_ge(pe.sem, pe.after("yT", i))
                    step(nc.vector.tensor_copy(hT[:, 0, :], B[6][:, :]), "y0", i, False)
                    ve.wait_ge(pe.sem, pe.after("out", i))
                    for n in range(2):
                        step(nc.vector.tensor_tensor(ao[:, 2 * n:2 * n + 2, :].rearrange("p t n -> p (t n)"), B[n][:, :],
                                                     xn[:, 2 * n:2 * n + 2, :].rearrange("p t n -> p (t n)"), ALU.add), f"ao{n}", i)
                    norm_half(c, ve, dve, pool, "3", i, lambda t: ao[:, t, :], lambda t: xn2[:, t, :], st, mv, rs)
                    ve.wait_ge(pe.sem, pe.after("zT", i))
                    for k in range(KC):
                        step(nc.vector.tensor_scalar(cT[:, k, :], B[2 + k][:, :], c.col("L1_attn_ln2_w", k), c.col("L1_attn_ln2_b", k),
                                                     ALU.mult, ALU.add), f"z{k}", i, False)
                    ve.wait_ge(dve.sem, dve.after("res1", i - 1))
                    norms(i + 1, 1 - i)
                    for f in range(FC):
                        ve.wait_ge(pe.sem, pe.after(f"w{f}", i))
                        ve.wait_ge(act.sem, act.after(f"u{f}", i))
                        step(nc.vector.tensor_tensor(pT[:, f, :], u[f % 2][:, :], B[2 * (f % 4) + 1][:, :], ALU.mult), f"p{f}", i, False)
                    xx = c.X[:, bass.ds(i * HT, HT), :]
                    step(nc.vector.tensor_tensor(xx, xx, ao[:, :, :], ALU.add), "xa", i)
                    ve.wait_ge(pe.sem, pe.after("mlp", i))
                    for n in range(2):
                        xx = c.X[:, bass.ds(i * HT + 2 * n, 2), :]
                        step(nc.vector.tensor_tensor(xx, xx, B[n][:, :].rearrange("p (t n) -> p t n", t=2), ALU.add), f"res{n}", i, False)


def stage_moe(c):
    nc = c.nc
    with ExitStack() as ctx:
        sb = lambda name, shape: c.sb(name, shape, ctx)
        xn, xnT = c.xn_late, sb("mo_xnT", [P, KC, HN])
        st, mv, rs = sb("mo_st", [P, HT, 6]), sb("mo_mv", [P, HT, 2]), sb("mo_rs", [P, 2 * HT])
        fT = sb("mo_fT", [P, KC, TB, S])
        sco = sb("mo_sco", [P, NE])
        more, same, rank = sb("mo_more", [P, NE, NE]), sb("mo_same", [P, NE, NE]), sb("mo_rank", [P, NE])
        G, GT, bias2 = sb("mo_G", [P, NE]), sb("mo_GT", [NE, P]), sb("mo_bias2", [P, D])
        hT = [sb(f"mo_hT{n}", [P, KC, HN]) for n in range(2)]
        E = range(NE)
        pe = c.steps(ctx, "mo_pe", "xT h0 " + " ".join((f"h{e+1} " if e < NE - 1 else "") + f"o{e}" for e in E))
        dve = c.steps(ctx, "mo_dve", "xT0 bias stats' moments' norm' " + " ".join(f"a{e} b{e}" for e in E))
        act = c.steps(ctx, "mo_act", "xT1 " + " ".join(f"h{e}" for e in E))
        pool = c.steps(ctx, "mo_pool", "vareps' rstd'")
        rv, rp = (c.sem("mo_route_" + n, ctx) for n in ("dve", "pe"))
        B = c.bank
        ident = c.ident()

        with nc.Block() as block:
            @block.gpsimd
            def _(gp):
                pool.first_turn(gp)
                with gp.Fori(0, 2) as i:
                    rstd_half(c, gp, pool, dve, "", i + 1, mv, rs)

            @block.tensor
            def _(te):
                pe.first_turn(te)
                for name in c.moe_loads:
                    te.wait_ge(c.loaded[name], 16)
                te.wait_ge(dve.sem, dve.after("norm", 0))
                for k in range(KC):
                    mm = nc.tensor.transpose(B[0][:, k * P:(k + 1) * P], xn[:, 0, k * P:(k + 1) * P], ident)
                mm.then_inc(rp, 1)
                te.wait_ge(rv, 1)
                for k in range(KC):
                    nc.tensor.matmul(B[1][:, 0:NE], fT[:, k, :, :].rearrange("p b s -> p (b s)"), c.Wr[:, k, :], start=(k == 0), stop=False)
                nc.tensor.matmul(B[1][:, 0:NE], c.ones[0:1, :], c.row("L1_ffn_br"), start=False, stop=True).then_inc(rp, 1)
                te.wait_ge(rv, 8)
                nc.tensor.transpose(B[2][0:NE, 0:P], G[:, :], ident).then_inc(rp, 1)
                te.wait_ge(rv, 9)
                nc.tensor.matmul(B[3][:, 0:D], GT[:, :], c.moe_b2[:, :], start=True, stop=True).then_inc(rp, 1)
                te.wait_ge(rv, 10)

                def hidden(e, i):
                    if e >= 2:
                        te.wait_ge(act.sem, act.after(f"h{e-2}", i))
                    for m in range(KC):
                        for k in range(KC):
                            mm = nc.tensor.matmul(B[2 * (e % 2) + m][:, :], c.moe_W1[:, KC * e + k, m * P:(m + 1) * P], xnT[:, k, :],
                                                  start=(k == 0), stop=(k == KC - 1))
                    mm.then_inc(pe.sem, 1)

                with te.Fori(0, 2) as i:
                    te.wait_ge(act.sem, act.after(f"h{NE-1}", i - 1))
                    te.wait_ge(dve.sem, dve.after("norm", i))
                    for t in range(HT):
                        for k in range(KC):
                            mm = nc.tensor.transpose(B[k][:, t * P:(t + 1) * P], xn[:, t, k * P:(k + 1) * P], ident)
                    mm.then_inc(pe.sem, 1)
                    te.wait_ge(dve.sem, dve.after("xT0", i))
                    te.wait_ge(act.sem, act.after("xT1", i))
                    hidden(0, i)
                    for e in E:
                        if e < NE - 1:
                            hidden(e + 1, i)
                        te.wait_ge(act.sem, act.after(f"h{e}", i))
                        te.wait_ge(dve.sem, dve.after(f"b{e-2}", i) if e >= 2 else dve.after(f"b{e+NE-2}", i - 1))
                        for t in range(HT):
                            for k in range(KC):
                                mm = nc.tensor.matmul(B[4 + 2 * (e % 2) + t // 2][:, (t % 2) * D:(t % 2 + 1) * D],
                                                      hT[e % 2][:, k, t * P:(t + 1) * P], c.moe_W2[:, KC * e + k, :],
                                                      start=(k == 0), stop=(k == KC - 1))
                        mm.then_inc(pe.sem, 1)

            @block.scalar
            def _(sc):
                act.first_turn(sc)
                with sc.Fori(0, 2) as i:
                    sc.wait_ge(pe.sem, pe.after("xT", i))
                    nc.scalar.copy(xnT[:, 1, :], B[1][:, :]).then_inc(act.sem, 1)
                    for e in E:
                        sc.wait_ge(pe.sem, pe.after(f"h{e}", i))
                        sc.wait_ge(pe.sem, pe.after(f"o{e-2}", i) if e >= 2 else pe.after(f"o{e+NE-2}", i - 1))
                        for m in range(KC):
                            op = nc.scalar.activation(hT[e % 2][:, m, :], B[2 * (e % 2) + m][:, :], ACT.Gelu,
                                                      bias=c.col("L1_ffn_b1", KC * e + m))
                        op.then_inc(act.sem, 1)

            @block.vector
            def _(ve):
                dve.first_turn(ve)
                ve.wait_ge(rp, 1)
                nc.vector.tensor_copy(fT[:, :, :, :], bc(B[0][:, 0:D].rearrange("p (k n) -> p k n", k=KC)[:, :, 0:S], 2, TB)).then_inc(rv, 1)
                ve.wait_ge(rp, 2)
                nc.vector.tensor_copy(sco[:, :], B[1][:, 0:NE]).then_inc(rv, 1)
                ve.wait_ge(rv, 2)
                other, self_ = bc(sco[:, :], 1, NE), bc(sco[:, :], 2, NE)
                nc.vector.tensor_tensor(more[:, :, :], other, self_, ALU.is_gt).then_inc(rv, 1)
                nc.vector.tensor_tensor(same[:, :, :], other, self_, ALU.is_equal).then_inc(rv, 1)
                ve.wait_ge(rv, 4)
                nc.vector.tensor_tensor(same[:, :, :], same[:, :, :], c.mask("earlier").rearrange("p (e j) -> p e j", e=NE), ALU.mult).then_inc(rv, 1)
                ve.wait_ge(rv, 5)
                nc.vector.tensor_tensor(more[:, :, :], more[:, :, :], same[:, :, :], ALU.add).then_inc(rv, 1)
                ve.wait_ge(rv, 6)
                nc.vector.tensor_reduce(rank[:, :], more[:, :, :], AX_X, ALU.add).then_inc(rv, 1)
                ve.wait_ge(rv, 7)
                nc.vector.tensor_scalar(G[:, :], rank[:, :], 2.0, 0.5, ALU.is_lt, ALU.mult).then_inc(rv, 1)
                ve.wait_ge(rp, 3)
                nc.vector.tensor_copy(GT[:, :], B[2][0:NE, 0:P]).then_inc(rv, 1)
                ve.wait_ge(rp, 4)
                nc.vector.tensor_copy(bias2[:, :], B[3][:, 0:D]).then_inc(rv, 1)
                ve.wait_ge(rv, 10)
                with ve.Fori(0, 2) as i:
                    ve.wait_ge(pe.sem, pe.after("xT", i))
                    nc.vector.tensor_copy(xnT[:, 0, :], B[0][:, :]).then_inc(dve.sem, 1)
                    xx = c.X[:, bass.ds(i * HT, HT), :]
                    nc.vector.tensor_tensor(xx, xx, bc(bias2[:, :], 1, HT), ALU.add).then_inc(dve.sem, 1)
                    ve.wait_ge(dve.sem, dve.after("bias", i))
                    ve.wait_ge(dve.sem, dve.after(f"b{NE-1}", i - 1))
                    norm_half(c, ve, dve, pool, "", i + 1, half_tiles(c, 1 - i), lambda t: xn[:, t, :], st, mv, rs)
                    for e in E:
                        ve.wait_ge(pe.sem, pe.after(f"o{e}", i))
                        if e:
                            ve.wait_ge(dve.sem, dve.after(f"b{e-1}", i))
                        for n in range(2):
                            xx = c.X[:, bass.ds(i * HT + 2 * n, 2), :]
                            nc.vector.scalar_tensor_tensor(out=xx, in0=B[4 + 2 * (e % 2) + n][:, :].rearrange("p (t n) -> p t n", t=2),
                                                           scalar=G[:, e:e + 1], in1=xx, op0=ALU.mult, op1=ALU.add).then_inc(dve.sem, 1)


def build(nc, dram):
    with ExitStack() as ctx:
        c = Core(nc, ctx, dram)
        stage_l0_cross(c)
        stage_l0_gla(c)
        stage_l0_ffn(c)
        c.l0.close()
        stage_l1_cross(c)
        c.cross.close()
        c.allocate_experts()
        stage_l1_linear(c)
        stage_moe(c)
        stored = c.sem("stored")
        with nc.Block() as block:
            @block.sync
            def _(sp):
                for j in range(TB):
                    sp.dma_start(by_column(dram["out"], j), c.X[j * S:(j + 1) * S, 0:NT, :]).then_inc(stored, 16)
                sp.wait_ge(stored, 16 * TB)


def masks():
    p = np.arange(P)
    inv_freq = 1.0 / np.float32(10000.0) ** (np.arange(0, 4, dtype=np.float32) * np.float32(2.0) / np.float32(8.0))
    angles = (p[:, None] % S).astype(np.float32) * inv_freq.astype(np.float32)[None]
    m = {
        "ident": np.eye(P),
        "fold": p[:, None] % S == np.arange(S),
        "hmask": p[:, None] // S == np.arange(4),
        "qmask": (p[:, None] // 16 == np.arange(8)) * 0.25,
        "causal": (p[:, None] // S == p // S) & (p[:, None] <= p),
        "spread": np.concatenate([p[:, None] == b * S + p % S for b in range(TB)], axis=1),
        "half": (p[:, None] // 64 == np.arange(2)) * 0.125,
        "cos": np.cos(angles), "sin": np.sin(angles),
        "earlier": np.broadcast_to((np.arange(NE)[None, :] < np.arange(NE)[:, None]).reshape(1, -1), (P, NE * NE)),
    }
    return np.concatenate([m[n].astype(np.float32) for n in MASKS], axis=1)


def kernel(**inputs):
    import concourse.bacc as _bacc
    from concourse.bass_utils import run_bass_kernel_spmd as _run

    a = {n: np.asarray(v) for n, v in inputs.items()}
    ctx = a["ctx_1024"]
    a["conv0"], a["conv1"] = a["L1_attn_conv_w"].T
    a["L1_attn_router_w"] = a["L1_attn_router_w"].transpose(0, 2, 1)
    a["L1_attn_Wqk"] = np.concatenate([a["L1_attn_Wq"], a["L1_attn_Wk"]], axis=1)
    for n in ("L1_attn_w1", "L1_attn_w3"):
        a[n] = np.pad(a[n], ((0, 0), (0, FFP - FF)))
    a["L1_attn_w2"] = np.pad(a["L1_attn_w2"], ((0, FFP - FF), (0, 0)))
    a["moe_W1"], a["moe_W2"] = a["L1_ffn_W1"].reshape(NE * D, D), a["L1_ffn_W2"].reshape(NE * D, D)
    arrays = {
        "x": a["x"].reshape(NT, P, D).transpose(1, 0, 2),
        "ctxT": np.pad(ctx.transpose(0, 2, 1), ((0, TB), (0, 0), (0, 0))),
        "ctx_lastT": ctx[:, KEYS - 1].T,
        "masks": masks(),
        "cols": np.concatenate([a[n].reshape(-1, P).T for n in COLS], axis=1),
        "repeated": np.broadcast_to(np.concatenate([a[n].reshape(-1) for n in REPEATED]), (P, REP_N)),
        "ctx": np.pad(ctx[:, 0:KEYS - 1].reshape(NB, 2, P, D).transpose(0, 2, 1, 3), ((0, TB), (0, 0), (0, 0), (0, 0))),
        "ctx_last": np.pad(ctx[:, KEYS - 1], ((0, TB), (0, 0))),
        "W_exp": a["L0_ffn_W_exp"],
        "W_conT": a["L0_ffn_W_con"].T,
        "b_exp": a["L0_ffn_b_exp"][None],
        "bf_weights": np.concatenate([w.reshape(STAGES_BF, F0 // 2, 4).transpose(0, 2, 1) for w in
                                      (a["L0_ffn_up_weights"], a["L0_ffn_down_weights"][::-1])]),
        "L0_attn_Wgk2": a["L0_attn_Wgk2"],
        "rows": np.concatenate([a[n] for n in ROWS])[None],
    }
    arrays["moe_b2"], arrays["L1_ffn_Wr"] = a["L1_ffn_b2"], a["L1_ffn_Wr"]
    arrays["moe_W1"], arrays["moe_W2"] = a["moe_W1"], a["moe_W2"]
    for n in (*WEIGHTS_L0, *WEIGHTS_CROSS, *WEIGHTS_L1):
        arrays[n] = a[n].T if n.startswith("L0_xattn") else a[n]
    nc = _bacc.Bacc("TRN2", target_bir_lowering=False, num_devices=1)
    dram, feed = {}, {}
    for n, v in arrays.items():
        feed["in_" + n] = np.ascontiguousarray(v)
        dram[n] = nc.dram_tensor("in_" + n, v.shape, F32, kind="ExternalInput").ap()
    dram["turned"] = nc.dram_tensor("turned", (NB, S, D), F32, kind="Internal").ap()
    dram["out"] = nc.dram_tensor("out_0", (NB, S, D), F32, kind="ExternalOutput").ap()
    build(nc, dram)
    r = _run(nc, [feed], core_ids=[0])
    return r.results[0]["out_0"]
```
